# Optimizing a Trainium2 kernel written in Bass

```python
import numpy as np
import jax
import jax.numpy as jnp

def _softmax(x, axis=-1):
    return jax.nn.softmax(x, axis=axis)

def _gelu(x):
    return jax.nn.gelu(x, approximate=True)

def _silu(x):
    return jax.nn.silu(x)

def _sigmoid(x):
    return jax.nn.sigmoid(x)

def _layernorm(x, axis=-1, eps=1e-05):
    m = jnp.mean(x, axis=axis, keepdims=True)
    v = jnp.var(x, axis=axis, keepdims=True)
    return (x - m) / jnp.sqrt(v + eps)

def _scatter_add(tgt, idx, src, axis=0):
    return tgt.at[idx].add(src)

def _segment_sum(src, seg, n):
    return jax.ops.segment_sum(src, seg, n)
kernel_name = 'mk_seq_preln_d4_jaxref_r8_ba65c3'

def setup_inputs(seed: int=0):
    np.random.seed(seed)
    _w = jnp.asarray

    def _L0_attn_setup():
        import jax, jax.numpy as jnp
        import numpy as np
        EMBED_DIM = 128
        NUM_HEADS = 16
        HEAD_DIM = EMBED_DIM // NUM_HEADS
        NUM_LANDMARKS = 64
        REG = 1e-06
        BATCH = 2
        SEQ = 1024

        def _sq_dists(X, L):
            Xn = jnp.sum(X * X, axis=-1, keepdims=True)
            Ln = jnp.sum(L * L, axis=-1, keepdims=True)
            XL = jnp.einsum('bhnd,bhkd->bhnk', X, L)
            return jnp.maximum(Xn + jnp.swapaxes(Ln, -2, -1) - 2.0 * XL, 0.0)
        key = jax.random.key(seed)
        ks = jax.random.split(key, 10)
        s = 0.02
        inp = {'query': jax.random.normal(ks[0], (BATCH, SEQ, EMBED_DIM), dtype=jnp.float32), 'Wq': jax.random.normal(ks[1], (EMBED_DIM, EMBED_DIM), dtype=jnp.float32) * s, 'bq': jnp.zeros((EMBED_DIM,), jnp.float32), 'Wk': jax.random.normal(ks[2], (EMBED_DIM, EMBED_DIM), dtype=jnp.float32) * s, 'bk': jnp.zeros((EMBED_DIM,), jnp.float32), 'Wv': jax.random.normal(ks[3], (EMBED_DIM, EMBED_DIM), dtype=jnp.float32) * s, 'bv': jnp.zeros((EMBED_DIM,), jnp.float32), 'Wo': jax.random.normal(ks[4], (EMBED_DIM, EMBED_DIM), dtype=jnp.float32) * s, 'bo': jnp.zeros((EMBED_DIM,), jnp.float32), 'temperature': jnp.asarray(float(HEAD_DIM), jnp.float32), 'landmark_idx': jnp.arange(NUM_LANDMARKS, dtype=jnp.int32) * (SEQ // NUM_LANDMARKS)}
        return inp
    _L0_attn_in = _L0_attn_setup()

    def _L0_ffn_setup():
        import jax, jax.numpy as jnp
        import numpy as np
        TOPK = 2
        CAPACITY_FACTOR = 1.0
        EPS = 1e-06
        B, S, D = (4, 512, 128)
        E = 8
        SUB_H = 256 // E
        key = jax.random.key(seed)
        ks = jax.random.split(key, 7)
        x = jax.random.normal(ks[0], (B, S, D), dtype=jnp.float32)
        w_gate_w = jax.random.normal(ks[1], (D, E), dtype=jnp.float32) * 0.02
        w_gate_b = jnp.zeros((E,), jnp.float32)
        W1 = jax.random.normal(ks[2], (E, D, SUB_H), dtype=jnp.float32) * 0.02
        b1 = jnp.zeros((E, SUB_H), jnp.float32)
        W2 = jax.random.normal(ks[3], (E, SUB_H, D), dtype=jnp.float32) * 0.02
        b2 = jnp.zeros((E, D), jnp.float32)
        return {'x': x, 'w_gate_w': w_gate_w, 'w_gate_b': w_gate_b, 'W1': W1, 'b1': b1, 'W2': W2, 'b2': b2}
    _L0_ffn_in = _L0_ffn_setup()

    def _L1_attn_setup():
        import jax, jax.numpy as jnp
        import numpy as np
        D = 128
        H = 16
        G = 4
        HD = D // H
        HPG = H // G
        THETA = 10000.0
        EPS = 1e-10

        def _l2_qk_norm(t):
            return t / (jnp.sqrt(jnp.sum(t * t, axis=-1, keepdims=True)) + EPS)

        def _rope(t):
            T = t.shape[1]
            half = HD // 2
            inv_freq = 1.0 / THETA ** (jnp.arange(half, dtype=jnp.float32) / half)
            ang = jnp.arange(T, dtype=jnp.float32)[:, None] * inv_freq[None, :]
            cos = jnp.cos(ang)[None, :, None, :]
            sin = jnp.sin(ang)[None, :, None, :]
            x1, x2 = (t[..., :half], t[..., half:])
            return jnp.concatenate([x1 * cos - x2 * sin, x2 * cos + x1 * sin], axis=-1)
        key = jax.random.key(seed)
        k1, k2, k3 = jax.random.split(key, 3)
        x = jax.random.normal(k1, (1, 512, D), jnp.float32)
        w_qkv = jax.random.normal(k2, (D, H * HD + 2 * G * HD), jnp.float32) * 0.02
        w_o = jax.random.normal(k3, (D, D), jnp.float32) * 0.02
        return {'x': x, 'w_qkv': w_qkv, 'w_o': w_o}
    _L1_attn_in = _L1_attn_setup()

    def _L1_ffn_setup():
        import jax, jax.numpy as jnp
        import numpy as np
        D = 128
        E = 12
        HS = 2 * D
        HR = 3 * D
        TAU = 1.5

        def _geglu(h):
            a, g = jnp.split(h, 2, axis=-1)
            return a * jax.nn.gelu(g, approximate=False)
        key = jax.random.key(seed)
        ks = jax.random.split(key, 12)

        def xavier(k, shape):
            fan_in, fan_out = (shape[-2], shape[-1])
            lim = jnp.sqrt(6.0 / (fan_in + fan_out))
            return jax.random.uniform(k, shape, jnp.float32, -lim, lim)
        x = jax.random.normal(ks[0], (2, 128, D), jnp.float32)
        Ws1 = xavier(ks[1], (D, 2 * HS))
        bs1 = jnp.zeros((2 * HS,), jnp.float32)
        Ws2 = xavier(ks[2], (HS, D))
        bs2 = jnp.zeros((D,), jnp.float32)
        We1 = xavier(ks[3], (E, D, 2 * HR))
        be1 = jnp.zeros((E, 2 * HR), jnp.float32)
        We2 = xavier(ks[4], (E, HR, D))
        be2 = jnp.zeros((E, D), jnp.float32)
        Wr = xavier(ks[5], (D, E))
        br = jnp.zeros((E,), jnp.float32)
        return {'x': x, 'Ws1': Ws1, 'bs1': bs1, 'Ws2': Ws2, 'bs2': bs2, 'We1': We1, 'be1': be1, 'We2': We2, 'be2': be2, 'Wr': Wr, 'br': br}
    _L1_ffn_in = _L1_ffn_setup()

    def _L2_attn_setup():
        import jax, jax.numpy as jnp
        import numpy as np
        D = 128
        H = 4
        HD = D // H
        K = 4
        EPS = 1e-06

        def _dwconv_silu(x, w):
            xc = jnp.transpose(x, (0, 2, 1))
            xp = jnp.pad(xc, ((0, 0), (0, 0), (K - 1, 0)))
            y = jax.lax.conv_general_dilated(xp, w, window_strides=(1,), padding='VALID', dimension_numbers=('NCH', 'OIH', 'NCH'), feature_group_count=D)
            return jax.nn.silu(jnp.transpose(y, (0, 2, 1)))

        def _l2norm(x):
            n = jnp.sqrt(jnp.sum(x * x, axis=-1, keepdims=True))
            return x / jnp.maximum(n, EPS)

        def _rmsnorm(x):
            ms = jnp.mean(x * x, axis=-1, keepdims=True)
            return x * jax.lax.rsqrt(ms + EPS)

        def _forward(x, W_in, W_ctrl, b_ctrl, w_q, w_k, w_v, W_out, b_out, ramp_logit):
            B, S, _ = x.shape
            qkv = jnp.einsum('bsd,de->bse', x, W_in)
            q_in, k_in, v_in = jnp.split(qkv, [D, 2 * D], axis=-1)
            ctrl = jnp.einsum('bsd,de->bse', x, W_ctrl) + b_ctrl
            alpha_in = ctrl[..., :H]
            beta_in = ctrl[..., H:2 * H]
            og_in = ctrl[..., 2 * H:]
            q = _l2norm(_dwconv_silu(q_in, w_q).reshape(B, S, H, HD))
            k = _l2norm(_dwconv_silu(k_in, w_k).reshape(B, S, H, HD))
            v = _dwconv_silu(v_in, w_v).reshape(B, S, H, HD)
            alpha = jax.nn.sigmoid(alpha_in) * 0.98 + 0.01
            beta = jax.nn.sigmoid(beta_in)
            og = jax.nn.sigmoid(og_in)
            ramp = jax.nn.sigmoid(ramp_logit)

            def step(state, inp):
                qt, kt, vt, at, bt, ot = inp
                old = jnp.einsum('bhvk,bhk->bhv', state, kt)
                erase = jnp.einsum('bhv,bhk->bhvk', old, kt)
                write = jnp.einsum('bhv,bhk->bhvk', vt, kt)
                a4 = at[:, :, None, None]
                b4 = bt[:, :, None, None]
                state = a4 * (state - b4 * erase) + b4 * write
                read = jnp.einsum('bhvk,bhk->bhv', state, qt)
                read = _rmsnorm(read).reshape(B, D)
                out = ot * (read @ W_out + b_out) * ramp
                return (state, out)
            state0 = jnp.zeros((B, H, HD, HD), x.dtype)
            xs = (jnp.swapaxes(q, 0, 1), jnp.swapaxes(k, 0, 1), jnp.swapaxes(v, 0, 1), jnp.swapaxes(alpha, 0, 1), jnp.swapaxes(beta, 0, 1), jnp.swapaxes(og, 0, 1))
            final_state, outs = jax.lax.scan(step, state0, xs)
            return (jnp.swapaxes(outs, 0, 1), final_state)

        def _reference_tuple_inner(x, W_in, W_ctrl, b_ctrl, w_q, w_k, w_v, W_out, b_out, ramp_logit):
            return _forward(x, W_in, W_ctrl, b_ctrl, w_q, w_k, w_v, W_out, b_out, ramp_logit)
        key = jax.random.key(seed)
        ks = jax.random.split(key, 6)
        x = jax.random.normal(ks[0], (4, 256, D), dtype=jnp.float32)
        W_in = jax.random.normal(ks[1], (D, 3 * D), dtype=jnp.float32) * 0.02
        W_ctrl = jax.random.normal(ks[2], (D, 2 * H + D), dtype=jnp.float32) * 0.02
        b_ctrl = jnp.concatenate([jnp.full((H,), 1.5, jnp.float32), jnp.full((H,), -2.0, jnp.float32), jnp.full((D,), -1.5, jnp.float32)])
        wconv = np.zeros((D, 1, K), dtype=np.float32)
        wconv[:, 0, -1] = 1.0
        w_q = jnp.asarray(wconv)
        w_k = jnp.asarray(wconv)
        w_v = jnp.asarray(wconv)
        lim = 0.1 * np.sqrt(6.0 / (D + D))
        W_out = jax.random.uniform(ks[3], (D, D), jnp.float32, -lim, lim)
        b_out = jnp.zeros((D,), jnp.float32)
        ramp_logit = jnp.full((D,), -2.1972246, jnp.float32)
        return {'x': x, 'W_in': W_in, 'W_ctrl': W_ctrl, 'b_ctrl': b_ctrl, 'w_q': w_q, 'w_k': w_k, 'w_v': w_v, 'W_out': W_out, 'b_out': b_out, 'ramp_logit': ramp_logit}
    _L2_attn_in = _L2_attn_setup()

    def _L2_ffn_setup():
        import jax, jax.numpy as jnp
        import numpy as np
        E = 8
        K = 2
        CF = 1.25
        key = jax.random.key(seed)
        kx, kr, kg, ku, kd = jax.random.split(key, 5)
        D, F = (128, 512)
        x = jax.random.normal(kx, (4, 256, D), dtype=jnp.float32)
        router_w = 0.02 * jax.random.normal(kr, (E, D), dtype=jnp.float32)
        wg = jax.random.normal(kg, (E, D, F), dtype=jnp.float32) / np.sqrt(D)
        wu = jax.random.normal(ku, (E, D, F), dtype=jnp.float32) / np.sqrt(D)
        wd = jax.random.normal(kd, (E, F, D), dtype=jnp.float32) / np.sqrt(F)
        return {'x': x, 'router_w': router_w, 'wg': wg, 'wu': wu, 'wd': wd}
    _L2_ffn_in = _L2_ffn_setup()

    def _L3_attn_setup():
        import math
        import jax, jax.numpy as jnp
        import numpy as np
        B, T, D_MODEL, N_HEADS = (2, 256, 128, 16)
        HEAD_DIM = D_MODEL // N_HEADS

        def _alibi_slopes(n_heads: int) -> np.ndarray:

            def pow2(n):
                start = 2.0 ** (-(8.0 / n))
                return [start * start ** i for i in range(n)]
            if math.log2(n_heads).is_integer():
                s = pow2(n_heads)
            else:
                cp = 2 ** math.floor(math.log2(n_heads))
                base = pow2(cp)
                extra = pow2(2 * cp)[1::2]
                s = base + extra[:n_heads - cp]
            return np.asarray(s, dtype=np.float32)
        SLOPES = jnp.asarray(_alibi_slopes(N_HEADS))
        key = jax.random.key(seed)
        k1, k2, k3 = jax.random.split(key, 3)
        x = jax.random.normal(k1, (B, T, D_MODEL), dtype=jnp.float32)
        Wqkv = jax.random.normal(k2, (D_MODEL, 3 * D_MODEL), dtype=jnp.float32) * 0.02
        Wout = jax.random.normal(k3, (D_MODEL, D_MODEL), dtype=jnp.float32) * 0.02
        return {'x': x, 'Wqkv': Wqkv, 'Wout': Wout}
    _L3_attn_in = _L3_attn_setup()

    def _L3_ffn_setup():
        import jax, jax.numpy as jnp
        import numpy as np
        SWIGLU_ALPHA = 1.702
        SWIGLU_LIMIT = 7.0
        TOP_K = 4
        key = jax.random.key(seed)
        k = jax.random.split(key, 5)
        B, S, D, E, I = (2, 128, 128, 8, 256)
        return {'hidden_states': jax.random.normal(k[0], (B, S, D), dtype=jnp.float32), 'router_weight': jax.random.normal(k[1], (E, D), dtype=jnp.float32) * 0.02, 'router_bias': jnp.zeros((E,), dtype=jnp.float32), 'gate_up_proj': jax.random.normal(k[2], (E, 2 * I, D), dtype=jnp.float32) * 0.02, 'gate_up_proj_bias': jnp.zeros((E, 2 * I), dtype=jnp.float32), 'down_proj': jax.random.normal(k[3], (E, D, I), dtype=jnp.float32) * 0.02, 'down_proj_bias': jnp.zeros((E, D), dtype=jnp.float32)}
    _L3_ffn_in = _L3_ffn_setup()
    _d = {'L0_attn_query': _L0_attn_in['query'], 'L0_attn_Wq': _L0_attn_in['Wq'], 'L0_attn_bq': _L0_attn_in['bq'], 'L0_attn_Wk': _L0_attn_in['Wk'], 'L0_attn_bk': _L0_attn_in['bk'], 'L0_attn_Wv': _L0_attn_in['Wv'], 'L0_attn_bv': _L0_attn_in['bv'], 'L0_attn_Wo': _L0_attn_in['Wo'], 'L0_attn_bo': _L0_attn_in['bo'], 'L0_attn_temperature': _L0_attn_in['temperature'], 'L0_attn_landmark_idx': _L0_attn_in['landmark_idx'], 'L0_ffn_w_gate_w': _L0_ffn_in['w_gate_w'], 'L0_ffn_w_gate_b': _L0_ffn_in['w_gate_b'], 'L0_ffn_W1': _L0_ffn_in['W1'], 'L0_ffn_b1': _L0_ffn_in['b1'], 'L0_ffn_W2': _L0_ffn_in['W2'], 'L0_ffn_b2': _L0_ffn_in['b2'], 'L1_attn_w_qkv': _L1_attn_in['w_qkv'], 'L1_attn_w_o': _L1_attn_in['w_o'], 'L1_ffn_Ws1': _L1_ffn_in['Ws1'], 'L1_ffn_bs1': _L1_ffn_in['bs1'], 'L1_ffn_Ws2': _L1_ffn_in['Ws2'], 'L1_ffn_bs2': _L1_ffn_in['bs2'], 'L1_ffn_We1': _L1_ffn_in['We1'], 'L1_ffn_be1': _L1_ffn_in['be1'], 'L1_ffn_We2': _L1_ffn_in['We2'], 'L1_ffn_be2': _L1_ffn_in['be2'], 'L1_ffn_Wr': _L1_ffn_in['Wr'], 'L1_ffn_br': _L1_ffn_in['br'], 'L2_attn_W_in': _L2_attn_in['W_in'], 'L2_attn_W_ctrl': _L2_attn_in['W_ctrl'], 'L2_attn_b_ctrl': _L2_attn_in['b_ctrl'], 'L2_attn_w_q': _L2_attn_in['w_q'], 'L2_attn_w_k': _L2_attn_in['w_k'], 'L2_attn_w_v': _L2_attn_in['w_v'], 'L2_attn_W_out': _L2_attn_in['W_out'], 'L2_attn_b_out': _L2_attn_in['b_out'], 'L2_attn_ramp_logit': _L2_attn_in['ramp_logit'], 'L2_ffn_router_w': _L2_ffn_in['router_w'], 'L2_ffn_wg': _L2_ffn_in['wg'], 'L2_ffn_wu': _L2_ffn_in['wu'], 'L2_ffn_wd': _L2_ffn_in['wd'], 'L3_attn_Wqkv': _L3_attn_in['Wqkv'], 'L3_attn_Wout': _L3_attn_in['Wout'], 'L3_ffn_router_weight': _L3_ffn_in['router_weight'], 'L3_ffn_router_bias': _L3_ffn_in['router_bias'], 'L3_ffn_gate_up_proj': _L3_ffn_in['gate_up_proj'], 'L3_ffn_gate_up_proj_bias': _L3_ffn_in['gate_up_proj_bias'], 'L3_ffn_down_proj': _L3_ffn_in['down_proj'], 'L3_ffn_down_proj_bias': _L3_ffn_in['down_proj_bias']}
    _x0 = _d['L0_attn_query']
    _d['L0_attn_query'] = jax.random.normal(jax.random.fold_in(jax.random.key(seed), 1), (8, 512, 128), dtype=_x0.dtype)
    del _x0
    return _d

def reference(L0_attn_query, L0_attn_Wq, L0_attn_bq, L0_attn_Wk, L0_attn_bk, L0_attn_Wv, L0_attn_bv, L0_attn_Wo, L0_attn_bo, L0_attn_temperature, L0_attn_landmark_idx, L0_ffn_w_gate_w, L0_ffn_w_gate_b, L0_ffn_W1, L0_ffn_b1, L0_ffn_W2, L0_ffn_b2, L1_attn_w_qkv, L1_attn_w_o, L1_ffn_Ws1, L1_ffn_bs1, L1_ffn_Ws2, L1_ffn_bs2, L1_ffn_We1, L1_ffn_be1, L1_ffn_We2, L1_ffn_be2, L1_ffn_Wr, L1_ffn_br, L2_attn_W_in, L2_attn_W_ctrl, L2_attn_b_ctrl, L2_attn_w_q, L2_attn_w_k, L2_attn_w_v, L2_attn_W_out, L2_attn_b_out, L2_attn_ramp_logit, L2_ffn_router_w, L2_ffn_wg, L2_ffn_wu, L2_ffn_wd, L3_attn_Wqkv, L3_attn_Wout, L3_ffn_router_weight, L3_ffn_router_bias, L3_ffn_gate_up_proj, L3_ffn_gate_up_proj_bias, L3_ffn_down_proj, L3_ffn_down_proj_bias):

    def _L0_attn_ref(query, Wq, bq, Wk, bk, Wv, bv, Wo, bo, temperature, landmark_idx):
        import jax, jax.numpy as jnp
        import numpy as np
        EMBED_DIM = 128
        NUM_HEADS = 16
        HEAD_DIM = EMBED_DIM // NUM_HEADS
        NUM_LANDMARKS = 64
        REG = 1e-06
        BATCH = 2
        SEQ = 1024

        def _sq_dists(X, L):
            Xn = jnp.sum(X * X, axis=-1, keepdims=True)
            Ln = jnp.sum(L * L, axis=-1, keepdims=True)
            XL = jnp.einsum('bhnd,bhkd->bhnk', X, L)
            return jnp.maximum(Xn + jnp.swapaxes(Ln, -2, -1) - 2.0 * XL, 0.0)
        b, n, _ = query.shape
        Q = (query @ Wq.T + bq).reshape(b, n, NUM_HEADS, HEAD_DIM).transpose(0, 2, 1, 3)
        K = (query @ Wk.T + bk).reshape(b, n, NUM_HEADS, HEAD_DIM).transpose(0, 2, 1, 3)
        V = (query @ Wv.T + bv).reshape(b, n, NUM_HEADS, HEAD_DIM).transpose(0, 2, 1, 3)
        landmarks = K[:, :, landmark_idx, :]
        C_Q = _sq_dists(Q, landmarks)
        C_K = _sq_dists(K, landmarks)
        W_sq = C_K[:, :, landmark_idx, :]
        Phi_Q = jnp.exp(-C_Q / temperature)
        Phi_K = jnp.exp(-C_K / temperature)
        W_kernel = jnp.exp(-W_sq / temperature) + REG * jnp.eye(NUM_LANDMARKS, dtype=query.dtype)
        Z = jnp.einsum('bhnk,bhnd->bhkd', Phi_K, V)
        Y = jnp.linalg.solve(W_kernel, Z)
        out_unnorm = jnp.einsum('bhnk,bhkd->bhnd', Phi_Q, Y)
        Phi_K_sum = jnp.sum(Phi_K, axis=-2)[..., None]
        norm = jnp.einsum('bhnk,bhko->bhno', Phi_Q, jnp.linalg.solve(W_kernel, Phi_K_sum))
        norm = jnp.maximum(norm, 1e-10)
        out = out_unnorm / norm
        out = out.transpose(0, 2, 1, 3).reshape(b, n, EMBED_DIM)
        return out @ Wo.T + bo

    def _L0_ffn_ref(x, w_gate_w, w_gate_b, W1, b1, W2, b2):
        import jax, jax.numpy as jnp
        import numpy as np
        TOPK = 2
        CAPACITY_FACTOR = 1.0
        EPS = 1e-06
        B, S, D = (4, 512, 128)
        E = 8
        SUB_H = 256 // E
        Bx, Sx, Dx = x.shape
        Ex = w_gate_b.shape[0]
        K = Sx // 2
        capacity = int(CAPACITY_FACTOR * Bx)
        gate_scores = jax.nn.softmax(x @ w_gate_w + w_gate_b, axis=-1)
        _, top_idx = jax.lax.top_k(gate_scores, TOPK)
        mask = jax.nn.one_hot(top_idx, Ex, dtype=gate_scores.dtype).sum(axis=-2)
        masked = gate_scores * mask
        denom = masked.sum(axis=0, keepdims=True) + EPS
        route = masked / denom * capacity
        route_eb = jnp.transpose(route, (2, 0, 1))
        _, seq_ids = jax.lax.top_k(route_eb, K)
        seq_ids = jnp.sort(seq_ids, axis=-1)
        xg = jax.vmap(lambda idx: jnp.take_along_axis(x, idx[..., None], axis=1))(seq_ids)
        h = jnp.einsum('ebkd,edh->ebkh', xg, W1) + b1[:, None, None, :]
        h = jax.nn.gelu(h, approximate=False)
        o = jnp.einsum('ebkh,ehd->ebkd', h, W2) + b2[:, None, None, :]
        flat_ids = (jnp.arange(Bx)[None, :, None] * Sx + seq_ids).reshape(-1)
        outs = jnp.zeros((Bx * Sx, Dx), x.dtype).at[flat_ids].add(o.reshape(-1, Dx))
        return outs.reshape(Bx, Sx, Dx)

    def _L1_attn_ref(x, w_qkv, w_o):
        import jax, jax.numpy as jnp
        import numpy as np
        D = 128
        H = 16
        G = 4
        HD = D // H
        HPG = H // G
        THETA = 10000.0
        EPS = 1e-10

        def _l2_qk_norm(t):
            return t / (jnp.sqrt(jnp.sum(t * t, axis=-1, keepdims=True)) + EPS)

        def _rope(t):
            T = t.shape[1]
            half = HD // 2
            inv_freq = 1.0 / THETA ** (jnp.arange(half, dtype=jnp.float32) / half)
            ang = jnp.arange(T, dtype=jnp.float32)[:, None] * inv_freq[None, :]
            cos = jnp.cos(ang)[None, :, None, :]
            sin = jnp.sin(ang)[None, :, None, :]
            x1, x2 = (t[..., :half], t[..., half:])
            return jnp.concatenate([x1 * cos - x2 * sin, x2 * cos + x1 * sin], axis=-1)
        B, T, _ = x.shape
        qkv = x @ w_qkv
        q, k, v = jnp.split(qkv, [H * HD, H * HD + G * HD], axis=-1)
        q = q.reshape(B, T, H, HD)
        k = k.reshape(B, T, G, HD)
        v = v.reshape(B, T, G, HD)
        q = _l2_qk_norm(q)
        k = _l2_qk_norm(k)
        q = _rope(q)
        k = _rope(k)
        k = jnp.repeat(k, HPG, axis=2)
        v = jnp.repeat(v, HPG, axis=2)
        q = jnp.transpose(q, (0, 2, 1, 3))
        k = jnp.transpose(k, (0, 2, 1, 3))
        v = jnp.transpose(v, (0, 2, 1, 3))
        scale = 1.0 / np.sqrt(HD).astype(np.float32)
        scores = jnp.einsum('bhqd,bhkd->bhqk', q, k) * scale
        causal = jnp.tril(jnp.ones((T, T), dtype=bool))
        scores = jnp.where(causal[None, None], scores, jnp.float32(-1e+30))
        attn = jax.nn.softmax(scores, axis=-1)
        out = jnp.einsum('bhqk,bhkd->bhqd', attn, v)
        out = jnp.transpose(out, (0, 2, 1, 3)).reshape(B, T, H * HD)
        return out @ w_o

    def _L1_ffn_ref(x, Ws1, bs1, Ws2, bs2, We1, be1, We2, be2, Wr, br):
        import jax, jax.numpy as jnp
        import numpy as np
        D = 128
        E = 12
        HS = 2 * D
        HR = 3 * D
        TAU = 1.5

        def _geglu(h):
            a, g = jnp.split(h, 2, axis=-1)
            return a * jax.nn.gelu(g, approximate=False)
        B, T, Dm = x.shape
        xf = x.reshape(-1, Dm)
        ys = _geglu(xf @ Ws1 + bs1) @ Ws2 + bs2
        logits = (xf @ Wr + br) / TAU
        top_val, top_idx = jax.lax.top_k(logits, 2)
        top_w = jax.nn.softmax(top_val, axis=-1)
        onehot = jax.nn.one_hot(top_idx, E, dtype=x.dtype)
        w = jnp.einsum('nke,nk->ne', onehot, top_w)
        h = jnp.einsum('nd,edh->enh', xf, We1) + be1[:, None, :]
        act = _geglu(h)
        yE = jnp.einsum('enh,ehd->end', act, We2) + be2[:, None, :]
        yr = jnp.einsum('end,ne->nd', yE, w)
        return (ys + yr).reshape(B, T, Dm)

    def _L2_attn_ref(x, W_in, W_ctrl, b_ctrl, w_q, w_k, w_v, W_out, b_out, ramp_logit):
        import jax, jax.numpy as jnp
        import numpy as np
        D = 128
        H = 4
        HD = D // H
        K = 4
        EPS = 1e-06

        def _dwconv_silu(x, w):
            xc = jnp.transpose(x, (0, 2, 1))
            xp = jnp.pad(xc, ((0, 0), (0, 0), (K - 1, 0)))
            y = jax.lax.conv_general_dilated(xp, w, window_strides=(1,), padding='VALID', dimension_numbers=('NCH', 'OIH', 'NCH'), feature_group_count=D)
            return jax.nn.silu(jnp.transpose(y, (0, 2, 1)))

        def _l2norm(x):
            n = jnp.sqrt(jnp.sum(x * x, axis=-1, keepdims=True))
            return x / jnp.maximum(n, EPS)

        def _rmsnorm(x):
            ms = jnp.mean(x * x, axis=-1, keepdims=True)
            return x * jax.lax.rsqrt(ms + EPS)

        def _forward(x, W_in, W_ctrl, b_ctrl, w_q, w_k, w_v, W_out, b_out, ramp_logit):
            B, S, _ = x.shape
            qkv = jnp.einsum('bsd,de->bse', x, W_in)
            q_in, k_in, v_in = jnp.split(qkv, [D, 2 * D], axis=-1)
            ctrl = jnp.einsum('bsd,de->bse', x, W_ctrl) + b_ctrl
            alpha_in = ctrl[..., :H]
            beta_in = ctrl[..., H:2 * H]
            og_in = ctrl[..., 2 * H:]
            q = _l2norm(_dwconv_silu(q_in, w_q).reshape(B, S, H, HD))
            k = _l2norm(_dwconv_silu(k_in, w_k).reshape(B, S, H, HD))
            v = _dwconv_silu(v_in, w_v).reshape(B, S, H, HD)
            alpha = jax.nn.sigmoid(alpha_in) * 0.98 + 0.01
            beta = jax.nn.sigmoid(beta_in)
            og = jax.nn.sigmoid(og_in)
            ramp = jax.nn.sigmoid(ramp_logit)

            def step(state, inp):
                qt, kt, vt, at, bt, ot = inp
                old = jnp.einsum('bhvk,bhk->bhv', state, kt)
                erase = jnp.einsum('bhv,bhk->bhvk', old, kt)
                write = jnp.einsum('bhv,bhk->bhvk', vt, kt)
                a4 = at[:, :, None, None]
                b4 = bt[:, :, None, None]
                state = a4 * (state - b4 * erase) + b4 * write
                read = jnp.einsum('bhvk,bhk->bhv', state, qt)
                read = _rmsnorm(read).reshape(B, D)
                out = ot * (read @ W_out + b_out) * ramp
                return (state, out)
            state0 = jnp.zeros((B, H, HD, HD), x.dtype)
            xs = (jnp.swapaxes(q, 0, 1), jnp.swapaxes(k, 0, 1), jnp.swapaxes(v, 0, 1), jnp.swapaxes(alpha, 0, 1), jnp.swapaxes(beta, 0, 1), jnp.swapaxes(og, 0, 1))
            final_state, outs = jax.lax.scan(step, state0, xs)
            return (jnp.swapaxes(outs, 0, 1), final_state)

        def _reference_tuple_inner(x, W_in, W_ctrl, b_ctrl, w_q, w_k, w_v, W_out, b_out, ramp_logit):
            return _forward(x, W_in, W_ctrl, b_ctrl, w_q, w_k, w_v, W_out, b_out, ramp_logit)
        return _reference_tuple_inner(x, W_in, W_ctrl, b_ctrl, w_q, w_k, w_v, W_out, b_out, ramp_logit)[0]

    def _L2_ffn_ref(x, router_w, wg, wu, wd):
        import jax, jax.numpy as jnp
        import numpy as np
        E = 8
        K = 2
        CF = 1.25
        B, L, D = x.shape
        xf = x.reshape(-1, D)
        N = xf.shape[0]
        capacity = max(1, int(CF * N / E))
        logits = xf @ router_w.T
        probs = jax.nn.softmax(logits, axis=-1)
        topw, topi = jax.lax.top_k(probs, K)
        topw = topw / (topw.sum(-1, keepdims=True) + 1e-06)
        fe = topi.reshape(-1)
        fw = topw.reshape(-1)
        ft = jnp.repeat(jnp.arange(N), K)
        order = jnp.lexsort((-fw, fe))
        se, sw, st = (fe[order], fw[order], ft[order])
        counts = jax.ops.segment_sum(jnp.ones_like(se), se, num_segments=E)
        starts = jnp.cumsum(counts) - counts
        rank = jnp.arange(N * K) - starts[se]
        keep = rank < capacity
        pos = jnp.where(keep, rank, capacity)
        disp = jnp.zeros((E, capacity + 1, D), x.dtype).at[se, pos].set(xf[st])
        disp = disp[:, :capacity]
        g = jnp.einsum('ecd,edf->ecf', disp, wg)
        u = jnp.einsum('ecd,edf->ecf', disp, wu)
        eo = jnp.einsum('ecf,efd->ecd', jax.nn.silu(g) * u, wd)
        gathered = eo[se, jnp.minimum(pos, capacity - 1)]
        contrib = gathered * (sw * keep.astype(x.dtype))[:, None]
        out = jnp.zeros_like(xf).at[st].add(contrib)
        return out.reshape(B, L, D)

    def _L3_attn_ref(x, Wqkv, Wout):
        import math
        import jax, jax.numpy as jnp
        import numpy as np
        B, T, D_MODEL, N_HEADS = (2, 256, 128, 16)
        HEAD_DIM = D_MODEL // N_HEADS

        def _alibi_slopes(n_heads: int) -> np.ndarray:

            def pow2(n):
                start = 2.0 ** (-(8.0 / n))
                return [start * start ** i for i in range(n)]
            if math.log2(n_heads).is_integer():
                s = pow2(n_heads)
            else:
                cp = 2 ** math.floor(math.log2(n_heads))
                base = pow2(cp)
                extra = pow2(2 * cp)[1::2]
                s = base + extra[:n_heads - cp]
            return np.asarray(s, dtype=np.float32)
        SLOPES = jnp.asarray(_alibi_slopes(N_HEADS))
        Bc, Tc, Dc = x.shape
        qkv = x @ Wqkv
        q, k, v = jnp.split(qkv, 3, axis=-1)
        q = q.reshape(Bc, Tc, N_HEADS, HEAD_DIM)
        k = k.reshape(Bc, Tc, N_HEADS, HEAD_DIM)
        v = v.reshape(Bc, Tc, N_HEADS, HEAD_DIM)
        scale = 1.0 / math.sqrt(HEAD_DIM)
        logits = jnp.einsum('bihd,bjhd->bhij', q, k) * scale
        pos = jnp.arange(Tc, dtype=jnp.float32)
        rel = pos[None, :] - pos[:, None]
        logits = logits + SLOPES[None, :, None, None] * rel[None, None, :, :]
        causal = pos[:, None] >= pos[None, :]
        logits = jnp.where(causal[None, None, :, :], logits, -jnp.inf)
        attn = jax.nn.softmax(logits, axis=-1)
        out = jnp.einsum('bhij,bjhd->bihd', attn, v).reshape(Bc, Tc, Dc)
        return out @ Wout

    def _L3_ffn_ref(hidden_states, router_weight, router_bias, gate_up_proj, gate_up_proj_bias, down_proj, down_proj_bias):
        import jax, jax.numpy as jnp
        import numpy as np
        SWIGLU_ALPHA = 1.702
        SWIGLU_LIMIT = 7.0
        TOP_K = 4
        B, S, D = hidden_states.shape
        E = router_weight.shape[0]
        x = hidden_states.reshape(-1, D)
        N = x.shape[0]
        logits = x @ router_weight.T + router_bias
        topk_logits, topk_idx = jax.lax.top_k(logits, TOP_K)
        topk_w = jax.nn.softmax(topk_logits.astype(jnp.float32), axis=-1)
        combine = jnp.zeros((N, E), dtype=jnp.float32)
        combine = combine.at[jnp.arange(N)[:, None], topk_idx].set(topk_w)
        gate_up = jnp.einsum('nd,ejd->nej', x, gate_up_proj) + gate_up_proj_bias
        gate, up = jnp.split(gate_up, 2, axis=-1)
        gate = jnp.minimum(gate, SWIGLU_LIMIT)
        up = jnp.clip(up, -SWIGLU_LIMIT, SWIGLU_LIMIT)
        act = (up + 1.0) * gate * jax.nn.sigmoid(SWIGLU_ALPHA * gate)
        out = jnp.einsum('nei,edi->ned', act, down_proj) + down_proj_bias
        y = jnp.einsum('ned,ne->nd', out, combine.astype(out.dtype))
        return y.reshape(B, S, D)
    x = L0_attn_query
    x = x + _L0_attn_ref(_layernorm(x, axis=-1), L0_attn_Wq, L0_attn_bq, L0_attn_Wk, L0_attn_bk, L0_attn_Wv, L0_attn_bv, L0_attn_Wo, L0_attn_bo, L0_attn_temperature, L0_attn_landmark_idx)
    x = x + _L0_ffn_ref(_layernorm(x, axis=-1), L0_ffn_w_gate_w, L0_ffn_w_gate_b, L0_ffn_W1, L0_ffn_b1, L0_ffn_W2, L0_ffn_b2)
    x = x + _L1_attn_ref(_layernorm(x, axis=-1), L1_attn_w_qkv, L1_attn_w_o)
    x = x + _L1_ffn_ref(_layernorm(x, axis=-1), L1_ffn_Ws1, L1_ffn_bs1, L1_ffn_Ws2, L1_ffn_bs2, L1_ffn_We1, L1_ffn_be1, L1_ffn_We2, L1_ffn_be2, L1_ffn_Wr, L1_ffn_br)
    x = x + _L2_attn_ref(_layernorm(x, axis=-1), L2_attn_W_in, L2_attn_W_ctrl, L2_attn_b_ctrl, L2_attn_w_q, L2_attn_w_k, L2_attn_w_v, L2_attn_W_out, L2_attn_b_out, L2_attn_ramp_logit)
    x = x + _L2_ffn_ref(_layernorm(x, axis=-1), L2_ffn_router_w, L2_ffn_wg, L2_ffn_wu, L2_ffn_wd)
    x = x + _L3_attn_ref(_layernorm(x, axis=-1), L3_attn_Wqkv, L3_attn_Wout)
    x = x + _L3_ffn_ref(_layernorm(x, axis=-1), L3_ffn_router_weight, L3_ffn_router_bias, L3_ffn_gate_up_proj, L3_ffn_gate_up_proj_bias, L3_ffn_down_proj, L3_ffn_down_proj_bias)
    return x

_drawn_inputs = setup_inputs


def setup_inputs(seed=0):
    import zlib

    import numpy as np

    out = dict(_drawn_inputs(seed))
    spreads = {'L0_attn_bq': (0.0, 0.8),
     'L0_attn_bk': (0.0, 0.753),
     'L0_attn_bv': (0.0, 0.1),
     'L0_attn_bo': (0.0, 0.1),
     'L0_ffn_w_gate_b': (0.0, 0.1),
     'L0_ffn_b1': (0.0, 0.1),
     'L0_ffn_b2': (0.0, 0.1),
     'L1_ffn_bs1': (0.0, 0.1),
     'L1_ffn_bs2': (0.0, 0.1),
     'L1_ffn_be1': (0.0, 0.1),
     'L1_ffn_be2': (0.0, 0.1),
     'L1_ffn_br': (0.0, 0.1),
     'L2_attn_b_out': (0.0, 1.516),
     'L2_attn_ramp_logit': (-2.1972246170043945, 0.6),
     'L3_ffn_router_bias': (0.0, 0.353),
     'L3_ffn_gate_up_proj_bias': (0.0, 0.8),
     'L3_ffn_down_proj_bias': (0.0, 0.1)}
    factors = {'L0_attn_Wq': 6.704,
     'L0_attn_Wk': 6.737,
     'L0_attn_Wv': 2.741,
     'L2_attn_W_in': 22.803,
     'L2_attn_W_ctrl': 28.335,
     'L2_attn_b_ctrl': 3.926,
     'L2_attn_w_q': 28.228,
     'L2_attn_w_k': 29.089,
     'L2_attn_w_v': 22.546,
     'L2_attn_W_out': 16.644,
     'L3_attn_Wqkv': 3.512,
     'L3_attn_Wout': 3.538,
     'L3_ffn_gate_up_proj': 3.218,
     'L3_ffn_down_proj': 2.919}
    for name, (base, spread) in spreads.items():
        noise = np.random.default_rng([zlib.crc32(name.encode()), seed]).standard_normal(out[name].shape)
        drawn = base * np.exp(spread * noise) if base else spread * noise
        out[name] = jnp.asarray(drawn.astype(out[name].dtype))
    for name, factor in factors.items():
        out[name] = (out[name] * factor).astype(out[name].dtype)
    return out
```

```python
from contextlib import ExitStack

import numpy as np

import concourse.bass as bass
from concourse import mybir

F32 = mybir.dt.float32
I32 = mybir.dt.int32
BF16 = mybir.dt.bfloat16
ALU = mybir.AluOpType
ACT = mybir.ActivationFunctionType
AX = mybir.AxisListType

P = 128
D = 128
BATCH, SEQ = 8, 512
N = BATCH * SEQ
TILES = N // P
BLK = 512
NBLK = N // BLK
TPB = BLK // P
LN_EPS = 1e-5
BIG = 3.0e38


class Core:

    def __init__(self, nc, ctx):
        self.nc, self.ctx, self.sems = nc, ctx, []
        self.x = self.sb("x", [P, TILES, D])
        self.xT = self.sb("xT", [P, N])
        self.ident = self.sb("ident", [P, P])
        self.neghalf = self.sb("neghalf", [P, 512])

    def sb(self, name, shape, dt=F32, ctx=None):
        return (ctx or self.ctx).enter_context(self.nc.sbuf_tensor(name, shape, dt))

    def ps(self, name, shape, dt=F32, ctx=None):
        return (ctx or self.ctx).enter_context(self.nc.psum_tensor(name, shape, dt))

    def sem(self, name):
        s = self.nc.alloc_semaphore(name)
        self.sems.append(s)
        return s

    def free_sems(self):
        self.nc.clear_and_free_semaphores(self.sems)
        self.nc.all_engine_barrier()
        self.sems = []

    def dram(self, name, shape, dt=F32):
        return self.nc.dram_tensor(name, shape, dt, kind="Internal").ap()


def start(core, x_in):
    nc = core.nc
    loaded, filled = core.sem("x_loaded"), core.sem("ident_filled")
    with nc.Block() as block:

        @block.sync
        def _(sp):
            sp.dma_start(core.x[:, :, :], x_in.rearrange("(t p) d -> p t d", p=P)).then_inc(loaded, 16)
            sp.wait_ge(loaded, 16)

        @block.gpsimd
        def _(pool):
            pool.memset(core.ident[:, :], 0.0).then_inc(filled, 1)
            pool.memset(core.neghalf[:, :], -0.5)
            pool.wait_ge(filled, 1)
            pool.affine_select(out=core.ident[:, :], in_=core.ident[:, :], compare_op=ALU.not_equal, fill=1.0,
                               base=0, pattern=[[-1, P]], channel_multiplier=1)


def store(core, x_out):
    nc = core.nc
    stored = core.sem("x_stored")
    with nc.Block() as block:

        @block.sync
        def _(sp):
            sp.dma_start(x_out.rearrange("(t p) d -> p t d", p=P), core.x[:, :, :]).then_inc(stored, 16)
            sp.wait_ge(stored, 16)


def layernorm(core, name):
    nc = core.nc
    var_ready, rstd_ready = core.sem(name + "_var_ready"), core.sem(name + "_rstd_ready")
    xn_ready, turned = core.sem(name + "_xn_ready"), core.sem(name + "_turned")
    copied = core.sem(name + "_copied")
    with ExitStack() as ctx:
        stats = core.sb(name + "_stats", [P, TPB, 6], ctx=ctx)
        mv = core.sb(name + "_mv", [P, 2, TPB, 2], ctx=ctx)
        rstd = core.sb(name + "_rstd", [P, 2, TPB], ctx=ctx)
        xn = core.sb(name + "_xn", [P, 2, TPB, D], ctx=ctx)
        turn = core.ps(name + "_turn", [P, 2, BLK], ctx=ctx)
        block = ctx.enter_context(nc.Block())

        def block_stats(dve, b):
            for t in range(TPB):
                dve.bn_stats(stats[:, t, :], core.x[:, TPB * b + t, :])
            dve.drain()
            for t in range(TPB):
                dve.bn_aggr(mv[:, b % 2, t, :], stats[:, t, :])
            dve.drain()
            dve.tensor_scalar(rstd[:, b % 2, :], mv[:, b % 2, :, 1], LN_EPS, None, ALU.add)\
               .then_inc(var_ready, 1)

        @block.vector
        def _(dve):
            block_stats(dve, 0)
            for b in range(NBLK):
                if b + 1 < NBLK:
                    if b >= 1:
                        dve.drain()
                    block_stats(dve, b + 1)
                dve.wait_ge(rstd_ready, b + 1)
                if b >= 2:
                    dve.wait_ge(turned, b - 1)
                for t in range(TPB):
                    last = dve.tensor_scalar(xn[:, b % 2, t, :], core.x[:, TPB * b + t, :],
                                             mv[:, b % 2, t, 0:1], rstd[:, b % 2, t:t + 1],
                                             ALU.subtract, ALU.mult)
                last.then_inc(xn_ready, 1)

        @block.gpsimd
        def _(pool):
            for b in range(NBLK):
                pool.wait_ge(var_ready, b + 1)
                pool.tensor_tensor(rstd[:, b % 2, :], rstd[:, b % 2, :], core.neghalf[:, 0:TPB], ALU.pow)\
                    .then_inc(rstd_ready, 1)

        @block.tensor
        def _(pe):
            for b in range(NBLK):
                pe.wait_ge(xn_ready, b + 1)
                if b >= 2:
                    pe.wait_ge(copied, b - 1)
                for t in range(TPB):
                    last = pe.transpose(turn[:, b % 2, t * P:(t + 1) * P], xn[:, b % 2, t, :], core.ident[:, :])
                last.then_inc(turned, 1)

        @block.scalar
        def _(act):
            for b in range(NBLK):
                act.wait_ge(turned, b + 1)
                act.activation(core.xT[:, b * BLK:(b + 1) * BLK], turn[:, b % 2, :], ACT.Copy)\
                   .then_inc(copied, 1)


def add_back(core, name, yT):
    nc = core.nc
    turned, added = core.sem(name + "_turned"), core.sem(name + "_added")
    with ExitStack() as ctx:
        turn = core.ps(name + "_turn", [P, 4, TPB, P], ctx=ctx)
        block = ctx.enter_context(nc.Block())

        @block.tensor
        def _(pe):
            for b in range(NBLK):
                if b >= 4:
                    pe.wait_ge(added, b - 3)
                for t in range(TPB):
                    c = b * BLK + t * P
                    last = pe.transpose(turn[:, b % 4, t, :], yT[:, c:c + P], core.ident[:, :])
                last.then_inc(turned, 1)

        @block.vector
        def _(dve):
            for b in range(NBLK):
                dve.wait_ge(turned, b + 1)
                xb = core.x[:, b * TPB:(b + 1) * TPB, :]
                dve.tensor_tensor(xb, xb, turn[:, b % 4, :, :], ALU.add).then_inc(added, 1)


def route(core, name, w_in, b_in, wts, E, K, mode, tau=1.0):
    nc = core.nc
    loaded, logits_ready, biased = core.sem(name + "_loaded"), core.sem(name + "_logits"), core.sem(name + "_biased")
    turned, const_ready = core.sem(name + "_turned"), core.sem(name + "_const")
    shifted, exped = core.sem(name + "_shifted"), core.sem(name + "_exped")
    with ExitStack() as ctx:
        sb = lambda n, s, dt=F32: core.sb(name + "_" + n, s, dt, ctx)
        w_sb, b_sb = sb("w", [P, E]), sb("b", [P, 1])
        lT = sb("lT", [P, N])
        logits, v, oh, mask = (sb(n, [P, TILES, E]) for n in ("logits", "v", "oh", "mask"))
        probs, shift = sb("probs", [P, TILES, E]), sb("shift", [P, TILES, E])
        m1, m, den = (sb(n, [P, TILES]) for n in ("m1", "m", "den"))
        rev = sb("rev", [P, E])
        ps_l = core.ps(name + "_ps_l", [P, 2, BLK], ctx=ctx)
        ps_t = core.ps(name + "_ps_t", [P, 512], ctx=ctx)
        block = ctx.enter_context(nc.Block())
        lv = ps_t[:, 0:TILES * E].rearrange("p (t e) -> p t e", e=E)
        each = lambda a: a[:, :].rearrange("p (t o) -> p t o", o=1).to_broadcast([P, TILES, E])

        @block.sync
        def _(sp):
            sp.dma_start(w_sb[:, :], w_in).then_inc(loaded, 16)
            if b_in is not None:
                sp.dma_start(b_sb[0:E, :], b_in).then_inc(loaded, 16)

        @block.gpsimd
        def _(pool):
            for e in range(E):
                last = pool.memset(rev[:, e:e + 1], float(E - e))
            last.then_inc(const_ready, 1)

        @block.tensor
        def _(pe):
            pe.wait_ge(loaded, 16 if b_in is None else 32)
            for b in range(NBLK):
                if b >= 2:
                    pe.wait_ge(biased, b - 1)
                pe.matmul(ps_l[0:E, b % 2, :], w_sb[:, :], core.xT[:, b * BLK:(b + 1) * BLK],
                          start=True, stop=True).then_inc(logits_ready, 1)
            for t in range(TILES):
                if t % TPB == 0:
                    pe.wait_ge(biased, t // TPB + 1)
                last = pe.transpose(ps_t[:, t * E:(t + 1) * E], lT[0:E, t * P:(t + 1) * P], core.ident[0:E, 0:E])
            last.then_inc(turned, 1)

        @block.scalar
        def _(act):
            act.wait_ge(shifted, 1)
            act.activation(probs[:, :, :], shift[:, :, :], ACT.Exp, scale=1.0 / tau).then_inc(exped, 1)

        @block.vector
        def _(dve):
            dve.wait_ge(loaded, 16 if b_in is None else 32)
            for b in range(NBLK):
                dve.wait_ge(logits_ready, b + 1)
                dve.tensor_scalar(lT[0:E, b * BLK:(b + 1) * BLK], ps_l[0:E, b % 2, :],
                                  0.0 if b_in is None else b_sb[0:E, 0:1], None, ALU.add).then_inc(biased, 1)
            dve.wait_ge(turned, 1)
            dve.tensor_reduce(m1[:, :], lv, AX.X, ALU.max)
            dve.tensor_copy(logits[:, :, :], lv)
            dve.tensor_copy(v[:, :, :], lv)
            dve.drain()
            dve.tensor_tensor(shift[:, :, :], logits[:, :, :], each(m1), ALU.subtract).then_inc(shifted, 1)
            dve.wait_ge(const_ready, 1)
            for k in range(K):
                if k:
                    dve.tensor_reduce(m[:, :], v[:, :, :], AX.X, ALU.max)
                    dve.drain()
                dve.tensor_tensor(oh[:, :, :], v[:, :, :], each(m if k else m1), ALU.is_equal)
                dve.drain()
                dve.tensor_tensor(oh[:, :, :], oh[:, :, :],
                                  rev[:, :].rearrange("p (o e) -> p o e", o=1).to_broadcast([P, TILES, E]), ALU.mult)
                dve.drain()
                dve.tensor_reduce(den[:, :], oh[:, :, :], AX.X, ALU.max)
                dve.drain()
                dve.tensor_tensor(oh[:, :, :], oh[:, :, :], each(den), ALU.is_equal)
                dve.drain()
                dve.scalar_tensor_tensor(out=v[:, :, :], in0=oh[:, :, :], scalar=-BIG, in1=v[:, :, :],
                                         op0=ALU.mult, op1=ALU.add)
                if k == 0:
                    dve.tensor_copy(mask[:, :, :], oh[:, :, :])
                else:
                    dve.tensor_tensor(mask[:, :, :], mask[:, :, :], oh[:, :, :], ALU.add)
                dve.drain()
            dve.wait_ge(exped, 1)
            if mode != "topk":
                dve.tensor_reduce(den[:, :], probs[:, :, :], AX.X, ALU.add)
                dve.drain()
                dve.reciprocal(den[:, :], den[:, :])
                dve.drain()
                dve.tensor_tensor(probs[:, :, :], probs[:, :, :], each(den), ALU.mult)
                dve.drain()
            dve.tensor_tensor(probs[:, :, :], probs[:, :, :], mask[:, :, :], ALU.mult)
            dve.drain()
            if mode == "batch":
                by = probs[:, :, :].rearrange("p (b s) e -> p (s e) b", b=BATCH)
                dsum = v[:, 0:TPB, :].rearrange("p s e -> p (s e)")
                dve.tensor_reduce(dsum, by, AX.X, ALU.add)
                dve.drain()
                dve.tensor_scalar(dsum, dsum, 1e-6, None, ALU.add)
                dve.drain()
                dve.reciprocal(dsum, dsum)
                dve.drain()
                dve.scalar_tensor_tensor(
                    out=wts[:, :, :].rearrange("p (b s) e -> p b (s e)", b=BATCH),
                    in0=probs[:, :, :].rearrange("p (b s) e -> p b (s e)", b=BATCH), scalar=float(BATCH),
                    in1=v[:, 0:TPB, :].rearrange("p (o s) e -> p o (s e)", o=1).to_broadcast([P, BATCH, TPB * E]),
                    op0=ALU.mult, op1=ALU.mult)
            else:
                dve.tensor_reduce(den[:, :], probs[:, :, :], AX.X, ALU.add)
                dve.drain()
                if mode == "probs":
                    dve.tensor_scalar(den[:, :], den[:, :], 1e-6, None, ALU.add)
                    dve.drain()
                dve.reciprocal(den[:, :], den[:, :])
                dve.drain()
                dve.tensor_tensor(wts[:, :, :], probs[:, :, :], each(den), ALU.mult)


def keep_best(core, name, wts, keep, group_in, before_in, bits_in, per_batch, times_weight):
    nc = core.nc
    E, HALF, TOP = 8, 2, 31
    ncol = HALF if per_batch else 1
    loaded, turned, rows_ready = core.sem(name + "_loaded"), core.sem(name + "_turned"), core.sem(name + "_rows")
    counted, summed = core.sem(name + "_counted"), core.sem(name + "_summed")
    tallied, spread = core.sem(name + "_tallied"), core.sem(name + "_spread")
    chosen, back = core.sem(name + "_chosen"), core.sem(name + "_back")
    with ExitStack() as ctx:
        sb = lambda n, s, dt=F32: core.sb(name + "_" + n, s, dt, ctx)
        group, before = sb("group", [P, P]), sb("before", [P, P])
        bits = sb("bits", [P, TOP], I32)
        rows, gt, eq, incl = (sb(n, [P, HALF, P]) for n in ("rows", "gt", "eq", "incl"))
        zeros = sb("zeros", [P, P])
        thr, cand, above = sb("thr", [P, ncol]), sb("cand", [P, ncol]), sb("above", [P, ncol])
        cnt = sb("cnt", [P, ncol])
        n_gt, n_eq, need, off = sb("n_gt", [P, ncol]), sb("n_eq", [P, HALF]), sb("need", [P, HALF]), sb("off", [P, HALF])
        ps_r = core.ps(name + "_ps_r", [P, HALF, P], ctx=ctx)
        ps_c = core.ps(name + "_ps_c", [P, 512], ctx=ctx)
        ps_o = core.ps(name + "_ps_o", [P, 512], ctx=ctx)
        ps_b = core.ps(name + "_ps_b", [P, HALF, P], ctx=ctx)
        flat = wts[:, :, :].rearrange("p t e -> p (t e)")
        shape = [P, ncol, HALF * P // ncol]
        cut = lambda a: a[:, :, :].rearrange("p h k -> p (h k)").rearrange("p (c k) -> p c k", c=ncol)
        wide = lambda a: a[:, :].rearrange("p (c o) -> p c o", o=1).to_broadcast(shape)
        block = ctx.enter_context(nc.Block())

        @block.sync
        def _(sp):
            sp.dma_start(group[:, :], group_in).then_inc(loaded, 16)
            sp.dma_start(before[:, :], before_in).then_inc(loaded, 16)
            sp.dma_start(bits[:, :], bits_in).then_inc(loaded, 16)

        @block.tensor
        def _(pe):
            for h in range(HALF):
                last = pe.transpose(ps_r[:, h, :], flat[:, h * P:(h + 1) * P], core.ident[:, :])
            last.then_inc(turned, 1)
            pe.wait_ge(loaded, 48)
            with pe.Fori(0, TOP) as i:
                pe.wait_ge(counted, i + 1)
                pe.matmul(ps_c[:, 0:ncol], group[:, :], cnt[:, :], start=True, stop=True).then_inc(summed, 1)
            pe.wait_ge(tallied, 1)
            pe.matmul(ps_c[:, 0:ncol], group[:, :], n_gt[:, :], start=True, stop=True)
            if per_batch:
                last = pe.matmul(ps_o[:, 0:HALF], before[:, :], n_eq[:, :], start=True, stop=True)
            else:
                pe.matmul(ps_o[:, 0:1], before[:, :], n_eq[:, 0:1], start=True, stop=True)
                pe.matmul(ps_o[:, 1:2], before[:, :], n_eq[:, 1:2], start=True, stop=False)
                last = pe.matmul(ps_o[:, 1:2], group[:, :], n_eq[:, 0:1], start=False, stop=True)
            last.then_inc(spread, 1)
            pe.wait_ge(chosen, 1)
            for h in range(HALF):
                last = pe.transpose(ps_b[:, h, :], gt[:, h, :], core.ident[:, :])
            last.then_inc(back, 1)

        @block.vector
        def _(dve):
            dve.memset(thr[:, :], 0.0)
            dve.memset(zeros[:, :], 0.0)
            dve.wait_ge(turned, 1)
            dve.tensor_copy(rows[:, :, :], ps_r[:, :, :])
            dve.wait_ge(loaded, 48)
            dve.drain()
            with dve.Fori(0, TOP) as i:
                dve.tensor_tensor(cand[:, :].bitcast(I32), thr[:, :].bitcast(I32),
                                  bits[:, bass.ds(i, 1)].to_broadcast([P, ncol]), ALU.bitwise_or)
                dve.drain()
                dve.tensor_tensor(cut(incl), cut(rows), wide(cand), ALU.is_ge)
                dve.drain()
                dve.tensor_reduce(cnt[:, :], cut(incl), AX.X, ALU.add).then_inc(counted, 1)
                dve.wait_ge(summed, i + 1)
                dve.scalar_tensor_tensor(out=above[:, :], in0=ps_c[:, 0:ncol], scalar=float(keep), in1=cand[:, :],
                                         op0=ALU.is_ge, op1=ALU.mult)
                dve.drain()
                dve.tensor_tensor(thr[:, :], thr[:, :], above[:, :], ALU.max)
                dve.drain()
            dve.scalar_tensor_tensor(out=thr[:, :], in0=thr[:, :], scalar=1.1754944e-38, in1=thr[:, :],
                                     op0=ALU.is_ge, op1=ALU.mult)
            dve.drain()
            dve.tensor_tensor(cut(gt), cut(rows), wide(thr), ALU.is_gt)
            dve.tensor_tensor(cut(eq), cut(rows), wide(thr), ALU.is_equal)
            dve.drain()
            dve.tensor_reduce(n_gt[:, :], cut(gt), AX.X, ALU.add)
            for h in range(HALF):
                dve.tensor_tensor_scan(incl[:, h, :], eq[:, h, :], zeros[:, :], 0.0, ALU.add, ALU.add)
            dve.tensor_reduce(n_eq[:, :], eq[:, :, :], AX.X, ALU.add).then_inc(tallied, 1)
            dve.wait_ge(spread, 1)
            dve.tensor_scalar(need[:, :], ps_c[:, 0:ncol].to_broadcast([P, HALF]) if ncol == 1 else ps_c[:, 0:HALF],
                              -1.0, float(keep), ALU.mult, ALU.add)
            dve.drain()
            dve.tensor_tensor(off[:, :], ps_o[:, 0:HALF], need[:, :], ALU.subtract)
            dve.drain()
            for h in range(HALF):
                dve.tensor_scalar(incl[:, h, :], incl[:, h, :], off[:, h:h + 1], 1.0, ALU.add, ALU.is_lt)
            dve.drain()
            dve.tensor_tensor(eq[:, :, :], eq[:, :, :], incl[:, :, :], ALU.mult)
            dve.drain()
            dve.tensor_tensor(gt[:, :, :], gt[:, :, :], eq[:, :, :], ALU.add).then_inc(chosen, 1)
            dve.wait_ge(back, 1)
            got = ps_b[:, :, :].rearrange("p h k -> p (h k)")
            if times_weight:
                dve.tensor_tensor(flat, flat, got, ALU.mult)
            else:
                dve.tensor_copy(flat, got)


def weight_rows(core, name, wts, E, rows_sb, rows_dram):
    nc = core.nc
    turned, copied, saved = core.sem(name + "_turned"), core.sem(name + "_copied"), core.sem(name + "_saved")
    with ExitStack() as ctx:
        turn = core.ps(name + "_turn", [P, 4, BLK], ctx=ctx)
        block = ctx.enter_context(nc.Block())

        @block.tensor
        def _(pe):
            for b in range(NBLK):
                if b >= 4:
                    pe.wait_ge(copied, b - 3)
                for t in range(TPB):
                    last = pe.transpose(turn[0:E, b % 4, t * P:(t + 1) * P], wts[:, b * TPB + t, :], core.ident[:, :])
                last.then_inc(turned, 1)

        @block.vector
        def _(dve):
            for b in range(NBLK):
                dve.wait_ge(turned, b + 1)
                dve.tensor_copy(rows_sb[0:E, b * BLK:(b + 1) * BLK], turn[0:E, b % 4, :]).then_inc(copied, 1)

        @block.sync
        def _(sp):
            sp.wait_ge(copied, NBLK)
            sp.dma_start(rows_dram, rows_sb[0:E, :]).then_inc(saved, 16)
            sp.wait_ge(saved, 16)


def expert_ffn(core, name, yT, w1_in, w2_in, b1_in, b2_in, rows_dram, E, C, kind, first):
    nc = core.nc
    PAR = min(E, 2)
    ROUNDS = E // PAR
    STEPS = NBLK * C
    w_ready = [core.sem(f"{name}_w_ready{k}") for k in range(PAR)]
    gu_ready, gate_done = core.sem(name + "_gu_ready"), core.sem(name + "_gate_done")
    act_done, down_done = core.sem(name + "_act_done"), core.sem(name + "_down_done")
    y_done, added = core.sem(name + "_y_done"), core.sem(name + "_added")
    pre_done = core.sem(name + "_pre_done")
    weighted = rows_dram is not None
    CREDIT = 2
    with ExitStack() as ctx:
        sb = lambda n, s, dt=F32: core.sb(name + "_" + n, s, dt, ctx)
        w1, w2 = sb("w1", [P, PAR, 2 * C, P]), sb("w2", [P, PAR, C, P])
        b1, b2 = sb("b1", [P, PAR, 2 * C]), sb("b2", [P, PAR])
        wb = sb("wb", [P, PAR, N]) if weighted else None
        gate, act_out = sb("gate", [P, 2, BLK]), sb("act", [P, 2, BLK])
        pre = sb("pre", [P, 2, 2, BLK]) if kind == "clipped" else None
        half = sb("half", [P, 2, BLK]) if kind == "clipped" else None
        y_sb = sb("y", [P, 2, BLK])
        ps_g = core.ps(name + "_ps_g", [P, 2, BLK], ctx=ctx)
        ps_u = core.ps(name + "_ps_u", [P, 2, BLK], ctx=ctx)
        ps_y = core.ps(name + "_ps_y", [P, 2, BLK], ctx=ctx)
        block = ctx.enter_context(nc.Block())
        loads = 2 + (b1_in is not None) + (b2_in is not None) + weighted

        def rounds(eng):
            return eng.Fori(0, ROUNDS)

        @block.sync
        def _(sp):
            with rounds(sp) as r:
                for k in range(PAR):
                    e = r * PAR + k
                    sp.wait_ge(y_done, (r * PAR + k - PAR + 1) * NBLK + PAR * NBLK)
                    sp.dma_start(w1[:, k, :, :], w1_in[bass.ds(e, 1)].rearrange("o p c f -> p (o c) f"))\
                        .then_inc(w_ready[k], 16)
                    sp.dma_start(w2[:, k, :, :], w2_in[bass.ds(e, 1)].rearrange("o p c f -> p (o c) f"))\
                        .then_inc(w_ready[k], 16)
                    if b1_in is not None:
                        sp.dma_start(b1[:, k, :], b1_in[bass.ds(e, 1)].rearrange("o p c -> p (o c)"))\
                            .then_inc(w_ready[k], 16)
                    if b2_in is not None:
                        sp.dma_start(b2[:, k:k + 1], b2_in[bass.ds(e, 1)].rearrange("o p c -> p (o c)"))\
                            .then_inc(w_ready[k], 16)
                    if weighted:
                        sp.dma_start(wb[:, k, :], rows_dram[bass.ds(e, 1), :].to_broadcast([P, N]))\
                            .then_inc(w_ready[k], 16)

        @block.tensor
        def _(pe):
            with rounds(pe) as r:
                base = r * (PAR * STEPS)

                def down(s):
                    k, c = s // STEPS, s % C
                    u = s // C
                    pe.wait_ge(act_done, base + s + 1 + CREDIT)
                    if c == 0:
                        pe.wait_ge(y_done, r * (PAR * NBLK) + (u - 1 + PAR * NBLK))
                    pe.matmul(ps_y[:, u % 2, :], w2[:, k, c, :], act_out[:, s % 2, :],
                              start=(c == 0), stop=(c == C - 1)).then_inc(down_done, 1)

                for s in range(PAR * STEPS):
                    k, b, c = s // STEPS, s // C % NBLK, s % C
                    if s % STEPS == 0:
                        pe.wait_ge(w_ready[k], (r + 1) * (16 * loads))
                    pe.wait_ge(act_done, base + s - 1 + CREDIT)
                    xb = core.xT[:, b * BLK:(b + 1) * BLK]
                    pe.matmul(ps_g[:, s % 2, :], w1[:, k, c, :], xb, start=True, stop=True)
                    pe.matmul(ps_u[:, s % 2, :], w1[:, k, C + c, :], xb, start=True, stop=True)\
                        .then_inc(gu_ready, 1)
                    if s >= 1:
                        down(s - 1)
                down(PAR * STEPS - 1)

        @block.scalar
        def _(act):
            with rounds(act) as r:
                base = r * (PAR * STEPS)
                for s in range(PAR * STEPS):
                    k, c = s // STEPS, s % C
                    if kind == "clipped":
                        act.wait_ge(pre_done, base + s + 1)
                        act.wait_ge(act_done, base + s - 1 + CREDIT)
                        act.activation(gate[:, s % 2, :], pre[:, s % 2, 0, :], ACT.Sigmoid, scale=1.702)\
                           .then_inc(gate_done, 1)
                        continue
                    act.wait_ge(gu_ready, base + s + 1)
                    act.wait_ge(act_done, base + s - 1 + CREDIT)
                    func = {"geglu": ACT.Gelu, "swiglu": ACT.Silu}[kind]
                    act.activation(gate[:, s % 2, :], ps_g[:, s % 2, :], func,
                                   bias=0.0 if b1_in is None else b1[:, k, c:c + 1]).then_inc(gate_done, 1)

        @block.vector
        def _(dve):
            dve.sem_inc(act_done, CREDIT)
            dve.sem_inc(y_done, PAR * NBLK)
            with rounds(dve) as r:
                base = r * (PAR * STEPS)

                def finish(u):
                    k, b = u // NBLK, u % NBLK
                    dve.wait_ge(down_done, base + (u + 1) * C)
                    if weighted:
                        dve.wait_ge(added, r * (PAR * NBLK) + u - 1 + CREDIT)
                        wv = wb[:, k, b * BLK:(b + 1) * BLK]
                        dve.scalar_tensor_tensor(out=y_sb[:, u % 2, :], in0=ps_y[:, u % 2, :],
                                                 scalar=0.0 if b2_in is None else b2[:, k:k + 1], in1=wv,
                                                 op0=ALU.add, op1=ALU.mult).then_inc(y_done, 1)
                    else:
                        dve.tensor_scalar(yT[:, b * BLK:(b + 1) * BLK], ps_y[:, u % 2, :], b2[:, k:k + 1], None,
                                          ALU.add).then_inc(y_done, 1)

                for s in range(PAR * STEPS):
                    k, c = s // STEPS, s % C
                    if s % STEPS == 0:
                        dve.wait_ge(w_ready[k], (r + 1) * (16 * loads))
                    if kind == "clipped":
                        dve.wait_ge(gu_ready, base + s + 1)
                        dve.tensor_scalar(pre[:, s % 2, 0, :], ps_g[:, s % 2, :], b1[:, k, c:c + 1], 7.0,
                                          ALU.add, ALU.min).then_inc(pre_done, 1)
                        dve.tensor_scalar(pre[:, s % 2, 1, :], ps_u[:, s % 2, :], b1[:, k, C + c:C + c + 1], 7.0,
                                          ALU.add, ALU.min)
                        dve.drain()
                        dve.tensor_scalar(pre[:, s % 2, 1, :], pre[:, s % 2, 1, :], -7.0, 1.0, ALU.max, ALU.add)
                        dve.drain()
                        dve.tensor_tensor(half[:, s % 2, :], pre[:, s % 2, 1, :], pre[:, s % 2, 0, :], ALU.mult)
                        dve.drain()
                    dve.wait_ge(gate_done, base + s + 1)
                    if s >= 2:
                        dve.wait_ge(down_done, base + s - 1)
                    if kind == "clipped":
                        dve.tensor_tensor(act_out[:, s % 2, :], half[:, s % 2, :], gate[:, s % 2, :], ALU.mult)\
                           .then_inc(act_done, 1)
                    else:
                        dve.scalar_tensor_tensor(out=act_out[:, s % 2, :], in0=ps_u[:, s % 2, :],
                                                 scalar=0.0 if b1_in is None else b1[:, k, C + c:C + c + 1],
                                                 in1=gate[:, s % 2, :], op0=ALU.add, op1=ALU.mult)\
                           .then_inc(act_done, 1)
                    if s >= C and s % C == 0:
                        finish(s // C - 1)
                finish(PAR * NBLK - 1)

        @block.gpsimd
        def _(pool):
            if weighted:
                if first:
                    pool.memset(yT[:, :], 0.0)
                    pool.drain()
                pool.sem_inc(added, CREDIT)
                with rounds(pool) as r:
                    for u in range(PAR * NBLK):
                        b = u % NBLK
                        pool.wait_ge(y_done, r * (PAR * NBLK) + (u + 1 + PAR * NBLK))
                        yb = yT[:, b * BLK:(b + 1) * BLK]
                        pool.tensor_tensor(yb, yb, y_sb[:, u % 2, :], ALU.add).then_inc(added, 1)


def masked_ffn(core, name, rows, rows_dram, w1_in, b1_in, w2_in, b2_in):
    nc = core.nc
    E, C, SUB = 8, 2, 32
    loaded, up_ready, gelu_done = core.sem(name + "_loaded"), core.sem(name + "_up_ready"), core.sem(name + "_gelu_done")
    act_done, y_ready, added = core.sem(name + "_act_done"), core.sem(name + "_y_ready"), core.sem(name + "_added")
    with ExitStack() as ctx:
        sb = lambda n, s, dt=F32: core.sb(name + "_" + n, s, dt, ctx)
        w1, w2, b1, b2 = sb("w1", [P, C, P]), sb("w2", [P, C, D]), sb("b1", [P, C]), sb("b2", [E, D])
        spread = sb("spread", [P, C, N])
        gelu, act_out = sb("gelu", [P, C, 2, BLK]), sb("act", [P, C, 2, BLK])
        ps_h = core.ps(name + "_ps_h", [P, C, 2, BLK], ctx=ctx)
        ps_y = core.ps(name + "_ps_y", [P, 2, TPB, D], ctx=ctx)
        block = ctx.enter_context(nc.Block())

        @block.sync
        def _(sp):
            sp.dma_start(w1[:, :, :], w1_in).then_inc(loaded, 16)
            sp.dma_start(w2[:, :, :], w2_in).then_inc(loaded, 16)
            sp.dma_start(b1[:, :], b1_in).then_inc(loaded, 16)
            sp.dma_start(b2[:, :], b2_in).then_inc(loaded, 16)
            for e in range(E):
                at = SUB * (e % 4)
                sp.dma_start(spread[at:at + SUB, e // 4, :], rows_dram[e:e + 1, :].to_broadcast([SUB, N]))\
                    .then_inc(loaded, 16)

        ALL = 16 * (4 + E)

        @block.tensor
        def _(pe):
            pe.wait_ge(loaded, ALL)

            def down(b):
                pe.wait_ge(act_done, C * (b + 1))
                if b >= 2:
                    pe.wait_ge(added, b - 1)
                for t in range(TPB):
                    cut = slice(t * P, (t + 1) * P)
                    for c in range(C):
                        pe.matmul(ps_y[:, b % 2, t, :], act_out[:, c, b % 2, cut], w2[:, c, :],
                                  start=(c == 0), stop=False)
                    last = pe.matmul(ps_y[:, b % 2, t, :], rows[0:E, b * BLK + t * P:b * BLK + (t + 1) * P], b2[:, :],
                                     start=False, stop=True)
                last.then_inc(y_ready, 1)

            for b in range(NBLK):
                if b >= 2:
                    pe.wait_ge(gelu_done, C * (b - 1))
                for c in range(C):
                    pe.matmul(ps_h[:, c, b % 2, :], w1[:, c, :], core.xT[:, b * BLK:(b + 1) * BLK],
                              start=True, stop=True).then_inc(up_ready, 1)
                if b >= 1:
                    down(b - 1)
            down(NBLK - 1)

        @block.scalar
        def _(act):
            for b in range(NBLK):
                for c in range(C):
                    act.wait_ge(up_ready, C * b + c + 1)
                    if b >= 2:
                        act.wait_ge(act_done, C * (b - 2) + c + 1)
                    act.activation(gelu[:, c, b % 2, :], ps_h[:, c, b % 2, :], ACT.Gelu, bias=b1[:, c:c + 1])\
                       .then_inc(gelu_done, 1)

        @block.vector
        def _(dve):
            dve.wait_ge(loaded, ALL)

            def add(b):
                dve.wait_ge(y_ready, b + 1)
                xb = core.x[:, b * TPB:(b + 1) * TPB, :]
                dve.tensor_tensor(xb, xb, ps_y[:, b % 2, :, :], ALU.add).then_inc(added, 1)

            for b in range(NBLK):
                for c in range(C):
                    dve.wait_ge(gelu_done, C * b + c + 1)
                    if b >= 2:
                        dve.wait_ge(y_ready, b - 1)
                    dve.tensor_tensor(act_out[:, c, b % 2, :], gelu[:, c, b % 2, :],
                                      spread[:, c, b * BLK:(b + 1) * BLK], ALU.mult).then_inc(act_done, 1)
                if b >= 1:
                    add(b - 1)
            add(NBLK - 1)


def layer0_ffn(core, A):
    layernorm(core, "l0f_ln")
    with ExitStack() as ctx:
        wts = core.sb("l0f_wts", [P, TILES, 8], ctx=ctx)
        rows = core.sb("l0f_rows", [P, N], ctx=ctx)
        rows_dram = core.dram("l0f_rows_dram", [8, N])
        route(core, "l0f_route", A["L0_router_w"], A["L0_router_b"], wts, 8, 2, "batch")
        keep_best(core, "l0f_keep", wts, SEQ // 2, A["c_same_batch"], A["c_before_batch"], A["c_bits"], True, False)
        weight_rows(core, "l0f_wr", wts, 8, rows, rows_dram)
        masked_ffn(core, "l0f", rows, rows_dram, A["L0_w1"], A["L0_b1"], A["L0_w2"], A["L0_b2"])


HEADS, HD = 16, 8
SPAN = 1280
KEY_AT = [0, 512, 1024, 896]
QUERY_AT = [896, 1024, 512, 0]
ROWS6 = 64
Q_PARTS, K_PARTS = (0, 0, 1, 1, 0, 2), (0, 1, 0, 1, 2, 0)


def causal_attention(core, name, wqkv_in, wo_in, mask_in, kind, extra):
    nc = core.nc
    rope = kind == "rope"
    KV = 4 if rope else HEADS
    QKV = (HEADS + 2 * KV) * HD
    PAIRS, KPAIRS = HEADS // 2, KV if rope else HEADS // 2
    QB, KB = PAIRS // 2, KPAIRS // 2
    ROWS = 6 * HD if rope else 6 * HD + 12
    SCALE = float(1.0 / np.sqrt(np.float32(HD)))
    S = {n: core.sem(f"{name}_{n}") for n in (
        "loaded", "const_ready", "xb_ready", "qkv_ready", "ss_ready", "norm_ready", "parts_ready", "turned",
        "copied", "max_scores", "max_taken", "max_parts", "s_ready", "exp_done", "pv_done", "o_copied",
        "o_turned", "o_normed", "a_turned", "a_copied", "y_ready", "x_added", "reset")}
    with ExitStack() as ctx:
        sb = lambda n, s, dt=F32: core.sb(name + "_" + n, s, dt, ctx)
        wqkv, wo = sb("wqkv", [P, QKV]), sb("wo", [P, D])
        mask_kq, mask_qk, identb = sb("mask_kq", [P, P], BF16), sb("mask_qk", [P, P], BF16), sb("identb", [P, P], BF16)
        xb = sb("xb", [P, BLK])
        HQK = HEADS + KV
        qk = sb("qk", [P, TPB, HQK, HD])
        rest = sb("rest", [P, TPB * HQK, HD])
        part = [sb(f"part{k}", [P, TPB * HQK, HD], BF16) for k in range(3)]
        q6 = sb("q6", [P, TPB, HEADS, ROWS6], BF16)
        k6 = sb("k6", [P, TPB, 2 * KPAIRS, ROWS6], BF16)
        qT6, kT6 = sb("qT6", [P, PAIRS, BLK], BF16), sb("kT6", [P, KPAIRS, BLK], BF16)
        vaug = sb("vaug", [P, TPB, KV, 32])
        pT = sb("pT", [P, 2, SPAN])
        oT, att, aT = sb("oT", [P, BLK]), sb("att", [P, TPB, HEADS, HD]), sb("aT", [P, BLK])
        rden = sb("rden", [P, TPB, 4])
        if rope:
            norm, half = sb("norm", [P, TPB * HQK]), sb("poshalf", [P, TPB * HQK])
            cos, sin = sb("cos", [P, TPB, 4]), sb("sin", [P, TPB, 4])
            rot, tmp = sb("rot", [P, TPB, HQK, HD]), sb("tmp", [P, 2, TPB, HQK, 4])
        else:
            q_tail, k_tail = sb("q_tail", [P, TPB * HEADS, 16], BF16), sb("k_tail", [P, TPB * HEADS, 16], BF16)
            negm, mrest = sb("negm", [P, TPB, HEADS]), sb("mrest", [P, TPB, HEADS])
            mpart = [sb(f"mpart{k}", [P, TPB, HEADS], BF16) for k in range(3)]
        ps_s = core.ps(name + "_ps_s", [P, 6 * 512], ctx=ctx)
        ps_o = core.ps(name + "_ps_o", [P, 512], ctx=ctx)
        ps_m = core.ps(name + "_ps_m", [P, 512], ctx=ctx)
        block = ctx.enter_context(nc.Block())
        WIDE = 256 if rope else 512
        qkv = ps_s[:, 0:TPB * WIDE].rearrange("p (t c) -> p t c", t=TPB)
        heads = lambda a: a.rearrange("p t h d -> p (t h) d")

        def bank16(n):
            return ps_s[:, (n % 6) * 512:(n % 6 + 1) * 512].bitcast(BF16)

        TURNS = QB + KB + (0 if rope else QB)

        def turned_to(n):
            if n < KB:
                return kT6[:, 2 * n:2 * n + 2, :].rearrange("p a k -> p (a k)")
            n = (n - KB) % QB
            return qT6[:, 2 * n:2 * n + 2, :].rearrange("p a k -> p (a k)")

        @block.sync
        def _(sp):
            sp.dma_start(wqkv[:, :], wqkv_in).then_inc(S["loaded"], 16)
            sp.dma_start(wo[:, :], wo_in).then_inc(S["loaded"], 16)
            sp.dma_start(mask_kq[:, :], mask_in[0]).then_inc(S["loaded"], 16)
            sp.dma_start(mask_qk[:, :], mask_in[1]).then_inc(S["loaded"], 16)
            sp.dma_start(identb[:, :], mask_in[2]).then_inc(S["loaded"], 16)
            if rope:
                sp.dma_start(cos[:, :, :], extra[0]).then_inc(S["loaded"], 16)
                sp.dma_start(sin[:, :, :], extra[1]).then_inc(S["loaded"], 16)
            else:
                sp.dma_start(q_tail[:, :, :], extra[0]).then_inc(S["loaded"], 16)
                sp.dma_start(k_tail[:, :, :], extra[1]).then_inc(S["loaded"], 16)

        ALL = 16 * 7

        @block.gpsimd
        def _(pool):
            pool.memset(q6[:, :, :, :], 0.0)
            pool.memset(k6[:, :, :, :], 0.0)
            pool.memset(vaug[:, :, :, :], 0.0)
            if rope:
                pool.memset(half[:, :], 0.5)
            pool.drain()
            pool.memset(vaug[:, :, :, HD:HD + 1], 1.0)
            if not rope:
                pool.wait_ge(S["loaded"], ALL)
                pool.tensor_copy(heads(k6[:, :, :, :])[:, :, 48:64], k_tail[:, :, :])
            pool.drain()
            pool.sem_inc(S["const_ready"], 1)
            with pool.Fori(0, BATCH) as b:
                pool.wait_ge(S["x_added"], b + 1)
                pool.tensor_copy(xb[:, :], core.xT[:, bass.ds(b * BLK, BLK)]).then_inc(S["xb_ready"], 1)
                if rope:
                    pool.wait_ge(S["ss_ready"], b + 1)
                    pool.tensor_tensor(norm[:, :], norm[:, :], half[:, :], ALU.pow).then_inc(S["norm_ready"], 1)
                else:
                    pool.tensor_copy(heads(q6[:, :, :, :])[:, :, 48:64], q_tail[:, :, :]).then_inc(S["reset"], 1)

        @block.tensor
        def _(pe):
            pe.wait_ge(S["loaded"], ALL)
            with pe.Fori(0, BATCH) as b:
                pe.wait_ge(S["xb_ready"], b + 1)
                for t in range(TPB):
                    last = pe.matmul(qkv[:, t, 0:QKV], xb[:, t * P:(t + 1) * P], wqkv[:, :], start=True, stop=True)
                last.then_inc(S["qkv_ready"], 1)
                pe.wait_ge(S["parts_ready"], b + 1)
                if not rope:
                    pe.wait_ge(S["reset"], b + 1)

                def turn(n, src, pair0):
                    if n >= 6:
                        pe.wait_ge(S["copied"], b * TURNS + n - 5)
                    for a in range(2):
                        for t in range(TPB):
                            at = (a * TPB + t) * P
                            last = pe.transpose(
                                bank16(n)[:, at:at + P],
                                src[:, t, 2 * (pair0 + a):2 * (pair0 + a) + 2, :].rearrange("p h r -> p (h r)"),
                                identb[:, :])
                    last.then_inc(S["turned"], 1)

                for n in range(KB):
                    turn(n, k6, 2 * n)
                for n in range(QB):
                    turn(KB + n, q6, 2 * n)
                pe.wait_ge(S["copied"], b * TURNS + KB + QB)

                def rows(h):
                    return slice(ROWS6 * (h % 2), ROWS6 * (h % 2) + ROWS)

                def keys(h):
                    return h // 4 if rope else h // 2

                if not rope:
                    for h in range(HEADS):
                        if h >= 2:
                            pe.wait_ge(S["max_taken"], b * HEADS + h - 1)
                        z = (h % 2) * 1536
                        for t in (3, 2, 0, 1):
                            at, w = z + QUERY_AT[t], (t + 1) * P
                            pe.matmul(ps_s[:, at:at + w], qT6[rows(h), h // 2, t * P:(t + 1) * P],
                                      kT6[rows(h), keys(h), 0:w], start=True, stop=False)
                            last = pe.matmul(ps_s[:, at + w - P:at + w], identb[:, :], mask_qk[:, :],
                                             start=False, stop=True)
                        last.then_inc(S["max_scores"], 1)
                    pe.wait_ge(S["max_parts"], b + 1)
                    for n in range(QB):
                        turn(6 + n, q6, 2 * n)
                    pe.wait_ge(S["copied"], b * TURNS + TURNS)

                def scores(h):
                    if h >= 2:
                        pe.wait_ge(S["exp_done"], b * HEADS + h - 1)
                    z = (h % 2) * 1536
                    for j in (0, 1, 3, 2):
                        at, w = z + KEY_AT[j], (TPB - j) * P
                        pe.matmul(ps_s[:, at:at + w], kT6[rows(h), keys(h), j * P:(j + 1) * P],
                                  qT6[rows(h), h // 2, j * P:BLK], start=True, stop=False)
                        last = pe.matmul(ps_s[:, at:at + P], identb[:, :], mask_kq[:, :], start=False, stop=True)
                    last.then_inc(S["s_ready"], 1)

                def values(h):
                    g, i = h // 4, h % 4
                    pe.wait_ge(S["exp_done"], b * HEADS + h + 1)
                    if i == 0 and g:
                        pe.wait_ge(S["o_copied"], b * 4 + g)
                    for j in range(TPB):
                        last = pe.matmul(ps_o[32 * i:32 * i + 32, j * P:BLK], vaug[:, j, g if rope else h, :],
                                         pT[:, h % 2, KEY_AT[j]:KEY_AT[j] + (TPB - j) * P],
                                         start=(j == 0), stop=(j == TPB - 1))
                    last.then_inc(S["pv_done"], 1)

                def turn_group(g):
                    pe.wait_ge(S["o_copied"], b * 4 + g + 1)
                    if g:
                        pe.wait_ge(S["o_normed"], b * 4 + g)
                    for t in range(TPB):
                        last = pe.transpose(ps_m[:, t * P:(t + 1) * P], oT[:, t * P:(t + 1) * P], core.ident[:, :])
                    last.then_inc(S["o_turned"], 1)

                scores(0)
                for h in range(1, HEADS):
                    scores(h)
                    values(h - 1)
                    if h > 4 and h % 4 == 1:
                        turn_group(h // 4 - 1)
                values(HEADS - 1)
                turn_group(3)
                pe.wait_ge(S["o_normed"], b * 4 + 4)
                for t in range(TPB):
                    last = pe.transpose(ps_m[:, t * P:(t + 1) * P],
                                        att[:, t, :, :].rearrange("p h d -> p (h d)"), core.ident[:, :])
                last.then_inc(S["a_turned"], 1)
                pe.wait_ge(S["a_copied"], b + 1)
                for t in range(TPB):
                    last = pe.matmul(ps_m[:, t * P:(t + 1) * P], aT[:, t * P:(t + 1) * P], wo[:, :],
                                     start=True, stop=True)
                last.then_inc(S["y_ready"], 1)

        @block.scalar
        def _(act):
            with act.Fori(0, BATCH) as b:
                for n in range(TURNS):
                    act.wait_ge(S["turned"], b * TURNS + n + 1)
                    at = n if n < KB + QB else 6 + n - KB - QB
                    act.activation(turned_to(n), bank16(at), ACT.Copy).then_inc(S["copied"], 1)
                for h in range(HEADS):
                    act.wait_ge(S["s_ready"], b * HEADS + h + 1)
                    if h >= 2:
                        act.wait_ge(S["pv_done"], b * HEADS + h - 1)
                    z = (h % 2) * 1536
                    act.activation(pT[:, h % 2, :], ps_s[:, z:z + SPAN], ACT.Exp, scale=SCALE)\
                       .then_inc(S["exp_done"], 1)

        @block.vector
        def _(dve):
            dve.wait_ge(S["loaded"], ALL)
            dve.wait_ge(S["const_ready"], 1)
            dve.sem_inc(S["x_added"], 1)
            with dve.Fori(0, BATCH) as b:
                dve.wait_ge(S["qkv_ready"], b + 1)
                src = heads(qk[:, :, :, :])
                for t in range(TPB):
                    dve.tensor_copy(qk[:, t, :, :].rearrange("p h d -> p (h d)"), qkv[:, t, 0:HQK * HD])
                    dve.tensor_copy(vaug[:, t, :, 0:HD],
                                    qkv[:, t, HQK * HD:QKV].rearrange("p (h d) -> p h d", d=HD))
                dve.drain()
                if rope:
                    flat = rest[:, :, :]
                    dve.tensor_tensor(flat, src, src, ALU.mult)
                    dve.drain()
                    dve.tensor_reduce(norm[:, :], flat, AX.X, ALU.add).then_inc(S["ss_ready"], 1)
                    dve.wait_ge(S["norm_ready"], b + 1)
                    dve.tensor_scalar(norm[:, :], norm[:, :], 1e-10, None, ALU.add)
                    dve.drain()
                    dve.reciprocal(norm[:, :], norm[:, :])
                    dve.drain()
                    dve.tensor_tensor(src, src, norm[:, :].rearrange("p (h o) -> p h o", o=1)
                                      .to_broadcast([P, TPB * HQK, HD]), ALU.mult)
                    dve.drain()
                    wide = lambda a: a[:, :, :].rearrange("p t (o f) -> p t o f", o=1).to_broadcast([P, TPB, HQK, 4])
                    lo, hi = qk[:, :, :, 0:4], qk[:, :, :, 4:8]
                    dve.tensor_tensor(rot[:, :, :, 0:4], lo, wide(cos), ALU.mult)
                    dve.tensor_tensor(rot[:, :, :, 4:8], hi, wide(cos), ALU.mult)
                    dve.tensor_tensor(tmp[:, 0, :, :, :], hi, wide(sin), ALU.mult)
                    dve.tensor_tensor(tmp[:, 1, :, :, :], lo, wide(sin), ALU.mult)
                    dve.drain()
                    dve.tensor_tensor(rot[:, :, :, 0:4], rot[:, :, :, 0:4], tmp[:, 0, :, :, :], ALU.subtract)
                    dve.tensor_tensor(rot[:, :, :, 4:8], rot[:, :, :, 4:8], tmp[:, 1, :, :, :], ALU.add)
                    dve.drain()
                    src = heads(rot[:, :, :, :])
                dve.tensor_copy(part[0][:, :, :], src)
                dve.drain()
                dve.tensor_tensor(rest[:, :, :], src, part[0][:, :, :], ALU.subtract)
                dve.drain()
                dve.tensor_copy(part[1][:, :, :], rest[:, :, :])
                dve.drain()
                dve.tensor_tensor(part[2][:, :, :], rest[:, :, :], part[1][:, :, :], ALU.subtract)
                dve.drain()
                by = lambda k: part[k][:, :, :].rearrange("p (t h) d -> p t h d", t=TPB)
                for n in range(6):
                    cut = slice(n * HD, (n + 1) * HD)
                    dve.tensor_copy(q6[:, :, :, cut], by(Q_PARTS[n])[:, :, 0:HEADS, :])
                    kp = by(K_PARTS[n])[:, :, HEADS:HQK, :]
                    if rope:
                        for twin in range(2):
                            last = dve.tensor_copy(k6[:, :, twin::2, cut], kp)
                    else:
                        last = dve.tensor_copy(k6[:, :, :, cut], kp)
                last.then_inc(S["parts_ready"], 1)
                if not rope:
                    for h in range(HEADS):
                        dve.wait_ge(S["max_scores"], b * HEADS + h + 1)
                        z = (h % 2) * 1536
                        for t in range(TPB):
                            at = z + QUERY_AT[t]
                            last = dve.tensor_reduce(negm[:, t, h:h + 1], ps_s[:, at:at + (t + 1) * P], AX.X, ALU.max,
                                                     negate=True)
                        last.then_inc(S["max_taken"], 1)
                    dve.drain()
                    dve.tensor_copy(mpart[0][:, :, :], negm[:, :, :])
                    dve.drain()
                    dve.tensor_tensor(mrest[:, :, :], negm[:, :, :], mpart[0][:, :, :], ALU.subtract)
                    dve.drain()
                    dve.tensor_copy(mpart[1][:, :, :], mrest[:, :, :])
                    dve.drain()
                    dve.tensor_tensor(mpart[2][:, :, :], mrest[:, :, :], mpart[1][:, :, :], ALU.subtract)
                    dve.drain()
                    for k in range(3):
                        last = dve.tensor_copy(q6[:, :, :, 57 + k:58 + k],
                                               mpart[k][:, :, :].rearrange("p t (h o) -> p t h o", o=1))
                    last.then_inc(S["max_parts"], 1)
                for g in range(4):
                    dve.wait_ge(S["pv_done"], b * HEADS + 4 * g + 4)
                    if g:
                        dve.wait_ge(S["o_turned"], b * 4 + g)
                    dve.tensor_copy(oT[:, :], ps_o[:, :]).then_inc(S["o_copied"], 1)
                    dve.wait_ge(S["o_turned"], b * 4 + g + 1)
                    by_head = ps_m[:, :].rearrange("p (t i c) -> p t i c", t=TPB, i=4)
                    dve.reciprocal(rden[:, :, :], by_head[:, :, :, HD:HD + 1].rearrange("p t i o -> p t (i o)"))
                    dve.drain()
                    dve.tensor_tensor(att[:, :, 4 * g:4 * g + 4, :], by_head[:, :, :, 0:HD],
                                      rden[:, :, :].rearrange("p t (i o) -> p t i o", o=1)
                                      .to_broadcast([P, TPB, 4, HD]), ALU.mult).then_inc(S["o_normed"], 1)
                dve.wait_ge(S["a_turned"], b + 1)
                dve.tensor_copy(aT[:, :], ps_m[:, :]).then_inc(S["a_copied"], 1)
                dve.wait_ge(S["y_ready"], b + 1)
                xr = core.x[:, bass.ds(b * TPB, TPB), :]
                dve.tensor_tensor(xr, xr, ps_m[:, :].rearrange("p (t d) -> p t d", t=TPB), ALU.add)\
                   .then_inc(S["x_added"], 1)


def layer1_attention(core, A):
    layernorm(core, "l1a_ln")
    causal_attention(core, "l1a", A["L1_wqkv"], A["L1_wo"], A["c_masks"], "rope", (A["c_cos"], A["c_sin"]))


def layer3_attention(core, A):
    layernorm(core, "l3a_ln")
    causal_attention(core, "l3a", A["L3_wqkv"], A["L3_wo"], A["c_masks"], "alibi", (A["c_q_tail"], A["c_k_tail"]))


LAND, REG = 64, 1e-6
COLS = LAND + HD + 1
RROWS = 6 * HD + 6


def landmark_sums(core, name, A, qT_all, land_all, w_dram, z_dram):
    nc = core.nc
    PAIRS, H2 = HEADS // 2, 2 * HEADS
    S = {n: core.sem(f"{name}_{n}") for n in (
        "loaded", "const_ready", "onehot_ready", "seq_done", "xb_ready", "qkv_ready", "parts_ready", "turned", "copied",
        "gathered", "land_ready", "w_ready", "w_clamped", "w_exped", "w_full", "dist_ready", "clamped", "phi_ready",
        "z_ready", "z_full", "saved")}
    with ExitStack() as ctx:
        sb = lambda n, s, dt=F32: core.sb(name + "_" + n, s, dt, ctx)
        wqkv, bias = sb("wqkv", [P, 3 * D]), sb("bias", [P, 3 * D])
        identb = sb("identb", [P, P], BF16)
        regeye = sb("regeye", [LAND, LAND])
        temp, scale = sb("temp", [P, 1]), sb("scale", [P, 1])
        idx_i, idx, neg = sb("idx_i", [P, LAND], I32), sb("idx", [P, LAND]), sb("neg", [P, LAND])
        pos_i, pos = sb("pos_i", [P, TPB], I32), sb("pos", [P, TPB])
        onehot = sb("onehot", [P, TPB, LAND], BF16)
        xb = sb("xb", [P, BLK])
        qk, rest = sb("qk", [P, TPB * H2, HD]), sb("rest", [P, TPB * H2, HD])
        part = [sb(f"part{k}", [P, TPB * H2, HD], BF16) for k in range(3)]
        sq, sqrest = sb("sq", [P, TPB * H2]), sb("sqrest", [P, TPB * H2])
        sqpart = [sb(f"sqpart{k}", [P, TPB * H2], BF16) for k in range(3)]
        x6 = sb("x6", [P, TPB, H2, ROWS6], BF16)
        l6 = sb("l6", [P, TPB, HEADS, ROWS6], BF16)
        kT6 = sb("kT6", [P, PAIRS, BLK], BF16)
        land = sb("land", [P, PAIRS, P], BF16)
        kland = sb("kland", [P, PAIRS, LAND], BF16)
        vaug = sb("vaug", [P, TPB, PAIRS, 17])
        phi = sb("phi", [P, TPB, PAIRS, P])
        w_sb = sb("w", [LAND, HEADS, LAND])
        z_sb = sb("z", [P, PAIRS, HD + 1])
        ps = core.ps(name + "_ps", [P, 8, 512], ctx=ctx)
        block = ctx.enter_context(nc.Block())
        by_head = lambda a: a[:, :, :].rearrange("p (t h) d -> p t h d", t=TPB)
        one = lambda a: a[:, :].rearrange("p (t h o) -> p t h o", t=TPB, o=1)
        BANK_OF_TURN = (4, 5, 6, 7, 0, 1, 2, 3)

        @block.sync
        def _(sp):
            for dst, src in ((wqkv[:, :], A["L0_wqkv"]), (bias[:, :], A["L0_bqkv"].to_broadcast([P, 3 * D])),
                             (identb[:, :], A["c_masks"][2]), (regeye[:, :], A["c_regeye"]),
                             (temp[:, :], A["L0_temp"].to_broadcast([P, 1])),
                             (idx_i[:, :], A["L0_idx"].to_broadcast([P, LAND]))):
                sp.dma_start(dst, src).then_inc(S["loaded"], 16)
            sp.sem_inc(S["seq_done"], 1)
            with sp.Fori(0, BATCH) as b:
                sp.wait_ge(S["w_full"], b + 1)
                sp.dma_start(w_dram[bass.ds(b * HEADS, HEADS)].rearrange("h i k -> i h k"), w_sb[:, :, :])\
                  .then_inc(S["saved"], 16)
                sp.wait_ge(S["z_full"], b + 1)
                for h2 in range(2):
                    zd = z_dram[bass.ds(b, 1), :, h2, :, :].rearrange("o a k c -> k (o a) c")
                    sp.dma_start(zd, z_sb[64 * h2:64 * h2 + 64, :, :]).then_inc(S["saved"], 16)
                sp.wait_ge(S["saved"], b * 48 + 48)
                sp.sem_inc(S["seq_done"], 1)

        @block.gpsimd
        def _(pool):
            pool.iota(pos_i[:, :], [[P, TPB]], base=0, channel_multiplier=1)
            pool.memset(x6[:, :, :, :], 0.0)
            pool.memset(l6[:, :, :, :], 0.0)
            pool.memset(land[:, :, :], 0.0)
            pool.drain()
            pool.memset(x6[:, :, :, 51:54], 1.0)
            pool.memset(l6[:, :, :, 48:51], 1.0)
            pool.memset(vaug[:, :, :, 16:17], 1.0)
            pool.drain()
            pool.sem_inc(S["const_ready"], 1)
            with pool.Fori(0, BATCH) as b:
                pool.wait_ge(S["seq_done"], b + 1)
                pool.tensor_copy(xb[:, :], core.xT[:, bass.ds(b * BLK, BLK)]).then_inc(S["xb_ready"], 1)

        @block.tensor
        def _(pe):
            pe.wait_ge(S["onehot_ready"], 1)
            with pe.Fori(0, BATCH) as b:
                pe.wait_ge(S["xb_ready"], b + 1)
                for t in range(TPB):
                    last = pe.matmul(ps[:, t, 0:3 * D], xb[:, t * P:(t + 1) * P], wqkv[:, :], start=True, stop=True)
                last.then_inc(S["qkv_ready"], 1)
                pe.wait_ge(S["parts_ready"], b + 1)
                for n in range(8):
                    for a in range(2):
                        for t in range(TPB):
                            at = (a * TPB + t) * P
                            last = pe.transpose(
                                ps[:, BANK_OF_TURN[n], :].bitcast(BF16)[:, at:at + P],
                                x6[:, t, 4 * n + 2 * a:4 * n + 2 * a + 2, :].rearrange("p h r -> p (h r)"), identb[:, :])
                    last.then_inc(S["turned"], 1)
                pe.wait_ge(S["copied"], b * 8 + 2)
                for bank, src, h0 in ((4, l6, 0), (5, x6, HEADS)):
                    for a in range(PAIRS):
                        for t in range(TPB):
                            last = pe.matmul(ps[:, bank, a * LAND:(a + 1) * LAND],
                                             src[:, t, h0 + 2 * a:h0 + 2 * a + 2, :].rearrange("p h r -> p (h r)"),
                                             onehot[:, t, :], start=(t == 0), stop=(t == TPB - 1))
                last.then_inc(S["gathered"], 1)
                pe.wait_ge(S["land_ready"], b + 1)
                pe.wait_ge(S["copied"], b * 8 + 4)
                for a in range(PAIRS):
                    last = pe.matmul(ps[0:LAND, 6 + a // 4, (a % 4) * P:(a % 4 + 1) * P], kland[:, a, :], land[:, a, :],
                                     start=True, stop=True)
                last.then_inc(S["w_ready"], 1)
                pe.wait_ge(S["copied"], b * 8 + 8)
                for t in range(TPB):
                    if t >= 2:
                        pe.wait_ge(S["clamped"], b * TPB + t - 1)
                    for a in range(PAIRS):
                        last = pe.matmul(ps[:, 2 * (t % 2) + a // 4, (a % 4) * P:(a % 4 + 1) * P],
                                         kT6[:, a, t * P:(t + 1) * P], land[:, a, :], start=True, stop=True)
                    last.then_inc(S["dist_ready"], 1)
                pe.wait_ge(S["phi_ready"], b * TPB + TPB)
                for a in range(PAIRS):
                    for t in range(TPB):
                        last = pe.matmul(ps[:, 4, a * 32:a * 32 + 17], phi[:, t, a, :], vaug[:, t, a, :],
                                         start=(t == 0), stop=(t == TPB - 1))
                last.then_inc(S["z_ready"], 1)

        @block.scalar
        def _(act):
            act.wait_ge(S["onehot_ready"], 1)
            with act.Fori(0, BATCH) as b:
                for n in range(8):
                    act.wait_ge(S["turned"], b * 8 + n + 1)
                    src = ps[:, BANK_OF_TURN[n], :].bitcast(BF16)
                    if n < 4:
                        dst = qT_all[:, bass.ds(b * (PAIRS * BLK) + n * 2 * BLK, 2 * BLK)]
                    else:
                        dst = kT6[:, 2 * (n - 4):2 * (n - 4) + 2, :].rearrange("p a k -> p (a k)")
                    act.activation(dst, src, ACT.Copy).then_inc(S["copied"], 1)
                act.wait_ge(S["w_clamped"], b + 1)
                act.activation(w_sb[:, :, :], w_sb[:, :, :], ACT.Exp, scale=scale[0:LAND, 0:1]).then_inc(S["w_exped"], 1)
                for t in range(TPB):
                    act.wait_ge(S["clamped"], b * TPB + t + 1)
                    act.activation(phi[:, t, :, :], phi[:, t, :, :], ACT.Exp, scale=scale[:, 0:1])\
                       .then_inc(S["phi_ready"], 1)

        @block.vector
        def _(dve):
            dve.wait_ge(S["loaded"], 96)
            dve.wait_ge(S["const_ready"], 1)
            dve.tensor_copy(idx[:, :], idx_i[:, :])
            dve.tensor_copy(pos[:, :], pos_i[:, :])
            dve.reciprocal(scale[:, :], temp[:, :])
            dve.drain()
            dve.tensor_scalar(neg[:, :], idx[:, :], 0.0, float(SEQ), ALU.is_lt, ALU.mult)
            dve.tensor_scalar(scale[:, :], scale[:, :], -1.0, None, ALU.mult)
            dve.drain()
            dve.tensor_tensor(idx[:, :], idx[:, :], neg[:, :], ALU.add)
            dve.drain()
            dve.tensor_scalar(idx[:, :], idx[:, :], 0.0, float(SEQ - 1), ALU.max, ALU.min)
            dve.drain()
            for t in range(TPB):
                last = dve.tensor_scalar(onehot[:, t, :], idx[:, :], pos[:, t:t + 1], None, ALU.is_equal)
            last.then_inc(S["onehot_ready"], 1)
            with dve.Fori(0, BATCH) as b:
                dve.wait_ge(S["qkv_ready"], b + 1)
                for t in range(TPB):
                    dve.tensor_tensor(by_head(qk)[:, t, :, :].rearrange("p h d -> p (h d)"), ps[:, t, 0:2 * D],
                                      bias[:, 0:2 * D], ALU.add)
                    dve.tensor_tensor(vaug[:, t, :, 0:16], ps[:, t, 2 * D:3 * D].rearrange("p (a c) -> p a c", a=PAIRS),
                                      bias[:, 2 * D:3 * D].rearrange("p (a c) -> p a c", a=PAIRS), ALU.add)
                dve.drain()
                dve.tensor_tensor(rest[:, :, :], qk[:, :, :], qk[:, :, :], ALU.mult)
                dve.tensor_copy(part[0][:, :, :], qk[:, :, :])
                dve.drain()
                dve.tensor_reduce(sq[:, :], rest[:, :, :], AX.X, ALU.add)
                dve.drain()
                dve.tensor_tensor(rest[:, :, :], qk[:, :, :], part[0][:, :, :], ALU.subtract)
                dve.tensor_copy(sqpart[0][:, :], sq[:, :])
                dve.drain()
                dve.tensor_copy(part[1][:, :, :], rest[:, :, :])
                dve.tensor_tensor(sqrest[:, :], sq[:, :], sqpart[0][:, :], ALU.subtract)
                dve.drain()
                dve.tensor_tensor(part[2][:, :, :], rest[:, :, :], part[1][:, :, :], ALU.subtract)
                dve.tensor_copy(sqpart[1][:, :], sqrest[:, :])
                dve.drain()
                dve.tensor_tensor(sqpart[2][:, :], sqrest[:, :], sqpart[1][:, :], ALU.subtract)
                dve.drain()
                for n in range(6):
                    cut = slice(n * HD, (n + 1) * HD)
                    dve.tensor_copy(x6[:, :, :, cut], by_head(part[Q_PARTS[n]]))
                    dve.tensor_scalar(l6[:, :, :, cut], by_head(part[K_PARTS[n]])[:, :, HEADS:H2, :], -2.0, None, ALU.mult)
                for k in range(3):
                    dve.tensor_copy(x6[:, :, :, 48 + k:49 + k], one(sqpart[k]))
                    last = dve.tensor_copy(l6[:, :, :, 51 + k:52 + k], one(sqpart[k])[:, :, HEADS:H2, :])
                last.then_inc(S["parts_ready"], 1)
                dve.wait_ge(S["gathered"], b + 1)
                for h2 in range(2):
                    rows, cols = slice(64 * h2, 64 * h2 + 64), slice(LAND * h2, LAND * h2 + LAND)
                    dve.tensor_copy(land[rows, :, cols], ps[rows, 4, :].rearrange("p (a k) -> p a k", a=PAIRS))
                dve.tensor_copy(kland[:, :, :], ps[:, 5, :].rearrange("p (a k) -> p a k", a=PAIRS)).then_inc(S["land_ready"], 1)
                dve.drain()
                dve.tensor_copy(land_all[:, bass.ds(b * (PAIRS * P), PAIRS * P)],
                                land[:, :, :].rearrange("p a k -> p (a k)"))
                dve.wait_ge(S["w_ready"], b + 1)
                dve.tensor_scalar(w_sb[:, :, :].rearrange("p h k -> p (h k)"),
                                  ps[0:LAND, 6:8, :].rearrange("p n k -> p (n k)"), 0.0, None, ALU.max)\
                   .then_inc(S["w_clamped"], 1)
                for t in range(TPB):
                    dve.wait_ge(S["dist_ready"], b * TPB + t + 1)
                    z = 2 * (t % 2)
                    dve.tensor_scalar(phi[:, t, :, :].rearrange("p a k -> p (a k)"),
                                      ps[:, z:z + 2, :].rearrange("p n k -> p (n k)"), 0.0, None, ALU.max)\
                       .then_inc(S["clamped"], 1)
                dve.wait_ge(S["w_exped"], b + 1)
                dve.tensor_tensor(w_sb[:, :, :], w_sb[:, :, :],
                                  regeye[:, :].rearrange("p (o k) -> p o k", o=1).to_broadcast([LAND, HEADS, LAND]),
                                  ALU.add).then_inc(S["w_full"], 1)
                dve.wait_ge(S["z_ready"], b + 1)
                zv = ps[:, 4, 0:PAIRS * 32].rearrange("p (a c) -> p a c", a=PAIRS)
                for h2 in range(2):
                    rows = slice(64 * h2, 64 * h2 + 64)
                    dve.tensor_copy(z_sb[rows, :, 0:HD], zv[rows, :, HD * h2:HD * h2 + HD])
                    last = dve.tensor_copy(z_sb[rows, :, HD:HD + 1], zv[rows, :, 16:17])
                last.then_inc(S["z_full"], 1)


def solve(core, name, w_dram, z_dram, y_dram):
    nc = core.nc
    OWN = 57
    loaded, pivot_ready = core.sem(name + "_loaded"), core.sem(name + "_pivot_ready")
    pool_done, solved, saved = core.sem(name + "_pool_done"), core.sem(name + "_solved"), core.sem(name + "_saved")
    with ExitStack() as ctx:
        sb = lambda n, s, dt=F32: core.sb(name + "_" + n, s, dt, ctx)
        m, rinv = sb("m", [P, LAND, COLS]), sb("rinv", [P, LAND])
        y = sb("y", [P, LAND, HD + 1])
        outer_p = sb("outer_p", [P, LAND, COLS - OWN])
        row_ps = core.ps(name + "_row", [P, 512], ctx=ctx)
        outer = core.ps(name + "_outer", [P, 7 * 512], ctx=ctx)
        block = ctx.enter_context(nc.Block())

        def outer_product(eng, out, col, row, shape):
            return eng.tensor_tensor(out, col.to_broadcast(shape),
                                     row.rearrange("p (o c) -> p o c", o=1).to_broadcast(shape), ALU.mult)

        @block.sync
        def _(sp):
            sp.dma_start(m[:, :, 0:LAND], w_dram).then_inc(loaded, 16)
            sp.dma_start(m[:, :, LAND:COLS], z_dram.rearrange("b a h k c -> (b a h) k c")).then_inc(loaded, 16)
            sp.wait_ge(solved, 1)
            sp.dma_start(y_dram.rearrange("b a h k c -> (b a h) k c"), y[:, :, :]).then_inc(saved, 16)
            sp.wait_ge(saved, 16)

        @block.vector
        def _(dve):
            dve.wait_ge(loaded, 32)
            for k in range(LAND):
                end = OWN if k < OWN else COLS
                if k == OWN:
                    dve.wait_ge(pool_done, OWN)
                dve.reciprocal(rinv[:, k:k + 1], m[:, k, k:k + 1]).then_inc(pivot_ready, 1)
                dve.wait_ge(pivot_ready, k + 1)
                w = end - k - 1
                if w == 0:
                    continue
                dve.tensor_scalar(row_ps[:, 0:w], m[:, k, k + 1:end], rinv[:, k:k + 1], None, ALU.mult)
                dve.drain()
                n = LAND - 1 - k
                at = 0
                while at < n:
                    rows = min(n - at, 7 * 512 // w)
                    shape = [P, rows, w]
                    r0 = k + 1 + at
                    out = outer[:, 0:rows * w].rearrange("p (r c) -> p r c", c=w)
                    outer_product(dve, out, m[:, r0:r0 + rows, k:k + 1], row_ps[:, 0:w], shape)
                    dve.drain()
                    dve.tensor_tensor(m[:, r0:r0 + rows, k + 1:end], m[:, r0:r0 + rows, k + 1:end], out, ALU.subtract)
                    dve.drain()
                    at += rows
                dve.tensor_copy(m[:, k, k + 1:end], row_ps[:, 0:w])
                dve.drain()
            for k in range(LAND - 1, 0, -1):
                shape = [P, k, HD + 1]
                out = outer[:, 0:k * (HD + 1)].rearrange("p (r c) -> p r c", c=HD + 1)
                outer_product(dve, out, m[:, 0:k, k:k + 1], m[:, k, LAND:COLS], shape)
                dve.drain()
                dve.tensor_tensor(m[:, 0:k, LAND:COLS], m[:, 0:k, LAND:COLS], out, ALU.subtract)
                dve.drain()
            dve.tensor_copy(y[:, :, :], m[:, :, LAND:COLS]).then_inc(solved, 1)

        @block.gpsimd
        def _(pool):
            pool.wait_ge(loaded, 32)
            for k in range(OWN):
                pool.wait_ge(pivot_ready, k + 1)
                pool.tensor_scalar(m[:, k, OWN:COLS], m[:, k, OWN:COLS], rinv[:, k:k + 1], None, ALU.mult)
                pool.drain()
                n = LAND - 1 - k
                shape = [P, n, COLS - OWN]
                outer_product(pool, outer_p[:, 0:n, :], m[:, k + 1:LAND, k:k + 1], m[:, k, OWN:COLS], shape)
                pool.drain()
                rest = m[:, k + 1:LAND, OWN:COLS]
                pool.tensor_tensor(rest, rest, outer_p[:, 0:n, :], ALU.subtract)
                pool.drain()
                pool.sem_inc(pool_done, 1)


def landmark_outputs(core, name, A, qT_all, land_all, y_dram):
    nc = core.nc
    PAIRS = HEADS // 2
    S = {n: core.sem(f"{name}_{n}") for n in (
        "loaded", "const_ready", "y_loaded", "land_ready", "dist_ready", "clamped", "phi_ready", "used", "o_ready", "o_copied",
        "o_turned", "o_normed", "a_turned", "a_copied", "y_ready", "x_added")}
    with ExitStack() as ctx:
        sb = lambda n, s, dt=F32: core.sb(name + "_" + n, s, dt, ctx)
        wo, bo, ones = sb("wo", [P, D]), sb("bo", [1, D]), sb("ones", [1, P])
        temp, scale = sb("temp", [P, 1]), sb("scale", [P, 1])
        land = sb("land", [P, PAIRS, P], BF16)
        y2 = sb("y2", [P, PAIRS, 32])
        phi = sb("phi", [P, 2, BLK])
        oT, att, aT = sb("oT", [P, 2, BLK]), sb("att", [P, TPB, HEADS, HD]), sb("aT", [P, BLK])
        den = sb("den", [P, 2, TPB, 8])
        ps_d = core.ps(name + "_ps_d", [P, 2, 512], ctx=ctx)
        ps_o = core.ps(name + "_ps_o", [P, 2, 512], ctx=ctx)
        ps_t = core.ps(name + "_ps_t", [P, 2, 512], ctx=ctx)
        ps_m = core.ps(name + "_ps_m", [P, 512], ctx=ctx)
        block = ctx.enter_context(nc.Block())

        @block.sync
        def _(sp):
            sp.dma_start(wo[:, :], A["L0_wo"]).then_inc(S["loaded"], 16)
            sp.dma_start(bo[:, :], A["L0_bo"]).then_inc(S["loaded"], 16)
            sp.dma_start(temp[:, :], A["L0_temp"].to_broadcast([P, 1])).then_inc(S["loaded"], 16)
            sp.wait_ge(S["const_ready"], 1)
            with sp.Fori(0, BATCH) as b:
                sp.wait_ge(S["x_added"], b + 1)
                for h2 in range(2):
                    src = y_dram[bass.ds(b, 1), :, h2, :, :].rearrange("o a k c -> k (o a) c")
                    sp.dma_start(y2[64 * h2:64 * h2 + 64, :, 16 * h2:16 * h2 + HD + 1], src).then_inc(S["y_loaded"], 16)

        @block.gpsimd
        def _(pool):
            pool.memset(y2[:, :, :], 0.0)
            pool.memset(ones[:, :], 1.0)
            pool.drain()
            pool.sem_inc(S["const_ready"], 1)
            with pool.Fori(0, BATCH) as b:
                pool.wait_ge(S["x_added"], b + 1)
                pool.tensor_copy(land[:, :, :].rearrange("p a k -> p (a k)"),
                                 land_all[:, bass.ds(b * (PAIRS * P), PAIRS * P)]).then_inc(S["land_ready"], 1)

        @block.tensor
        def _(pe):
            pe.wait_ge(S["loaded"], 48)
            pe.wait_ge(S["const_ready"], 1)
            with pe.Fori(0, BATCH) as b:
                pe.wait_ge(S["land_ready"], b + 1)

                def outputs(a):
                    if a == 0:
                        pe.wait_ge(S["y_loaded"], b * 32 + 32)
                    pe.wait_ge(S["phi_ready"], b * PAIRS + a + 1)
                    pe.matmul(ps_o[32 * (a % 4):32 * (a % 4) + 32, a // 4, :], y2[:, a, :], phi[:, a % 2, :],
                              start=True, stop=True).then_inc(S["used"], 1)

                for a in range(PAIRS):
                    if a >= 2:
                        pe.wait_ge(S["clamped"], b * PAIRS + a - 1)
                    pe.matmul(ps_d[:, a % 2, :], land[:, a, :], qT_all[:, bass.ds((b * PAIRS + a) * BLK, BLK)],
                              start=True, stop=True).then_inc(S["dist_ready"], 1)
                    if a >= 1:
                        outputs(a - 1)
                outputs(PAIRS - 1)
                for g in range(2):
                    pe.wait_ge(S["o_copied"], b * 2 + g + 1)
                    for t in range(TPB):
                        last = pe.transpose(ps_t[:, g, t * P:(t + 1) * P], oT[:, g, t * P:(t + 1) * P], core.ident[:, :])
                    last.then_inc(S["o_turned"], 1)
                pe.wait_ge(S["o_normed"], b * 2 + 2)
                for t in range(TPB):
                    last = pe.transpose(ps_m[:, t * P:(t + 1) * P], att[:, t, :, :].rearrange("p h d -> p (h d)"),
                                        core.ident[:, :])
                last.then_inc(S["a_turned"], 1)
                pe.wait_ge(S["a_copied"], b + 1)
                for t in range(TPB):
                    pe.matmul(ps_m[:, t * P:(t + 1) * P], aT[:, t * P:(t + 1) * P], wo[:, :], start=True, stop=False)
                    last = pe.matmul(ps_m[:, t * P:(t + 1) * P], ones[:, :], bo[:, :], start=False, stop=True)
                last.then_inc(S["y_ready"], 1)

        @block.scalar
        def _(act):
            with act.Fori(0, BATCH) as b:
                for a in range(PAIRS):
                    act.wait_ge(S["clamped"], b * PAIRS + a + 1)
                    act.activation(phi[:, a % 2, :], phi[:, a % 2, :], ACT.Exp, scale=scale[:, 0:1])\
                       .then_inc(S["phi_ready"], 1)

        @block.vector
        def _(dve):
            dve.wait_ge(S["loaded"], 48)
            dve.reciprocal(scale[:, :], temp[:, :])
            dve.drain()
            dve.tensor_scalar(scale[:, :], scale[:, :], -1.0, None, ALU.mult)
            dve.drain()
            dve.sem_inc(S["x_added"], 1)
            with dve.Fori(0, BATCH) as b:
                for a in range(PAIRS):
                    dve.wait_ge(S["dist_ready"], b * PAIRS + a + 1)
                    if a >= 2:
                        dve.wait_ge(S["used"], b * PAIRS + a - 1)
                    dve.tensor_scalar(phi[:, a % 2, :], ps_d[:, a % 2, :], 0.0, None, ALU.max).then_inc(S["clamped"], 1)
                    if a == 5:
                        dve.wait_ge(S["used"], b * PAIRS + 4)
                        dve.tensor_copy(oT[:, 0, :], ps_o[:, 0, :]).then_inc(S["o_copied"], 1)
                dve.wait_ge(S["used"], b * PAIRS + 8)
                dve.tensor_copy(oT[:, 1, :], ps_o[:, 1, :]).then_inc(S["o_copied"], 1)
                for g in range(2):
                    dve.wait_ge(S["o_turned"], b * 2 + g + 1)
                    bh = ps_t[:, g, :].rearrange("p (t i c) -> p t i c", t=TPB, i=8)
                    dve.tensor_scalar(den[:, g, :, :], bh[:, :, :, HD:HD + 1].rearrange("p t i o -> p t (i o)"), 1e-10,
                                      None, ALU.max)
                    dve.drain()
                    dve.reciprocal(den[:, g, :, :], den[:, g, :, :])
                    dve.drain()
                    dve.tensor_tensor(att[:, :, 8 * g:8 * g + 8, :], bh[:, :, :, 0:HD],
                                      den[:, g, :, :].rearrange("p t (i o) -> p t i o", o=1)
                                      .to_broadcast([P, TPB, 8, HD]), ALU.mult).then_inc(S["o_normed"], 1)
                dve.wait_ge(S["a_turned"], b + 1)
                dve.tensor_copy(aT[:, :], ps_m[:, :]).then_inc(S["a_copied"], 1)
                dve.wait_ge(S["y_ready"], b + 1)
                xr = core.x[:, bass.ds(b * TPB, TPB), :]
                dve.tensor_tensor(xr, xr, ps_m[:, :].rearrange("p (t d) -> p t d", t=TPB), ALU.add)\
                   .then_inc(S["x_added"], 1)


def layer0_attention(core, A):
    layernorm(core, "l0a_ln")
    with ExitStack() as ctx:
        qT_all = core.sb("l0a_qT_all", [P, BATCH * (HEADS // 2) * BLK], BF16, ctx)
        land_all = core.sb("l0a_land_all", [P, BATCH * (HEADS // 2) * P], BF16, ctx)
        w_dram = core.dram("l0a_w_dram", [BATCH * HEADS, LAND, LAND])
        z_dram = core.dram("l0a_z_dram", [BATCH, HEADS // 2, 2, LAND, HD + 1])
        y_dram = core.dram("l0a_y_dram", [BATCH, HEADS // 2, 2, LAND, HD + 1])
        landmark_sums(core, "l0s", A, qT_all, land_all, w_dram, z_dram)
        solve(core, "l0v", w_dram, z_dram, y_dram)
        landmark_outputs(core, "l0o", A, qT_all, land_all, y_dram)


RHEADS, RD, CHUNK = 4, 32, 32
CHUNKS = SEQ // CHUNK


def chunk_products(core, name, A, store):
    nc = core.nc
    S = {n: core.sem(f"{name}_{n}") for n in (
        "loaded", "const_ready", "taps_ready", "seq_done", "conv_ready", "ctrl_ready", "silu_done", "square_done", "gates_done",
        "spread_ready", "ss_ready", "norm_ready", "recip_ready", "r_turned", "r_copied", "expanded", "kdiag_ready",
        "prod_ready", "l_ready", "all_read", "l_saved")}
    with ExitStack() as ctx:
        sb = lambda n, s, dt=F32: core.sb(name + "_" + n, s, dt, ctx)
        w_in, taps, w_taps = sb("w_in", [P, 3, D]), sb("taps", [P, 3, 4, D]), sb("w_taps", [P, 3, 4, D])
        w_ctrl, b8, bog = sb("w_ctrl", [P, 8 + D]), sb("b8", [8, 1]), sb("bog", [P, 1])
        chunk_c = sb("chunk_c", [P, 4, SEQ])
        ones4, pick_ab, pick_r = sb("ones4", [P, RHEADS]), sb("pick_ab", [8, 2, P]), sb("pick_r", [32, 8, P])
        qkv_s, sq = sb("qkv_s", [P, 3, SEQ]), sb("sq", [P, 2, SEQ])
        gates8 = sb("gates8", [8, SEQ])
        a_all, a_in, a_start, b_all = (sb(n, [P, SEQ]) for n in ("a_all", "a_in", "a_start", "b_all"))
        dec, gam, dec_b, gam_b = (sb(n, [P, SEQ]) for n in ("dec", "gam", "dec_b", "gam_b"))
        nrm, rT = sb("nrm", [P, 32]), sb("rT", [32, P])
        kq_n, ktok = sb("kq_n", [P, 2, SEQ]), sb("ktok", [P, SEQ])
        kdiag = sb("kdiag", [P, CHUNKS, P])
        l_sb = sb("l_sb", [P, CHUNKS, CHUNK])
        ps = core.ps(name + "_ps", [P, 8, 512], ctx=ctx)
        block = ctx.enter_context(nc.Block())
        chunks = lambda a: a.rearrange("p (c t) -> p c t", t=CHUNK)
        NOT_START, START, SAME, BEFORE = range(4)

        @block.sync
        def _(sp):
            for dst, src in ((w_in[:, :, :], A["L2_w_in"]), (taps[:, :, :, :].rearrange("p s j f -> p (s j f)"), A["L2_taps"].to_broadcast([P, 12 * D])),
                             (w_ctrl[:, :], A["L2_w_ctrl"]), (b8[:, :], A["L2_b8"]), (bog[:, :], A["L2_bog"]),
                             (chunk_c[:, :, :], A["c_chunk"]), (ones4[:, :], A["c_ones4"]), (pick_ab[:, :, :], A["c_pick_ab"]),
                             (pick_r[:, :, :], A["c_pick_r"])):
                sp.dma_start(dst, src).then_inc(S["loaded"], 16)
            sp.sem_inc(S["seq_done"], 1)
            with sp.Fori(0, BATCH) as b:
                sp.wait_ge(S["l_ready"], b + 1)
                for h in range(RHEADS):
                    dst = store.l_dram[bass.ds(b, 1), h].rearrange("o c s t -> (o s) c t")
                    sp.dma_start(dst, l_sb[32 * h:32 * h + 32, :, :]).then_inc(S["l_saved"], 16)
                sp.wait_ge(S["l_saved"], b * 64 + 64)
                sp.wait_ge(S["all_read"], b + 1)
                sp.sem_inc(S["seq_done"], 1)

        ALL = 16 * 9

        @block.gpsimd
        def _(pool):
            pool.memset(kdiag[:, :, :], 0.0)
            pool.drain()
            pool.sem_inc(S["const_ready"], 1)

        @block.tensor
        def _(pe):
            pe.wait_ge(S["taps_ready"], 1)
            pe.wait_ge(S["loaded"], ALL)
            with pe.Fori(0, BATCH) as b:
                pe.wait_ge(S["seq_done"], b + 1)
                for s in (1, 0, 2):
                    for j in range(4):
                        last = pe.matmul(ps[:, s, j:SEQ], w_taps[:, s, j, :], core.xT[:, bass.ds(b * SEQ, SEQ - j)],
                                         start=(j == 0), stop=(j == 3))
                    last.then_inc(S["conv_ready"], 1)
                xb = core.xT[:, bass.ds(b * SEQ, SEQ)]
                pe.matmul(ps[0:8, 3, :], w_ctrl[:, 0:8], xb, start=True, stop=True)
                pe.matmul(ps[:, 4, :], w_ctrl[:, 8:8 + D], xb, start=True, stop=True).then_inc(S["ctrl_ready"], 1)
                for s in range(2):
                    pe.wait_ge(S["square_done"], b * 2 + s + 1)
                    for t in range(TPB):
                        at = (s * TPB + t) * RHEADS
                        last = pe.matmul(ps[:, 7, at:at + RHEADS], sq[:, s, t * P:(t + 1) * P], ones4[:, :],
                                         start=True, stop=True)
                last.then_inc(S["ss_ready"], 1)
                pe.wait_ge(S["gates_done"], b + 1)
                for k in range(2):
                    last = pe.matmul(ps[:, 5 + k, :], pick_ab[:, k, :], gates8[:, :], start=True, stop=True)
                last.then_inc(S["spread_ready"], 1)
                pe.wait_ge(S["recip_ready"], b + 1)
                pe.transpose(ps[0:32, 7, P:2 * P], nrm[:, :], core.ident[:, :]).then_inc(S["r_turned"], 1)
                pe.wait_ge(S["r_copied"], b + 1)
                pe.wait_ge(S["silu_done"], b * 3 + 3)
                for s in range(2):
                    for t in range(TPB):
                        last = pe.matmul(ps[:, s, t * P:(t + 1) * P], pick_r[:, s * TPB + t, :], rT[:, :],
                                         start=True, stop=True)
                last.then_inc(S["expanded"], 1)
                pe.wait_ge(S["kdiag_ready"], b + 1)
                for c in range(CHUNKS):
                    last = pe.matmul(ps[:, 2 + c // 8, (c % 8) * 64:(c % 8 + 1) * 64], kdiag[:, c, :],
                                     kq_n[:, :, c * CHUNK:(c + 1) * CHUNK], start=True, stop=True)
                last.then_inc(S["prod_ready"], 1)

        @block.scalar
        def _(act):
            act.wait_ge(S["loaded"], ALL)
            with act.Fori(0, BATCH) as b:
                for n, s in enumerate((1, 0, 2)):
                    act.wait_ge(S["conv_ready"], b * 3 + n + 1)
                    act.activation(qkv_s[:, s, :], ps[:, s, :], ACT.Silu).then_inc(S["silu_done"], 1)
                act.drain()
                for n, s in enumerate((1, 0)):
                    act.activation(sq[:, n, :], qkv_s[:, s, :], ACT.Square).then_inc(S["square_done"], 1)
                act.wait_ge(S["ctrl_ready"], b + 1)
                act.activation(gates8[:, :], ps[0:8, 3, :], ACT.Sigmoid, bias=b8[:, 0:1]).then_inc(S["gates_done"], 1)
                act.activation(store.og[:, bass.ds(b * SEQ, SEQ)], ps[:, 4, :], ACT.Sigmoid, bias=bog[:, 0:1])
                act.wait_ge(S["ss_ready"], b + 1)
                act.activation(nrm[:, :], ps[:, 7, 0:32], ACT.Sqrt).then_inc(S["norm_ready"], 1)

        @block.vector
        def _(dve):
            dve.wait_ge(S["loaded"], ALL)
            dve.wait_ge(S["const_ready"], 1)
            for s in range(3):
                last = dve.tensor_tensor(w_taps[:, s, :, :], taps[:, s, :, :],
                                         w_in[:, s, :].rearrange("p (o f) -> p o f", o=1).to_broadcast([P, 4, D]), ALU.mult)
            last.then_inc(S["taps_ready"], 1)
            with dve.Fori(0, BATCH) as b:
                dve.wait_ge(S["norm_ready"], b + 1)
                dve.tensor_scalar(nrm[:, :], nrm[:, :], 1e-6, None, ALU.max)
                dve.drain()
                dve.reciprocal(nrm[:, :], nrm[:, :]).then_inc(S["recip_ready"], 1)
                dve.wait_ge(S["spread_ready"], b + 1)
                dve.tensor_scalar(a_all[:, :], ps[:, 5, :], 0.01, None, ALU.add)
                dve.tensor_copy(b_all[:, :], ps[:, 6, :])
                dve.wait_ge(S["r_turned"], b + 1)
                dve.tensor_copy(rT[:, :], ps[0:32, 7, P:2 * P]).then_inc(S["r_copied"], 1)
                dve.drain()
                dve.tensor_tensor(a_in[:, :], a_all[:, :], chunk_c[:, NOT_START, :], ALU.mult)
                dve.tensor_tensor(a_start[:, :], a_all[:, :], chunk_c[:, START, :], ALU.mult)
                dve.drain()
                dve.tensor_tensor_scan(dec[:, :], a_in[:, :], chunk_c[:, SAME, :], 0.0, ALU.mult, ALU.add)
                dve.tensor_tensor_scan(gam[:, :], a_in[:, :], a_start[:, :], 0.0, ALU.mult, ALU.add)
                dve.drain()
                dve.wait_ge(S["expanded"], b + 1)
                dve.tensor_tensor(kq_n[:, 0, :], qkv_s[:, 1, :], ps[:, 0, :], ALU.mult)
                dve.tensor_tensor(kq_n[:, 1, :], qkv_s[:, 0, :], ps[:, 1, :], ALU.mult)
                dve.tensor_tensor(dec_b[:, :], dec[:, :], b_all[:, :], ALU.mult)
                dve.tensor_tensor(gam_b[:, :], gam[:, :], b_all[:, :], ALU.mult)
                dve.drain()
                for h in range(RHEADS):
                    rows = slice(32 * h, 32 * h + 32)
                    last = dve.tensor_copy(kdiag[rows, :, 32 * h:32 * h + 32], chunks(kq_n[rows, 0, :]))
                last.then_inc(S["kdiag_ready"], 1)
                dve.tensor_tensor(dec_b[:, :], dec_b[:, :], chunk_c[:, BEFORE, :], ALU.mult)
                dve.transpose(ktok[:, :], kq_n[:, 0, :])
                dve.tensor_tensor(store.kq[:, :, bass.ds(b, 1), 0:32], chunks(kq_n[:, 0, :]), chunks(gam_b[:, :]), ALU.mult)
                dve.tensor_tensor(store.kq[:, :, bass.ds(b, 1), 32:64], chunks(kq_n[:, 1, :]), chunks(gam[:, :]), ALU.mult)
                dve.tensor_tensor(store.vb[:, :, bass.ds(b, 1), :], chunks(qkv_s[:, 2, :]), chunks(b_all[:, :]), ALU.mult)
                dve.tensor_copy(store.last[:, :, bass.ds(b, 1)], chunks(gam[:, :])[:, :, CHUNK - 1:CHUNK])
                dve.drain()
                dve.tensor_tensor(store.ak[:, :, bass.ds(b, 1), 32:64], chunks(ktok[:, :]),
                                  chunks(dec[:, :])[:, :, CHUNK - 1:CHUNK].to_broadcast([P, CHUNKS, CHUNK]), ALU.mult)
                dve.wait_ge(S["prod_ready"], b + 1)
                prod = ps[:, 2:4, :].rearrange("p n (c k) -> p (n c) k", k=64)
                dve.tensor_tensor(l_sb[:, :, :], prod[:, :, 0:32], chunks(dec_b[:, :]), ALU.mult).then_inc(S["l_ready"], 1)
                dve.tensor_tensor(store.ak[:, :, bass.ds(b, 1), 0:32], prod[:, :, 32:64], chunks(dec[:, :]), ALU.mult)\
                   .then_inc(S["all_read"], 1)


def invert_chunks(core, name, l_dram, t_dram):
    nc = core.nc
    SYS, MINE = 4, 3
    loaded, started, done, saved = (core.sem(f"{name}_{n}") for n in ("loaded", "started", "done", "saved"))
    with ExitStack() as ctx:
        sb = lambda n, s, dt=F32: core.sb(name + "_" + n, s, dt, ctx)
        l_sb, t_sb = sb("l", [P, SYS, CHUNK, CHUNK]), sb("t", [P, SYS, CHUNK, CHUNK])
        outer_p = sb("outer_p", [P, 1, CHUNK * CHUNK // 4 + CHUNK])
        outer = core.ps(name + "_outer", [P, MINE * 512], ctx=ctx)
        block = ctx.enter_context(nc.Block())

        def rows_off(eng, s0, n, buf):
            for j in range(CHUNK - 1):
                shape = [P, n, j + 1, CHUNK - 1 - j]
                size = shape[2] * shape[3]
                out = buf(n, size).rearrange("p s (l i) -> p s l i", i=shape[3])
                eng.tensor_tensor(out, l_sb[:, s0:s0 + n, j:j + 1, j + 1:CHUNK].to_broadcast(shape),
                                  t_sb[:, s0:s0 + n, 0:j + 1, j:j + 1].to_broadcast(shape), ALU.mult)
                eng.drain()
                rest = t_sb[:, s0:s0 + n, 0:j + 1, j + 1:CHUNK]
                eng.tensor_tensor(rest, rest, out, ALU.subtract)
                eng.drain()
            eng.sem_inc(done, 1)

        @block.sync
        def _(sp):
            sp.dma_start(l_sb[:, :, :, :], l_dram.rearrange("b h (g c) s t -> (b h g) c s t", c=SYS)).then_inc(loaded, 16)
            sp.wait_ge(done, 2)
            sp.dma_start(t_dram.rearrange("b h (g c) s t -> (b h g) c s t", c=SYS), t_sb[:, :, :, :]).then_inc(saved, 16)
            sp.wait_ge(saved, 16)

        @block.gpsimd
        def _(pool):
            pool.memset(t_sb[:, :, :, :], 0.0)
            pool.drain()
            pool.memset(t_sb[:, :, :, :].rearrange("p c s t -> p c (s t)")[:, :, 0:CHUNK * CHUNK:CHUNK + 1], 1.0)
            pool.drain()
            pool.sem_inc(started, 1)
            pool.wait_ge(loaded, 16)
            rows_off(pool, MINE, 1, lambda n, size: outer_p[:, :, 0:size])

        @block.vector
        def _(dve):
            dve.wait_ge(started, 1)
            dve.wait_ge(loaded, 16)
            rows_off(dve, 0, MINE, lambda n, size: outer[:, :].rearrange("p (s k) -> p s k", s=MINE)[:, :, 0:size])


def chunk_recurrence(core, name, store, t_dram, o_all):
    nc = core.nc
    HB = BATCH // 2
    S = {n: core.sem(f"{name}_{n}") for n in (
        "loaded", "const_ready", "operands", "step_done", "s_ready", "so_ready", "x_ready", "o1_done", "u_ready", "u_diag_a", "u_diag_v",
        "c_ready", "s_turned", "s_diag_a", "s_diag_v")}
    with ExitStack() as ctx:
        sb = lambda n, s, dt=F32: core.sb(name + "_" + n, s, dt, ctx)
        t_all = sb("t_all", [P, BATCH, CHUNKS, CHUNK])
        kq, ak = sb("kq", [P, 2, BATCH, 64]), sb("ak", [P, 2, BATCH, 64])
        tdiag = sb("tdiag", [P, 2, BATCH, P])
        state, turned = sb("state", [P, BATCH, RD]), sb("turned", [P, BATCH, RD])
        sdiag, udiag = sb("sdiag", [P, BATCH, P]), sb("udiag", [P, BATCH, P])
        xT, xtok, o1 = sb("xT", [P, BATCH, RD]), sb("xtok", [P, BATCH, RD]), sb("o1", [P, BATCH, RD])
        ps_a = core.ps(name + "_ps_a", [P, 2, 512], ctx=ctx)
        ps_u = core.ps(name + "_ps_u", [P, 2, 512], ctx=ctx)
        ps_c = core.ps(name + "_ps_c", [P, 2, 512], ctx=ctx)
        block = ctx.enter_context(nc.Block())
        of = lambda ps, g, w: ps[:, g, 0:HB * w].rearrange("p (b k) -> p b k", b=HB)

        @block.sync
        def _(sp):
            with sp.Fori(0, BATCH) as b:
                for h in range(RHEADS):
                    dst = t_all[32 * h:32 * h + 32, bass.ds(b, 1), :, :].rearrange("s o c t -> s (o c) t")
                    sp.dma_start(dst, t_dram[bass.ds(b, 1), h].rearrange("o c s t -> s (o c) t")).then_inc(S["loaded"], 16)

        @block.gpsimd
        def _(pool):
            pool.memset(sdiag[:, :, :], 0.0)
            pool.memset(udiag[:, :, :], 0.0)
            pool.memset(tdiag[:, :, :, :], 0.0)
            pool.memset(state[:, :, :], 0.0)
            pool.drain()
            pool.sem_inc(S["const_ready"], 1)

        @block.tensor
        def _(pe):
            pe.wait_ge(S["const_ready"], 1)
            with pe.Fori(0, CHUNKS // 2) as r:
                for k in range(2):
                    pe.wait_ge(S["operands"], r * 2 + k + 1)
                    for g in range(2):
                        n = 2 * k + g
                        pe.wait_ge(S["s_diag_a"], r * 4 + n + 1)
                        pe.wait_ge(S["s_diag_v"], r * 4 + n + 1)
                        for b in range(HB * g, HB * g + HB):
                            last = pe.matmul(of(ps_a, g, 64)[:, b - HB * g, :], sdiag[:, b, :], kq[:, k, b, :],
                                             start=True, stop=True)
                        last.then_inc(S["so_ready"], 1)
                    for g in range(2):
                        n = 2 * k + g
                        pe.wait_ge(S["x_ready"], r * 4 + n + 1)
                        for b in range(HB * g, HB * g + HB):
                            last = pe.matmul(of(ps_u, g, RD)[:, b - HB * g, :], tdiag[:, k, b, :], xtok[:, b, :],
                                             start=True, stop=True)
                        last.then_inc(S["u_ready"], 1)
                    for g in range(2):
                        n = 2 * k + g
                        pe.wait_ge(S["u_diag_a"], r * 4 + n + 1)
                        pe.wait_ge(S["u_diag_v"], r * 4 + n + 1)
                        for b in range(HB * g, HB * g + HB):
                            last = pe.matmul(of(ps_c, g, 64)[:, b - HB * g, :], udiag[:, b, :], ak[:, k, b, :],
                                             start=True, stop=True)
                        last.then_inc(S["c_ready"], 1)

        @block.scalar
        def _(act):
            act.wait_ge(S["const_ready"], 1)
            act.wait_ge(S["loaded"], 64 * BATCH)
            act.sem_inc(S["s_diag_a"], 2)
            with act.Fori(0, CHUNKS // 2) as r:
                def operands(k):
                    c = r * 2 + k
                    act.wait_ge(S["step_done"], r * 2 + k + 1)
                    act.activation(kq[:, k, :, :], store.kq[:, bass.ds(c, 1), :, :].rearrange("p o b k -> p (o b) k"), ACT.Copy)
                    act.activation(ak[:, k, :, :], store.ak[:, bass.ds(c, 1), :, :].rearrange("p o b k -> p (o b) k"), ACT.Copy)
                    for h in range(RHEADS):
                        rows = slice(32 * h, 32 * h + 32)
                        last = act.activation(tdiag[rows, k, :, 32 * h:32 * h + 32],
                                              t_all[rows, :, bass.ds(c, 1), :].rearrange("p b o k -> p b (o k)"), ACT.Copy)
                    act.drain()
                    act.sem_inc(S["operands"], 1)

                for k in range(2):
                    operands(k)
                    for g in range(2):
                        n = 2 * k + g
                        act.wait_ge(S["x_ready"], r * 4 + n + 1)
                        act.activation(o1[:, HB * g:HB * g + HB, :], of(ps_a, g, 64)[:, :, 32:64], ACT.Copy)\
                           .then_inc(S["o1_done"], 1)
                    for g in range(2):
                        n = 2 * k + g
                        act.wait_ge(S["u_ready"], r * 4 + n + 1)
                        for h in (2, 3):
                            rows = slice(32 * h, 32 * h + 32)
                            last = act.activation(udiag[rows, HB * g:HB * g + HB, 32 * h:32 * h + 32],
                                                  of(ps_u, g, RD)[rows, :, :], ACT.Copy)
                        last.then_inc(S["u_diag_a"], 1)
                    for g in range(2):
                        n = 2 * k + g
                        act.wait_ge(S["s_turned"], r * 4 + n + 1)
                        for h in (2, 3):
                            rows = slice(32 * h, 32 * h + 32)
                            last = act.activation(sdiag[rows, HB * g:HB * g + HB, 32 * h:32 * h + 32],
                                                  turned[rows, HB * g:HB * g + HB, :], ACT.Copy)
                        last.then_inc(S["s_diag_a"], 1)

        @block.vector
        def _(dve):
            dve.wait_ge(S["const_ready"], 1)
            dve.sem_inc(S["step_done"], 2)
            dve.sem_inc(S["s_diag_v"], 2)
            with dve.Fori(0, CHUNKS // 2) as r:
                for k in range(2):
                    c = r * 2 + k
                    for g in range(2):
                        n = 2 * k + g
                        mine = slice(HB * g, HB * g + HB)
                        dve.wait_ge(S["so_ready"], r * 4 + n + 1)
                        dve.tensor_tensor(xT[:, mine, :],
                                          store.vb[:, bass.ds(c, 1), mine, :].rearrange("p o b k -> p (o b) k"),
                                          of(ps_a, g, 64)[:, :, 0:32], ALU.subtract)
                        dve.drain()
                        dve.transpose(xtok[:, mine, :].rearrange("p b k -> p (b k)"),
                                      xT[:, mine, :].rearrange("p b k -> p (b k)")).then_inc(S["x_ready"], 1)
                        dve.tensor_tensor(state[:, mine, :], state[:, mine, :],
                                          store.last[:, bass.ds(c, 1), mine].rearrange("p o (b u) -> p (o b) u", u=1)
                                          .to_broadcast([P, HB, RD]), ALU.mult)
                    for g in range(2):
                        n = 2 * k + g
                        dve.wait_ge(S["u_ready"], r * 4 + n + 1)
                        for h in (0, 1):
                            rows = slice(32 * h, 32 * h + 32)
                            last = dve.tensor_copy(udiag[rows, HB * g:HB * g + HB, 32 * h:32 * h + 32],
                                                   of(ps_u, g, RD)[rows, :, :])
                        last.then_inc(S["u_diag_v"], 1)
                    for g in range(2):
                        n = 2 * k + g
                        mine = slice(HB * g, HB * g + HB)
                        dve.wait_ge(S["c_ready"], r * 4 + n + 1)
                        dve.tensor_tensor(state[:, mine, :], state[:, mine, :], of(ps_c, g, 64)[:, :, 32:64], ALU.add)
                        dve.drain()
                        dve.transpose(turned[:, mine, :].rearrange("p b k -> p (b k)"),
                                      state[:, mine, :].rearrange("p b k -> p (b k)")).then_inc(S["s_turned"], 1)
                        dve.wait_ge(S["o1_done"], r * 4 + n + 1)
                        dve.tensor_tensor(o_all[:, bass.ds(c, 1), mine, :].rearrange("p o b k -> p (o b) k"), o1[:, mine, :],
                                          of(ps_c, g, 64)[:, :, 0:32], ALU.add)
                        dve.drain()
                        for h in (0, 1):
                            rows = slice(32 * h, 32 * h + 32)
                            last = dve.tensor_copy(sdiag[rows, mine, 32 * h:32 * h + 32], turned[rows, mine, :])
                        last.then_inc(S["s_diag_v"], 1)
                    dve.sem_inc(S["step_done"], 1)


def gated_output(core, name, A, o_all, og):
    nc = core.nc
    S = {n: core.sem(f"{name}_{n}") for n in (
        "loaded", "ramp_exp", "x_added", "squared", "ss_ready", "root_ready", "recip_ready", "r_turned", "r_copied", "expanded",
        "o_normed", "y_ready", "gated", "turned")}
    with ExitStack() as ctx:
        sb = lambda n, s, dt=F32: core.sb(name + "_" + n, s, dt, ctx)
        w_out, b_out, ramp = sb("w_out", [P, D]), sb("b_out", [P, 1]), sb("ramp", [P, 1])
        ones4, pick = sb("ones4", [P, RHEADS]), sb("pick", [16, TPB, P])
        epsb = sb("eps", [P, 1])
        o_s, sq, on, y = (sb(n, [P, SEQ]) for n in ("o_s", "sq", "on", "y"))
        r, rT = sb("r", [P, 16]), sb("rT", [16, P])
        ps = core.ps(name + "_ps", [P, 4, 512], ctx=ctx)
        block = ctx.enter_context(nc.Block())

        @block.sync
        def _(sp):
            for dst, src in ((w_out[:, :], A["L2_w_out"]), (b_out[:, :], A["L2_b_out"]), (ramp[:, :], A["L2_ramp"]),
                             (ones4[:, :], A["c_ones4"]), (pick[:, :, :], A["c_pick_o"])):
                sp.dma_start(dst, src).then_inc(S["loaded"], 16)

        @block.tensor
        def _(pe):
            pe.wait_ge(S["loaded"], 80)
            with pe.Fori(0, BATCH) as b:
                pe.wait_ge(S["squared"], b + 1)
                for t in range(TPB):
                    last = pe.matmul(ps[:, 0, t * RHEADS:(t + 1) * RHEADS], sq[:, t * P:(t + 1) * P], ones4[:, :],
                                     start=True, stop=True)
                last.then_inc(S["ss_ready"], 1)
                pe.wait_ge(S["recip_ready"], b + 1)
                pe.transpose(ps[0:16, 0, P:2 * P], r[:, :], core.ident[:, :]).then_inc(S["r_turned"], 1)
                pe.wait_ge(S["r_copied"], b + 1)
                for t in range(TPB):
                    last = pe.matmul(ps[:, 1, t * P:(t + 1) * P], pick[:, t, :], rT[:, :], start=True, stop=True)
                last.then_inc(S["expanded"], 1)
                pe.wait_ge(S["o_normed"], b + 1)
                pe.matmul(ps[:, 2, :], w_out[:, :], on[:, :], start=True, stop=True).then_inc(S["y_ready"], 1)
                pe.wait_ge(S["gated"], b + 1)
                for t in range(TPB):
                    last = pe.transpose(ps[:, 3, t * P:(t + 1) * P], y[:, t * P:(t + 1) * P], core.ident[:, :])
                last.then_inc(S["turned"], 1)

        @block.scalar
        def _(act):
            act.wait_ge(S["loaded"], 80)
            act.activation(ramp[:, :], ramp[:, :], ACT.Sigmoid).then_inc(S["ramp_exp"], 1)
            with act.Fori(0, BATCH) as b:
                act.wait_ge(S["x_added"], b + 1)
                src = o_all[:, :, bass.ds(b, 1), :].rearrange("p c o t -> p c (o t)")
                act.activation(sq[:, :].rearrange("p (c t) -> p c t", t=CHUNK), src, ACT.Square).then_inc(S["squared"], 1)
                act.activation(o_s[:, :].rearrange("p (c t) -> p c t", t=CHUNK), src, ACT.Copy)
                act.wait_ge(S["ss_ready"], b + 1)
                act.activation(r[:, :], ps[:, 0, 0:16], ACT.Sqrt, scale=1.0 / RD, bias=epsb[:, 0:1])\
                   .then_inc(S["root_ready"], 1)

        @block.vector
        def _(dve):
            dve.memset(epsb[:, :], 1e-6)
            dve.wait_ge(S["ramp_exp"], 1)
            dve.drain()
            dve.sem_inc(S["x_added"], 1)
            with dve.Fori(0, BATCH) as b:
                dve.wait_ge(S["root_ready"], b + 1)
                dve.reciprocal(r[:, :], r[:, :]).then_inc(S["recip_ready"], 1)
                dve.wait_ge(S["r_turned"], b + 1)
                dve.tensor_copy(rT[:, :], ps[0:16, 0, P:2 * P]).then_inc(S["r_copied"], 1)
                dve.wait_ge(S["expanded"], b + 1)
                dve.tensor_tensor(on[:, :], o_s[:, :], ps[:, 1, :], ALU.mult).then_inc(S["o_normed"], 1)
                dve.wait_ge(S["y_ready"], b + 1)
                dve.tensor_scalar(y[:, :], ps[:, 2, :], b_out[:, 0:1], ramp[:, 0:1], ALU.add, ALU.mult)
                dve.drain()
                dve.tensor_tensor(y[:, :], y[:, :], og[:, bass.ds(b * SEQ, SEQ)], ALU.mult).then_inc(S["gated"], 1)
                dve.wait_ge(S["turned"], b + 1)
                xr = core.x[:, bass.ds(b * TPB, TPB), :]
                dve.tensor_tensor(xr, xr, ps[:, 3, :].rearrange("p (t d) -> p t d", t=TPB), ALU.add)\
                   .then_inc(S["x_added"], 1)


class ChunkStore:

    def __init__(self, core, ctx):
        self.kq = core.sb("l2a_kq", [P, CHUNKS, BATCH, 64], ctx=ctx)
        self.ak = core.sb("l2a_ak", [P, CHUNKS, BATCH, 64], ctx=ctx)
        self.vb = core.sb("l2a_vb", [P, CHUNKS, BATCH, RD], ctx=ctx)
        self.last = core.sb("l2a_last", [P, CHUNKS, BATCH], ctx=ctx)
        self.l_dram = core.dram("l2a_l_dram", [BATCH, RHEADS, CHUNKS, CHUNK, CHUNK])


def layer2_attention(core, A):
    layernorm(core, "l2a_ln")
    with ExitStack() as outer:
        og = core.sb("l2a_og", [P, N], ctx=outer)
        o_all = core.xT[:, :].rearrange("p (c b t) -> p c b t", c=CHUNKS, b=BATCH)
        t_dram = core.dram("l2a_t_dram", [BATCH, RHEADS, CHUNKS, CHUNK, CHUNK])
        with ExitStack() as ctx:
            store = ChunkStore(core, ctx)
            store.og = og
            chunk_products(core, "l2p", A, store)
            invert_chunks(core, "l2i", store.l_dram, t_dram)
            chunk_recurrence(core, "l2r", store, t_dram, o_all)
        gated_output(core, "l2g", A, o_all, og)


def layer3_ffn(core, A):
    layernorm(core, "l3f_ln")
    with ExitStack() as ctx:
        wts = core.sb("l3f_wts", [P, TILES, 8], ctx=ctx)
        rows = core.sb("l3f_rows", [P, N], ctx=ctx)
        rows_dram = core.dram("l3f_rows_dram", [8, N])
        route(core, "l3f_route", A["L3_router_w"], A["L3_router_b"], wts, 8, 4, "topk")
        weight_rows(core, "l3f_wr", wts, 8, rows, rows_dram)
        expert_ffn(core, "l3f", rows, A["L3_w1"], A["L3_w2"], A["L3_b1"], A["L3_b2"], rows_dram, 8, 2, "clipped", True)
        add_back(core, "l3f_add", rows)


def layer2_ffn(core, A):
    layernorm(core, "l2f_ln")
    with ExitStack() as ctx:
        wts = core.sb("l2f_wts", [P, TILES, 8], ctx=ctx)
        rows = core.sb("l2f_rows", [P, N], ctx=ctx)
        rows_dram = core.dram("l2f_rows_dram", [8, N])
        route(core, "l2f_route", A["L2_router_w"], None, wts, 8, 2, "probs")
        keep_best(core, "l2f_keep", wts, 640, A["c_same_expert"], A["c_before_expert"], A["c_bits"], False, True)
        weight_rows(core, "l2f_wr", wts, 8, rows, rows_dram)
        expert_ffn(core, "l2f", rows, A["L2_w1"], A["L2_w2"], None, None, rows_dram, 8, 4, "swiglu", True)
        add_back(core, "l2f_add", rows)


def layer1_ffn(core, A):
    layernorm(core, "l1f_ln")
    with ExitStack() as ctx:
        wts = core.sb("l1f_wts", [P, TILES, 12], ctx=ctx)
        rows = core.sb("l1f_rows", [P, N], ctx=ctx)
        rows_dram = core.dram("l1f_rows_dram", [12, N])
        route(core, "l1f_route", A["L1_router_w"], A["L1_router_b"], wts, 12, 2, "topk", 1.5)
        weight_rows(core, "l1f_wr", wts, 12, rows, rows_dram)
        expert_ffn(core, "l1fs", rows, A["L1_ws1"], A["L1_ws2"], A["L1_bs1"], A["L1_bs2"], None, 1, 2, "geglu", True)
        expert_ffn(core, "l1f", rows, A["L1_w1"], A["L1_w2"], A["L1_b1"], A["L1_b2"], rows_dram, 12, 3, "geglu", False)
        add_back(core, "l1f_add", rows)


def packed(inputs):
    g = {k: np.asarray(v) for k, v in inputs.items()}
    c = np.ascontiguousarray

    def w1(w):
        e, d, f = w.shape
        return c(w.reshape(e, d, f // P, P))

    def w2(w):
        e, f, d = w.shape
        return c(w.reshape(e, f // P, P, d).transpose(0, 2, 1, 3))

    def cols(b):
        e, f = b.shape
        return c(b.reshape(e, f // P, P).transpose(0, 2, 1))

    def gate_first(w):
        h = w.shape[-1] // 2
        return np.concatenate([w[..., h:], w[..., :h]], -1)

    t, e = np.arange(P) // 8, np.arange(P) % 8
    same_e = e[:, None] == e[None, :]
    same_b = (t[:, None] // TPB) == (t[None, :] // TPB)
    earlier = t[:, None] < t[None, :]
    bits = np.zeros((P, 31), np.int32)
    bits[:] = [1 << b for b in range(30, -1, -1)]
    bf16 = mybir.dt.np(BF16)
    later = np.arange(P)[:, None] > np.arange(P)[None, :]
    masks = np.stack([np.where(later, -1e30, 0), np.where(later.T, -1e30, 0), np.eye(P)]).astype(bf16)
    half = HD // 2
    inv_freq = np.float32(1.0) / np.float32(10000.0) ** (np.arange(half, dtype=np.float32) / np.float32(half))
    angle = np.arange(SEQ, dtype=np.float32)[:, None] * inv_freq[None, :]
    by_tile = lambda a: c(a.reshape(TPB, P, half).transpose(1, 0, 2))

    def parts(a):
        hi = a.astype(bf16)
        mid = (a - hi.astype(np.float64)).astype(bf16)
        return np.stack([hi, mid, (a - hi.astype(np.float64) - mid.astype(np.float64)).astype(bf16)], -1)

    slope = np.float32(2.0) ** (-np.arange(1, HEADS + 1, dtype=np.float32) / 2)
    pos = np.arange(SEQ, dtype=np.float64)
    steep = slope.astype(np.float64) * np.sqrt(np.float64(HD))
    q_tail = np.zeros((SEQ, HEADS, 16), bf16)
    q_tail[:, :, 0:3] = q_tail[:, :, 3:6] = parts(steep)[None]
    q_tail[:, :, 6:9] = parts(-pos[:, None] * steep[None, :])
    k_tail = np.zeros((SEQ, HEADS, 16), bf16)
    k_tail[:, :, 0:3] = (pos - pos % 2)[:, None, None]
    k_tail[:, :, 3:6] = (pos % 2)[:, None, None]
    k_tail[:, :, 6:12] = 1
    tail = lambda a: c(a.reshape(TPB, P, HEADS, 16).transpose(1, 0, 2, 3).reshape(P, TPB * HEADS, 16))
    col, row = np.arange(SEQ) % CHUNK, (np.arange(P) % CHUNK)[:, None]
    chunk_c = np.stack([np.broadcast_to(a, (P, SEQ)) for a in (col != 0, col == 0, row == col, row < col)], 1)
    chunk_c = c(chunk_c.astype(np.float32))
    quadrant = np.arange(P) // RD
    by_quadrant = c((quadrant[:, None] == np.arange(RHEADS)[None, :]).astype(np.float32))
    pick_ab = np.zeros((8, 2, P), np.float32)
    pick_ab[0:4, 0] = 0.98 * by_quadrant.T
    pick_ab[4:8, 1] = by_quadrant.T

    def pick(n):
        a = np.zeros((n, RHEADS, n, P), np.float32)
        for i in range(n):
            a[i, :, i] = by_quadrant.T
        return a.reshape(n * RHEADS, n, P)

    return {
        "c_masks": masks, "c_cos": by_tile(np.cos(angle)), "c_sin": by_tile(np.sin(angle)),
        "c_q_tail": tail(q_tail), "c_k_tail": tail(k_tail),
        "c_chunk": chunk_c, "c_ones4": by_quadrant, "c_pick_ab": pick_ab, "c_pick_r": pick(8), "c_pick_o": pick(4),
        "L2_w_in": c(g["L2_attn_W_in"].reshape(D, 3, D)),
        "L2_taps": c(np.stack([g["L2_attn_w_q"], g["L2_attn_w_k"], g["L2_attn_w_v"]])[:, :, 0, ::-1]
                     .transpose(0, 2, 1).reshape(1, 12 * D)),
        "L2_w_ctrl": g["L2_attn_W_ctrl"], "L2_b8": c(g["L2_attn_b_ctrl"][:8].reshape(8, 1)),
        "L2_bog": c(g["L2_attn_b_ctrl"][8:].reshape(D, 1)), "L2_w_out": g["L2_attn_W_out"],
        "L2_b_out": g["L2_attn_b_out"].reshape(D, 1), "L2_ramp": g["L2_attn_ramp_logit"].reshape(D, 1),
        "c_regeye": (np.eye(LAND) * REG).astype(np.float32),
        "L0_wqkv": c(np.concatenate([g["L0_attn_Wq"].T, g["L0_attn_Wk"].T, g["L0_attn_Wv"].T], 1)),
        "L0_bqkv": np.concatenate([g["L0_attn_bq"], g["L0_attn_bk"], g["L0_attn_bv"]]).reshape(1, 3 * D),
        "L0_temp": g["L0_attn_temperature"].reshape(1, 1), "L0_idx": g["L0_attn_landmark_idx"].reshape(1, LAND),
        "L0_wo": c(g["L0_attn_Wo"].T), "L0_bo": g["L0_attn_bo"].reshape(1, D),
        "L1_wqkv": g["L1_attn_w_qkv"], "L1_wo": g["L1_attn_w_o"],
        "L3_wqkv": g["L3_attn_Wqkv"], "L3_wo": g["L3_attn_Wout"],
        "x_in": c(g["L0_attn_query"].reshape(N, D)),
        "c_bits": bits,
        "c_same_expert": same_e.astype(np.float32),
        "c_before_expert": (same_e & earlier).astype(np.float32),
        "c_same_batch": (same_e & same_b).astype(np.float32),
        "c_before_batch": (same_e & same_b & earlier).astype(np.float32),
        "L0_router_w": g["L0_ffn_w_gate_w"], "L0_router_b": g["L0_ffn_w_gate_b"].reshape(-1, 1),
        "L0_w1": c(g["L0_ffn_W1"].transpose(1, 0, 2).reshape(D, 2, P)), "L0_b1": c(g["L0_ffn_b1"].reshape(2, P).T),
        "L0_w2": c(g["L0_ffn_W2"].reshape(2, P, D).transpose(1, 0, 2)), "L0_b2": g["L0_ffn_b2"],
        "L1_router_w": g["L1_ffn_Wr"], "L1_router_b": g["L1_ffn_br"].reshape(-1, 1),
        "L1_ws1": w1(gate_first(g["L1_ffn_Ws1"][None])), "L1_ws2": w2(g["L1_ffn_Ws2"][None]),
        "L1_bs1": cols(gate_first(g["L1_ffn_bs1"][None])), "L1_bs2": g["L1_ffn_bs2"].reshape(1, D, 1),
        "L1_w1": w1(gate_first(g["L1_ffn_We1"])), "L1_w2": w2(g["L1_ffn_We2"]),
        "L1_b1": cols(gate_first(g["L1_ffn_be1"])), "L1_b2": c(g["L1_ffn_be2"][:, :, None]),
        "L2_router_w": c(g["L2_ffn_router_w"].T),
        "L2_w1": w1(np.concatenate([g["L2_ffn_wg"], g["L2_ffn_wu"]], 2)), "L2_w2": w2(g["L2_ffn_wd"]),
        "L3_router_w": c(g["L3_ffn_router_weight"].T), "L3_router_b": g["L3_ffn_router_bias"].reshape(-1, 1),
        "L3_w1": w1(g["L3_ffn_gate_up_proj"].transpose(0, 2, 1)), "L3_w2": w2(g["L3_ffn_down_proj"].transpose(0, 2, 1)),
        "L3_b1": cols(g["L3_ffn_gate_up_proj_bias"]), "L3_b2": c(g["L3_ffn_down_proj_bias"][:, :, None]),
    }


def forward(nc, A, x_out):
    with ExitStack() as ctx:
        core = Core(nc, ctx)
        start(core, A["x_in"])
        for layer in (layer0_attention, layer0_ffn, layer1_attention, layer1_ffn,
                      layer2_attention, layer2_ffn, layer3_attention, layer3_ffn):
            layer(core, A)
            core.free_sems()
        store(core, x_out)


def kernel(**inputs):
    import concourse.bacc as _bacc
    from concourse.bass_utils import run_bass_kernel_spmd as _run

    arrays = packed(inputs)
    nc = _bacc.Bacc("TRN2", target_bir_lowering=False, num_devices=1)
    A = {k: nc.dram_tensor(k, a.shape, mybir.dt.from_np(a.dtype), kind="ExternalInput").ap()
         for k, a in arrays.items()}
    x_out = nc.dram_tensor("x_out", [N, D], F32, kind="ExternalOutput").ap()
    forward(nc, A, x_out)
    r = _run(nc, [arrays], core_ids=[0])
    return r.results[0]["x_out"].reshape(BATCH, SEQ, D)
```

```python
from contextlib import ExitStack

import numpy as np

import concourse.bass as bass
from concourse import mybir

F32 = mybir.dt.float32
I32 = mybir.dt.int32
U32 = mybir.dt.uint32
BF16 = mybir.dt.bfloat16
ALU = mybir.AluOpType
ACT = mybir.ActivationFunctionType
AX = mybir.AxisListType

P = 128
D = 128
BATCH, SEQ = 8, 512
N = BATCH * SEQ
TILES = N // P
BLK = 512
NBLK = N // BLK
TPB = BLK // P
LN_EPS = 1e-5
BIG = 3.0e38
TABLE_ROWS = 1 + 44 * 256


class Core:

    def __init__(self, nc, ctx):
        self.nc, self.ctx, self.sems = nc, ctx, []
        self.x = self.sb("x", [P, TILES, D])
        self.xT = self.sb("xT", [P, N])
        self.ident = self.sb("ident", [P, P])
        self.neghalf = self.sb("neghalf", [P, 512])
        self.zeros = self.sb("zeros", [P, 4 * D])
        self.table_x, self.table_y = (self.dram(n, [TABLE_ROWS, D]) for n in ("table_x", "table_y"))
        self.table_filled = nc.alloc_semaphore("table_filled")

    def sb(self, name, shape, dt=F32, ctx=None):
        return (ctx or self.ctx).enter_context(self.nc.sbuf_tensor(name, shape, dt))

    def ps(self, name, shape, dt=F32, ctx=None):
        return (ctx or self.ctx).enter_context(self.nc.psum_tensor(name, shape, dt))

    def sem(self, name):
        s = self.nc.alloc_semaphore(name)
        self.sems.append(s)
        return s

    def free_sems(self):
        self.nc.clear_and_free_semaphores(self.sems)
        self.nc.all_engine_barrier()
        self.sems = []

    def dram(self, name, shape, dt=F32):
        return self.nc.dram_tensor(name, shape, dt, kind="Internal").ap()


def start(core, x_in):
    nc = core.nc
    loaded, filled, zeroed = core.sem("x_loaded"), core.sem("ident_filled"), core.sem("zeroed")
    with nc.Block() as block:

        @block.sync
        def _(sp):
            sp.dma_start(core.x[:, :, :], x_in.rearrange("(t p) d -> p t d", p=P)).then_inc(loaded, 16)
            sp.wait_ge(zeroed, 1)
            sp.dma_start(core.table_x[0:1, :], core.zeros[0:1, 0:D]).then_inc(core.table_filled, 16)
            sp.dma_start(core.table_y[0:1, :], core.zeros[0:1, 0:D]).then_inc(core.table_filled, 16)
            sp.dma_start(core.table_x[1:TABLE_ROWS, :].rearrange("(p n k) d -> p n (k d)", p=P, k=4),
                         core.zeros[:, :].rearrange("p (o k) -> p o k", o=1)
                         .to_broadcast([P, (TABLE_ROWS - 1) // P // 4, 4 * D])).then_inc(core.table_filled, 16)
            sp.wait_ge(loaded, 16)

        @block.gpsimd
        def _(pool):
            pool.memset(core.zeros[:, :], 0.0).then_inc(zeroed, 1)
            pool.memset(core.ident[:, :], 0.0).then_inc(filled, 1)
            pool.memset(core.neghalf[:, :], -0.5)
            pool.wait_ge(filled, 1)
            pool.affine_select(out=core.ident[:, :], in_=core.ident[:, :], compare_op=ALU.not_equal, fill=1.0,
                               base=0, pattern=[[-1, P]], channel_multiplier=1)


def store(core, x_out):
    nc = core.nc
    stored = core.sem("x_stored")
    with nc.Block() as block:

        @block.sync
        def _(sp):
            sp.dma_start(x_out.rearrange("(t p) d -> p t d", p=P), core.x[:, :, :]).then_inc(stored, 16)
            sp.wait_ge(stored, 16)
            sp.wait_ge(core.table_filled, 48)


def layernorm(core, name, xn_all=None):
    nc = core.nc
    var_ready, rstd_ready = core.sem(name + "_var_ready"), core.sem(name + "_rstd_ready")
    xn_ready, turned = core.sem(name + "_xn_ready"), core.sem(name + "_turned")
    copied = core.sem(name + "_copied")
    with ExitStack() as ctx:
        stats = core.sb(name + "_stats", [P, TPB, 6], ctx=ctx)
        mv = core.sb(name + "_mv", [P, 2, TPB, 2], ctx=ctx)
        rstd = core.sb(name + "_rstd", [P, 2, TPB], ctx=ctx)
        ring = 2 if xn_all is None else NBLK
        xn = core.sb(name + "_xn", [P, 2, TPB, D], ctx=ctx) if xn_all is None \
            else xn_all[:, :, :].rearrange("p (b t) d -> p b t d", t=TPB)
        turn = core.ps(name + "_turn", [P, 2, BLK], ctx=ctx)
        block = ctx.enter_context(nc.Block())

        def block_stats(dve, b):
            for t in range(TPB):
                dve.bn_stats(stats[:, t, :], core.x[:, TPB * b + t, :])
            dve.drain()
            for t in range(TPB):
                dve.bn_aggr(mv[:, b % 2, t, :], stats[:, t, :])
            dve.drain()
            dve.tensor_scalar(rstd[:, b % 2, :], mv[:, b % 2, :, 1], LN_EPS, None, ALU.add)\
               .then_inc(var_ready, 1)

        @block.vector
        def _(dve):
            block_stats(dve, 0)
            for b in range(NBLK):
                if b + 1 < NBLK:
                    if b >= 1:
                        dve.drain()
                    block_stats(dve, b + 1)
                dve.wait_ge(rstd_ready, b + 1)
                if b >= ring:
                    dve.wait_ge(turned, b - 1)
                for t in range(TPB):
                    last = dve.tensor_scalar(xn[:, b % ring, t, :], core.x[:, TPB * b + t, :],
                                             mv[:, b % 2, t, 0:1], rstd[:, b % 2, t:t + 1],
                                             ALU.subtract, ALU.mult)
                last.then_inc(xn_ready, 1)

        @block.gpsimd
        def _(pool):
            for b in range(NBLK):
                pool.wait_ge(var_ready, b + 1)
                pool.tensor_tensor(rstd[:, b % 2, :], rstd[:, b % 2, :], core.neghalf[:, 0:TPB], ALU.pow)\
                    .then_inc(rstd_ready, 1)

        @block.tensor
        def _(pe):
            for b in range(NBLK):
                pe.wait_ge(xn_ready, b + 1)
                if b >= 2:
                    pe.wait_ge(copied, b - 1)
                for t in range(TPB):
                    last = pe.transpose(turn[:, b % 2, t * P:(t + 1) * P], xn[:, b % ring, t, :], core.ident[:, :])
                last.then_inc(turned, 1)

        @block.scalar
        def _(act):
            for b in range(NBLK):
                act.wait_ge(turned, b + 1)
                act.activation(core.xT[:, b * BLK:(b + 1) * BLK], turn[:, b % 2, :], ACT.Copy)\
                   .then_inc(copied, 1)


def add_back(core, name, yT):
    nc = core.nc
    turned, added = core.sem(name + "_turned"), core.sem(name + "_added")
    with ExitStack() as ctx:
        turn = core.ps(name + "_turn", [P, 4, TPB, P], ctx=ctx)
        block = ctx.enter_context(nc.Block())

        @block.tensor
        def _(pe):
            for b in range(NBLK):
                if b >= 4:
                    pe.wait_ge(added, b - 3)
                for t in range(TPB):
                    c = b * BLK + t * P
                    last = pe.transpose(turn[:, b % 4, t, :], yT[:, c:c + P], core.ident[:, :])
                last.then_inc(turned, 1)

        @block.vector
        def _(dve):
            for b in range(NBLK):
                dve.wait_ge(turned, b + 1)
                xb = core.x[:, b * TPB:(b + 1) * TPB, :]
                dve.tensor_tensor(xb, xb, turn[:, b % 4, :, :], ALU.add).then_inc(added, 1)


def route(core, name, w_in, b_in, wts, E, K, mode, tau=1.0):
    nc = core.nc
    loaded, logits_ready, biased = core.sem(name + "_loaded"), core.sem(name + "_logits"), core.sem(name + "_biased")
    turned, const_ready = core.sem(name + "_turned"), core.sem(name + "_const")
    shifted, exped = core.sem(name + "_shifted"), core.sem(name + "_exped")
    with ExitStack() as ctx:
        sb = lambda n, s, dt=F32: core.sb(name + "_" + n, s, dt, ctx)
        w_sb, b_sb = sb("w", [P, E]), sb("b", [P, 1])
        lT = sb("lT", [P, N])
        logits, v, oh, mask = (sb(n, [P, TILES, E]) for n in ("logits", "v", "oh", "mask"))
        probs, shift = sb("probs", [P, TILES, E]), sb("shift", [P, TILES, E])
        m1, m, den = (sb(n, [P, TILES]) for n in ("m1", "m", "den"))
        rev = sb("rev", [P, E])
        ps_l = core.ps(name + "_ps_l", [P, 2, BLK], ctx=ctx)
        ps_t = core.ps(name + "_ps_t", [P, 512], ctx=ctx)
        block = ctx.enter_context(nc.Block())
        lv = ps_t[:, 0:TILES * E].rearrange("p (t e) -> p t e", e=E)
        each = lambda a: a[:, :].rearrange("p (t o) -> p t o", o=1).to_broadcast([P, TILES, E])

        @block.sync
        def _(sp):
            sp.dma_start(w_sb[:, :], w_in).then_inc(loaded, 16)
            if b_in is not None:
                sp.dma_start(b_sb[0:E, :], b_in).then_inc(loaded, 16)

        @block.gpsimd
        def _(pool):
            for e in range(E):
                last = pool.memset(rev[:, e:e + 1], float(E - e))
            last.then_inc(const_ready, 1)

        @block.tensor
        def _(pe):
            pe.wait_ge(loaded, 16 if b_in is None else 32)
            for b in range(NBLK):
                if b >= 2:
                    pe.wait_ge(biased, b - 1)
                pe.matmul(ps_l[0:E, b % 2, :], w_sb[:, :], core.xT[:, b * BLK:(b + 1) * BLK],
                          start=True, stop=True).then_inc(logits_ready, 1)
            for t in range(TILES):
                if t % TPB == 0:
                    pe.wait_ge(biased, t // TPB + 1)
                last = pe.transpose(ps_t[:, t * E:(t + 1) * E], lT[0:E, t * P:(t + 1) * P], core.ident[0:E, 0:E])
            last.then_inc(turned, 1)

        @block.scalar
        def _(act):
            act.wait_ge(shifted, 1)
            act.activation(probs[:, :, :], shift[:, :, :], ACT.Exp, scale=1.0 / tau).then_inc(exped, 1)

        @block.vector
        def _(dve):
            dve.wait_ge(loaded, 16 if b_in is None else 32)
            for b in range(NBLK):
                dve.wait_ge(logits_ready, b + 1)
                dve.tensor_scalar(lT[0:E, b * BLK:(b + 1) * BLK], ps_l[0:E, b % 2, :],
                                  0.0 if b_in is None else b_sb[0:E, 0:1], None, ALU.add).then_inc(biased, 1)
            dve.wait_ge(turned, 1)
            dve.tensor_reduce(m1[:, :], lv, AX.X, ALU.max)
            dve.tensor_copy(logits[:, :, :], lv)
            dve.tensor_copy(v[:, :, :], lv)
            dve.drain()
            dve.tensor_tensor(shift[:, :, :], logits[:, :, :], each(m1), ALU.subtract).then_inc(shifted, 1)
            dve.wait_ge(const_ready, 1)
            for k in range(K):
                if k:
                    dve.tensor_reduce(m[:, :], v[:, :, :], AX.X, ALU.max)
                    dve.drain()
                dve.tensor_tensor(oh[:, :, :], v[:, :, :], each(m if k else m1), ALU.is_equal)
                dve.drain()
                dve.tensor_tensor(oh[:, :, :], oh[:, :, :],
                                  rev[:, :].rearrange("p (o e) -> p o e", o=1).to_broadcast([P, TILES, E]), ALU.mult)
                dve.drain()
                dve.tensor_reduce(den[:, :], oh[:, :, :], AX.X, ALU.max)
                dve.drain()
                dve.tensor_tensor(oh[:, :, :], oh[:, :, :], each(den), ALU.is_equal)
                dve.drain()
                dve.scalar_tensor_tensor(out=v[:, :, :], in0=oh[:, :, :], scalar=-BIG, in1=v[:, :, :],
                                         op0=ALU.mult, op1=ALU.add)
                if k == 0:
                    dve.tensor_copy(mask[:, :, :], oh[:, :, :])
                else:
                    dve.tensor_tensor(mask[:, :, :], mask[:, :, :], oh[:, :, :], ALU.add)
                dve.drain()
            dve.wait_ge(exped, 1)
            if mode != "topk":
                dve.tensor_reduce(den[:, :], probs[:, :, :], AX.X, ALU.add)
                dve.drain()
                dve.reciprocal(den[:, :], den[:, :])
                dve.drain()
                dve.tensor_tensor(probs[:, :, :], probs[:, :, :], each(den), ALU.mult)
                dve.drain()
            dve.tensor_tensor(probs[:, :, :], probs[:, :, :], mask[:, :, :], ALU.mult)
            dve.drain()
            if mode == "batch":
                by = probs[:, :, :].rearrange("p (b s) e -> p (s e) b", b=BATCH)
                dsum = v[:, 0:TPB, :].rearrange("p s e -> p (s e)")
                dve.tensor_reduce(dsum, by, AX.X, ALU.add)
                dve.drain()
                dve.tensor_scalar(dsum, dsum, 1e-6, None, ALU.add)
                dve.drain()
                dve.reciprocal(dsum, dsum)
                dve.drain()
                dve.scalar_tensor_tensor(
                    out=wts[:, :, :].rearrange("p (b s) e -> p b (s e)", b=BATCH),
                    in0=probs[:, :, :].rearrange("p (b s) e -> p b (s e)", b=BATCH), scalar=float(BATCH),
                    in1=v[:, 0:TPB, :].rearrange("p (o s) e -> p o (s e)", o=1).to_broadcast([P, BATCH, TPB * E]),
                    op0=ALU.mult, op1=ALU.mult)
            else:
                dve.tensor_reduce(den[:, :], probs[:, :, :], AX.X, ALU.add)
                dve.drain()
                if mode == "probs":
                    dve.tensor_scalar(den[:, :], den[:, :], 1e-6, None, ALU.add)
                    dve.drain()
                dve.reciprocal(den[:, :], den[:, :])
                dve.drain()
                dve.tensor_tensor(wts[:, :, 0:E], probs[:, :, :], each(den), ALU.mult)


def keep_best(core, name, wts, keep, group_in, before_in, bits_in, per_batch, times_weight):
    nc = core.nc
    E, HALF, TOP = 8, 2, 31
    ncol = HALF if per_batch else 1
    loaded, turned, rows_ready = core.sem(name + "_loaded"), core.sem(name + "_turned"), core.sem(name + "_rows")
    counted, summed = core.sem(name + "_counted"), core.sem(name + "_summed")
    tallied, spread = core.sem(name + "_tallied"), core.sem(name + "_spread")
    chosen, back = core.sem(name + "_chosen"), core.sem(name + "_back")
    with ExitStack() as ctx:
        sb = lambda n, s, dt=F32: core.sb(name + "_" + n, s, dt, ctx)
        group, before = sb("group", [P, P]), sb("before", [P, P])
        bits = sb("bits", [P, TOP], I32)
        rows, gt, eq, incl = (sb(n, [P, HALF, P]) for n in ("rows", "gt", "eq", "incl"))
        zeros = sb("zeros", [P, P])
        thr, cand, above = sb("thr", [P, ncol]), sb("cand", [P, ncol]), sb("above", [P, ncol])
        cnt = sb("cnt", [P, ncol])
        n_gt, n_eq, need, off = sb("n_gt", [P, ncol]), sb("n_eq", [P, HALF]), sb("need", [P, HALF]), sb("off", [P, HALF])
        ps_r = core.ps(name + "_ps_r", [P, HALF, P], ctx=ctx)
        ps_c = core.ps(name + "_ps_c", [P, 512], ctx=ctx)
        ps_o = core.ps(name + "_ps_o", [P, 512], ctx=ctx)
        ps_b = core.ps(name + "_ps_b", [P, HALF, P], ctx=ctx)
        flat = wts[:, :, :].rearrange("p t e -> p (t e)")
        shape = [P, ncol, HALF * P // ncol]
        cut = lambda a: a[:, :, :].rearrange("p h k -> p (h k)").rearrange("p (c k) -> p c k", c=ncol)
        wide = lambda a: a[:, :].rearrange("p (c o) -> p c o", o=1).to_broadcast(shape)
        block = ctx.enter_context(nc.Block())

        @block.sync
        def _(sp):
            sp.dma_start(group[:, :], group_in).then_inc(loaded, 16)
            sp.dma_start(before[:, :], before_in).then_inc(loaded, 16)
            sp.dma_start(bits[:, :], bits_in).then_inc(loaded, 16)

        @block.tensor
        def _(pe):
            for h in range(HALF):
                last = pe.transpose(ps_r[:, h, :], flat[:, h * P:(h + 1) * P], core.ident[:, :])
            last.then_inc(turned, 1)
            pe.wait_ge(loaded, 48)
            with pe.Fori(0, TOP) as i:
                pe.wait_ge(counted, i + 1)
                pe.matmul(ps_c[:, 0:ncol], group[:, :], cnt[:, :], start=True, stop=True).then_inc(summed, 1)
            pe.wait_ge(tallied, 1)
            pe.matmul(ps_c[:, 0:ncol], group[:, :], n_gt[:, :], start=True, stop=True)
            if per_batch:
                last = pe.matmul(ps_o[:, 0:HALF], before[:, :], n_eq[:, :], start=True, stop=True)
            else:
                pe.matmul(ps_o[:, 0:1], before[:, :], n_eq[:, 0:1], start=True, stop=True)
                pe.matmul(ps_o[:, 1:2], before[:, :], n_eq[:, 1:2], start=True, stop=False)
                last = pe.matmul(ps_o[:, 1:2], group[:, :], n_eq[:, 0:1], start=False, stop=True)
            last.then_inc(spread, 1)
            pe.wait_ge(chosen, 1)
            for h in range(HALF):
                last = pe.transpose(ps_b[:, h, :], gt[:, h, :], core.ident[:, :])
            last.then_inc(back, 1)

        @block.vector
        def _(dve):
            dve.memset(thr[:, :], 0.0)
            dve.memset(zeros[:, :], 0.0)
            dve.wait_ge(turned, 1)
            dve.tensor_copy(rows[:, :, :], ps_r[:, :, :])
            dve.wait_ge(loaded, 48)
            dve.drain()
            with dve.Fori(0, TOP) as i:
                dve.tensor_tensor(cand[:, :].bitcast(I32), thr[:, :].bitcast(I32),
                                  bits[:, bass.ds(i, 1)].to_broadcast([P, ncol]), ALU.bitwise_or)
                dve.drain()
                dve.tensor_tensor(cut(incl), cut(rows), wide(cand), ALU.is_ge)
                dve.drain()
                dve.tensor_reduce(cnt[:, :], cut(incl), AX.X, ALU.add).then_inc(counted, 1)
                dve.wait_ge(summed, i + 1)
                dve.scalar_tensor_tensor(out=above[:, :], in0=ps_c[:, 0:ncol], scalar=float(keep), in1=cand[:, :],
                                         op0=ALU.is_ge, op1=ALU.mult)
                dve.drain()
                dve.tensor_tensor(thr[:, :], thr[:, :], above[:, :], ALU.max)
                dve.drain()
            dve.scalar_tensor_tensor(out=thr[:, :], in0=thr[:, :], scalar=1.1754944e-38, in1=thr[:, :],
                                     op0=ALU.is_ge, op1=ALU.mult)
            dve.drain()
            dve.tensor_tensor(cut(gt), cut(rows), wide(thr), ALU.is_gt)
            dve.tensor_tensor(cut(eq), cut(rows), wide(thr), ALU.is_equal)
            dve.drain()
            dve.tensor_reduce(n_gt[:, :], cut(gt), AX.X, ALU.add)
            for h in range(HALF):
                dve.tensor_tensor_scan(incl[:, h, :], eq[:, h, :], zeros[:, :], 0.0, ALU.add, ALU.add)
            dve.tensor_reduce(n_eq[:, :], eq[:, :, :], AX.X, ALU.add).then_inc(tallied, 1)
            dve.wait_ge(spread, 1)
            dve.tensor_scalar(need[:, :], ps_c[:, 0:ncol].to_broadcast([P, HALF]) if ncol == 1 else ps_c[:, 0:HALF],
                              -1.0, float(keep), ALU.mult, ALU.add)
            dve.drain()
            dve.tensor_tensor(off[:, :], ps_o[:, 0:HALF], need[:, :], ALU.subtract)
            dve.drain()
            for h in range(HALF):
                dve.tensor_scalar(incl[:, h, :], incl[:, h, :], off[:, h:h + 1], 1.0, ALU.add, ALU.is_lt)
            dve.drain()
            dve.tensor_tensor(eq[:, :, :], eq[:, :, :], incl[:, :, :], ALU.mult)
            dve.drain()
            dve.tensor_tensor(gt[:, :, :], gt[:, :, :], eq[:, :, :], ALU.add).then_inc(chosen, 1)
            dve.wait_ge(back, 1)
            got = ps_b[:, :, :].rearrange("p h k -> p (h k)")
            if times_weight:
                dve.tensor_tensor(flat, flat, got, ALU.mult)
            else:
                dve.tensor_copy(flat, got)


def weight_rows(core, name, wts, E, rows_sb, rows_dram):
    nc = core.nc
    turned, copied, saved = core.sem(name + "_turned"), core.sem(name + "_copied"), core.sem(name + "_saved")
    with ExitStack() as ctx:
        turn = core.ps(name + "_turn", [P, 4, BLK], ctx=ctx)
        block = ctx.enter_context(nc.Block())

        @block.tensor
        def _(pe):
            for b in range(NBLK):
                if b >= 4:
                    pe.wait_ge(copied, b - 3)
                for t in range(TPB):
                    last = pe.transpose(turn[0:E, b % 4, t * P:(t + 1) * P], wts[:, b * TPB + t, :], core.ident[:, :])
                last.then_inc(turned, 1)

        @block.vector
        def _(dve):
            for b in range(NBLK):
                dve.wait_ge(turned, b + 1)
                dve.tensor_copy(rows_sb[0:E, b * BLK:(b + 1) * BLK], turn[0:E, b % 4, :]).then_inc(copied, 1)

        @block.sync
        def _(sp):
            if rows_dram is not None:
                sp.wait_ge(copied, NBLK)
                sp.dma_start(rows_dram, rows_sb[0:E, :]).then_inc(saved, 16)
                sp.wait_ge(saved, 16)


def expert_ffn(core, name, yT, w1_in, w2_in, b1_in, b2_in, rows_dram, E, C, kind, first):
    nc = core.nc
    PAR = min(E, 2)
    ROUNDS = E // PAR
    STEPS = NBLK * C
    w_ready = [core.sem(f"{name}_w_ready{k}") for k in range(PAR)]
    gu_ready, gate_done = core.sem(name + "_gu_ready"), core.sem(name + "_gate_done")
    act_done, down_done = core.sem(name + "_act_done"), core.sem(name + "_down_done")
    y_done, added = core.sem(name + "_y_done"), core.sem(name + "_added")
    pre_done, half_done = core.sem(name + "_pre_done"), core.sem(name + "_half_done")
    weighted = rows_dram is not None
    LAG = 2 if kind == "clipped" else 1
    CREDIT = 2
    with ExitStack() as ctx:
        sb = lambda n, s, dt=F32: core.sb(name + "_" + n, s, dt, ctx)
        w1, w2 = sb("w1", [P, PAR, 2 * C, P]), sb("w2", [P, PAR, C, P])
        b1, b2 = sb("b1", [P, PAR, 2 * C]), sb("b2", [P, PAR])
        wb = sb("wb", [P, PAR, N]) if weighted else None
        gate, act_out = sb("gate", [P, 2, BLK]), sb("act", [P, 2, BLK])
        g_sb, up, half = (sb(n, [P, 2, BLK]) for n in ("g", "up", "half")) if kind == "clipped" else (None,) * 3
        y_sb = sb("y", [P, 2, BLK])
        ps_g = core.ps(name + "_ps_g", [P, 2, BLK], ctx=ctx)
        ps_u = core.ps(name + "_ps_u", [P, 2, BLK], ctx=ctx)
        ps_y = core.ps(name + "_ps_y", [P, 2, BLK], ctx=ctx)
        block = ctx.enter_context(nc.Block())
        loads = 2 + (b1_in is not None) + (b2_in is not None) + weighted

        def rounds(eng):
            return eng.Fori(0, ROUNDS)

        @block.sync
        def _(sp):
            with rounds(sp) as r:
                for k in range(PAR):
                    e = r * PAR + k
                    sp.wait_ge(y_done, (r * PAR + k - PAR + 1) * NBLK + PAR * NBLK)
                    sp.dma_start(w1[:, k, :, :], w1_in[bass.ds(e, 1)].rearrange("o p c f -> p (o c) f"))\
                        .then_inc(w_ready[k], 16)
                    sp.dma_start(w2[:, k, :, :], w2_in[bass.ds(e, 1)].rearrange("o p c f -> p (o c) f"))\
                        .then_inc(w_ready[k], 16)
                    if b1_in is not None:
                        sp.dma_start(b1[:, k, :], b1_in[bass.ds(e, 1)].rearrange("o p c -> p (o c)"))\
                            .then_inc(w_ready[k], 16)
                    if b2_in is not None:
                        sp.dma_start(b2[:, k:k + 1], b2_in[bass.ds(e, 1)].rearrange("o p c -> p (o c)"))\
                            .then_inc(w_ready[k], 16)
                    if weighted:
                        sp.dma_start(wb[:, k, :], rows_dram[bass.ds(e, 1), :].to_broadcast([P, N]))\
                            .then_inc(w_ready[k], 16)

        @block.tensor
        def _(pe):
            with rounds(pe) as r:
                base = r * (PAR * STEPS)

                def down(s):
                    k, c = s // STEPS, s % C
                    u = s // C
                    pe.wait_ge(act_done, base + s + 1 + CREDIT)
                    if c == 0:
                        pe.wait_ge(y_done, r * (PAR * NBLK) + (u - 1 + PAR * NBLK))
                    pe.matmul(ps_y[:, u % 2, :], w2[:, k, c, :], act_out[:, s % 2, :],
                              start=(c == 0), stop=(c == C - 1)).then_inc(down_done, 1)

                for s in range(PAR * STEPS):
                    k, b, c = s // STEPS, s // C % NBLK, s % C
                    if s % STEPS == 0:
                        pe.wait_ge(w_ready[k], (r + 1) * (16 * loads))
                    pe.wait_ge(pre_done if kind == "clipped" else act_done, base + s - 1 + CREDIT)
                    xb = core.xT[:, b * BLK:(b + 1) * BLK]
                    pe.matmul(ps_g[:, s % 2, :], w1[:, k, c, :], xb, start=True, stop=True)
                    pe.matmul(ps_u[:, s % 2, :], w1[:, k, C + c, :], xb, start=True, stop=True)\
                        .then_inc(gu_ready, 1)
                    if s >= LAG:
                        down(s - LAG)
                for s in range(PAR * STEPS - LAG, PAR * STEPS):
                    down(s)

        @block.scalar
        def _(act):
            with rounds(act) as r:
                base = r * (PAR * STEPS)
                for s in range(PAR * STEPS):
                    k, c = s // STEPS, s % C
                    if kind == "clipped":
                        act.wait_ge(pre_done, base + s + 1 + CREDIT)
                        act.wait_ge(act_done, base + s - 1 + CREDIT)
                        act.activation(gate[:, s % 2, :], g_sb[:, s % 2, :], ACT.Sigmoid, scale=1.702)\
                           .then_inc(gate_done, 1)
                        continue
                    act.wait_ge(gu_ready, base + s + 1)
                    act.wait_ge(act_done, base + s - 1 + CREDIT)
                    func = {"geglu": ACT.Gelu, "swiglu": ACT.Silu}[kind]
                    act.activation(gate[:, s % 2, :], ps_g[:, s % 2, :], func,
                                   bias=0.0 if b1_in is None else b1[:, k, c:c + 1]).then_inc(gate_done, 1)

        @block.vector
        def _(dve):
            dve.sem_inc(act_done, CREDIT)
            if kind == "clipped":
                dve.sem_inc(pre_done, CREDIT)
                dve.sem_inc(gate_done, CREDIT)
            dve.sem_inc(y_done, PAR * NBLK)
            with rounds(dve) as r:
                base = r * (PAR * STEPS)

                def finish(u):
                    k, b = u // NBLK, u % NBLK
                    dve.wait_ge(down_done, base + (u + 1) * C)
                    if weighted:
                        dve.wait_ge(added, r * (PAR * NBLK) + u - 1 + CREDIT)
                        wv = wb[:, k, b * BLK:(b + 1) * BLK]
                        dve.scalar_tensor_tensor(out=y_sb[:, u % 2, :], in0=ps_y[:, u % 2, :],
                                                 scalar=0.0 if b2_in is None else b2[:, k:k + 1], in1=wv,
                                                 op0=ALU.add, op1=ALU.mult).then_inc(y_done, 1)
                    else:
                        dve.tensor_scalar(yT[:, b * BLK:(b + 1) * BLK], ps_y[:, u % 2, :], b2[:, k:k + 1], None,
                                          ALU.add).then_inc(y_done, 1)

                for s in range(PAR * STEPS):
                    k, c = s // STEPS, s % C
                    if s % STEPS == 0:
                        dve.wait_ge(w_ready[k], (r + 1) * (16 * loads))
                    if kind == "clipped":
                        if s % STEPS == 0:
                            dve.tensor_scalar(b1[:, k, C:2 * C], b1[:, k, C:2 * C], 1.0, None, ALU.add)
                            dve.drain()
                        dve.wait_ge(gate_done, base + s - 1 + CREDIT)
                        dve.wait_ge(gu_ready, base + s + 1)
                        dve.tensor_scalar(g_sb[:, s % 2, :], ps_g[:, s % 2, :], b1[:, k, c:c + 1], 7.0,
                                          ALU.add, ALU.min)
                        dve.tensor_scalar(up[:, s % 2, :], ps_u[:, s % 2, :], b1[:, k, C + c:C + c + 1], 8.0,
                                          ALU.add, ALU.min).then_inc(pre_done, 1)
                        dve.drain()
                        dve.wait_ge(act_done, base + s - 1 + CREDIT)
                        dve.scalar_tensor_tensor(out=half[:, s % 2, :], in0=up[:, s % 2, :], scalar=-6.0,
                                                 in1=g_sb[:, s % 2, :], op0=ALU.max, op1=ALU.mult)\
                           .then_inc(half_done, 1)
                    else:
                        dve.wait_ge(gate_done, base + s + 1)
                        if s >= 2:
                            dve.wait_ge(down_done, base + s - 1)
                        dve.scalar_tensor_tensor(out=act_out[:, s % 2, :], in0=ps_u[:, s % 2, :],
                                                 scalar=0.0 if b1_in is None else b1[:, k, C + c:C + c + 1],
                                                 in1=gate[:, s % 2, :], op0=ALU.add, op1=ALU.mult)\
                           .then_inc(act_done, 1)
                    if s >= C + LAG - 1 and (s - LAG + 1) % C == 0:
                        finish((s - LAG + 1) // C - 1)
                for u in range((PAR * STEPS - LAG) // C, PAR * NBLK):
                    finish(u)

        @block.gpsimd
        def _(pool):
            if weighted:
                if first:
                    pool.memset(yT[:, :], 0.0)
                    pool.drain()
                pool.sem_inc(added, CREDIT)
                with rounds(pool) as r:
                    base = r * (PAR * STEPS)

                    def add(u):
                        b = u % NBLK
                        pool.wait_ge(y_done, r * (PAR * NBLK) + (u + 1 + PAR * NBLK))
                        yb = yT[:, b * BLK:(b + 1) * BLK]
                        pool.tensor_tensor(yb, yb, y_sb[:, u % 2, :], ALU.add).then_inc(added, 1)

                    for s in range(PAR * STEPS):
                        if kind == "clipped":
                            pool.wait_ge(gate_done, base + s + 1 + CREDIT)
                            pool.wait_ge(half_done, base + s + 1)
                            if s >= 2:
                                pool.wait_ge(down_done, base + s - 1)
                            pool.tensor_tensor(act_out[:, s % 2, :], half[:, s % 2, :], gate[:, s % 2, :], ALU.mult)\
                                .then_inc(act_done, 1)
                        if s >= C + LAG and (s - LAG) % C == 0:
                            add((s - LAG) // C - 1)
                    for u in range((PAR * STEPS - 1 - LAG) // C, PAR * NBLK):
                        add(u)


def masked_ffn(core, name, rows, rows_dram, w1_in, b1_in, w2_in, b2_in):
    nc = core.nc
    E, C, SUB = 8, 2, 32
    loaded, up_ready, gelu_done = core.sem(name + "_loaded"), core.sem(name + "_up_ready"), core.sem(name + "_gelu_done")
    act_done, y_ready, added = core.sem(name + "_act_done"), core.sem(name + "_y_ready"), core.sem(name + "_added")
    with ExitStack() as ctx:
        sb = lambda n, s, dt=F32: core.sb(name + "_" + n, s, dt, ctx)
        w1, w2, b1, b2 = sb("w1", [P, C, P]), sb("w2", [P, C, D]), sb("b1", [P, C]), sb("b2", [E, D])
        spread = sb("spread", [P, C, N])
        gelu, act_out = sb("gelu", [P, C, 2, BLK]), sb("act", [P, C, 2, BLK])
        ps_h = core.ps(name + "_ps_h", [P, C, 2, BLK], ctx=ctx)
        ps_y = core.ps(name + "_ps_y", [P, 2, TPB, D], ctx=ctx)
        block = ctx.enter_context(nc.Block())

        @block.sync
        def _(sp):
            sp.dma_start(w1[:, :, :], w1_in).then_inc(loaded, 16)
            sp.dma_start(w2[:, :, :], w2_in).then_inc(loaded, 16)
            sp.dma_start(b1[:, :], b1_in).then_inc(loaded, 16)
            sp.dma_start(b2[:, :], b2_in).then_inc(loaded, 16)
            for e in range(E):
                at = SUB * (e % 4)
                sp.dma_start(spread[at:at + SUB, e // 4, :], rows_dram[e:e + 1, :].to_broadcast([SUB, N]))\
                    .then_inc(loaded, 16)

        ALL = 16 * (4 + E)

        @block.tensor
        def _(pe):
            pe.wait_ge(loaded, ALL)

            def down(b):
                pe.wait_ge(act_done, C * (b + 1))
                if b >= 2:
                    pe.wait_ge(added, b - 1)
                for t in range(TPB):
                    cut = slice(t * P, (t + 1) * P)
                    for c in range(C):
                        pe.matmul(ps_y[:, b % 2, t, :], act_out[:, c, b % 2, cut], w2[:, c, :],
                                  start=(c == 0), stop=False)
                    last = pe.matmul(ps_y[:, b % 2, t, :], rows[0:E, b * BLK + t * P:b * BLK + (t + 1) * P], b2[:, :],
                                     start=False, stop=True)
                last.then_inc(y_ready, 1)

            for b in range(NBLK):
                if b >= 2:
                    pe.wait_ge(gelu_done, C * (b - 1))
                for c in range(C):
                    pe.matmul(ps_h[:, c, b % 2, :], w1[:, c, :], core.xT[:, b * BLK:(b + 1) * BLK],
                              start=True, stop=True).then_inc(up_ready, 1)
                if b >= 1:
                    down(b - 1)
            down(NBLK - 1)

        @block.scalar
        def _(act):
            for b in range(NBLK):
                for c in range(C):
                    act.wait_ge(up_ready, C * b + c + 1)
                    if b >= 2:
                        act.wait_ge(act_done, C * (b - 2) + c + 1)
                    act.activation(gelu[:, c, b % 2, :], ps_h[:, c, b % 2, :], ACT.Gelu, bias=b1[:, c:c + 1])\
                       .then_inc(gelu_done, 1)

        @block.vector
        def _(dve):
            dve.wait_ge(loaded, ALL)

            def add(b):
                dve.wait_ge(y_ready, b + 1)
                xb = core.x[:, b * TPB:(b + 1) * TPB, :]
                dve.tensor_tensor(xb, xb, ps_y[:, b % 2, :, :], ALU.add).then_inc(added, 1)

            for b in range(NBLK):
                for c in range(C):
                    dve.wait_ge(gelu_done, C * b + c + 1)
                    if b >= 2:
                        dve.wait_ge(y_ready, b - 1)
                    dve.tensor_tensor(act_out[:, c, b % 2, :], gelu[:, c, b % 2, :],
                                      spread[:, c, b * BLK:(b + 1) * BLK], ALU.mult).then_inc(act_done, 1)
                if b >= 1:
                    add(b - 1)
            add(NBLK - 1)


def layer0_ffn(core, A):
    layernorm(core, "l0f_ln")
    with ExitStack() as ctx:
        wts = core.sb("l0f_wts", [P, TILES, 8], ctx=ctx)
        rows = core.sb("l0f_rows", [P, N], ctx=ctx)
        rows_dram = core.dram("l0f_rows_dram", [8, N])
        route(core, "l0f_route", A["L0_router_w"], A["L0_router_b"], wts, 8, 2, "batch")
        keep_best(core, "l0f_keep", wts, SEQ // 2, A["c_same_batch"], A["c_before_batch"], A["c_bits"], True, False)
        weight_rows(core, "l0f_wr", wts, 8, rows, rows_dram)
        masked_ffn(core, "l0f", rows, rows_dram, A["L0_w1"], A["L0_b1"], A["L0_w2"], A["L0_b2"])


HEADS, HD = 16, 8
SPAN = 1280
KEY_AT = [0, 512, 1024, 896]
QUERY_AT = [896, 1024, 512, 0]
ROWS6 = 64
Q_PARTS, K_PARTS = (0, 0, 1, 1, 0, 2), (0, 1, 0, 1, 2, 0)


def causal_attention(core, name, wqkv_in, wo_in, mask_in, kind, extra):
    nc = core.nc
    rope = kind == "rope"
    KV = 4 if rope else HEADS
    QKV = (HEADS + 2 * KV) * HD
    PAIRS, KPAIRS = HEADS // 2, KV if rope else HEADS // 2
    QB, KB = PAIRS // 2, KPAIRS // 2
    ROWS = 6 * HD if rope else 6 * HD + 12
    SCALE = float(1.0 / np.sqrt(np.float32(HD)))
    S = {n: core.sem(f"{name}_{n}") for n in (
        "loaded", "const_ready", "xb_ready", "qkv_ready", "ss_ready", "norm_ready", "parts_ready", "turned",
        "copied", "max_scores", "max_taken", "max_parts", "s_ready", "exp_done", "pv_done", "o_copied",
        "o_turned", "o_normed", "a_turned", "a_copied", "y_ready", "x_added", "reset")}
    with ExitStack() as ctx:
        sb = lambda n, s, dt=F32: core.sb(name + "_" + n, s, dt, ctx)
        wqkv, wo = sb("wqkv", [P, QKV]), sb("wo", [P, D])
        mask_kq, mask_qk, identb = sb("mask_kq", [P, P], BF16), sb("mask_qk", [P, P], BF16), sb("identb", [P, P], BF16)
        xb = sb("xb", [P, BLK])
        HQK = HEADS + KV
        qk = sb("qk", [P, TPB, HQK, HD])
        rest = sb("rest", [P, TPB * HQK, HD])
        part = [sb(f"part{k}", [P, TPB * HQK, HD], BF16) for k in range(3)]
        q6 = sb("q6", [P, TPB, HEADS, ROWS6], BF16)
        k6 = sb("k6", [P, TPB, 2 * KPAIRS, ROWS6], BF16)
        qT6, kT6 = sb("qT6", [P, PAIRS, BLK], BF16), sb("kT6", [P, KPAIRS, BLK], BF16)
        vaug = sb("vaug", [P, TPB, KV, 32])
        pT = sb("pT", [P, 2, SPAN])
        oT, att, aT = sb("oT", [P, BLK]), sb("att", [P, TPB, HEADS, HD]), sb("aT", [P, BLK])
        rden = sb("rden", [P, TPB, 4])
        if rope:
            norm = sb("norm", [P, TPB * HQK])
            cos, sin = sb("cos", [P, TPB, 4]), sb("sin", [P, TPB, 4])
            rot, tmp = sb("rot", [P, TPB, HQK, HD]), sb("tmp", [P, 2, TPB, HQK, 4])
        else:
            q_tail, k_tail = sb("q_tail", [P, TPB * HEADS, 16], BF16), sb("k_tail", [P, TPB * HEADS, 16], BF16)
            no_tail = sb("no_tail", [P, TPB * HEADS, 16], BF16)
            negm, mrest = sb("negm", [P, TPB, HEADS]), sb("mrest", [P, TPB, HEADS])
            mpart = [sb(f"mpart{k}", [P, TPB, HEADS], BF16) for k in range(3)]
        ps_s = core.ps(name + "_ps_s", [P, 6 * 512], ctx=ctx)
        ps_o = core.ps(name + "_ps_o", [P, 512], ctx=ctx)
        ps_m = core.ps(name + "_ps_m", [P, 512], ctx=ctx)
        block = ctx.enter_context(nc.Block())
        WIDE = 256 if rope else 512
        qkv = ps_s[:, 0:TPB * WIDE].rearrange("p (t c) -> p t c", t=TPB)
        heads = lambda a: a.rearrange("p t h d -> p (t h) d")

        def bank16(n):
            return ps_s[:, (n % 6) * 512:(n % 6 + 1) * 512].bitcast(BF16)

        TURNS = QB + KB + (0 if rope else QB)

        def turned_to(n):
            if n < KB:
                return kT6[:, 2 * n:2 * n + 2, :].rearrange("p a k -> p (a k)")
            n = (n - KB) % QB
            return qT6[:, 2 * n:2 * n + 2, :].rearrange("p a k -> p (a k)")

        @block.sync
        def _(sp):
            sp.dma_start(wqkv[:, :], wqkv_in).then_inc(S["loaded"], 16)
            sp.dma_start(wo[:, :], wo_in).then_inc(S["loaded"], 16)
            sp.dma_start(mask_kq[:, :], mask_in[0]).then_inc(S["loaded"], 16)
            sp.dma_start(mask_qk[:, :], mask_in[1]).then_inc(S["loaded"], 16)
            sp.dma_start(identb[:, :], mask_in[2]).then_inc(S["loaded"], 16)
            if rope:
                sp.dma_start(cos[:, :, :], extra[0]).then_inc(S["loaded"], 16)
                sp.dma_start(sin[:, :, :], extra[1]).then_inc(S["loaded"], 16)
            else:
                sp.dma_start(q_tail[:, :, :], extra[0]).then_inc(S["loaded"], 16)
                sp.dma_start(k_tail[:, :, :], extra[1]).then_inc(S["loaded"], 16)

        ALL = 16 * 7

        @block.gpsimd
        def _(pool):
            pool.memset(q6[:, :, :, :], 0.0)
            pool.memset(k6[:, :, :, :], 0.0)
            pool.memset(vaug[:, :, :, :], 0.0)
            pool.drain()
            pool.memset(vaug[:, :, :, HD:HD + 1], 1.0)
            if not rope:
                pool.memset(no_tail[:, :, :], 0.0)
                pool.wait_ge(S["loaded"], ALL)
                pool.tensor_copy(heads(k6[:, :, :, :])[:, :, 48:64], k_tail[:, :, :])
            pool.drain()
            pool.sem_inc(S["const_ready"], 1)
            if rope:
                return
            with pool.Fori(0, BATCH) as b:
                pool.wait_ge(S["x_added"], b + 1)
                pool.tensor_tensor(heads(q6[:, :, :, :])[:, :, 48:64], q_tail[:, :, :], no_tail[:, :, :], ALU.add)\
                    .then_inc(S["reset"], 1)

        @block.tensor
        def _(pe):
            pe.wait_ge(S["loaded"], ALL)
            with pe.Fori(0, BATCH) as b:
                pe.wait_ge(S["xb_ready"], b + 1)
                for t in range(TPB):
                    last = pe.matmul(qkv[:, t, 0:QKV], xb[:, t * P:(t + 1) * P], wqkv[:, :], start=True, stop=True)
                last.then_inc(S["qkv_ready"], 1)
                pe.wait_ge(S["parts_ready"], b + 1)
                if not rope:
                    pe.wait_ge(S["reset"], b + 1)

                def turn(n, src, pair0):
                    if n >= 6:
                        pe.wait_ge(S["copied"], b * TURNS + n - 5)
                    for a in range(2):
                        for t in range(TPB):
                            at = (a * TPB + t) * P
                            last = pe.transpose(
                                bank16(n)[:, at:at + P],
                                src[:, t, 2 * (pair0 + a):2 * (pair0 + a) + 2, :].rearrange("p h r -> p (h r)"),
                                identb[:, :])
                    last.then_inc(S["turned"], 1)

                for n in range(KB):
                    turn(n, k6, 2 * n)
                for n in range(QB):
                    turn(KB + n, q6, 2 * n)
                pe.wait_ge(S["copied"], b * TURNS + KB + QB)

                def rows(h):
                    return slice(ROWS6 * (h % 2), ROWS6 * (h % 2) + ROWS)

                def keys(h):
                    return h // 4 if rope else h // 2

                if not rope:
                    for h in range(HEADS):
                        if h >= 2:
                            pe.wait_ge(S["max_taken"], b * HEADS + h - 1)
                        z = (h % 2) * 1536
                        for t in (3, 2, 0, 1):
                            at, w = z + QUERY_AT[t], (t + 1) * P
                            pe.matmul(ps_s[:, at:at + w], qT6[rows(h), h // 2, t * P:(t + 1) * P],
                                      kT6[rows(h), keys(h), 0:w], start=True, stop=False)
                            last = pe.matmul(ps_s[:, at + w - P:at + w], identb[:, :], mask_qk[:, :],
                                             start=False, stop=True)
                        last.then_inc(S["max_scores"], 1)
                    pe.wait_ge(S["max_parts"], b + 1)
                    for n in range(QB):
                        turn(6 + n, q6, 2 * n)
                    pe.wait_ge(S["copied"], b * TURNS + TURNS)

                def scores(h):
                    if h >= 2:
                        pe.wait_ge(S["exp_done"], b * HEADS + h - 1)
                    z = (h % 2) * 1536
                    for j in (0, 1, 3, 2):
                        at, w = z + KEY_AT[j], (TPB - j) * P
                        pe.matmul(ps_s[:, at:at + w], kT6[rows(h), keys(h), j * P:(j + 1) * P],
                                  qT6[rows(h), h // 2, j * P:BLK], start=True, stop=False)
                        last = pe.matmul(ps_s[:, at:at + P], identb[:, :], mask_kq[:, :], start=False, stop=True)
                    last.then_inc(S["s_ready"], 1)

                def values(h):
                    g, i = h // 4, h % 4
                    pe.wait_ge(S["exp_done"], b * HEADS + h + 1)
                    if i == 0 and g:
                        pe.wait_ge(S["o_copied"], b * 4 + g)
                    for j in range(TPB):
                        last = pe.matmul(ps_o[32 * i:32 * i + 32, j * P:BLK], vaug[:, j, g if rope else h, :],
                                         pT[:, h % 2, KEY_AT[j]:KEY_AT[j] + (TPB - j) * P],
                                         start=(j == 0), stop=(j == TPB - 1))
                    last.then_inc(S["pv_done"], 1)

                def turn_group(g):
                    pe.wait_ge(S["o_copied"], b * 4 + g + 1)
                    if g:
                        pe.wait_ge(S["o_normed"], b * 4 + g)
                    for t in range(TPB):
                        last = pe.transpose(ps_m[:, t * P:(t + 1) * P], oT[:, t * P:(t + 1) * P], core.ident[:, :])
                    last.then_inc(S["o_turned"], 1)

                scores(0)
                for h in range(1, HEADS):
                    scores(h)
                    values(h - 1)
                    if h > 4 and h % 4 == 1:
                        turn_group(h // 4 - 1)
                values(HEADS - 1)
                turn_group(3)
                pe.wait_ge(S["o_normed"], b * 4 + 4)
                for t in range(TPB):
                    last = pe.transpose(ps_m[:, t * P:(t + 1) * P],
                                        att[:, t, :, :].rearrange("p h d -> p (h d)"), core.ident[:, :])
                last.then_inc(S["a_turned"], 1)
                pe.wait_ge(S["a_copied"], b + 1)
                for t in range(TPB):
                    last = pe.matmul(ps_m[:, t * P:(t + 1) * P], aT[:, t * P:(t + 1) * P], wo[:, :],
                                     start=True, stop=True)
                last.then_inc(S["y_ready"], 1)

        @block.scalar
        def _(act):
            with act.Fori(0, BATCH) as b:
                act.wait_ge(S["x_added"], b + 1)
                act.activation(xb[:, :], core.xT[:, bass.ds(b * BLK, BLK)], ACT.Copy).then_inc(S["xb_ready"], 1)
                if rope:
                    act.wait_ge(S["ss_ready"], b + 1)
                    act.activation(norm[:, :], norm[:, :], ACT.Sqrt).then_inc(S["norm_ready"], 1)
                for n in range(TURNS):
                    act.wait_ge(S["turned"], b * TURNS + n + 1)
                    at = n if n < KB + QB else 6 + n - KB - QB
                    act.activation(turned_to(n), bank16(at), ACT.Copy).then_inc(S["copied"], 1)
                for h in range(HEADS):
                    act.wait_ge(S["s_ready"], b * HEADS + h + 1)
                    if h >= 2:
                        act.wait_ge(S["pv_done"], b * HEADS + h - 1)
                    z = (h % 2) * 1536
                    act.activation(pT[:, h % 2, :], ps_s[:, z:z + SPAN], ACT.Exp, scale=SCALE)\
                       .then_inc(S["exp_done"], 1)

        @block.vector
        def _(dve):
            dve.wait_ge(S["loaded"], ALL)
            dve.wait_ge(S["const_ready"], 1)
            dve.sem_inc(S["x_added"], 1)
            with dve.Fori(0, BATCH) as b:
                dve.wait_ge(S["qkv_ready"], b + 1)
                src = heads(qk[:, :, :, :])
                for t in range(TPB):
                    dve.tensor_copy(qk[:, t, :, :].rearrange("p h d -> p (h d)"), qkv[:, t, 0:HQK * HD])
                    dve.tensor_copy(vaug[:, t, :, 0:HD],
                                    qkv[:, t, HQK * HD:QKV].rearrange("p (h d) -> p h d", d=HD))
                dve.drain()
                if rope:
                    flat = rest[:, :, :]
                    dve.tensor_tensor(flat, src, src, ALU.mult)
                    dve.drain()
                    dve.tensor_reduce(norm[:, :], flat, AX.X, ALU.add).then_inc(S["ss_ready"], 1)
                    dve.wait_ge(S["norm_ready"], b + 1)
                    dve.tensor_scalar(norm[:, :], norm[:, :], 1e-10, None, ALU.add)
                    dve.drain()
                    dve.reciprocal(norm[:, :], norm[:, :])
                    dve.drain()
                    dve.tensor_tensor(src, src, norm[:, :].rearrange("p (h o) -> p h o", o=1)
                                      .to_broadcast([P, TPB * HQK, HD]), ALU.mult)
                    dve.drain()
                    wide = lambda a: a[:, :, :].rearrange("p t (o f) -> p t o f", o=1).to_broadcast([P, TPB, HQK, 4])
                    lo, hi = qk[:, :, :, 0:4], qk[:, :, :, 4:8]
                    dve.tensor_tensor(rot[:, :, :, 0:4], lo, wide(cos), ALU.mult)
                    dve.tensor_tensor(rot[:, :, :, 4:8], hi, wide(cos), ALU.mult)
                    dve.tensor_tensor(tmp[:, 0, :, :, :], hi, wide(sin), ALU.mult)
                    dve.tensor_tensor(tmp[:, 1, :, :, :], lo, wide(sin), ALU.mult)
                    dve.drain()
                    dve.tensor_tensor(rot[:, :, :, 0:4], rot[:, :, :, 0:4], tmp[:, 0, :, :, :], ALU.subtract)
                    dve.tensor_tensor(rot[:, :, :, 4:8], rot[:, :, :, 4:8], tmp[:, 1, :, :, :], ALU.add)
                    dve.drain()
                    src = heads(rot[:, :, :, :])
                dve.tensor_copy(part[0][:, :, :], src)
                dve.drain()
                dve.tensor_tensor(rest[:, :, :], src, part[0][:, :, :], ALU.subtract)
                dve.drain()
                dve.tensor_copy(part[1][:, :, :], rest[:, :, :])
                dve.drain()
                dve.tensor_tensor(part[2][:, :, :], rest[:, :, :], part[1][:, :, :], ALU.subtract)
                dve.drain()
                by = lambda k: part[k][:, :, :].rearrange("p (t h) d -> p t h d", t=TPB)
                for n in range(6):
                    cut = slice(n * HD, (n + 1) * HD)
                    dve.tensor_copy(q6[:, :, :, cut], by(Q_PARTS[n])[:, :, 0:HEADS, :])
                    kp = by(K_PARTS[n])[:, :, HEADS:HQK, :]
                    if rope:
                        for twin in range(2):
                            last = dve.tensor_copy(k6[:, :, twin::2, cut], kp)
                    else:
                        last = dve.tensor_copy(k6[:, :, :, cut], kp)
                last.then_inc(S["parts_ready"], 1)
                if not rope:
                    for h in range(HEADS):
                        dve.wait_ge(S["max_scores"], b * HEADS + h + 1)
                        z = (h % 2) * 1536
                        for t in range(TPB):
                            at = z + QUERY_AT[t]
                            last = dve.tensor_reduce(negm[:, t, h:h + 1], ps_s[:, at:at + (t + 1) * P], AX.X, ALU.max,
                                                     negate=True)
                        last.then_inc(S["max_taken"], 1)
                    dve.drain()
                    dve.tensor_copy(mpart[0][:, :, :], negm[:, :, :])
                    dve.drain()
                    dve.tensor_tensor(mrest[:, :, :], negm[:, :, :], mpart[0][:, :, :], ALU.subtract)
                    dve.drain()
                    dve.tensor_copy(mpart[1][:, :, :], mrest[:, :, :])
                    dve.drain()
                    dve.tensor_tensor(mpart[2][:, :, :], mrest[:, :, :], mpart[1][:, :, :], ALU.subtract)
                    dve.drain()
                    for k in range(3):
                        last = dve.tensor_copy(q6[:, :, :, 57 + k:58 + k],
                                               mpart[k][:, :, :].rearrange("p t (h o) -> p t h o", o=1))
                    last.then_inc(S["max_parts"], 1)
                for g in range(4):
                    dve.wait_ge(S["pv_done"], b * HEADS + 4 * g + 4)
                    if g:
                        dve.wait_ge(S["o_turned"], b * 4 + g)
                    dve.tensor_copy(oT[:, :], ps_o[:, :]).then_inc(S["o_copied"], 1)
                    dve.wait_ge(S["o_turned"], b * 4 + g + 1)
                    by_head = ps_m[:, :].rearrange("p (t i c) -> p t i c", t=TPB, i=4)
                    dve.reciprocal(rden[:, :, :], by_head[:, :, :, HD:HD + 1].rearrange("p t i o -> p t (i o)"))
                    dve.drain()
                    dve.tensor_tensor(att[:, :, 4 * g:4 * g + 4, :], by_head[:, :, :, 0:HD],
                                      rden[:, :, :].rearrange("p t (i o) -> p t i o", o=1)
                                      .to_broadcast([P, TPB, 4, HD]), ALU.mult).then_inc(S["o_normed"], 1)
                dve.wait_ge(S["a_turned"], b + 1)
                dve.tensor_copy(aT[:, :], ps_m[:, :]).then_inc(S["a_copied"], 1)
                dve.wait_ge(S["y_ready"], b + 1)
                xr = core.x[:, bass.ds(b * TPB, TPB), :]
                dve.tensor_tensor(xr, xr, ps_m[:, :].rearrange("p (t d) -> p t d", t=TPB), ALU.add)\
                   .then_inc(S["x_added"], 1)


def layer1_attention(core, A):
    layernorm(core, "l1a_ln")
    causal_attention(core, "l1a", A["L1_wqkv"], A["L1_wo"], A["c_masks"], "rope", (A["c_cos"], A["c_sin"]))


def layer3_attention(core, A):
    layernorm(core, "l3a_ln")
    causal_attention(core, "l3a", A["L3_wqkv"], A["L3_wo"], A["c_masks"], "alibi", (A["c_q_tail"], A["c_k_tail"]))


LAND, REG = 64, 1e-6
COLS = LAND + HD + 1
RROWS = 6 * HD + 6


def landmark_sums(core, name, A, qT_all, land_all, w_dram, z_dram):
    nc = core.nc
    PAIRS, H2 = HEADS // 2, 2 * HEADS
    S = {n: core.sem(f"{name}_{n}") for n in (
        "loaded", "const_ready", "onehot_ready", "seq_done", "xb_ready", "qkv_ready", "parts_ready", "turned", "copied",
        "gathered", "land_ready", "w_ready", "w_clamped", "w_exped", "w_full", "dist_ready", "clamped", "phi_ready",
        "z_ready", "z_full", "saved")}
    with ExitStack() as ctx:
        sb = lambda n, s, dt=F32: core.sb(name + "_" + n, s, dt, ctx)
        wqkv, bias = sb("wqkv", [P, 3 * D]), sb("bias", [P, 3 * D])
        identb = sb("identb", [P, P], BF16)
        regeye = sb("regeye", [LAND, LAND])
        temp, scale = sb("temp", [P, 1]), sb("scale", [P, 1])
        idx_i, idx, neg = sb("idx_i", [P, LAND], I32), sb("idx", [P, LAND]), sb("neg", [P, LAND])
        pos_i, pos = sb("pos_i", [P, TPB], I32), sb("pos", [P, TPB])
        onehot = sb("onehot", [P, TPB, LAND], BF16)
        xb = sb("xb", [P, BLK])
        qk, rest = sb("qk", [P, TPB * H2, HD]), sb("rest", [P, TPB * H2, HD])
        part = [sb(f"part{k}", [P, TPB * H2, HD], BF16) for k in range(3)]
        sq, sqrest = sb("sq", [P, TPB * H2]), sb("sqrest", [P, TPB * H2])
        sqpart = [sb(f"sqpart{k}", [P, TPB * H2], BF16) for k in range(3)]
        x6 = sb("x6", [P, TPB, H2, ROWS6], BF16)
        l6 = sb("l6", [P, TPB, HEADS, ROWS6], BF16)
        kT6 = sb("kT6", [P, PAIRS, BLK], BF16)
        land = sb("land", [P, PAIRS, P], BF16)
        kland = sb("kland", [P, PAIRS, LAND], BF16)
        vaug = sb("vaug", [P, TPB, PAIRS, 17])
        phi = sb("phi", [P, TPB, PAIRS, P])
        w_sb = sb("w", [LAND, HEADS, LAND])
        z_sb = sb("z", [P, PAIRS, HD + 1])
        ps = core.ps(name + "_ps", [P, 8, 512], ctx=ctx)
        block = ctx.enter_context(nc.Block())
        by_head = lambda a: a[:, :, :].rearrange("p (t h) d -> p t h d", t=TPB)
        one = lambda a: a[:, :].rearrange("p (t h o) -> p t h o", t=TPB, o=1)
        BANK_OF_TURN = (4, 5, 6, 7, 0, 1, 2, 3)

        @block.sync
        def _(sp):
            for dst, src in ((wqkv[:, :], A["L0_wqkv"]), (bias[:, :], A["L0_bqkv"].to_broadcast([P, 3 * D])),
                             (identb[:, :], A["c_masks"][2]), (regeye[:, :], A["c_regeye"]),
                             (temp[:, :], A["L0_temp"].to_broadcast([P, 1])),
                             (idx_i[:, :], A["L0_idx"].to_broadcast([P, LAND]))):
                sp.dma_start(dst, src).then_inc(S["loaded"], 16)
            sp.sem_inc(S["seq_done"], 1)
            with sp.Fori(0, BATCH) as b:
                sp.wait_ge(S["w_full"], b + 1)
                sp.dma_start(w_dram[bass.ds(b * HEADS, HEADS)].rearrange("h i k -> i h k"), w_sb[:, :, :])\
                  .then_inc(S["saved"], 16)
                sp.wait_ge(S["z_full"], b + 1)
                for h2 in range(2):
                    zd = z_dram[bass.ds(b, 1), :, h2, :, :].rearrange("o a k c -> k (o a) c")
                    sp.dma_start(zd, z_sb[64 * h2:64 * h2 + 64, :, :]).then_inc(S["saved"], 16)
                sp.wait_ge(S["saved"], b * 48 + 48)
                sp.sem_inc(S["seq_done"], 1)

        @block.gpsimd
        def _(pool):
            pool.iota(pos_i[:, :], [[P, TPB]], base=0, channel_multiplier=1)
            pool.memset(x6[:, :, :, :], 0.0)
            pool.memset(l6[:, :, :, :], 0.0)
            pool.memset(land[:, :, :], 0.0)
            pool.drain()
            pool.memset(x6[:, :, :, 51:54], 1.0)
            pool.memset(l6[:, :, :, 48:51], 1.0)
            pool.memset(vaug[:, :, :, 16:17], 1.0)
            pool.drain()
            pool.sem_inc(S["const_ready"], 1)

        @block.tensor
        def _(pe):
            pe.wait_ge(S["onehot_ready"], 1)
            with pe.Fori(0, BATCH) as b:
                pe.wait_ge(S["xb_ready"], b + 1)
                for t in range(TPB):
                    last = pe.matmul(ps[:, t, 0:3 * D], xb[:, t * P:(t + 1) * P], wqkv[:, :], start=True, stop=True)
                last.then_inc(S["qkv_ready"], 1)
                pe.wait_ge(S["parts_ready"], b + 1)
                for n in range(8):
                    for a in range(2):
                        for t in range(TPB):
                            at = (a * TPB + t) * P
                            last = pe.transpose(
                                ps[:, BANK_OF_TURN[n], :].bitcast(BF16)[:, at:at + P],
                                x6[:, t, 4 * n + 2 * a:4 * n + 2 * a + 2, :].rearrange("p h r -> p (h r)"), identb[:, :])
                    last.then_inc(S["turned"], 1)
                pe.wait_ge(S["copied"], b * 8 + 2)
                for bank, src, h0 in ((4, l6, 0), (5, x6, HEADS)):
                    for a in range(PAIRS):
                        for t in range(TPB):
                            last = pe.matmul(ps[:, bank, a * LAND:(a + 1) * LAND],
                                             src[:, t, h0 + 2 * a:h0 + 2 * a + 2, :].rearrange("p h r -> p (h r)"),
                                             onehot[:, t, :], start=(t == 0), stop=(t == TPB - 1))
                last.then_inc(S["gathered"], 1)
                pe.wait_ge(S["land_ready"], b + 1)
                pe.wait_ge(S["copied"], b * 8 + 4)
                for a in range(PAIRS):
                    last = pe.matmul(ps[0:LAND, 6 + a // 4, (a % 4) * P:(a % 4 + 1) * P], kland[:, a, :], land[:, a, :],
                                     start=True, stop=True)
                last.then_inc(S["w_ready"], 1)
                pe.wait_ge(S["copied"], b * 8 + 8)
                for t in range(TPB):
                    if t >= 2:
                        pe.wait_ge(S["clamped"], b * TPB + t - 1)
                    for a in range(PAIRS):
                        last = pe.matmul(ps[:, 2 * (t % 2) + a // 4, (a % 4) * P:(a % 4 + 1) * P],
                                         kT6[:, a, t * P:(t + 1) * P], land[:, a, :], start=True, stop=True)
                    last.then_inc(S["dist_ready"], 1)
                pe.wait_ge(S["phi_ready"], b * TPB + TPB)
                for a in range(PAIRS):
                    for t in range(TPB):
                        last = pe.matmul(ps[:, 4, a * 32:a * 32 + 17], phi[:, t, a, :], vaug[:, t, a, :],
                                         start=(t == 0), stop=(t == TPB - 1))
                last.then_inc(S["z_ready"], 1)

        @block.scalar
        def _(act):
            act.wait_ge(S["onehot_ready"], 1)
            with act.Fori(0, BATCH) as b:
                act.activation(xb[:, :], core.xT[:, bass.ds(b * BLK, BLK)], ACT.Copy).then_inc(S["xb_ready"], 1)
                for n in range(8):
                    act.wait_ge(S["turned"], b * 8 + n + 1)
                    src = ps[:, BANK_OF_TURN[n], :].bitcast(BF16)
                    if n < 4:
                        dst = qT_all[:, bass.ds(b * (PAIRS * BLK) + n * 2 * BLK, 2 * BLK)]
                    else:
                        dst = kT6[:, 2 * (n - 4):2 * (n - 4) + 2, :].rearrange("p a k -> p (a k)")
                    act.activation(dst, src, ACT.Copy).then_inc(S["copied"], 1)
                act.wait_ge(S["w_clamped"], b + 1)
                act.activation(w_sb[:, :, :], w_sb[:, :, :], ACT.Exp, scale=scale[0:LAND, 0:1]).then_inc(S["w_exped"], 1)
                for t in range(TPB):
                    act.wait_ge(S["clamped"], b * TPB + t + 1)
                    act.activation(phi[:, t, :, :], phi[:, t, :, :], ACT.Exp, scale=scale[:, 0:1])\
                       .then_inc(S["phi_ready"], 1)

        @block.vector
        def _(dve):
            dve.wait_ge(S["loaded"], 96)
            dve.wait_ge(S["const_ready"], 1)
            dve.tensor_copy(idx[:, :], idx_i[:, :])
            dve.tensor_copy(pos[:, :], pos_i[:, :])
            dve.reciprocal(scale[:, :], temp[:, :])
            dve.drain()
            dve.tensor_scalar(neg[:, :], idx[:, :], 0.0, float(SEQ), ALU.is_lt, ALU.mult)
            dve.tensor_scalar(scale[:, :], scale[:, :], -1.0, None, ALU.mult)
            dve.drain()
            dve.tensor_tensor(idx[:, :], idx[:, :], neg[:, :], ALU.add)
            dve.drain()
            dve.tensor_scalar(idx[:, :], idx[:, :], 0.0, float(SEQ - 1), ALU.max, ALU.min)
            dve.drain()
            for t in range(TPB):
                last = dve.tensor_scalar(onehot[:, t, :], idx[:, :], pos[:, t:t + 1], None, ALU.is_equal)
            last.then_inc(S["onehot_ready"], 1)
            with dve.Fori(0, BATCH) as b:
                dve.wait_ge(S["qkv_ready"], b + 1)
                for t in range(TPB):
                    dve.tensor_tensor(by_head(qk)[:, t, :, :].rearrange("p h d -> p (h d)"), ps[:, t, 0:2 * D],
                                      bias[:, 0:2 * D], ALU.add)
                    dve.tensor_tensor(vaug[:, t, :, 0:16], ps[:, t, 2 * D:3 * D].rearrange("p (a c) -> p a c", a=PAIRS),
                                      bias[:, 2 * D:3 * D].rearrange("p (a c) -> p a c", a=PAIRS), ALU.add)
                dve.drain()
                dve.tensor_tensor(rest[:, :, :], qk[:, :, :], qk[:, :, :], ALU.mult)
                dve.tensor_copy(part[0][:, :, :], qk[:, :, :])
                dve.drain()
                dve.tensor_reduce(sq[:, :], rest[:, :, :], AX.X, ALU.add)
                dve.drain()
                dve.tensor_tensor(rest[:, :, :], qk[:, :, :], part[0][:, :, :], ALU.subtract)
                dve.tensor_copy(sqpart[0][:, :], sq[:, :])
                dve.drain()
                dve.tensor_copy(part[1][:, :, :], rest[:, :, :])
                dve.tensor_tensor(sqrest[:, :], sq[:, :], sqpart[0][:, :], ALU.subtract)
                dve.drain()
                dve.tensor_tensor(part[2][:, :, :], rest[:, :, :], part[1][:, :, :], ALU.subtract)
                dve.tensor_copy(sqpart[1][:, :], sqrest[:, :])
                dve.drain()
                dve.tensor_tensor(sqpart[2][:, :], sqrest[:, :], sqpart[1][:, :], ALU.subtract)
                dve.drain()
                for n in range(6):
                    cut = slice(n * HD, (n + 1) * HD)
                    dve.tensor_copy(x6[:, :, :, cut], by_head(part[Q_PARTS[n]]))
                    dve.tensor_scalar(l6[:, :, :, cut], by_head(part[K_PARTS[n]])[:, :, HEADS:H2, :], -2.0, None, ALU.mult)
                for k in range(3):
                    dve.tensor_copy(x6[:, :, :, 48 + k:49 + k], one(sqpart[k]))
                    last = dve.tensor_copy(l6[:, :, :, 51 + k:52 + k], one(sqpart[k])[:, :, HEADS:H2, :])
                last.then_inc(S["parts_ready"], 1)
                dve.wait_ge(S["gathered"], b + 1)
                for h2 in range(2):
                    rows, cols = slice(64 * h2, 64 * h2 + 64), slice(LAND * h2, LAND * h2 + LAND)
                    dve.tensor_copy(land[rows, :, cols], ps[rows, 4, :].rearrange("p (a k) -> p a k", a=PAIRS))
                dve.tensor_copy(kland[:, :, :], ps[:, 5, :].rearrange("p (a k) -> p a k", a=PAIRS)).then_inc(S["land_ready"], 1)
                dve.drain()
                dve.tensor_copy(land_all[:, bass.ds(b * (PAIRS * P), PAIRS * P)],
                                land[:, :, :].rearrange("p a k -> p (a k)"))
                dve.wait_ge(S["seq_done"], b + 1)
                dve.wait_ge(S["w_ready"], b + 1)
                dve.tensor_scalar(w_sb[:, :, :].rearrange("p h k -> p (h k)"),
                                  ps[0:LAND, 6:8, :].rearrange("p n k -> p (n k)"), 0.0, None, ALU.max)\
                   .then_inc(S["w_clamped"], 1)
                for t in range(TPB):
                    dve.wait_ge(S["dist_ready"], b * TPB + t + 1)
                    z = 2 * (t % 2)
                    dve.tensor_scalar(phi[:, t, :, :].rearrange("p a k -> p (a k)"),
                                      ps[:, z:z + 2, :].rearrange("p n k -> p (n k)"), 0.0, None, ALU.max)\
                       .then_inc(S["clamped"], 1)
                dve.wait_ge(S["w_exped"], b + 1)
                dve.tensor_tensor(w_sb[:, :, :], w_sb[:, :, :],
                                  regeye[:, :].rearrange("p (o k) -> p o k", o=1).to_broadcast([LAND, HEADS, LAND]),
                                  ALU.add).then_inc(S["w_full"], 1)
                dve.wait_ge(S["z_ready"], b + 1)
                zv = ps[:, 4, 0:PAIRS * 32].rearrange("p (a c) -> p a c", a=PAIRS)
                for h2 in range(2):
                    rows = slice(64 * h2, 64 * h2 + 64)
                    dve.tensor_copy(z_sb[rows, :, 0:HD], zv[rows, :, HD * h2:HD * h2 + HD])
                    last = dve.tensor_copy(z_sb[rows, :, HD:HD + 1], zv[rows, :, 16:17])
                last.then_inc(S["z_full"], 1)


def solve(core, name, w_dram, z_dram, y_dram):
    nc = core.nc
    OWN = 60
    BAND = 13
    loaded, pivot_ready = core.sem(name + "_loaded"), core.sem(name + "_pivot_ready")
    pool_done, solved, saved = core.sem(name + "_pool_done"), core.sem(name + "_solved"), core.sem(name + "_saved")
    with ExitStack() as ctx:
        sb = lambda n, s, dt=F32: core.sb(name + "_" + n, s, dt, ctx)
        m, rinv = sb("m", [P, LAND, COLS]), sb("rinv", [P, LAND])
        y = sb("y", [P, LAND, HD + 1])
        scaled = sb("scaled", [P, OWN, COLS - OWN])
        outer_p = sb("outer_p", [P, LAND, COLS - OWN])
        row_ps = core.ps(name + "_row", [P, 512], ctx=ctx)
        outer = core.ps(name + "_outer", [P, 7 * 512], ctx=ctx)
        block = ctx.enter_context(nc.Block())

        def outer_product(eng, out, col, row, shape):
            return eng.tensor_tensor(out, col.rearrange("p (r o) -> p r o", o=1).to_broadcast(shape),
                                     row.rearrange("p (o c) -> p o c", o=1).to_broadcast(shape), ALU.mult)

        @block.sync
        def _(sp):
            sp.dma_start(m[:, :, 0:LAND], w_dram).then_inc(loaded, 16)
            sp.dma_start(m[:, :, LAND:COLS], z_dram.rearrange("b a h k c -> (b a h) k c")).then_inc(loaded, 16)
            sp.wait_ge(solved, 1)
            sp.dma_start(y_dram.rearrange("b a h k c -> (b a h) k c"), y[:, :, :]).then_inc(saved, 16)
            sp.wait_ge(saved, 16)

        @block.vector
        def _(dve):
            dve.wait_ge(loaded, 32)
            for k in range(LAND):
                end = OWN if k < OWN else COLS
                last_row = OWN if k < OWN else LAND
                if k == OWN:
                    dve.wait_ge(pool_done, OWN)
                dve.reciprocal(rinv[:, k:k + 1], m[:, k, k:k + 1])
                dve.drain()
                w, n = end - k - 1, last_row - k - 1
                if w:
                    dve.tensor_scalar(row_ps[:, 0:w], m[:, k, k + 1:end], rinv[:, k:k + 1], None, ALU.mult)
                    dve.drain()
                bands, at = [], 0
                for band in range(max(1, round(n / BAND)) if n else 0):
                    r0 = k + 1 + band * n // max(1, round(n / BAND))
                    r1 = k + 1 + (band + 1) * n // max(1, round(n / BAND))
                    size = (r1 - r0) * (end - r0)
                    bands.append((r0, r1, outer[:, at:at + size].rearrange("p (r c) -> p r c", c=end - r0)))
                    at += size
                for r0, r1, out in bands:
                    outer_product(dve, out, m[:, k, r0:r1], row_ps[:, r0 - k - 1:w], [P, r1 - r0, end - r0])
                dve.drain()
                for r0, r1, out in bands:
                    dve.tensor_tensor(m[:, r0:r1, r0:end], m[:, r0:r1, r0:end], out, ALU.subtract)
                if w:
                    dve.tensor_copy(m[:, k, k + 1:end], row_ps[:, 0:w])
                dve.drain()
                if k < OWN:
                    dve.sem_inc(pivot_ready, 1)
            for k in range(LAND - 1, 0, -1):
                shape = [P, k, HD + 1]
                out = outer[:, 0:k * (HD + 1)].rearrange("p (r c) -> p r c", c=HD + 1)
                outer_product(dve, out, m[:, 0:k, k:k + 1].rearrange("p r o -> p (r o)"), m[:, k, LAND:COLS], shape)
                dve.drain()
                dve.tensor_tensor(m[:, 0:k, LAND:COLS], m[:, 0:k, LAND:COLS], out, ALU.subtract)
                dve.drain()
            dve.tensor_copy(y[:, :, :], m[:, :, LAND:COLS]).then_inc(solved, 1)

        @block.gpsimd
        def _(pool):
            pool.wait_ge(loaded, 32)
            for k in range(OWN):
                pool.wait_ge(pivot_ready, k + 1)
                pool.tensor_scalar(scaled[:, k, :], m[:, k, OWN:COLS], rinv[:, k:k + 1], None, ALU.mult)
                pool.drain()
                n = OWN - 1 - k
                if n:
                    outer_product(pool, outer_p[:, k + 1:OWN, :], m[:, k, k + 1:OWN], m[:, k, OWN:COLS],
                                  [P, n, COLS - OWN])
                outer_product(pool, outer_p[:, OWN:LAND, :], m[:, k, OWN:LAND], scaled[:, k, :],
                              [P, LAND - OWN, COLS - OWN])
                pool.drain()
                rest = m[:, k + 1:LAND, OWN:COLS]
                pool.tensor_tensor(rest, rest, outer_p[:, k + 1:LAND, :], ALU.subtract)
                pool.drain()
            pool.tensor_copy(m[:, 0:OWN, OWN:COLS], scaled[:, :, :])
            pool.drain()
            pool.sem_inc(pool_done, OWN)


def landmark_outputs(core, name, A, qT_all, land_all, y_dram):
    nc = core.nc
    PAIRS = HEADS // 2
    S = {n: core.sem(f"{name}_{n}") for n in (
        "loaded", "const_ready", "y_loaded", "land_ready", "dist_ready", "clamped", "phi_ready", "used", "o_ready", "o_copied",
        "o_turned", "o_normed", "a_turned", "a_copied", "y_ready", "x_added")}
    with ExitStack() as ctx:
        sb = lambda n, s, dt=F32: core.sb(name + "_" + n, s, dt, ctx)
        wo, bo, ones = sb("wo", [P, D]), sb("bo", [1, D]), sb("ones", [1, P])
        temp, scale = sb("temp", [P, 1]), sb("scale", [P, 1])
        land = sb("land", [P, PAIRS, P], BF16)
        y2 = sb("y2", [P, PAIRS, 32])
        phi = sb("phi", [P, 2, BLK])
        oT, att, aT = sb("oT", [P, 2, BLK]), sb("att", [P, TPB, HEADS, HD]), sb("aT", [P, BLK])
        den = sb("den", [P, 2, TPB, 8])
        ps_d = core.ps(name + "_ps_d", [P, 2, 512], ctx=ctx)
        ps_o = core.ps(name + "_ps_o", [P, 2, 512], ctx=ctx)
        ps_t = core.ps(name + "_ps_t", [P, 2, 512], ctx=ctx)
        ps_m = core.ps(name + "_ps_m", [P, 512], ctx=ctx)
        block = ctx.enter_context(nc.Block())

        @block.sync
        def _(sp):
            sp.dma_start(wo[:, :], A["L0_wo"]).then_inc(S["loaded"], 16)
            sp.dma_start(bo[:, :], A["L0_bo"]).then_inc(S["loaded"], 16)
            sp.dma_start(temp[:, :], A["L0_temp"].to_broadcast([P, 1])).then_inc(S["loaded"], 16)
            sp.wait_ge(S["const_ready"], 1)
            with sp.Fori(0, BATCH) as b:
                sp.wait_ge(S["x_added"], b + 1)
                for h2 in range(2):
                    src = y_dram[bass.ds(b, 1), :, h2, :, :].rearrange("o a k c -> k (o a) c")
                    sp.dma_start(y2[64 * h2:64 * h2 + 64, :, 16 * h2:16 * h2 + HD + 1], src).then_inc(S["y_loaded"], 16)

        @block.gpsimd
        def _(pool):
            pool.memset(y2[:, :, :], 0.0)
            pool.memset(ones[:, :], 1.0)
            pool.drain()
            pool.sem_inc(S["const_ready"], 1)

        @block.tensor
        def _(pe):
            pe.wait_ge(S["loaded"], 48)
            pe.wait_ge(S["const_ready"], 1)
            with pe.Fori(0, BATCH) as b:
                pe.wait_ge(S["land_ready"], b + 1)

                def outputs(a):
                    if a == 0:
                        pe.wait_ge(S["y_loaded"], b * 32 + 32)
                    pe.wait_ge(S["phi_ready"], b * PAIRS + a + 1)
                    pe.matmul(ps_o[32 * (a % 4):32 * (a % 4) + 32, a // 4, :], y2[:, a, :], phi[:, a % 2, :],
                              start=True, stop=True).then_inc(S["used"], 1)

                for a in range(PAIRS):
                    if a >= 2:
                        pe.wait_ge(S["clamped"], b * PAIRS + a - 1)
                    pe.matmul(ps_d[:, a % 2, :], land[:, a, :], qT_all[:, bass.ds((b * PAIRS + a) * BLK, BLK)],
                              start=True, stop=True).then_inc(S["dist_ready"], 1)
                    if a >= 1:
                        outputs(a - 1)
                outputs(PAIRS - 1)
                for g in range(2):
                    pe.wait_ge(S["o_copied"], b * 2 + g + 1)
                    for t in range(TPB):
                        last = pe.transpose(ps_t[:, g, t * P:(t + 1) * P], oT[:, g, t * P:(t + 1) * P], core.ident[:, :])
                    last.then_inc(S["o_turned"], 1)
                pe.wait_ge(S["o_normed"], b * 2 + 2)
                for t in range(TPB):
                    last = pe.transpose(ps_m[:, t * P:(t + 1) * P], att[:, t, :, :].rearrange("p h d -> p (h d)"),
                                        core.ident[:, :])
                last.then_inc(S["a_turned"], 1)
                pe.wait_ge(S["a_copied"], b + 1)
                for t in range(TPB):
                    pe.matmul(ps_m[:, t * P:(t + 1) * P], aT[:, t * P:(t + 1) * P], wo[:, :], start=True, stop=False)
                    last = pe.matmul(ps_m[:, t * P:(t + 1) * P], ones[:, :], bo[:, :], start=False, stop=True)
                last.then_inc(S["y_ready"], 1)

        @block.scalar
        def _(act):
            with act.Fori(0, BATCH) as b:
                act.wait_ge(S["x_added"], b + 1)
                act.activation(land[:, :, :].rearrange("p a k -> p (a k)"),
                               land_all[:, bass.ds(b * (PAIRS * P), PAIRS * P)], ACT.Copy).then_inc(S["land_ready"], 1)
                for a in range(PAIRS):
                    act.wait_ge(S["clamped"], b * PAIRS + a + 1)
                    act.activation(phi[:, a % 2, :], phi[:, a % 2, :], ACT.Exp, scale=scale[:, 0:1])\
                       .then_inc(S["phi_ready"], 1)

        @block.vector
        def _(dve):
            dve.wait_ge(S["loaded"], 48)
            dve.reciprocal(scale[:, :], temp[:, :])
            dve.drain()
            dve.tensor_scalar(scale[:, :], scale[:, :], -1.0, None, ALU.mult)
            dve.drain()
            dve.sem_inc(S["x_added"], 1)
            with dve.Fori(0, BATCH) as b:
                for a in range(PAIRS):
                    dve.wait_ge(S["dist_ready"], b * PAIRS + a + 1)
                    if a >= 2:
                        dve.wait_ge(S["used"], b * PAIRS + a - 1)
                    dve.tensor_scalar(phi[:, a % 2, :], ps_d[:, a % 2, :], 0.0, None, ALU.max).then_inc(S["clamped"], 1)
                    if a == 5:
                        dve.wait_ge(S["used"], b * PAIRS + 4)
                        dve.tensor_copy(oT[:, 0, :], ps_o[:, 0, :]).then_inc(S["o_copied"], 1)
                dve.wait_ge(S["used"], b * PAIRS + 8)
                dve.tensor_copy(oT[:, 1, :], ps_o[:, 1, :]).then_inc(S["o_copied"], 1)
                for g in range(2):
                    dve.wait_ge(S["o_turned"], b * 2 + g + 1)
                    bh = ps_t[:, g, :].rearrange("p (t i c) -> p t i c", t=TPB, i=8)
                    dve.tensor_scalar(den[:, g, :, :], bh[:, :, :, HD:HD + 1].rearrange("p t i o -> p t (i o)"), 1e-10,
                                      None, ALU.max)
                    dve.drain()
                    dve.reciprocal(den[:, g, :, :], den[:, g, :, :])
                    dve.drain()
                    dve.tensor_tensor(att[:, :, 8 * g:8 * g + 8, :], bh[:, :, :, 0:HD],
                                      den[:, g, :, :].rearrange("p t (i o) -> p t i o", o=1)
                                      .to_broadcast([P, TPB, 8, HD]), ALU.mult).then_inc(S["o_normed"], 1)
                dve.wait_ge(S["a_turned"], b + 1)
                dve.tensor_copy(aT[:, :], ps_m[:, :]).then_inc(S["a_copied"], 1)
                dve.wait_ge(S["y_ready"], b + 1)
                xr = core.x[:, bass.ds(b * TPB, TPB), :]
                dve.tensor_tensor(xr, xr, ps_m[:, :].rearrange("p (t d) -> p t d", t=TPB), ALU.add)\
                   .then_inc(S["x_added"], 1)


def layer0_attention(core, A):
    layernorm(core, "l0a_ln")
    with ExitStack() as ctx:
        qT_all = core.sb("l0a_qT_all", [P, BATCH * (HEADS // 2) * BLK], BF16, ctx)
        land_all = core.sb("l0a_land_all", [P, BATCH * (HEADS // 2) * P], BF16, ctx)
        w_dram = core.dram("l0a_w_dram", [BATCH * HEADS, LAND, LAND])
        z_dram = core.dram("l0a_z_dram", [BATCH, HEADS // 2, 2, LAND, HD + 1])
        y_dram = core.dram("l0a_y_dram", [BATCH, HEADS // 2, 2, LAND, HD + 1])
        landmark_sums(core, "l0s", A, qT_all, land_all, w_dram, z_dram)
        solve(core, "l0v", w_dram, z_dram, y_dram)
        landmark_outputs(core, "l0o", A, qT_all, land_all, y_dram)


RHEADS, RD, CHUNK = 4, 32, 32
CHUNKS = SEQ // CHUNK


def chunk_products(core, name, A, store):
    nc = core.nc
    S = {n: core.sem(f"{name}_{n}") for n in (
        "loaded", "const_ready", "taps_ready", "seq_done", "conv_ready", "ctrl_ready", "silu_done", "square_done", "gates_done",
        "spread_ready", "ss_ready", "norm_ready", "recip_ready", "r_turned", "r_copied", "expanded", "kdiag_ready",
        "prod_ready", "l_ready", "all_read", "l_saved", "qkv_read")}
    with ExitStack() as ctx:
        sb = lambda n, s, dt=F32: core.sb(name + "_" + n, s, dt, ctx)
        w_in, taps, w_taps = sb("w_in", [P, 3, D]), sb("taps", [P, 3, 4, D]), sb("w_taps", [P, 3, 4, D])
        w_ctrl, b8, bog = sb("w_ctrl", [P, 8 + D]), sb("b8", [8, 1]), sb("bog", [P, 1])
        chunk_c = sb("chunk_c", [P, 4, SEQ])
        ones4, pick_ab, pick_r = sb("ones4", [P, RHEADS]), sb("pick_ab", [8, 2, P]), sb("pick_r", [32, 8, P])
        qkv_s, sq = sb("qkv_s", [P, 3, SEQ]), sb("sq", [P, 2, SEQ])
        gates8 = sb("gates8", [8, SEQ])
        a_all, a_in, a_start, b_all = (sb(n, [P, SEQ]) for n in ("a_all", "a_in", "a_start", "b_all"))
        dec, gam, dec_b, gam_b = (sb(n, [P, SEQ]) for n in ("dec", "gam", "dec_b", "gam_b"))
        nrm, rT = sb("nrm", [P, 32]), sb("rT", [32, P])
        kq_n, ktok = sb("kq_n", [P, 2, SEQ]), sb("ktok", [P, SEQ])
        kdiag = sb("kdiag", [P, CHUNKS, P])
        l_sb = sb("l_sb", [P, CHUNKS, CHUNK])
        ps = core.ps(name + "_ps", [P, 8, 512], ctx=ctx)
        block = ctx.enter_context(nc.Block())
        chunks = lambda a: a.rearrange("p (c t) -> p c t", t=CHUNK)
        NOT_START, START, SAME, BEFORE = range(4)

        @block.sync
        def _(sp):
            for dst, src in ((w_in[:, :, :], A["L2_w_in"]), (taps[:, :, :, :].rearrange("p s j f -> p (s j f)"), A["L2_taps"].to_broadcast([P, 12 * D])),
                             (w_ctrl[:, :], A["L2_w_ctrl"]), (b8[:, :], A["L2_b8"]), (bog[:, :], A["L2_bog"]),
                             (chunk_c[:, :, :], A["c_chunk"]), (ones4[:, :], A["c_ones4"]), (pick_ab[:, :, :], A["c_pick_ab"]),
                             (pick_r[:, :, :], A["c_pick_r"])):
                sp.dma_start(dst, src).then_inc(S["loaded"], 16)
            sp.sem_inc(S["seq_done"], 1)
            with sp.Fori(0, BATCH) as b:
                sp.wait_ge(S["l_ready"], b + 1)
                for h in range(RHEADS):
                    dst = store.l_dram[bass.ds(b, 1), h].rearrange("o c s t -> (o s) c t")
                    sp.dma_start(dst, l_sb[32 * h:32 * h + 32, :, :]).then_inc(S["l_saved"], 16)
                sp.wait_ge(S["l_saved"], b * 64 + 64)
                sp.wait_ge(S["all_read"], b + 1)
                sp.sem_inc(S["seq_done"], 1)

        ALL = 16 * 9

        @block.gpsimd
        def _(pool):
            pool.memset(kdiag[:, :, :], 0.0)
            pool.drain()
            pool.sem_inc(S["const_ready"], 1)

        @block.tensor
        def _(pe):
            pe.wait_ge(S["taps_ready"], 1)
            pe.wait_ge(S["loaded"], ALL)
            with pe.Fori(0, BATCH) as b:
                pe.wait_ge(S["silu_done"], b * 3 + 3)
                for s in (1, 0, 2):
                    for j in range(4):
                        last = pe.matmul(ps[:, s, j:SEQ], w_taps[:, s, j, :], core.xT[:, bass.ds(b * SEQ, SEQ - j)],
                                         start=(j == 0), stop=(j == 3))
                    last.then_inc(S["conv_ready"], 1)
                xb = core.xT[:, bass.ds(b * SEQ, SEQ)]
                pe.wait_ge(S["seq_done"], b + 1)
                pe.matmul(ps[:, 4, :], w_ctrl[:, 8:8 + D], xb, start=True, stop=True)
                pe.matmul(ps[0:8, 3, :], w_ctrl[:, 0:8], xb, start=True, stop=True).then_inc(S["ctrl_ready"], 1)
                for s in range(2):
                    pe.wait_ge(S["square_done"], b * 2 + s + 1)
                    for t in range(TPB):
                        at = (s * TPB + t) * RHEADS
                        last = pe.matmul(ps[:, 7, at:at + RHEADS], sq[:, s, t * P:(t + 1) * P], ones4[:, :],
                                         start=True, stop=True)
                last.then_inc(S["ss_ready"], 1)
                pe.wait_ge(S["gates_done"], b + 1)
                for k in range(2):
                    last = pe.matmul(ps[:, 5 + k, :], pick_ab[:, k, :], gates8[:, :], start=True, stop=True)
                last.then_inc(S["spread_ready"], 1)
                pe.wait_ge(S["recip_ready"], b + 1)
                pe.transpose(ps[0:32, 7, P:2 * P], nrm[:, :], core.ident[:, :]).then_inc(S["r_turned"], 1)
                pe.wait_ge(S["r_copied"], b + 1)
                pe.wait_ge(S["silu_done"], b * 3 + 6)
                for s in range(2):
                    for t in range(TPB):
                        last = pe.matmul(ps[:, 5 + s, t * P:(t + 1) * P], pick_r[:, s * TPB + t, :], rT[:, :],
                                         start=True, stop=True)
                last.then_inc(S["expanded"], 1)
                pe.wait_ge(S["kdiag_ready"], b + 1)
                for c in range(CHUNKS):
                    last = pe.matmul(ps[:, 3 + c // 8, (c % 8) * 64:(c % 8 + 1) * 64], kdiag[:, c, :],
                                     kq_n[:, :, c * CHUNK:(c + 1) * CHUNK], start=True, stop=True)
                last.then_inc(S["prod_ready"], 1)

        @block.scalar
        def _(act):
            act.wait_ge(S["loaded"], ALL)
            act.sem_inc(S["silu_done"], 3)
            with act.Fori(0, BATCH) as b:
                act.wait_ge(S["qkv_read"], b + 1)
                for n, s in enumerate((1, 0, 2)):
                    act.wait_ge(S["conv_ready"], b * 3 + n + 1)
                    act.activation(qkv_s[:, s, :], ps[:, s, :], ACT.Silu).then_inc(S["silu_done"], 1)
                act.drain()
                for n, s in enumerate((1, 0)):
                    act.activation(sq[:, n, :], qkv_s[:, s, :], ACT.Square).then_inc(S["square_done"], 1)
                act.wait_ge(S["ctrl_ready"], b + 1)
                act.activation(gates8[:, :], ps[0:8, 3, :], ACT.Sigmoid, bias=b8[:, 0:1]).then_inc(S["gates_done"], 1)
                act.activation(store.og[:, bass.ds(b * SEQ, SEQ)], ps[:, 4, :], ACT.Sigmoid, bias=bog[:, 0:1])
                act.wait_ge(S["ss_ready"], b + 1)
                act.activation(nrm[:, :], ps[:, 7, 0:32], ACT.Sqrt).then_inc(S["norm_ready"], 1)

        @block.vector
        def _(dve):
            dve.wait_ge(S["loaded"], ALL)
            dve.wait_ge(S["const_ready"], 1)
            for s in range(3):
                last = dve.tensor_tensor(w_taps[:, s, :, :], taps[:, s, :, :],
                                         w_in[:, s, :].rearrange("p (o f) -> p o f", o=1).to_broadcast([P, 4, D]), ALU.mult)
            last.then_inc(S["taps_ready"], 1)
            dve.sem_inc(S["qkv_read"], 1)
            with dve.Fori(0, BATCH) as b:
                dve.wait_ge(S["norm_ready"], b + 1)
                dve.tensor_scalar(nrm[:, :], nrm[:, :], 1e-6, None, ALU.max)
                dve.drain()
                dve.reciprocal(nrm[:, :], nrm[:, :]).then_inc(S["recip_ready"], 1)
                dve.wait_ge(S["spread_ready"], b + 1)
                dve.tensor_scalar(a_all[:, :], ps[:, 5, :], 0.01, None, ALU.add)
                dve.tensor_copy(b_all[:, :], ps[:, 6, :])
                dve.wait_ge(S["r_turned"], b + 1)
                dve.tensor_copy(rT[:, :], ps[0:32, 7, P:2 * P]).then_inc(S["r_copied"], 1)
                dve.drain()
                dve.tensor_tensor(a_in[:, :], a_all[:, :], chunk_c[:, NOT_START, :], ALU.mult)
                dve.tensor_tensor(a_start[:, :], a_all[:, :], chunk_c[:, START, :], ALU.mult)
                dve.drain()
                dve.tensor_tensor_scan(dec[:, :], a_in[:, :], chunk_c[:, SAME, :], 0.0, ALU.mult, ALU.add)
                dve.tensor_tensor_scan(gam[:, :], a_in[:, :], a_start[:, :], 0.0, ALU.mult, ALU.add)
                dve.drain()
                dve.wait_ge(S["expanded"], b + 1)
                dve.tensor_tensor(kq_n[:, 0, :], qkv_s[:, 1, :], ps[:, 5, :], ALU.mult)
                dve.tensor_tensor(kq_n[:, 1, :], qkv_s[:, 0, :], ps[:, 6, :], ALU.mult)
                dve.tensor_tensor(store.vb[:, :, bass.ds(b, 1), :], chunks(qkv_s[:, 2, :]), chunks(b_all[:, :]), ALU.mult)\
                   .then_inc(S["qkv_read"], 1)
                dve.tensor_tensor(dec_b[:, :], dec[:, :], b_all[:, :], ALU.mult)
                dve.tensor_tensor(gam_b[:, :], gam[:, :], b_all[:, :], ALU.mult)
                dve.drain()
                for h in range(RHEADS):
                    rows = slice(32 * h, 32 * h + 32)
                    last = dve.tensor_copy(kdiag[rows, :, 32 * h:32 * h + 32], chunks(kq_n[rows, 0, :]))
                last.then_inc(S["kdiag_ready"], 1)
                dve.tensor_tensor(dec_b[:, :], dec_b[:, :], chunk_c[:, BEFORE, :], ALU.mult)
                dve.transpose(ktok[:, :], kq_n[:, 0, :])
                dve.tensor_tensor(store.kq[:, :, bass.ds(b, 1), 0:32], chunks(kq_n[:, 0, :]), chunks(gam_b[:, :]), ALU.mult)
                dve.tensor_tensor(store.kq[:, :, bass.ds(b, 1), 32:64], chunks(kq_n[:, 1, :]), chunks(gam[:, :]), ALU.mult)
                dve.tensor_copy(store.last[:, :, bass.ds(b, 1)], chunks(gam[:, :])[:, :, CHUNK - 1:CHUNK])
                dve.drain()
                dve.tensor_tensor(store.ak[:, :, bass.ds(b, 1), 32:64], chunks(ktok[:, :]),
                                  chunks(dec[:, :])[:, :, CHUNK - 1:CHUNK].to_broadcast([P, CHUNKS, CHUNK]), ALU.mult)
                dve.wait_ge(S["prod_ready"], b + 1)
                dve.wait_ge(S["seq_done"], b + 1)
                prod = ps[:, 3:5, :].rearrange("p n (c k) -> p (n c) k", k=64)
                dve.tensor_tensor(l_sb[:, :, :], prod[:, :, 0:32], chunks(dec_b[:, :]), ALU.mult).then_inc(S["l_ready"], 1)
                dve.tensor_tensor(store.ak[:, :, bass.ds(b, 1), 0:32], prod[:, :, 32:64], chunks(dec[:, :]), ALU.mult)\
                   .then_inc(S["all_read"], 1)


def invert_chunks(core, name, l_dram, t_dram):
    nc = core.nc
    SYS, MINE = 4, 3
    loaded, started, done, saved = (core.sem(f"{name}_{n}") for n in ("loaded", "started", "done", "saved"))
    with ExitStack() as ctx:
        sb = lambda n, s, dt=F32: core.sb(name + "_" + n, s, dt, ctx)
        l_sb, t_sb = sb("l", [P, SYS, CHUNK, CHUNK]), sb("t", [P, SYS, CHUNK, CHUNK])
        outer_p = sb("outer_p", [P, 1, CHUNK * CHUNK // 4 + CHUNK])
        outer = core.ps(name + "_outer", [P, MINE * 512], ctx=ctx)
        block = ctx.enter_context(nc.Block())

        def rows_off(eng, s0, n, buf):
            for j in range(CHUNK - 1):
                shape = [P, n, j + 1, CHUNK - 1 - j]
                size = shape[2] * shape[3]
                out = buf(n, size).rearrange("p s (l i) -> p s l i", i=shape[3])
                eng.tensor_tensor(out, l_sb[:, s0:s0 + n, j:j + 1, j + 1:CHUNK].to_broadcast(shape),
                                  t_sb[:, s0:s0 + n, 0:j + 1, j:j + 1].to_broadcast(shape), ALU.mult)
                eng.drain()
                rest = t_sb[:, s0:s0 + n, 0:j + 1, j + 1:CHUNK]
                eng.tensor_tensor(rest, rest, out, ALU.subtract)
                eng.drain()
            eng.sem_inc(done, 1)

        @block.sync
        def _(sp):
            sp.dma_start(l_sb[:, :, :, :], l_dram.rearrange("b h (g c) s t -> (b h g) c s t", c=SYS)).then_inc(loaded, 16)
            sp.wait_ge(done, 2)
            sp.dma_start(t_dram.rearrange("b h (g c) s t -> (b h g) c s t", c=SYS), t_sb[:, :, :, :]).then_inc(saved, 16)
            sp.wait_ge(saved, 16)

        @block.gpsimd
        def _(pool):
            pool.memset(t_sb[:, :, :, :], 0.0)
            pool.drain()
            pool.memset(t_sb[:, :, :, :].rearrange("p c s t -> p c (s t)")[:, :, 0:CHUNK * CHUNK:CHUNK + 1], 1.0)
            pool.drain()
            pool.sem_inc(started, 1)
            pool.wait_ge(loaded, 16)
            rows_off(pool, MINE, 1, lambda n, size: outer_p[:, :, 0:size])

        @block.vector
        def _(dve):
            dve.wait_ge(started, 1)
            dve.wait_ge(loaded, 16)
            rows_off(dve, 0, MINE, lambda n, size: outer[:, :].rearrange("p (s k) -> p s k", s=MINE)[:, :, 0:size])


def chunk_recurrence(core, name, store, t_dram, o_all):
    nc = core.nc
    HB = BATCH // 2
    S = {n: core.sem(f"{name}_{n}") for n in (
        "loaded", "const_ready", "operands", "step_done", "s_ready", "so_ready", "x_ready", "o1_done", "u_ready", "u_diag_a", "u_diag_v",
        "c_ready", "s_turned", "s_diag_a", "s_diag_v")}
    with ExitStack() as ctx:
        sb = lambda n, s, dt=F32: core.sb(name + "_" + n, s, dt, ctx)
        t_all = sb("t_all", [P, BATCH, CHUNKS, CHUNK])
        kq, ak = sb("kq", [P, 2, BATCH, 64]), sb("ak", [P, 2, BATCH, 64])
        tdiag = sb("tdiag", [P, 2, BATCH, P])
        state, turned = sb("state", [P, BATCH, RD]), sb("turned", [P, BATCH, RD])
        sdiag, udiag = sb("sdiag", [P, BATCH, P]), sb("udiag", [P, BATCH, P])
        xT, xtok, o1 = sb("xT", [P, BATCH, RD]), sb("xtok", [P, BATCH, RD]), sb("o1", [P, BATCH, RD])
        ps_a = core.ps(name + "_ps_a", [P, 2, 512], ctx=ctx)
        ps_u = core.ps(name + "_ps_u", [P, 2, 512], ctx=ctx)
        ps_c = core.ps(name + "_ps_c", [P, 2, 512], ctx=ctx)
        block = ctx.enter_context(nc.Block())
        of = lambda ps, g, w: ps[:, g, 0:HB * w].rearrange("p (b k) -> p b k", b=HB)

        @block.sync
        def _(sp):
            with sp.Fori(0, BATCH) as b:
                for h in range(RHEADS):
                    dst = t_all[32 * h:32 * h + 32, bass.ds(b, 1), :, :].rearrange("s o c t -> s (o c) t")
                    sp.dma_start(dst, t_dram[bass.ds(b, 1), h].rearrange("o c s t -> s (o c) t")).then_inc(S["loaded"], 16)

        @block.gpsimd
        def _(pool):
            pool.memset(sdiag[:, :, :], 0.0)
            pool.memset(udiag[:, :, :], 0.0)
            pool.memset(tdiag[:, :, :, :], 0.0)
            pool.memset(state[:, :, :], 0.0)
            pool.drain()
            pool.sem_inc(S["const_ready"], 1)

        @block.tensor
        def _(pe):
            pe.wait_ge(S["const_ready"], 1)
            with pe.Fori(0, CHUNKS // 2) as r:
                for k in range(2):
                    pe.wait_ge(S["operands"], r * 2 + k + 1)
                    for g in range(2):
                        n = 2 * k + g
                        pe.wait_ge(S["s_diag_a"], r * 4 + n + 1)
                        pe.wait_ge(S["s_diag_v"], r * 4 + n + 1)
                        for b in range(HB * g, HB * g + HB):
                            last = pe.matmul(of(ps_a, g, 64)[:, b - HB * g, :], sdiag[:, b, :], kq[:, k, b, :],
                                             start=True, stop=True)
                        last.then_inc(S["so_ready"], 1)
                    for g in range(2):
                        n = 2 * k + g
                        pe.wait_ge(S["x_ready"], r * 4 + n + 1)
                        for b in range(HB * g, HB * g + HB):
                            last = pe.matmul(of(ps_u, g, RD)[:, b - HB * g, :], tdiag[:, k, b, :], xtok[:, b, :],
                                             start=True, stop=True)
                        last.then_inc(S["u_ready"], 1)
                    for g in range(2):
                        n = 2 * k + g
                        pe.wait_ge(S["u_diag_a"], r * 4 + n + 1)
                        pe.wait_ge(S["u_diag_v"], r * 4 + n + 1)
                        for b in range(HB * g, HB * g + HB):
                            last = pe.matmul(of(ps_c, g, 64)[:, b - HB * g, :], udiag[:, b, :], ak[:, k, b, :],
                                             start=True, stop=True)
                        last.then_inc(S["c_ready"], 1)

        @block.scalar
        def _(act):
            act.wait_ge(S["const_ready"], 1)
            act.wait_ge(S["loaded"], 64 * BATCH)
            act.sem_inc(S["s_diag_a"], 2)
            with act.Fori(0, CHUNKS // 2) as r:
                def operands(k):
                    c = r * 2 + k
                    act.wait_ge(S["step_done"], r * 2 + k + 1)
                    act.activation(kq[:, k, :, :], store.kq[:, bass.ds(c, 1), :, :].rearrange("p o b k -> p (o b) k"), ACT.Copy)
                    act.activation(ak[:, k, :, :], store.ak[:, bass.ds(c, 1), :, :].rearrange("p o b k -> p (o b) k"), ACT.Copy)
                    for h in range(RHEADS):
                        rows = slice(32 * h, 32 * h + 32)
                        last = act.activation(tdiag[rows, k, :, 32 * h:32 * h + 32],
                                              t_all[rows, :, bass.ds(c, 1), :].rearrange("p b o k -> p b (o k)"), ACT.Copy)
                    act.drain()
                    act.sem_inc(S["operands"], 1)

                for k in range(2):
                    operands(k)
                    for g in range(2):
                        n = 2 * k + g
                        act.wait_ge(S["x_ready"], r * 4 + n + 1)
                        act.activation(o1[:, HB * g:HB * g + HB, :], of(ps_a, g, 64)[:, :, 32:64], ACT.Copy)\
                           .then_inc(S["o1_done"], 1)
                    for g in range(2):
                        n = 2 * k + g
                        act.wait_ge(S["u_ready"], r * 4 + n + 1)
                        for h in (2, 3):
                            rows = slice(32 * h, 32 * h + 32)
                            last = act.activation(udiag[rows, HB * g:HB * g + HB, 32 * h:32 * h + 32],
                                                  of(ps_u, g, RD)[rows, :, :], ACT.Copy)
                        last.then_inc(S["u_diag_a"], 1)
                    for g in range(2):
                        n = 2 * k + g
                        act.wait_ge(S["s_turned"], r * 4 + n + 1)
                        for h in (2, 3):
                            rows = slice(32 * h, 32 * h + 32)
                            last = act.activation(sdiag[rows, HB * g:HB * g + HB, 32 * h:32 * h + 32],
                                                  turned[rows, HB * g:HB * g + HB, :], ACT.Copy)
                        last.then_inc(S["s_diag_a"], 1)

        @block.vector
        def _(dve):
            dve.wait_ge(S["const_ready"], 1)
            dve.sem_inc(S["step_done"], 2)
            dve.sem_inc(S["s_diag_v"], 2)
            with dve.Fori(0, CHUNKS // 2) as r:
                for k in range(2):
                    c = r * 2 + k
                    for g in range(2):
                        n = 2 * k + g
                        mine = slice(HB * g, HB * g + HB)
                        dve.wait_ge(S["so_ready"], r * 4 + n + 1)
                        dve.tensor_tensor(xT[:, mine, :],
                                          store.vb[:, bass.ds(c, 1), mine, :].rearrange("p o b k -> p (o b) k"),
                                          of(ps_a, g, 64)[:, :, 0:32], ALU.subtract)
                        dve.drain()
                        dve.transpose(xtok[:, mine, :].rearrange("p b k -> p (b k)"),
                                      xT[:, mine, :].rearrange("p b k -> p (b k)")).then_inc(S["x_ready"], 1)
                        dve.tensor_tensor(state[:, mine, :], state[:, mine, :],
                                          store.last[:, bass.ds(c, 1), mine].rearrange("p o (b u) -> p (o b) u", u=1)
                                          .to_broadcast([P, HB, RD]), ALU.mult)
                    for g in range(2):
                        n = 2 * k + g
                        dve.wait_ge(S["u_ready"], r * 4 + n + 1)
                        for h in (0, 1):
                            rows = slice(32 * h, 32 * h + 32)
                            last = dve.tensor_copy(udiag[rows, HB * g:HB * g + HB, 32 * h:32 * h + 32],
                                                   of(ps_u, g, RD)[rows, :, :])
                        last.then_inc(S["u_diag_v"], 1)
                    for g in range(2):
                        n = 2 * k + g
                        mine = slice(HB * g, HB * g + HB)
                        dve.wait_ge(S["c_ready"], r * 4 + n + 1)
                        dve.tensor_tensor(state[:, mine, :], state[:, mine, :], of(ps_c, g, 64)[:, :, 32:64], ALU.add)
                        dve.drain()
                        dve.transpose(turned[:, mine, :].rearrange("p b k -> p (b k)"),
                                      state[:, mine, :].rearrange("p b k -> p (b k)")).then_inc(S["s_turned"], 1)
                        dve.wait_ge(S["o1_done"], r * 4 + n + 1)
                        dve.tensor_tensor(o_all[:, bass.ds(c, 1), mine, :].rearrange("p o b k -> p (o b) k"), o1[:, mine, :],
                                          of(ps_c, g, 64)[:, :, 0:32], ALU.add)
                        dve.drain()
                        for h in (0, 1):
                            rows = slice(32 * h, 32 * h + 32)
                            last = dve.tensor_copy(sdiag[rows, mine, 32 * h:32 * h + 32], turned[rows, mine, :])
                        last.then_inc(S["s_diag_v"], 1)
                    dve.sem_inc(S["step_done"], 1)


def gated_output(core, name, A, o_all, og):
    nc = core.nc
    S = {n: core.sem(f"{name}_{n}") for n in (
        "loaded", "ramp_exp", "x_added", "squared", "ss_ready", "root_ready", "recip_ready", "r_turned", "r_copied", "expanded",
        "o_normed", "y_ready", "gated", "turned")}
    with ExitStack() as ctx:
        sb = lambda n, s, dt=F32: core.sb(name + "_" + n, s, dt, ctx)
        w_out, b_out, ramp = sb("w_out", [P, D]), sb("b_out", [P, 1]), sb("ramp", [P, 1])
        ones4, pick = sb("ones4", [P, RHEADS]), sb("pick", [16, TPB, P])
        epsb = sb("eps", [P, 1])
        o_s, sq, on, y = (sb(n, [P, SEQ]) for n in ("o_s", "sq", "on", "y"))
        r, rT = sb("r", [P, 16]), sb("rT", [16, P])
        ps = core.ps(name + "_ps", [P, 4, 512], ctx=ctx)
        block = ctx.enter_context(nc.Block())

        @block.sync
        def _(sp):
            for dst, src in ((w_out[:, :], A["L2_w_out"]), (b_out[:, :], A["L2_b_out"]), (ramp[:, :], A["L2_ramp"]),
                             (ones4[:, :], A["c_ones4"]), (pick[:, :, :], A["c_pick_o"])):
                sp.dma_start(dst, src).then_inc(S["loaded"], 16)

        @block.tensor
        def _(pe):
            pe.wait_ge(S["loaded"], 80)
            with pe.Fori(0, BATCH) as b:
                pe.wait_ge(S["squared"], b + 1)
                for t in range(TPB):
                    last = pe.matmul(ps[:, 0, t * RHEADS:(t + 1) * RHEADS], sq[:, t * P:(t + 1) * P], ones4[:, :],
                                     start=True, stop=True)
                last.then_inc(S["ss_ready"], 1)
                pe.wait_ge(S["recip_ready"], b + 1)
                pe.transpose(ps[0:16, 0, P:2 * P], r[:, :], core.ident[:, :]).then_inc(S["r_turned"], 1)
                pe.wait_ge(S["r_copied"], b + 1)
                for t in range(TPB):
                    last = pe.matmul(ps[:, 1, t * P:(t + 1) * P], pick[:, t, :], rT[:, :], start=True, stop=True)
                last.then_inc(S["expanded"], 1)
                pe.wait_ge(S["o_normed"], b + 1)
                pe.matmul(ps[:, 2, :], w_out[:, :], on[:, :], start=True, stop=True).then_inc(S["y_ready"], 1)
                pe.wait_ge(S["gated"], b + 1)
                for t in range(TPB):
                    last = pe.transpose(ps[:, 3, t * P:(t + 1) * P], y[:, t * P:(t + 1) * P], core.ident[:, :])
                last.then_inc(S["turned"], 1)

        @block.scalar
        def _(act):
            act.wait_ge(S["loaded"], 80)
            act.activation(ramp[:, :], ramp[:, :], ACT.Sigmoid).then_inc(S["ramp_exp"], 1)
            with act.Fori(0, BATCH) as b:
                act.wait_ge(S["x_added"], b + 1)
                src = o_all[:, :, bass.ds(b, 1), :].rearrange("p c o t -> p c (o t)")
                act.activation(sq[:, :].rearrange("p (c t) -> p c t", t=CHUNK), src, ACT.Square).then_inc(S["squared"], 1)
                act.activation(o_s[:, :].rearrange("p (c t) -> p c t", t=CHUNK), src, ACT.Copy)
                act.wait_ge(S["ss_ready"], b + 1)
                act.activation(r[:, :], ps[:, 0, 0:16], ACT.Sqrt, scale=1.0 / RD, bias=epsb[:, 0:1])\
                   .then_inc(S["root_ready"], 1)

        @block.vector
        def _(dve):
            dve.memset(epsb[:, :], 1e-6)
            dve.wait_ge(S["ramp_exp"], 1)
            dve.drain()
            dve.sem_inc(S["x_added"], 1)
            with dve.Fori(0, BATCH) as b:
                dve.wait_ge(S["root_ready"], b + 1)
                dve.reciprocal(r[:, :], r[:, :]).then_inc(S["recip_ready"], 1)
                dve.wait_ge(S["r_turned"], b + 1)
                dve.tensor_copy(rT[:, :], ps[0:16, 0, P:2 * P]).then_inc(S["r_copied"], 1)
                dve.wait_ge(S["expanded"], b + 1)
                dve.tensor_tensor(on[:, :], o_s[:, :], ps[:, 1, :], ALU.mult).then_inc(S["o_normed"], 1)
                dve.wait_ge(S["y_ready"], b + 1)
                dve.tensor_scalar(y[:, :], ps[:, 2, :], b_out[:, 0:1], ramp[:, 0:1], ALU.add, ALU.mult)
                dve.drain()
                dve.tensor_tensor(y[:, :], y[:, :], og[:, bass.ds(b * SEQ, SEQ)], ALU.mult).then_inc(S["gated"], 1)
                dve.wait_ge(S["turned"], b + 1)
                xr = core.x[:, bass.ds(b * TPB, TPB), :]
                dve.tensor_tensor(xr, xr, ps[:, 3, :].rearrange("p (t d) -> p t d", t=TPB), ALU.add)\
                   .then_inc(S["x_added"], 1)


class ChunkStore:

    def __init__(self, core, ctx):
        self.kq = core.sb("l2a_kq", [P, CHUNKS, BATCH, 64], ctx=ctx)
        self.ak = core.sb("l2a_ak", [P, CHUNKS, BATCH, 64], ctx=ctx)
        self.vb = core.sb("l2a_vb", [P, CHUNKS, BATCH, RD], ctx=ctx)
        self.last = core.sb("l2a_last", [P, CHUNKS, BATCH], ctx=ctx)
        self.l_dram = core.dram("l2a_l_dram", [BATCH, RHEADS, CHUNKS, CHUNK, CHUNK])


def layer2_attention(core, A):
    layernorm(core, "l2a_ln")
    with ExitStack() as outer:
        og = core.sb("l2a_og", [P, N], ctx=outer)
        o_all = core.xT[:, :].rearrange("p (c b t) -> p c b t", c=CHUNKS, b=BATCH)
        t_dram = core.dram("l2a_t_dram", [BATCH, RHEADS, CHUNKS, CHUNK, CHUNK])
        with ExitStack() as ctx:
            store = ChunkStore(core, ctx)
            store.og = og
            chunk_products(core, "l2p", A, store)
            invert_chunks(core, "l2i", store.l_dram, t_dram)
            chunk_recurrence(core, "l2r", store, t_dram, o_all)
        gated_output(core, "l2g", A, o_all, og)


def place_tokens(core, name, wts, E, span, slots, weights, skip, blk_row=None):
    nc = core.nc
    COLS = TILES * E
    NB = (TABLE_ROWS - 1) // span
    made, masked, summed = core.sem(name + "_made"), core.sem(name + "_masked"), core.sem(name + "_summed")
    with ExitStack() as ctx:
        sb = lambda n, s, dt=F32: core.sb(name + "_" + n, s, dt, ctx)
        before, ones = sb("before", [P, P]), sb("ones", [P, P])
        mask, at, hit = (sb(n, [P, TILES, E]) for n in ("mask", "at", "hit"))
        incl = sb("incl", [P, E, TILES])
        zeros, size, first = sb("zeros", [P, 32]), sb("size", [P, E]), sb("first", [P, E])
        a, b = sb("a", [P, TILES]), sb("b", [P, TILES])
        iota, begun = sb("iota", [P, NB]), sb("begun", [P, NB, E])
        ps_b = core.ps(name + "_ps_b", [P, BLK], ctx=ctx)
        ps_t = core.ps(name + "_ps_t", [P, BLK], ctx=ctx)
        flat = lambda v: v[:, :, :].rearrange("p t e -> p (t e)")
        count = ps_t[:, 0:COLS].rearrange("p (t e) -> p t e", e=E)
        each = lambda v, m: v[:, :].rearrange("p (t o) -> p t o", o=1).to_broadcast([P, m, E])
        by_e = lambda v, m: v[:, :].rearrange("p (o e) -> p o e", o=1).to_broadcast([P, m, E])
        block = ctx.enter_context(nc.Block())

        @block.gpsimd
        def _(pool):
            pool.memset(ones[:, :], 1.0)
            pool.drain()
            pool.affine_select(out=before[:, :], in_=ones[:, :], compare_op=ALU.is_gt, fill=0.0,
                               base=0, pattern=[[1, P]], channel_multiplier=-1)
            pool.iota(iota[:, :], pattern=[[span, NB]], base=0, channel_multiplier=0,
                      allow_small_or_imprecise_dtypes=True)
            pool.iota(a[:, 0:1], pattern=[[0, 1]], base=-P, channel_multiplier=1,
                      allow_small_or_imprecise_dtypes=True)
            pool.drain()
            pool.sem_inc(made, 1)

        @block.tensor
        def _(pe):
            pe.wait_ge(made, 1)
            pe.wait_ge(masked, 1)
            pe.matmul(ps_b[:, 0:COLS], before[:, :], flat(mask), start=True, stop=True)
            pe.matmul(ps_t[:, 0:COLS], ones[:, :], flat(mask), start=True, stop=True).then_inc(summed, 1)

        @block.vector
        def _(dve):
            dve.tensor_scalar(mask[:, :, :], wts[:, :, 0:E], 0.0, None, ALU.is_gt).then_inc(masked, 1)
            if blk_row is not None:
                dve.memset(wts[:, :, E:E + 1], 1.0)
            dve.memset(zeros[:, :], 0.0)
            dve.wait_ge(summed, 1)
            dve.drain()
            for e in range(E):
                dve.tensor_tensor_scan(incl[:, e, :], count[:, :, e], zeros[:, 0:TILES], 0.0, ALU.add, ALU.add)
            dve.drain()
            dve.tensor_scalar(size[:, :], incl[:, :, TILES - 1], span / 2 - 0.5, 1.0 / span, ALU.add, ALU.mult)
            dve.tensor_tensor(at[:, :, :], ps_b[:, 0:COLS].rearrange("p (t e) -> p t e", e=E),
                              incl[:, :, :].rearrange("p e t -> p t e"), ALU.add)
            dve.drain()
            dve.tensor_tensor(at[:, :, :], at[:, :, :], count, ALU.subtract)
            if blk_row is None:
                for e in range(E):
                    last = dve.memset(first[:, e:e + 1], float(e * span))
            else:
                dve.tensor_scalar(size[:, :], size[:, :], 8388608.0, None, ALU.add)
                dve.drain()
                dve.tensor_scalar(size[:, :], size[:, :], -8388608.0, float(span), ALU.add, ALU.mult)
                dve.drain()
                dve.tensor_tensor_scan(first[:, :], size[:, :], zeros[:, 0:E], 0.0, ALU.add, ALU.add)
                dve.drain()
                dve.tensor_tensor(first[:, :], first[:, :], size[:, :], ALU.subtract)
                dve.drain()
                wide = iota[:, :].rearrange("p (n o) -> p n o", o=1).to_broadcast([P, NB, E])
                dve.wait_ge(made, 1)
                dve.tensor_tensor(begun[:, :, :], by_e(first, NB), wide, ALU.is_le)
                dve.tensor_copy(size[:, 0:1], a[:, 0:1])
                dve.drain()
                dve.tensor_reduce(iota[:, :], begun[:, :, :], AX.X, ALU.add)
                dve.drain()
                dve.tensor_scalar(blk_row[:, :], iota[:, :], float(P), size[:, 0:1], ALU.mult, ALU.add)
            dve.drain()
            dve.scalar_tensor_tensor(out=at[:, :, :], in0=at[:, :, :], scalar=1.0, in1=by_e(first, TILES),
                                     op0=ALU.add, op1=ALU.add)
            dve.drain()
            dve.tensor_tensor(at[:, :, :], at[:, :, :], mask[:, :, :], ALU.mult)
            dve.drain()
            dve.tensor_reduce(a[:, :], at[:, :, :], AX.X, ALU.max)
            dve.tensor_reduce(b[:, :], at[:, :, :], AX.X, ALU.add)
            dve.drain()
            dve.tensor_tensor(b[:, :], b[:, :], a[:, :], ALU.subtract)
            dve.tensor_tensor(hit[:, :, :], at[:, :, :], each(a, TILES), ALU.is_equal)
            dve.drain()
            dve.tensor_tensor(hit[:, :, :], hit[:, :, :], wts[:, :, 0:E], ALU.mult)
            for k, v in enumerate((a, b)):
                dve.tensor_copy(slots[:, k, :], v[:, :])
                dve.tensor_scalar(incl[:, k, :], v[:, :], 0.0, 1.0e6, ALU.is_equal, ALU.mult)
            dve.drain()
            for k, v in enumerate((a, b)):
                dve.tensor_tensor(skip[:, k, :], incl[:, k, :], v[:, :], ALU.add)
            dve.tensor_reduce(weights[:, 0, :], hit[:, :, :], AX.X, ALU.add)
            dve.tensor_reduce(weights[:, 1, :], wts[:, :, 0:E], AX.X, ALU.add)
            dve.drain()
            dve.tensor_tensor(weights[:, 1, :], weights[:, 1, :], weights[:, 0, :], ALU.subtract)


def scatter_tokens(core, pool, xn, skip, scattered):
    pool.wait_ge(core.table_filled, 48)
    for k in range(2):
        for t in range(TILES):
            pool.indirect_dma_start(out=core.table_x[:, :], in_=xn[:, t, :], in_offset=None,
                                    out_offset=bass.IndirectOffsetOnAxis(ap=skip[:, k, t:t + 1], axis=0),
                                    bounds_check=TABLE_ROWS - 1, oob_is_err=False).then_inc(scattered, 16)
    pool.wait_ge(scattered, 2 * TILES * 16)


def scatter_block(core, name, xn, skip):
    scattered = core.sem(name + "_scattered")
    with core.nc.Block() as block:

        @block.gpsimd
        def _(pool):
            scatter_tokens(core, pool, xn, skip, scattered)


def shared_expert(core, name, rows, w1_in, b1_in, w2_in, b2_in, xn, skip):
    nc = core.nc
    E, C = b2_in.shape[0], 2
    loaded, gu_ready, gelu_done = core.sem(name + "_loaded"), core.sem(name + "_gu_ready"), core.sem(name + "_gelu_done")
    act_done, y_ready, added = core.sem(name + "_act_done"), core.sem(name + "_y_ready"), core.sem(name + "_added")
    scattered = core.sem(name + "_scattered")
    with ExitStack() as ctx:
        sb = lambda n, s, dt=F32: core.sb(name + "_" + n, s, dt, ctx)
        w1, w2, b1, b2 = sb("w1", [P, 2 * C, P]), sb("w2", [P, C, D]), sb("b1", [P, 2 * C]), sb("b2", [E, D])
        gelu, act_out = sb("gelu", [P, 2, BLK]), sb("act", [P, 2, C, BLK])
        ps_g = core.ps(name + "_ps_g", [P, 2, BLK], ctx=ctx)
        ps_u = core.ps(name + "_ps_u", [P, 2, BLK], ctx=ctx)
        ps_y = core.ps(name + "_ps_y", [P, 2, TPB, D], ctx=ctx)
        block = ctx.enter_context(nc.Block())

        @block.sync
        def _(sp):
            sp.dma_start(w1[:, :, :], w1_in[0]).then_inc(loaded, 16)
            sp.dma_start(w2[:, :, :], w2_in[0]).then_inc(loaded, 16)
            sp.dma_start(b1[:, :], b1_in[0]).then_inc(loaded, 16)
            sp.dma_start(b2[:, :], b2_in).then_inc(loaded, 16)

        @block.gpsimd
        def _(pool):
            scatter_tokens(core, pool, xn, skip, scattered)

        @block.tensor
        def _(pe):
            pe.wait_ge(loaded, 64)

            def down(b):
                pe.wait_ge(act_done, C * (b + 1))
                if b >= 2:
                    pe.wait_ge(added, b - 1)
                for t in range(TPB):
                    for c in range(C):
                        pe.matmul(ps_y[:, b % 2, t, :], act_out[:, b % 2, c, t * P:(t + 1) * P], w2[:, c, :],
                                  start=(c == 0), stop=False)
                    last = pe.matmul(ps_y[:, b % 2, t, :], rows[0:E, b * BLK + t * P:b * BLK + (t + 1) * P],
                                     b2[:, :], start=False, stop=True)
                last.then_inc(y_ready, 1)

            for b in range(NBLK):
                for c in range(C):
                    s = C * b + c
                    if s >= 2:
                        pe.wait_ge(act_done, s - 1)
                    xb = core.xT[:, b * BLK:(b + 1) * BLK]
                    pe.matmul(ps_g[:, s % 2, :], w1[:, c, :], xb, start=True, stop=True)
                    pe.matmul(ps_u[:, s % 2, :], w1[:, C + c, :], xb, start=True, stop=True).then_inc(gu_ready, 1)
                if b >= 1:
                    down(b - 1)
            down(NBLK - 1)

        @block.scalar
        def _(act):
            act.wait_ge(loaded, 64)
            for s in range(C * NBLK):
                act.wait_ge(gu_ready, s + 1)
                if s >= 2:
                    act.wait_ge(act_done, s - 1)
                act.activation(gelu[:, s % 2, :], ps_g[:, s % 2, :], ACT.Gelu, bias=b1[:, s % C:s % C + 1])\
                   .then_inc(gelu_done, 1)

        @block.vector
        def _(dve):
            dve.wait_ge(loaded, 64)

            def add(b):
                dve.wait_ge(y_ready, b + 1)
                xb = core.x[:, b * TPB:(b + 1) * TPB, :]
                dve.tensor_tensor(xb, xb, ps_y[:, b % 2, :, :], ALU.add).then_inc(added, 1)

            for b in range(NBLK):
                for c in range(C):
                    s = C * b + c
                    dve.wait_ge(gelu_done, s + 1)
                    if b >= 2:
                        dve.wait_ge(y_ready, b - 1)
                    dve.scalar_tensor_tensor(out=act_out[:, b % 2, c, :], in0=ps_u[:, s % 2, :],
                                             scalar=b1[:, C + c:C + c + 1], in1=gelu[:, s % 2, :],
                                             op0=ALU.add, op1=ALU.mult).then_inc(act_done, 1)
                if b >= 1:
                    add(b - 1)
            add(NBLK - 1)


def slot_ffn(core, name, rounds, sizes, C, func, w_in, w_cols, blk_row=None):
    nc = core.nc
    gathered = blk_row is not None
    U = len(sizes)
    BPW = 1 if gathered else 2
    NW = U // BPW
    MAXT, FROM = max(sizes), [sum(sizes[:k]) * P for k in range(U)]
    ROUND_ROWS = sum(sizes) * P
    x_loaded = [core.sem(f"{name}_x_loaded{k}") for k in range(U)]
    w_loaded = [core.sem(f"{name}_w_loaded{m}") for m in range(NW)]
    y_stored = [core.sem(f"{name}_y_stored{k}") for k in range(U)]
    turned, copied = core.sem(name + "_turned"), core.sem(name + "_copied")
    gu_ready, gate_done, act_done = (core.sem(f"{name}_{n}") for n in ("gu_ready", "gate_done", "act_done"))
    y_ready, y_copied = core.sem(name + "_y_ready"), core.sem(name + "_y_copied")
    with ExitStack() as ctx:
        sb = lambda n, s, dt=F32: core.sb(name + "_" + n, s, dt, ctx)
        w = sb("w", [P, NW, w_cols])
        idx = sb("idx", [P, NW], U32) if gathered else None
        xs, xsT = sb("xs", [P, U, MAXT, D]), sb("xsT", [P, U, MAXT * P])
        gate, act_out = sb("gate", [P, 2, MAXT * P]), sb("act", [P, U, C, MAXT * P])
        y_sb = sb("y", [P, U, MAXT, D])
        ps_t, ps_g, ps_u, ps_y = (core.ps(f"{name}_ps_{n}", [P, 2, BLK], ctx=ctx) for n in ("t", "g", "u", "y"))
        block = ctx.enter_context(nc.Block())
        w1 = lambda k, c: w[:, k // BPW, c * P:(c + 1) * P]
        w2 = lambda k, c: w[:, k // BPW, (2 * C + c) * P:(2 * C + c + 1) * P]
        b1 = lambda k, c: w[:, k // BPW, 3 * C * P + c:3 * C * P + c + 1] if gathered else 0.0

        def slots_of(table, r, k):
            n = sizes[k] * P
            at = slice(1 + FROM[k], 1 + FROM[k] + n) if type(r) is int and r == 0 \
                else bass.ds(r * ROUND_ROWS + (1 + FROM[k]), n)
            return table[at, :].rearrange("(t p) d -> p t d", p=P)

        def load_weights(sp, r, m):
            at = slice(m * P, (m + 1) * P) if type(r) is int and r == 0 else bass.ds(r * (NW * P) + m * P, P)
            sp.dma_start(w[:, m, :], w_in[at, :]).then_inc(w_loaded[m], 16)

        @block.sync
        def _(sp):
            for k in range(U):
                if not gathered and k % BPW == 0:
                    load_weights(sp, 0, k // BPW)
                sp.dma_start(xs[:, k, 0:sizes[k], :], slots_of(core.table_x, 0, k)).then_inc(x_loaded[k], 16)

            def store(r, k):
                sp.wait_ge(y_copied, r * U + (k + 1))
                sp.dma_start(slots_of(core.table_y, r, k), y_sb[:, k, 0:sizes[k], :]).then_inc(y_stored[k], 16)

            with sp.Fori(0, rounds - 1) as r:
                for k in range(U):
                    sp.wait_ge(turned, r * U + (k + 1))
                    sp.dma_start(xs[:, k, 0:sizes[k], :], slots_of(core.table_x, r + 1, k))\
                        .then_inc(x_loaded[k], 16)
                    store(r, k)
                    if not gathered and k % BPW == BPW - 1:
                        sp.wait_ge(y_ready, r * U + (k + 1))
                        load_weights(sp, r + 1, k // BPW)
            for k in range(U):
                store(rounds - 1, k)
            for k in range(U):
                sp.wait_ge(y_stored[k], 16 * rounds + 16)

        @block.gpsimd
        def _(pool):
            if gathered:
                def gather_weights(r, k):
                    at = slice(k, k + 1) if type(r) is int else bass.ds(r * U + k, 1)
                    pool.tensor_copy(idx[:, k:k + 1], blk_row[:, at])
                    pool.drain()
                    pool.indirect_dma_start(out=w[:, k, :], out_offset=None, in_=w_in[:, :],
                                            in_offset=bass.IndirectOffsetOnAxis(ap=idx[:, k:k + 1], axis=0),
                                            bounds_check=w_in.shape[0] - 1, oob_is_err=False)\
                        .then_inc(w_loaded[k], 16)

                for k in range(U):
                    gather_weights(0, k)
                with pool.Fori(1, rounds) as r:
                    for k in range(U):
                        pool.wait_ge(y_ready, r * U + (k + 1 - U))
                        gather_weights(r, k)

        @block.tensor
        def _(pe):
            def turn(r, k, first):
                pe.wait_ge(x_loaded[k], r * 16 + 16)
                if not (first and k < 2):
                    pe.wait_ge(copied, r * U + (k - 1))
                for t in range(sizes[k]):
                    last = pe.transpose(ps_t[:, k % 2, t * P:(t + 1) * P], xs[:, k, t, :], core.ident[:, :])
                last.then_inc(turned, 1)

            def up(r, k, first):
                n = sizes[k] * P
                pe.wait_ge(copied, r * U + (k + 1))
                if k % BPW == 0:
                    pe.wait_ge(w_loaded[k // BPW], r * 16 + 16)
                for c in range(C):
                    q = (k * C + c) % 2
                    if not (first and k * C + c < 2):
                        pe.wait_ge(act_done, r * (U * C) + (k * C + c - 1))
                    pe.matmul(ps_g[:, q, 0:n], w1(k, c), xsT[:, k, 0:n], start=True, stop=True)
                    pe.matmul(ps_u[:, q, 0:n], w1(k, C + c), xsT[:, k, 0:n], start=True, stop=True)\
                        .then_inc(gu_ready, 1)

            def down(r, k, first):
                pe.wait_ge(act_done, r * (U * C) + (k + 1) * C)
                if not (first and k < 2):
                    pe.wait_ge(y_copied, r * U + (k - 1))
                for t in range(sizes[k]):
                    for c in range(C):
                        last = pe.matmul(ps_y[:, k % 2, t * P:(t + 1) * P], act_out[:, k, c, t * P:(t + 1) * P],
                                         w2(k, c), start=(c == 0), stop=(c == C - 1))
                last.then_inc(y_ready, 1)

            for k in range(U):
                turn(0, k, True)
                if k >= 1:
                    up(0, k - 1, True)
                if k >= 2:
                    down(0, k - 2, True)
            with pe.Fori(1, rounds) as r:
                for k in range(U):
                    turn(r, k, False)
                    if k >= 1:
                        up(r, k - 1, False)
                    else:
                        up(r - 1, U - 1, False)
                    if k >= 2:
                        down(r, k - 2, False)
                    else:
                        down(r - 1, U + k - 2, False)
            up(rounds - 1, U - 1, False)
            down(rounds - 1, U - 2, False)
            down(rounds - 1, U - 1, False)

        @block.scalar
        def _(act):
            def copy(r, k):
                n = sizes[k] * P
                act.wait_ge(turned, r * U + (k + 1))
                act.activation(xsT[:, k, 0:n], ps_t[:, k % 2, 0:n], ACT.Copy).then_inc(copied, 1)

            def gates(r, k, first):
                n = sizes[k] * P
                for c in range(C):
                    q = (k * C + c) % 2
                    act.wait_ge(gu_ready, r * (U * C) + (k * C + c + 1))
                    if not (first and k * C + c < 2):
                        act.wait_ge(act_done, r * (U * C) + (k * C + c - 1))
                    act.activation(gate[:, q, 0:n], ps_g[:, q, 0:n], func, bias=b1(k, c)).then_inc(gate_done, 1)

            for k in range(U):
                if gathered:
                    act.wait_ge(w_loaded[k], 16)
                copy(0, k)
                if k >= 1:
                    gates(0, k - 1, True)
            with act.Fori(1, rounds) as r:
                for k in range(U):
                    if gathered:
                        act.wait_ge(w_loaded[k], r * 16 + 16)
                    copy(r, k)
                    if k >= 1:
                        gates(r, k - 1, False)
                    else:
                        gates(r - 1, U - 1, False)
            gates(rounds - 1, U - 1, False)

        @block.vector
        def _(dve):
            def products(r, k, first):
                n = sizes[k] * P
                for c in range(C):
                    q = (k * C + c) % 2
                    dve.wait_ge(gate_done, r * (U * C) + (k * C + c + 1))
                    if c == 0 and gathered:
                        dve.wait_ge(w_loaded[k], r * 16 + 16)
                    if c == 0 and not first:
                        dve.wait_ge(y_ready, r * U + (k + 1 - U))
                    if gathered:
                        dve.scalar_tensor_tensor(out=act_out[:, k, c, 0:n], in0=ps_u[:, q, 0:n],
                                                 scalar=b1(k, C + c), in1=gate[:, q, 0:n],
                                                 op0=ALU.add, op1=ALU.mult).then_inc(act_done, 1)
                    else:
                        dve.tensor_tensor(act_out[:, k, c, 0:n], ps_u[:, q, 0:n], gate[:, q, 0:n], ALU.mult)\
                           .then_inc(act_done, 1)

            def copy_out(r, k, first):
                n = sizes[k] * P
                dve.wait_ge(y_ready, r * U + (k + 1))
                if not first:
                    dve.wait_ge(y_stored[k], r * 16 + 16)
                dve.tensor_copy(y_sb[:, k, 0:sizes[k], :].rearrange("p t d -> p (t d)"), ps_y[:, k % 2, 0:n])\
                   .then_inc(y_copied, 1)

            for k in range(U):
                dve.sem_inc(y_stored[k], 16)
            for k in range(U):
                products(0, k, True)
                if k >= 1:
                    copy_out(0, k - 1, True)
            with dve.Fori(1, rounds) as r:
                for k in range(U):
                    products(r, k, False)
                    if k >= 1:
                        copy_out(r, k - 1, False)
                    else:
                        copy_out(r - 1, U - 1, False)
            copy_out(rounds - 1, U - 1, False)


def combine(core, name, slots, weights, table_rows):
    nc = core.nc
    fetched = [core.sem(f"{name}_fetched{k}") for k in range(4)]
    with ExitStack() as ctx:
        y = core.sb(name + "_y", [P, 2, TILES, D], ctx=ctx)
        block = ctx.enter_context(nc.Block())
        SL = TILES // 4

        @block.gpsimd
        def _(pool):
            for t in range(TILES):
                for k in range(2):
                    pool.indirect_dma_start(out=y[:, k, t, :], out_offset=None, in_=core.table_y[0:table_rows, :],
                                            in_offset=bass.IndirectOffsetOnAxis(ap=slots[:, k, t:t + 1], axis=0),
                                            bounds_check=table_rows - 1, oob_is_err=False)\
                        .then_inc(fetched[t // SL], 16)

        @block.vector
        def _(dve):
            for q in range(4):
                dve.wait_ge(fetched[q], 16 * 2 * SL)
                for k in range(2):
                    for t in range(q * SL, (q + 1) * SL):
                        dve.scalar_tensor_tensor(out=core.x[:, t, :], in0=y[:, k, t, :],
                                                 scalar=weights[:, k, t:t + 1], in1=core.x[:, t, :],
                                                 op0=ALU.mult, op1=ALU.add)
                    if k == 0:
                        dve.drain()


def layer2_ffn(core, A):
    with ExitStack() as ctx:
        xn = core.sb("l2f_xn", [P, TILES, D], ctx=ctx)
        wts = core.sb("l2f_wts", [P, TILES, 8], ctx=ctx)
        slots, skip = (core.sb("l2f_" + n, [P, 2, TILES], U32, ctx) for n in ("slots", "skip"))
        weights = core.sb("l2f_weights", [P, 2, TILES], ctx=ctx)
        layernorm(core, "l2f_ln", xn)
        route(core, "l2f_route", A["L2_router_w"], None, wts, 8, 2, "probs")
        keep_best(core, "l2f_keep", wts, 640, A["c_same_expert"], A["c_before_expert"], A["c_bits"], False, True)
        place_tokens(core, "l2f_place", wts, 8, 640, slots, weights, skip)
        scatter_block(core, "l2f_scatter", xn, skip)
        slot_ffn(core, "l2f", 4, [3, 2, 3, 2], 4, ACT.Silu, A["L2_w"], 12 * P)
        combine(core, "l2f_combine", slots, weights, 1 + 8 * 640)


def layer1_ffn(core, A):
    NB = (TABLE_ROWS - 1) // 256
    with ExitStack() as ctx:
        xn = core.sb("l1f_xn", [P, TILES, D], ctx=ctx)
        wts = core.sb("l1f_wts", [P, TILES, 13], ctx=ctx)
        slots, skip = (core.sb("l1f_" + n, [P, 2, TILES], U32, ctx) for n in ("slots", "skip"))
        weights = core.sb("l1f_weights", [P, 2, TILES], ctx=ctx)
        blk_row = core.sb("l1f_blk_row", [P, NB], U32, ctx)
        rows = core.sb("l1f_rows", [P, N], ctx=ctx)
        layernorm(core, "l1f_ln", xn)
        route(core, "l1f_route", A["L1_router_w"], A["L1_router_b"], wts, 12, 2, "topk", 1.5)
        place_tokens(core, "l1f_place", wts, 12, 256, slots, weights, skip, blk_row)
        weight_rows(core, "l1f_wr", wts, 13, rows, None)
        shared_expert(core, "l1fs", rows, A["L1_ws1"], A["L1_bs1"], A["L1_ws2"], A["L1_b2"], xn, skip)
        slot_ffn(core, "l1f", NB // 4, [2, 2, 2, 2], 3, ACT.Gelu, A["L1_w"], 9 * P + 6, blk_row)
        combine(core, "l1f_combine", slots, weights, TABLE_ROWS)


def layer3_ffn(core, A):
    layernorm(core, "l3f_ln")
    with ExitStack() as ctx:
        wts = core.sb("l3f_wts", [P, TILES, 8], ctx=ctx)
        rows = core.sb("l3f_rows", [P, N], ctx=ctx)
        rows_dram = core.dram("l3f_rows_dram", [8, N])
        route(core, "l3f_route", A["L3_router_w"], A["L3_router_b"], wts, 8, 4, "topk")
        weight_rows(core, "l3f_wr", wts, 8, rows, rows_dram)
        expert_ffn(core, "l3f", rows, A["L3_w1"], A["L3_w2"], A["L3_b1"], A["L3_b2"], rows_dram, 8, 2, "clipped", True)
        add_back(core, "l3f_add", rows)


def packed(inputs):
    g = {k: np.asarray(v) for k, v in inputs.items()}
    c = np.ascontiguousarray

    def w1(w):
        e, d, f = w.shape
        return c(w.reshape(e, d, f // P, P))

    def w2(w):
        e, f, d = w.shape
        return c(w.reshape(e, f // P, P, d).transpose(0, 2, 1, 3))

    def cols(b):
        e, f = b.shape
        return c(b.reshape(e, f // P, P).transpose(0, 2, 1))

    def by_row(*parts):
        return np.concatenate([a.reshape(a.shape[0] * P, -1) for a in parts], 1)

    def gate_first(w):
        h = w.shape[-1] // 2
        return np.concatenate([w[..., h:], w[..., :h]], -1)

    t, e = np.arange(P) // 8, np.arange(P) % 8
    same_e = e[:, None] == e[None, :]
    same_b = (t[:, None] // TPB) == (t[None, :] // TPB)
    earlier = t[:, None] < t[None, :]
    bits = np.zeros((P, 31), np.int32)
    bits[:] = [1 << b for b in range(30, -1, -1)]
    bf16 = mybir.dt.np(BF16)
    later = np.arange(P)[:, None] > np.arange(P)[None, :]
    masks = np.stack([np.where(later, -1e30, 0), np.where(later.T, -1e30, 0), np.eye(P)]).astype(bf16)
    half = HD // 2
    inv_freq = np.float32(1.0) / np.float32(10000.0) ** (np.arange(half, dtype=np.float32) / np.float32(half))
    angle = np.arange(SEQ, dtype=np.float32)[:, None] * inv_freq[None, :]
    by_tile = lambda a: c(a.reshape(TPB, P, half).transpose(1, 0, 2))

    def parts(a):
        hi = a.astype(bf16)
        mid = (a - hi.astype(np.float64)).astype(bf16)
        return np.stack([hi, mid, (a - hi.astype(np.float64) - mid.astype(np.float64)).astype(bf16)], -1)

    slope = np.float32(2.0) ** (-np.arange(1, HEADS + 1, dtype=np.float32) / 2)
    pos = np.arange(SEQ, dtype=np.float64)
    steep = slope.astype(np.float64) * np.sqrt(np.float64(HD))
    q_tail = np.zeros((SEQ, HEADS, 16), bf16)
    q_tail[:, :, 0:3] = q_tail[:, :, 3:6] = parts(steep)[None]
    q_tail[:, :, 6:9] = parts(-pos[:, None] * steep[None, :])
    k_tail = np.zeros((SEQ, HEADS, 16), bf16)
    k_tail[:, :, 0:3] = (pos - pos % 2)[:, None, None]
    k_tail[:, :, 3:6] = (pos % 2)[:, None, None]
    k_tail[:, :, 6:12] = 1
    tail = lambda a: c(a.reshape(TPB, P, HEADS, 16).transpose(1, 0, 2, 3).reshape(P, TPB * HEADS, 16))
    col, row = np.arange(SEQ) % CHUNK, (np.arange(P) % CHUNK)[:, None]
    chunk_c = np.stack([np.broadcast_to(a, (P, SEQ)) for a in (col != 0, col == 0, row == col, row < col)], 1)
    chunk_c = c(chunk_c.astype(np.float32))
    quadrant = np.arange(P) // RD
    by_quadrant = c((quadrant[:, None] == np.arange(RHEADS)[None, :]).astype(np.float32))
    pick_ab = np.zeros((8, 2, P), np.float32)
    pick_ab[0:4, 0] = 0.98 * by_quadrant.T
    pick_ab[4:8, 1] = by_quadrant.T

    def pick(n):
        a = np.zeros((n, RHEADS, n, P), np.float32)
        for i in range(n):
            a[i, :, i] = by_quadrant.T
        return a.reshape(n * RHEADS, n, P)

    return {
        "c_masks": masks, "c_cos": by_tile(np.cos(angle)), "c_sin": by_tile(np.sin(angle)),
        "c_q_tail": tail(q_tail), "c_k_tail": tail(k_tail),
        "c_chunk": chunk_c, "c_ones4": by_quadrant, "c_pick_ab": pick_ab, "c_pick_r": pick(8), "c_pick_o": pick(4),
        "L2_w_in": c(g["L2_attn_W_in"].reshape(D, 3, D)),
        "L2_taps": c(np.stack([g["L2_attn_w_q"], g["L2_attn_w_k"], g["L2_attn_w_v"]])[:, :, 0, ::-1]
                     .transpose(0, 2, 1).reshape(1, 12 * D)),
        "L2_w_ctrl": g["L2_attn_W_ctrl"], "L2_b8": c(g["L2_attn_b_ctrl"][:8].reshape(8, 1)),
        "L2_bog": c(g["L2_attn_b_ctrl"][8:].reshape(D, 1)), "L2_w_out": g["L2_attn_W_out"],
        "L2_b_out": g["L2_attn_b_out"].reshape(D, 1), "L2_ramp": g["L2_attn_ramp_logit"].reshape(D, 1),
        "c_regeye": (np.eye(LAND) * REG).astype(np.float32),
        "L0_wqkv": c(np.concatenate([g["L0_attn_Wq"].T, g["L0_attn_Wk"].T, g["L0_attn_Wv"].T], 1)),
        "L0_bqkv": np.concatenate([g["L0_attn_bq"], g["L0_attn_bk"], g["L0_attn_bv"]]).reshape(1, 3 * D),
        "L0_temp": g["L0_attn_temperature"].reshape(1, 1), "L0_idx": g["L0_attn_landmark_idx"].reshape(1, LAND),
        "L0_wo": c(g["L0_attn_Wo"].T), "L0_bo": g["L0_attn_bo"].reshape(1, D),
        "L1_wqkv": g["L1_attn_w_qkv"], "L1_wo": g["L1_attn_w_o"],
        "L3_wqkv": g["L3_attn_Wqkv"], "L3_wo": g["L3_attn_Wout"],
        "x_in": c(g["L0_attn_query"].reshape(N, D)),
        "c_bits": bits,
        "c_same_expert": same_e.astype(np.float32),
        "c_before_expert": (same_e & earlier).astype(np.float32),
        "c_same_batch": (same_e & same_b).astype(np.float32),
        "c_before_batch": (same_e & same_b & earlier).astype(np.float32),
        "L0_router_w": g["L0_ffn_w_gate_w"], "L0_router_b": g["L0_ffn_w_gate_b"].reshape(-1, 1),
        "L0_w1": c(g["L0_ffn_W1"].transpose(1, 0, 2).reshape(D, 2, P)), "L0_b1": c(g["L0_ffn_b1"].reshape(2, P).T),
        "L0_w2": c(g["L0_ffn_W2"].reshape(2, P, D).transpose(1, 0, 2)), "L0_b2": g["L0_ffn_b2"],
        "L1_router_w": g["L1_ffn_Wr"], "L1_router_b": g["L1_ffn_br"].reshape(-1, 1),
        "L1_ws1": w1(gate_first(g["L1_ffn_Ws1"][None])), "L1_ws2": w2(g["L1_ffn_Ws2"][None]),
        "L1_bs1": cols(gate_first(g["L1_ffn_bs1"][None])),
        "L1_w": by_row(w1(gate_first(g["L1_ffn_We1"])), w2(g["L1_ffn_We2"]), cols(gate_first(g["L1_ffn_be1"]))),
        "L1_b2": np.concatenate([g["L1_ffn_be2"], g["L1_ffn_bs2"].reshape(1, D)]),
        "L2_router_w": c(g["L2_ffn_router_w"].T),
        "L2_w": by_row(w1(np.concatenate([g["L2_ffn_wg"], g["L2_ffn_wu"]], 2)), w2(g["L2_ffn_wd"])),
        "L3_router_w": c(g["L3_ffn_router_weight"].T), "L3_router_b": g["L3_ffn_router_bias"].reshape(-1, 1),
        "L3_w1": w1(g["L3_ffn_gate_up_proj"].transpose(0, 2, 1)), "L3_w2": w2(g["L3_ffn_down_proj"].transpose(0, 2, 1)),
        "L3_b1": cols(g["L3_ffn_gate_up_proj_bias"]), "L3_b2": c(g["L3_ffn_down_proj_bias"][:, :, None]),
    }


def forward(nc, A, x_out):
    with ExitStack() as ctx:
        core = Core(nc, ctx)
        start(core, A["x_in"])
        for layer in (layer0_attention, layer0_ffn, layer1_attention, layer1_ffn,
                      layer2_attention, layer2_ffn, layer3_attention, layer3_ffn):
            layer(core, A)
            core.free_sems()
        store(core, x_out)


def kernel(**inputs):
    import concourse.bacc as _bacc
    from concourse.bass_utils import run_bass_kernel_spmd as _run

    arrays = packed(inputs)
    nc = _bacc.Bacc("TRN2", target_bir_lowering=False, num_devices=1)
    A = {k: nc.dram_tensor(k, a.shape, mybir.dt.from_np(a.dtype), kind="ExternalInput").ap()
         for k, a in arrays.items()}
    x_out = nc.dram_tensor("x_out", [N, D], F32, kind="ExternalOutput").ap()
    forward(nc, A, x_out)
    r = _run(nc, [arrays], core_ids=[0])
    return r.results[0]["x_out"].reshape(BATCH, SEQ, D)
```

```python
from contextlib import ExitStack

import numpy as np

import concourse.bass as bass
from concourse import mybir

F32 = mybir.dt.float32
I32 = mybir.dt.int32
U32 = mybir.dt.uint32
BF16 = mybir.dt.bfloat16
ALU = mybir.AluOpType
ACT = mybir.ActivationFunctionType
AX = mybir.AxisListType

P = 128
D = 128
BATCH, SEQ = 8, 512
N = BATCH * SEQ
TILES = N // P
BLK = 512
NBLK = N // BLK
TPB = BLK // P
LN_EPS = 1e-5
BIG = 3.0e38
TABLE_ROWS = 1 + 44 * 256


class Core:

    def __init__(self, nc, ctx):
        self.nc, self.ctx, self.sems = nc, ctx, []
        self.x = self.sb("x", [P, TILES, D])
        self.xT = self.sb("xT", [P, N])
        self.ident = self.sb("ident", [P, P])
        self.neghalf = self.sb("neghalf", [P, 512])
        self.zeros = self.sb("zeros", [P, 4 * D])
        self.table_x, self.table_y = (self.dram(n, [TABLE_ROWS, D]) for n in ("table_x", "table_y"))
        self.table_filled = nc.alloc_semaphore("table_filled")

    def sb(self, name, shape, dt=F32, ctx=None):
        return (ctx or self.ctx).enter_context(self.nc.sbuf_tensor(name, shape, dt))

    def ps(self, name, shape, dt=F32, ctx=None):
        return (ctx or self.ctx).enter_context(self.nc.psum_tensor(name, shape, dt))

    def sem(self, name):
        s = self.nc.alloc_semaphore(name)
        self.sems.append(s)
        return s

    def free_sems(self):
        self.nc.clear_and_free_semaphores(self.sems)
        self.nc.all_engine_barrier()
        self.sems = []

    def dram(self, name, shape, dt=F32):
        return self.nc.dram_tensor(name, shape, dt, kind="Internal").ap()


def start(core, x_in):
    nc = core.nc
    loaded, filled, zeroed = core.sem("x_loaded"), core.sem("ident_filled"), core.sem("zeroed")
    with nc.Block() as block:

        @block.sync
        def _(sp):
            sp.dma_start(core.x[:, :, :], x_in.rearrange("(t p) d -> p t d", p=P)).then_inc(loaded, 16)
            sp.wait_ge(zeroed, 1)
            sp.dma_start(core.table_x[0:1, :], core.zeros[0:1, 0:D]).then_inc(core.table_filled, 16)
            sp.dma_start(core.table_y[0:1, :], core.zeros[0:1, 0:D]).then_inc(core.table_filled, 16)
            sp.dma_start(core.table_x[1:TABLE_ROWS, :].rearrange("(p n k) d -> p n (k d)", p=P, k=4),
                         core.zeros[:, :].rearrange("p (o k) -> p o k", o=1)
                         .to_broadcast([P, (TABLE_ROWS - 1) // P // 4, 4 * D])).then_inc(core.table_filled, 16)
            sp.wait_ge(loaded, 16)

        @block.gpsimd
        def _(pool):
            pool.memset(core.zeros[:, :], 0.0).then_inc(zeroed, 1)
            pool.memset(core.ident[:, :], 0.0).then_inc(filled, 1)
            pool.memset(core.neghalf[:, :], -0.5)
            pool.wait_ge(filled, 1)
            pool.affine_select(out=core.ident[:, :], in_=core.ident[:, :], compare_op=ALU.not_equal, fill=1.0,
                               base=0, pattern=[[-1, P]], channel_multiplier=1)


def store(core, x_out):
    nc = core.nc
    stored = core.sem("x_stored")
    with nc.Block() as block:

        @block.sync
        def _(sp):
            sp.dma_start(x_out.rearrange("(t p) d -> p t d", p=P), core.x[:, :, :]).then_inc(stored, 16)
            sp.wait_ge(stored, 16)
            sp.wait_ge(core.table_filled, 48)


def layernorm(core, name, xn_all=None, combined=None):
    nc = core.nc
    var_ready, rstd_ready = core.sem(name + "_var_ready"), core.sem(name + "_rstd_ready")
    xn_ready, turned = core.sem(name + "_xn_ready"), core.sem(name + "_turned")
    copied = core.sem(name + "_copied")
    with ExitStack() as ctx:
        if combined is not None:
            slots, weights, table_rows = combined
            fetched = [core.sem(f"{name}_fetched{b}") for b in range(NBLK)]
            y = core.sb(name + "_y", [P, 2, TILES, D], ctx=ctx)
        stats = core.sb(name + "_stats", [P, TPB, 6], ctx=ctx)
        mv = core.sb(name + "_mv", [P, 2, TPB, 2], ctx=ctx)
        rstd, shift = (core.sb(f"{name}_{n}", [P, 2, TPB], ctx=ctx) for n in ("rstd", "shift"))
        ring = 2 if xn_all is None else NBLK
        xn = core.sb(name + "_xn", [P, 2, TPB, D], ctx=ctx) if xn_all is None \
            else xn_all[:, :, :].rearrange("p (b t) d -> p b t d", t=TPB)
        turn = core.ps(name + "_turn", [P, 2, BLK], ctx=ctx)
        block = ctx.enter_context(nc.Block())

        def block_stats(dve, b):
            for t in range(TPB):
                dve.bn_stats(stats[:, t, :], core.x[:, TPB * b + t, :])
            dve.drain()
            for t in range(TPB):
                dve.bn_aggr(mv[:, b % 2, t, :], stats[:, t, :])
            dve.drain()
            if b >= 2:
                dve.wait_ge(xn_ready, b - 1)
            dve.tensor_scalar(rstd[:, b % 2, :], mv[:, b % 2, :, 1], LN_EPS, None, ALU.add)
            dve.tensor_scalar(shift[:, b % 2, :], mv[:, b % 2, :, 0], -1.0, None, ALU.mult).then_inc(var_ready, 1)

        def fetch(pool, b):
            for t in range(b * TPB, (b + 1) * TPB):
                for k in range(2):
                    pool.indirect_dma_start(out=y[:, k, t, :], out_offset=None, in_=core.table_y[0:table_rows, :],
                                            in_offset=bass.IndirectOffsetOnAxis(ap=slots[:, k, t:t + 1], axis=0),
                                            bounds_check=table_rows - 1, oob_is_err=False).then_inc(fetched[b], 16)

        @block.vector
        def _(dve):
            for b in range(NBLK):
                if b:
                    dve.drain()
                if combined is not None:
                    dve.wait_ge(fetched[b], 2 * TPB * 16)
                    for k in range(2):
                        for t in range(b * TPB, (b + 1) * TPB):
                            dve.scalar_tensor_tensor(out=core.x[:, t, :], in0=y[:, k, t, :],
                                                     scalar=weights[:, k, t:t + 1], in1=core.x[:, t, :],
                                                     op0=ALU.mult, op1=ALU.add)
                        dve.drain()
                block_stats(dve, b)

        @block.gpsimd
        def _(pool):
            if combined is not None:
                fetch(pool, 0)
            for b in range(NBLK):
                if combined is not None and b + 1 < NBLK:
                    fetch(pool, b + 1)
                pool.wait_ge(var_ready, b + 1)
                pool.tensor_tensor(rstd[:, b % 2, :], rstd[:, b % 2, :], core.neghalf[:, 0:TPB], ALU.pow)
                pool.drain()
                pool.tensor_tensor(shift[:, b % 2, :], shift[:, b % 2, :], rstd[:, b % 2, :], ALU.mult)\
                    .then_inc(rstd_ready, 1)

        @block.tensor
        def _(pe):
            for b in range(NBLK):
                pe.wait_ge(xn_ready, b + 1)
                if b >= 2:
                    pe.wait_ge(copied, b - 1)
                for t in range(TPB):
                    last = pe.transpose(turn[:, b % 2, t * P:(t + 1) * P], xn[:, b % ring, t, :], core.ident[:, :])
                last.then_inc(turned, 1)

        @block.scalar
        def _(act):
            def copy_out(b):
                act.wait_ge(turned, b + 1)
                act.activation(core.xT[:, b * BLK:(b + 1) * BLK], turn[:, b % 2, :], ACT.Copy)\
                   .then_inc(copied, 1)

            for b in range(NBLK):
                act.wait_ge(rstd_ready, b + 1)
                if b >= ring:
                    act.wait_ge(turned, b - 1)
                for t in range(TPB):
                    last = act.activation(xn[:, b % ring, t, :], core.x[:, TPB * b + t, :], ACT.Identity,
                                          scale=rstd[:, b % 2, t:t + 1], bias=shift[:, b % 2, t:t + 1])
                last.then_inc(xn_ready, 1)
                if b:
                    copy_out(b - 1)
            copy_out(NBLK - 1)


def add_back(core, name, yT):
    nc = core.nc
    turned, added = core.sem(name + "_turned"), core.sem(name + "_added")
    with ExitStack() as ctx:
        turn = core.ps(name + "_turn", [P, 4, TPB, P], ctx=ctx)
        block = ctx.enter_context(nc.Block())

        @block.tensor
        def _(pe):
            for b in range(NBLK):
                if b >= 4:
                    pe.wait_ge(added, b - 3)
                for t in range(TPB):
                    c = b * BLK + t * P
                    last = pe.transpose(turn[:, b % 4, t, :], yT[:, c:c + P], core.ident[:, :])
                last.then_inc(turned, 1)

        @block.vector
        def _(dve):
            for b in range(NBLK):
                dve.wait_ge(turned, b + 1)
                xb = core.x[:, b * TPB:(b + 1) * TPB, :]
                dve.tensor_tensor(xb, xb, turn[:, b % 4, :, :], ALU.add).then_inc(added, 1)


def route(core, name, w_in, b_in, wts, E, K, mode, tau=1.0):
    nc = core.nc
    loaded, logits_ready, biased = core.sem(name + "_loaded"), core.sem(name + "_logits"), core.sem(name + "_biased")
    turned, const_ready = core.sem(name + "_turned"), core.sem(name + "_const")
    shifted, exped = core.sem(name + "_shifted"), core.sem(name + "_exped")
    with ExitStack() as ctx:
        sb = lambda n, s, dt=F32: core.sb(name + "_" + n, s, dt, ctx)
        w_sb, b_sb = sb("w", [P, E]), sb("b", [P, 1])
        lT = sb("lT", [P, N])
        logits, v, oh, mask = (sb(n, [P, TILES, E]) for n in ("logits", "v", "oh", "mask"))
        probs, shift = sb("probs", [P, TILES, E]), sb("shift", [P, TILES, E])
        m1, m, den = (sb(n, [P, TILES]) for n in ("m1", "m", "den"))
        rev = sb("rev", [P, E])
        ps_l = core.ps(name + "_ps_l", [P, 2, BLK], ctx=ctx)
        ps_t = core.ps(name + "_ps_t", [P, 512], ctx=ctx)
        block = ctx.enter_context(nc.Block())
        lv = ps_t[:, 0:TILES * E].rearrange("p (t e) -> p t e", e=E)
        each = lambda a: a[:, :].rearrange("p (t o) -> p t o", o=1).to_broadcast([P, TILES, E])

        @block.sync
        def _(sp):
            sp.dma_start(w_sb[:, :], w_in).then_inc(loaded, 16)
            if b_in is not None:
                sp.dma_start(b_sb[0:E, :], b_in).then_inc(loaded, 16)

        @block.gpsimd
        def _(pool):
            for e in range(E):
                last = pool.memset(rev[:, e:e + 1], float(E - e))
            last.then_inc(const_ready, 1)

        @block.tensor
        def _(pe):
            pe.wait_ge(loaded, 16 if b_in is None else 32)
            for b in range(NBLK):
                if b >= 2:
                    pe.wait_ge(biased, b - 1)
                pe.matmul(ps_l[0:E, b % 2, :], w_sb[:, :], core.xT[:, b * BLK:(b + 1) * BLK],
                          start=True, stop=True).then_inc(logits_ready, 1)
            for t in range(TILES):
                if t % TPB == 0:
                    pe.wait_ge(biased, t // TPB + 1)
                last = pe.transpose(ps_t[:, t * E:(t + 1) * E], lT[0:E, t * P:(t + 1) * P], core.ident[0:E, 0:E])
            last.then_inc(turned, 1)

        @block.scalar
        def _(act):
            act.wait_ge(shifted, 1)
            act.activation(probs[:, :, :], shift[:, :, :], ACT.Exp, scale=1.0 / tau).then_inc(exped, 1)

        @block.vector
        def _(dve):
            dve.wait_ge(loaded, 16 if b_in is None else 32)
            for b in range(NBLK):
                dve.wait_ge(logits_ready, b + 1)
                dve.tensor_scalar(lT[0:E, b * BLK:(b + 1) * BLK], ps_l[0:E, b % 2, :],
                                  0.0 if b_in is None else b_sb[0:E, 0:1], None, ALU.add).then_inc(biased, 1)
            dve.wait_ge(turned, 1)
            dve.tensor_reduce(m1[:, :], lv, AX.X, ALU.max)
            dve.tensor_copy(logits[:, :, :], lv)
            dve.tensor_copy(v[:, :, :], lv)
            dve.drain()
            dve.tensor_tensor(shift[:, :, :], logits[:, :, :], each(m1), ALU.subtract).then_inc(shifted, 1)
            dve.wait_ge(const_ready, 1)
            for k in range(K):
                if k:
                    dve.tensor_reduce(m[:, :], v[:, :, :], AX.X, ALU.max)
                    dve.drain()
                dve.tensor_tensor(oh[:, :, :], v[:, :, :], each(m if k else m1), ALU.is_equal)
                dve.drain()
                dve.tensor_tensor(oh[:, :, :], oh[:, :, :],
                                  rev[:, :].rearrange("p (o e) -> p o e", o=1).to_broadcast([P, TILES, E]), ALU.mult)
                dve.drain()
                dve.tensor_reduce(den[:, :], oh[:, :, :], AX.X, ALU.max)
                dve.drain()
                dve.tensor_tensor(oh[:, :, :], oh[:, :, :], each(den), ALU.is_equal)
                dve.drain()
                dve.scalar_tensor_tensor(out=v[:, :, :], in0=oh[:, :, :], scalar=-BIG, in1=v[:, :, :],
                                         op0=ALU.mult, op1=ALU.add)
                if k == 0:
                    dve.tensor_copy(mask[:, :, :], oh[:, :, :])
                else:
                    dve.tensor_tensor(mask[:, :, :], mask[:, :, :], oh[:, :, :], ALU.add)
                dve.drain()
            dve.wait_ge(exped, 1)
            if mode != "topk":
                dve.tensor_reduce(den[:, :], probs[:, :, :], AX.X, ALU.add)
                dve.drain()
                dve.reciprocal(den[:, :], den[:, :])
                dve.drain()
                dve.tensor_tensor(probs[:, :, :], probs[:, :, :], each(den), ALU.mult)
                dve.drain()
            dve.tensor_tensor(probs[:, :, :], probs[:, :, :], mask[:, :, :], ALU.mult)
            dve.drain()
            if mode == "batch":
                by = probs[:, :, :].rearrange("p (b s) e -> p (s e) b", b=BATCH)
                dsum = v[:, 0:TPB, :].rearrange("p s e -> p (s e)")
                dve.tensor_reduce(dsum, by, AX.X, ALU.add)
                dve.drain()
                dve.tensor_scalar(dsum, dsum, 1e-6, None, ALU.add)
                dve.drain()
                dve.reciprocal(dsum, dsum)
                dve.drain()
                dve.scalar_tensor_tensor(
                    out=wts[:, :, :].rearrange("p (b s) e -> p b (s e)", b=BATCH),
                    in0=probs[:, :, :].rearrange("p (b s) e -> p b (s e)", b=BATCH), scalar=float(BATCH),
                    in1=v[:, 0:TPB, :].rearrange("p (o s) e -> p o (s e)", o=1).to_broadcast([P, BATCH, TPB * E]),
                    op0=ALU.mult, op1=ALU.mult)
            else:
                dve.tensor_reduce(den[:, :], probs[:, :, :], AX.X, ALU.add)
                dve.drain()
                if mode == "probs":
                    dve.tensor_scalar(den[:, :], den[:, :], 1e-6, None, ALU.add)
                    dve.drain()
                dve.reciprocal(den[:, :], den[:, :])
                dve.drain()
                dve.tensor_tensor(wts[:, :, 0:E], probs[:, :, :], each(den), ALU.mult)


def keep_best(core, name, wts, keep, group_in, before_in, bits_in, per_batch, times_weight):
    nc = core.nc
    E, HALF, TOP = 8, 2, 32
    ncol = HALF if per_batch else 1
    loaded, turned, rows_ready = core.sem(name + "_loaded"), core.sem(name + "_turned"), core.sem(name + "_rows")
    counted, summed = core.sem(name + "_counted"), core.sem(name + "_summed")
    tallied, spread = core.sem(name + "_tallied"), core.sem(name + "_spread")
    chosen, back = core.sem(name + "_chosen"), core.sem(name + "_back")
    with ExitStack() as ctx:
        sb = lambda n, s, dt=F32: core.sb(name + "_" + n, s, dt, ctx)
        group, before = sb("group", [P, P]), sb("before", [P, P])
        bits = sb("bits", [P, TOP], I32)
        rows, gt, eq, incl = (sb(n, [P, HALF, P]) for n in ("rows", "gt", "eq", "incl"))
        zeros = sb("zeros", [P, P])
        thr, cand, above = sb("thr", [P, ncol]), sb("cand", [P, ncol]), sb("above", [P, ncol])
        cnt = sb("cnt", [P, ncol])
        n_gt, n_eq, need, off = sb("n_gt", [P, ncol]), sb("n_eq", [P, HALF]), sb("need", [P, HALF]), sb("off", [P, HALF])
        ps_r = core.ps(name + "_ps_r", [P, HALF, P], ctx=ctx)
        ps_c = core.ps(name + "_ps_c", [P, 512], ctx=ctx)
        ps_o = core.ps(name + "_ps_o", [P, 512], ctx=ctx)
        ps_b = core.ps(name + "_ps_b", [P, HALF, P], ctx=ctx)
        flat = wts[:, :, :].rearrange("p t e -> p (t e)")
        shape = [P, ncol, HALF * P // ncol]
        cut = lambda a: a[:, :, :].rearrange("p h k -> p (h k)").rearrange("p (c k) -> p c k", c=ncol)
        wide = lambda a: a[:, :].rearrange("p (c o) -> p c o", o=1).to_broadcast(shape)
        block = ctx.enter_context(nc.Block())

        @block.sync
        def _(sp):
            sp.dma_start(group[:, :], group_in).then_inc(loaded, 16)
            sp.dma_start(before[:, :], before_in).then_inc(loaded, 16)
            sp.dma_start(bits[:, :], bits_in).then_inc(loaded, 16)

        @block.tensor
        def _(pe):
            for h in range(HALF):
                last = pe.transpose(ps_r[:, h, :], flat[:, h * P:(h + 1) * P], core.ident[:, :])
            last.then_inc(turned, 1)
            pe.wait_ge(loaded, 48)
            with pe.Fori(0, TOP // 4) as r:
                for k in range(4):
                    pe.wait_ge(counted, r * 4 + (k + 1))
                    pe.matmul(ps_c[:, 0:ncol], group[:, :], cnt[:, :], start=True, stop=True).then_inc(summed, 1)
            pe.wait_ge(tallied, 1)
            pe.matmul(ps_c[:, 0:ncol], group[:, :], n_gt[:, :], start=True, stop=True)
            if per_batch:
                last = pe.matmul(ps_o[:, 0:HALF], before[:, :], n_eq[:, :], start=True, stop=True)
            else:
                pe.matmul(ps_o[:, 0:1], before[:, :], n_eq[:, 0:1], start=True, stop=True)
                pe.matmul(ps_o[:, 1:2], before[:, :], n_eq[:, 1:2], start=True, stop=False)
                last = pe.matmul(ps_o[:, 1:2], group[:, :], n_eq[:, 0:1], start=False, stop=True)
            last.then_inc(spread, 1)
            pe.wait_ge(chosen, 1)
            for h in range(HALF):
                last = pe.transpose(ps_b[:, h, :], gt[:, h, :], core.ident[:, :])
            last.then_inc(back, 1)

        @block.vector
        def _(dve):
            dve.memset(thr[:, :], 0.0)
            dve.memset(zeros[:, :], 0.0)
            dve.wait_ge(turned, 1)
            dve.tensor_copy(rows[:, :, :], ps_r[:, :, :])
            dve.wait_ge(loaded, 48)
            dve.drain()
            def next_bit(i):
                dve.tensor_tensor(cand[:, :].bitcast(I32), thr[:, :].bitcast(I32),
                                  bits[:, bass.ds(i, 1)].to_broadcast([P, ncol]), ALU.bitwise_or)
                dve.drain()
                dve.tensor_tensor(cut(incl), cut(rows), wide(cand), ALU.is_ge)
                dve.drain()
                dve.tensor_reduce(cnt[:, :], cut(incl), AX.X, ALU.add).then_inc(counted, 1)
                dve.wait_ge(summed, i + 1)
                dve.scalar_tensor_tensor(out=above[:, :], in0=ps_c[:, 0:ncol], scalar=float(keep), in1=cand[:, :],
                                         op0=ALU.is_ge, op1=ALU.mult)
                dve.drain()
                dve.tensor_tensor(thr[:, :], thr[:, :], above[:, :], ALU.max)
                dve.drain()
            with dve.Fori(0, TOP // 4) as r:
                for k in range(4):
                    next_bit(r * 4 + k)
            dve.scalar_tensor_tensor(out=thr[:, :], in0=thr[:, :], scalar=1.1754944e-38, in1=thr[:, :],
                                     op0=ALU.is_ge, op1=ALU.mult)
            dve.drain()
            dve.tensor_tensor(cut(gt), cut(rows), wide(thr), ALU.is_gt)
            dve.tensor_tensor(cut(eq), cut(rows), wide(thr), ALU.is_equal)
            dve.drain()
            dve.tensor_reduce(n_gt[:, :], cut(gt), AX.X, ALU.add)
            for h in range(HALF):
                dve.tensor_tensor_scan(incl[:, h, :], eq[:, h, :], zeros[:, :], 0.0, ALU.add, ALU.add)
            dve.tensor_reduce(n_eq[:, :], eq[:, :, :], AX.X, ALU.add).then_inc(tallied, 1)
            dve.wait_ge(spread, 1)
            dve.tensor_scalar(need[:, :], ps_c[:, 0:ncol].to_broadcast([P, HALF]) if ncol == 1 else ps_c[:, 0:HALF],
                              -1.0, float(keep), ALU.mult, ALU.add)
            dve.drain()
            dve.tensor_tensor(off[:, :], ps_o[:, 0:HALF], need[:, :], ALU.subtract)
            dve.drain()
            for h in range(HALF):
                dve.tensor_scalar(incl[:, h, :], incl[:, h, :], off[:, h:h + 1], 1.0, ALU.add, ALU.is_lt)
            dve.drain()
            dve.tensor_tensor(eq[:, :, :], eq[:, :, :], incl[:, :, :], ALU.mult)
            dve.drain()
            dve.tensor_tensor(gt[:, :, :], gt[:, :, :], eq[:, :, :], ALU.add).then_inc(chosen, 1)
            dve.wait_ge(back, 1)
            got = ps_b[:, :, :].rearrange("p h k -> p (h k)")
            if times_weight:
                dve.tensor_tensor(flat, flat, got, ALU.mult)
            else:
                dve.tensor_copy(flat, got)


def weight_rows(core, name, wts, E, rows_sb, rows_dram):
    nc = core.nc
    turned, copied, saved = core.sem(name + "_turned"), core.sem(name + "_copied"), core.sem(name + "_saved")
    with ExitStack() as ctx:
        turn = core.ps(name + "_turn", [P, 4, BLK], ctx=ctx)
        block = ctx.enter_context(nc.Block())

        @block.tensor
        def _(pe):
            for b in range(NBLK):
                if b >= 4:
                    pe.wait_ge(copied, b - 3)
                for t in range(TPB):
                    last = pe.transpose(turn[0:E, b % 4, t * P:(t + 1) * P], wts[:, b * TPB + t, :], core.ident[:, :])
                last.then_inc(turned, 1)

        @block.vector
        def _(dve):
            for b in range(NBLK):
                dve.wait_ge(turned, b + 1)
                dve.tensor_copy(rows_sb[0:E, b * BLK:(b + 1) * BLK], turn[0:E, b % 4, :]).then_inc(copied, 1)

        @block.sync
        def _(sp):
            if rows_dram is not None:
                sp.wait_ge(copied, NBLK)
                sp.dma_start(rows_dram, rows_sb[0:E, :]).then_inc(saved, 16)
                sp.wait_ge(saved, 16)


def expert_ffn(core, name, yT, w1_in, w2_in, b1_in, b2_in, rows_dram, E, C):
    nc = core.nc
    PAR = 2
    ROUNDS = E // PAR
    STEPS = NBLK * C
    w_ready = [core.sem(f"{name}_w_ready{k}") for k in range(PAR)]
    wb_ready = [core.sem(f"{name}_wb_ready{k}") for k in range(PAR)]
    gu_ready, gate_done = core.sem(name + "_gu_ready"), core.sem(name + "_gate_done")
    act_done, down_done = core.sem(name + "_act_done"), core.sem(name + "_down_done")
    y_done, added = core.sem(name + "_y_done"), core.sem(name + "_added")
    pre_done, half_done = core.sem(name + "_pre_done"), core.sem(name + "_half_done")
    LAG = 2
    CREDIT = 2
    with ExitStack() as ctx:
        sb = lambda n, s, dt=F32: core.sb(name + "_" + n, s, dt, ctx)
        w1, w2 = sb("w1", [P, PAR, 2 * C, P]), sb("w2", [P, PAR, C, P])
        b1, b2 = sb("b1", [P, PAR, 2 * C]), sb("b2", [P, PAR])
        wb = sb("wb", [P, PAR, N])
        gate, act_out = sb("gate", [P, 2, BLK]), sb("act", [P, 2, BLK])
        g_sb, up, half = (sb(n, [P, 2, BLK]) for n in ("g", "up", "half"))
        y_sb = sb("y", [P, 2, BLK])
        ps_g = core.ps(name + "_ps_g", [P, 2, BLK], ctx=ctx)
        ps_u = core.ps(name + "_ps_u", [P, 2, BLK], ctx=ctx)
        ps_y = core.ps(name + "_ps_y", [P, 2, BLK], ctx=ctx)
        block = ctx.enter_context(nc.Block())
        loads = 4

        def rounds(eng):
            return eng.Fori(0, ROUNDS)

        @block.sync
        def _(sp):
            with rounds(sp) as r:
                for k in range(PAR):
                    e = r * PAR + k
                    sp.wait_ge(y_done, (r * PAR + k - PAR + 1) * NBLK + PAR * NBLK)
                    sp.dma_start(w1[:, k, :, :], w1_in[bass.ds(e, 1)].rearrange("o p c f -> p (o c) f"))\
                        .then_inc(w_ready[k], 16)
                    sp.dma_start(w2[:, k, :, :], w2_in[bass.ds(e, 1)].rearrange("o p c f -> p (o c) f"))\
                        .then_inc(w_ready[k], 16)
                    sp.dma_start(b1[:, k, :], b1_in[bass.ds(e, 1)].rearrange("o p c -> p (o c)"))\
                        .then_inc(w_ready[k], 16)
                    sp.dma_start(b2[:, k:k + 1], b2_in[bass.ds(e, 1)].rearrange("o p c -> p (o c)"))\
                        .then_inc(w_ready[k], 16)
                    sp.dma_start(wb[:, k, :], rows_dram[bass.ds(e, 1), :].to_broadcast([P, N]))\
                        .then_inc(wb_ready[k], 16)

        @block.tensor
        def _(pe):
            with rounds(pe) as r:
                base = r * (PAR * STEPS)

                def down(s):
                    k, c = s // STEPS, s % C
                    u = s // C
                    pe.wait_ge(act_done, base + s + 1 + CREDIT)
                    if c == 0:
                        pe.wait_ge(y_done, r * (PAR * NBLK) + (u - 1 + PAR * NBLK))
                    pe.matmul(ps_y[:, u % 2, :], w2[:, k, c, :], act_out[:, s % 2, :],
                              start=(c == 0), stop=(c == C - 1)).then_inc(down_done, 1)

                for s in range(PAR * STEPS):
                    k, b, c = s // STEPS, s // C % NBLK, s % C
                    if s % STEPS == 0:
                        pe.wait_ge(w_ready[k], (r + 1) * (16 * loads))
                    pe.wait_ge(pre_done, base + s - 1 + CREDIT)
                    xb = core.xT[:, b * BLK:(b + 1) * BLK]
                    pe.matmul(ps_g[:, s % 2, :], w1[:, k, c, :], xb, start=True, stop=True)
                    pe.matmul(ps_u[:, s % 2, :], w1[:, k, C + c, :], xb, start=True, stop=True)\
                        .then_inc(gu_ready, 1)
                    if s >= LAG:
                        down(s - LAG)
                for s in range(PAR * STEPS - LAG, PAR * STEPS):
                    down(s)

        @block.scalar
        def _(act):
            with rounds(act) as r:
                base = r * (PAR * STEPS)
                for s in range(PAR * STEPS):
                    k, c = s // STEPS, s % C
                    act.wait_ge(pre_done, base + s + 1 + CREDIT)
                    act.wait_ge(act_done, base + s - 1 + CREDIT)
                    act.activation(gate[:, s % 2, :], g_sb[:, s % 2, :], ACT.Sigmoid, scale=1.702)\
                       .then_inc(gate_done, 1)

        @block.vector
        def _(dve):
            dve.sem_inc(act_done, CREDIT)
            dve.sem_inc(pre_done, CREDIT)
            dve.sem_inc(gate_done, CREDIT)
            dve.sem_inc(y_done, PAR * NBLK)
            with rounds(dve) as r:
                base = r * (PAR * STEPS)

                def finish(u):
                    k, b = u // NBLK, u % NBLK
                    dve.wait_ge(down_done, base + (u + 1) * C)
                    dve.wait_ge(added, r * (PAR * NBLK) + u - 1 + CREDIT)
                    if b == 0:
                        dve.wait_ge(wb_ready[k], r * 16 + 16)
                    dve.scalar_tensor_tensor(out=y_sb[:, u % 2, :], in0=ps_y[:, u % 2, :], scalar=b2[:, k:k + 1],
                                             in1=wb[:, k, b * BLK:(b + 1) * BLK], op0=ALU.add, op1=ALU.mult)\
                       .then_inc(y_done, 1)

                for s in range(PAR * STEPS):
                    k, c = s // STEPS, s % C
                    if s % STEPS == 0:
                        dve.wait_ge(w_ready[k], (r + 1) * (16 * loads))
                    if s % STEPS == 0:
                        dve.tensor_scalar(b1[:, k, C:2 * C], b1[:, k, C:2 * C], 1.0, None, ALU.add)
                        dve.drain()
                    dve.wait_ge(gate_done, base + s - 1 + CREDIT)
                    dve.wait_ge(gu_ready, base + s + 1)
                    dve.tensor_scalar(g_sb[:, s % 2, :], ps_g[:, s % 2, :], b1[:, k, c:c + 1], 7.0,
                                      ALU.add, ALU.min)
                    dve.tensor_scalar(up[:, s % 2, :], ps_u[:, s % 2, :], b1[:, k, C + c:C + c + 1], 8.0,
                                      ALU.add, ALU.min).then_inc(pre_done, 1)
                    dve.drain()
                    dve.wait_ge(act_done, base + s - 1 + CREDIT)
                    dve.scalar_tensor_tensor(out=half[:, s % 2, :], in0=up[:, s % 2, :], scalar=-6.0,
                                             in1=g_sb[:, s % 2, :], op0=ALU.max, op1=ALU.mult)\
                       .then_inc(half_done, 1)
                    if s >= C + LAG - 1 and (s - LAG + 1) % C == 0:
                        finish((s - LAG + 1) // C - 1)
                for u in range((PAR * STEPS - LAG) // C, PAR * NBLK):
                    finish(u)

        @block.gpsimd
        def _(pool):
            pool.memset(yT[:, :], 0.0)
            pool.drain()
            pool.sem_inc(added, CREDIT)
            with rounds(pool) as r:
                base = r * (PAR * STEPS)

                def add(u):
                    b = u % NBLK
                    pool.wait_ge(y_done, r * (PAR * NBLK) + (u + 1 + PAR * NBLK))
                    yb = yT[:, b * BLK:(b + 1) * BLK]
                    pool.tensor_tensor(yb, yb, y_sb[:, u % 2, :], ALU.add).then_inc(added, 1)

                for s in range(PAR * STEPS):
                    pool.wait_ge(gate_done, base + s + 1 + CREDIT)
                    pool.wait_ge(half_done, base + s + 1)
                    if s >= 2:
                        pool.wait_ge(down_done, base + s - 1)
                    pool.tensor_tensor(act_out[:, s % 2, :], half[:, s % 2, :], gate[:, s % 2, :], ALU.mult)\
                        .then_inc(act_done, 1)
                    if s >= C + LAG and (s - LAG) % C == 0:
                        add((s - LAG) // C - 1)
                for u in range((PAR * STEPS - 1 - LAG) // C, PAR * NBLK):
                    add(u)


def masked_ffn(core, name, rows, rows_dram, w1_in, b1_in, w2_in, b2_in):
    nc = core.nc
    E, C, SUB = 8, 2, 32
    loaded, up_ready, gelu_done = core.sem(name + "_loaded"), core.sem(name + "_up_ready"), core.sem(name + "_gelu_done")
    act_done, y_ready, added = core.sem(name + "_act_done"), core.sem(name + "_y_ready"), core.sem(name + "_added")
    with ExitStack() as ctx:
        sb = lambda n, s, dt=F32: core.sb(name + "_" + n, s, dt, ctx)
        w1, w2, b1, b2 = sb("w1", [P, C, P]), sb("w2", [P, C, D]), sb("b1", [P, C]), sb("b2", [E, D])
        spread = sb("spread", [P, C, N])
        gelu, act_out = sb("gelu", [P, C, 2, BLK]), sb("act", [P, C, 2, BLK])
        ps_h = core.ps(name + "_ps_h", [P, C, 2, BLK], ctx=ctx)
        ps_y = core.ps(name + "_ps_y", [P, 2, TPB, D], ctx=ctx)
        block = ctx.enter_context(nc.Block())

        @block.sync
        def _(sp):
            sp.dma_start(w1[:, :, :], w1_in).then_inc(loaded, 16)
            sp.dma_start(w2[:, :, :], w2_in).then_inc(loaded, 16)
            sp.dma_start(b1[:, :], b1_in).then_inc(loaded, 16)
            sp.dma_start(b2[:, :], b2_in).then_inc(loaded, 16)
            for e in range(E):
                at = SUB * (e % 4)
                sp.dma_start(spread[at:at + SUB, e // 4, :], rows_dram[e:e + 1, :].to_broadcast([SUB, N]))\
                    .then_inc(loaded, 16)

        ALL = 16 * (4 + E)

        @block.tensor
        def _(pe):
            pe.wait_ge(loaded, ALL)

            def down(b):
                pe.wait_ge(act_done, C * (b + 1))
                if b >= 2:
                    pe.wait_ge(added, b - 1)
                for t in range(TPB):
                    cut = slice(t * P, (t + 1) * P)
                    for c in range(C):
                        pe.matmul(ps_y[:, b % 2, t, :], act_out[:, c, b % 2, cut], w2[:, c, :],
                                  start=(c == 0), stop=False)
                    last = pe.matmul(ps_y[:, b % 2, t, :], rows[0:E, b * BLK + t * P:b * BLK + (t + 1) * P], b2[:, :],
                                     start=False, stop=True)
                last.then_inc(y_ready, 1)

            for b in range(NBLK):
                if b >= 2:
                    pe.wait_ge(gelu_done, C * (b - 1))
                for c in range(C):
                    pe.matmul(ps_h[:, c, b % 2, :], w1[:, c, :], core.xT[:, b * BLK:(b + 1) * BLK],
                              start=True, stop=True).then_inc(up_ready, 1)
                if b >= 1:
                    down(b - 1)
            down(NBLK - 1)

        @block.scalar
        def _(act):
            for b in range(NBLK):
                for c in range(C):
                    act.wait_ge(up_ready, C * b + c + 1)
                    if b >= 2:
                        act.wait_ge(act_done, C * (b - 2) + c + 1)
                    act.activation(gelu[:, c, b % 2, :], ps_h[:, c, b % 2, :], ACT.Gelu, bias=b1[:, c:c + 1])\
                       .then_inc(gelu_done, 1)

        @block.vector
        def _(dve):
            dve.wait_ge(loaded, ALL)

            def add(b):
                dve.wait_ge(y_ready, b + 1)
                xb = core.x[:, b * TPB:(b + 1) * TPB, :]
                dve.tensor_tensor(xb, xb, ps_y[:, b % 2, :, :], ALU.add).then_inc(added, 1)

            for b in range(NBLK):
                for c in range(C):
                    dve.wait_ge(gelu_done, C * b + c + 1)
                    if b >= 2:
                        dve.wait_ge(y_ready, b - 1)
                    dve.tensor_tensor(act_out[:, c, b % 2, :], gelu[:, c, b % 2, :],
                                      spread[:, c, b * BLK:(b + 1) * BLK], ALU.mult).then_inc(act_done, 1)
                if b >= 1:
                    add(b - 1)
            add(NBLK - 1)


def layer0_ffn(core, A):
    layernorm(core, "l0f_ln")
    with ExitStack() as ctx:
        wts = core.sb("l0f_wts", [P, TILES, 8], ctx=ctx)
        rows = core.sb("l0f_rows", [P, N], ctx=ctx)
        rows_dram = core.dram("l0f_rows_dram", [8, N])
        route(core, "l0f_route", A["L0_router_w"], A["L0_router_b"], wts, 8, 2, "batch")
        keep_best(core, "l0f_keep", wts, SEQ // 2, A["c_same_batch"], A["c_before_batch"], A["c_bits"], True, False)
        weight_rows(core, "l0f_wr", wts, 8, rows, rows_dram)
        masked_ffn(core, "l0f", rows, rows_dram, A["L0_w1"], A["L0_b1"], A["L0_w2"], A["L0_b2"])


HEADS, HD = 16, 8
SPAN = 1280
KEY_AT = [0, 512, 1024, 896]
QUERY_AT = [896, 1024, 512, 0]
ROWS6 = 64
Q_PARTS, K_PARTS = (0, 0, 1, 1, 0, 2), (0, 1, 0, 1, 2, 0)


def causal_attention(core, name, wqkv_in, wo_in, mask_in, kind, extra):
    nc = core.nc
    rope = kind == "rope"
    KV = 4 if rope else HEADS
    QKV = (HEADS + 2 * KV) * HD
    PAIRS, KPAIRS = HEADS // 2, KV if rope else HEADS // 2
    QB, KB = PAIRS // 2, KPAIRS // 2
    ROWS = 6 * HD if rope else 6 * HD + 12
    SCALE = float(1.0 / np.sqrt(np.float32(HD)))
    S = {n: core.sem(f"{name}_{n}") for n in (
        "loaded", "const_ready", "xb_ready", "qkv_ready", "qkv_taken", "ss_ready", "norm_ready", "parts_ready", "turned",
        "copied", "max_scores", "max_taken", "max_parts", "s_ready", "exp_done", "pv_done", "o_copied",
        "o_turned", "o_normed", "a_turned", "a_copied", "y_ready", "x_added", "reset")}
    with ExitStack() as ctx:
        sb = lambda n, s, dt=F32: core.sb(name + "_" + n, s, dt, ctx)
        wqkv, wo = sb("wqkv", [P, QKV]), sb("wo", [P, D])
        mask_kq, mask_qk, identb = sb("mask_kq", [P, P], BF16), sb("mask_qk", [P, P], BF16), sb("identb", [P, P], BF16)
        xb = sb("xb", [P, BLK])
        HQK = HEADS + KV
        qk = sb("qk", [P, TPB, HQK, HD])
        rest = sb("rest", [P, TPB * HQK, HD])
        part = [sb(f"part{k}", [P, TPB * HQK, HD], BF16) for k in range(3)]
        q6 = sb("q6", [P, TPB, HEADS, ROWS6], BF16)
        k6 = sb("k6", [P, TPB, 2 * KPAIRS, ROWS6], BF16)
        qT6, kT6 = sb("qT6", [P, 2, PAIRS, BLK], BF16), sb("kT6", [P, 2, KPAIRS, BLK], BF16)
        vaug = sb("vaug", [P, 2, TPB, KV, 32])
        pT = sb("pT", [P, 2, SPAN])
        oT, att, aT = sb("oT", [P, BLK]), sb("att", [P, TPB, HEADS, HD]), sb("aT", [P, BLK])
        rden = sb("rden", [P, TPB, 4])
        if rope:
            norm = sb("norm", [P, TPB * HQK])
            cos, sin = sb("cos", [P, TPB, 4]), sb("sin", [P, TPB, 4])
            rot, tmp = sb("rot", [P, TPB, HQK, HD]), sb("tmp", [P, 2, TPB, HQK, 4])
        else:
            q_tail, k_tail = sb("q_tail", [P, TPB * HEADS, 16], BF16), sb("k_tail", [P, TPB * HEADS, 16], BF16)
            no_tail = sb("no_tail", [P, TPB * HEADS, 16], BF16)
            negm, mrest = sb("negm", [P, TPB, HEADS]), sb("mrest", [P, TPB, HEADS])
            mpart = [sb(f"mpart{k}", [P, TPB, HEADS], BF16) for k in range(3)]
        AB, OB = (2, 2) if rope else (3, 1)
        ps_s = core.ps(name + "_ps_s", [P, SPAN + 256], ctx=ctx)
        ps_a = core.ps(name + "_ps_a", [P, AB, 512], ctx=ctx)
        ps_o = core.ps(name + "_ps_o", [P, OB, 512], ctx=ctx)
        ps_m = core.ps(name + "_ps_m", [P, 512], ctx=ctx)
        block = ctx.enter_context(nc.Block())
        heads = lambda a: a.rearrange("p t h d -> p (t h) d")
        PER = 512 // 256 if rope else 1

        def qkv(t):
            at = (t % PER) * 256
            return ps_a[:, t // PER % AB, at:at + QKV]

        TURNS = QB + KB + (0 if rope else QB)
        PIECES = 3 * HEADS
        FIRST = QB + KB

        def turn_of(n):
            if n >= FIRST:
                return "q", n - FIRST
            if rope:
                return ("k", n) if n < KB else ("q", n - KB)
            return ("q", n // 2) if n % 2 else ("k", n // 2)

        def wait(eng, sem, value):
            if type(value) is not int or value > 0:
                eng.wait_ge(sem, value)

        def sequences(eng, prepare, head, wrap_up):
            for slot in range(HEADS + 1):
                prepare(0, 0, slot)

            def one(b, par, wrap, prep):
                for slot in range(HEADS):
                    if wrap:
                        wrap_up(b - 1, slot)
                    head(b, par, slot, lambda: prepare(b + 1, 1 - par, slot) if prep else None)
                if prep:
                    prepare(b + 1, 1 - par, HEADS)

            one(0, 0, False, True)
            with eng.Fori(0, (BATCH - 2) // 2) as i:
                one(i * 2 + 1, 1, True, True)
                one(i * 2 + 2, 0, True, True)
            one(BATCH - 1, 1, True, False)
            for slot in range(HEADS):
                wrap_up(BATCH - 1, slot)

        PROJECT = 1
        TURN = 10 if rope else 6
        MAX = 8

        @block.sync
        def _(sp):
            sp.dma_start(wqkv[:, :], wqkv_in).then_inc(S["loaded"], 16)
            sp.dma_start(wo[:, :], wo_in).then_inc(S["loaded"], 16)
            sp.dma_start(mask_kq[:, :], mask_in[0]).then_inc(S["loaded"], 16)
            sp.dma_start(mask_qk[:, :], mask_in[1]).then_inc(S["loaded"], 16)
            sp.dma_start(identb[:, :], mask_in[2]).then_inc(S["loaded"], 16)
            if rope:
                sp.dma_start(cos[:, :, :], extra[0]).then_inc(S["loaded"], 16)
                sp.dma_start(sin[:, :, :], extra[1]).then_inc(S["loaded"], 16)
            else:
                sp.dma_start(q_tail[:, :, :], extra[0]).then_inc(S["loaded"], 16)
                sp.dma_start(k_tail[:, :, :], extra[1]).then_inc(S["loaded"], 16)

        ALL = 16 * 7

        @block.gpsimd
        def _(pool):
            pool.memset(q6[:, :, :, :], 0.0)
            pool.memset(k6[:, :, :, :], 0.0)
            pool.memset(vaug[:, :, :, :, :], 0.0)
            pool.drain()
            pool.memset(vaug[:, :, :, :, HD:HD + 1], 1.0)
            if not rope:
                pool.memset(no_tail[:, :, :], 0.0)
                pool.wait_ge(S["loaded"], ALL)
                pool.tensor_copy(heads(k6[:, :, :, :])[:, :, 48:64], k_tail[:, :, :])
            pool.drain()
            pool.sem_inc(S["const_ready"], 1)
            if rope:
                return
            with pool.Fori(0, BATCH) as b:
                pool.wait_ge(S["qkv_ready"], b * TPB + 1)
                pool.tensor_tensor(heads(q6[:, :, :, :])[:, :, 48:64], q_tail[:, :, :], no_tail[:, :, :], ALU.add)\
                    .then_inc(S["reset"], 1)

        @block.tensor
        def _(pe):
            pe.wait_ge(S["loaded"], ALL)
            rows = lambda h: slice(ROWS6 * (h % 2), ROWS6 * (h % 2) + ROWS)
            keys = lambda h: h // 4 if rope else h // 2

            def turn(b, n):
                if AB <= n < FIRST or n >= FIRST + AB:
                    pe.wait_ge(S["copied"], b * TURNS + n - AB + 1)
                what, bank = turn_of(n)
                src = q6 if what == "q" else k6
                for a in range(2):
                    for t in range(TPB):
                        at = (a * TPB + t) * P
                        last = pe.transpose(
                            ps_a[:, n % AB, :].bitcast(BF16)[:, at:at + P],
                            src[:, t, 2 * (2 * bank + a):2 * (2 * bank + a) + 2, :].rearrange("p h r -> p (h r)"),
                            identb[:, :])
                last.then_inc(S["turned"], 1)

            def first_pass(b, par, h):
                for u, tiles in enumerate(((3,), (2, 0), (1,))):
                    if h == 0:
                        pe.wait_ge(S["copied"], b * TURNS + FIRST)
                    if h:
                        pe.wait_ge(S["max_taken"], b * PIECES + 3 * (h - 1) + u + 1)
                    for t in tiles:
                        at, w = (384 if t == 0 else 0), (t + 1) * P
                        pe.matmul(ps_a[:, u, at:at + w], qT6[rows(h), par, h // 2, t * P:(t + 1) * P],
                                  kT6[rows(h), par, keys(h), 0:w], start=True, stop=False)
                        last = pe.matmul(ps_a[:, u, at + w - P:at + w], identb[:, :], mask_qk[:, :],
                                         start=False, stop=True)
                    last.then_inc(S["max_scores"], 1)

            def prepare(b, par, slot):
                if slot == PROJECT:
                    wait(pe, S["copied"], b * TURNS)
                    pe.wait_ge(S["xb_ready"], b + 1)
                    for t in range(TPB):
                        if t >= AB * PER:
                            pe.wait_ge(S["qkv_taken"], b * TPB + t - AB * PER + 1)
                        pe.matmul(qkv(t), xb[:, t * P:(t + 1) * P], wqkv[:, :], start=True, stop=True)\
                            .then_inc(S["qkv_ready"], 1)
                if slot == TURN:
                    pe.wait_ge(S["parts_ready"], b + 1)
                    if not rope:
                        pe.wait_ge(S["reset"], b + 1)
                at = slot - TURN
                if rope and 0 <= at < TURNS:
                    turn(b, at)
                if not rope:
                    if 0 <= at < 2:
                        for n in range(4 * at, 4 * at + 4):
                            turn(b, n)
                    if slot == HEADS:
                        pe.wait_ge(S["max_parts"], b + 1)
                        for n in range(FIRST, TURNS):
                            turn(b, n)

            def scores(b, par, h):
                if h % 4 == 0:
                    pe.wait_ge(S["copied"], b * TURNS + (KB + h // 4 + 1 if rope else FIRST + h // 4 + 1))
                for j in (0, 1, 3, 2):
                    if j < 2:
                        wait(pe, S["exp_done"], (b * HEADS + h) * 2 - 1 + j)
                    at, w = KEY_AT[j], (TPB - j) * P
                    pe.matmul(ps_s[:, at:at + w], kT6[rows(h), par, keys(h), j * P:(j + 1) * P],
                              qT6[rows(h), par, h // 2, j * P:BLK], start=True, stop=False)
                    last = pe.matmul(ps_s[:, at:at + P], identb[:, :], mask_kq[:, :], start=False, stop=True)
                    if j in (0, 2):
                        last.then_inc(S["s_ready"], 1)

            def values(b, par, h):
                g, i = h // 4, h % 4
                if i == 0:
                    wait(pe, S["o_copied"], b * 4 + g - (OB - 1))
                for j in range(TPB):
                    if j < 2:
                        pe.wait_ge(S["exp_done"], (b * HEADS + h) * 2 + 1 + j)
                    last = pe.matmul(ps_o[32 * i:32 * i + 32, g % OB, j * P:BLK], vaug[:, par, j, g if rope else h, :],
                                     pT[:, h % 2, KEY_AT[j]:KEY_AT[j] + (TPB - j) * P],
                                     start=(j == 0), stop=(j == TPB - 1))
                last.then_inc(S["pv_done"], 1)

            def turn_group(b, g):
                pe.wait_ge(S["o_copied"], b * 4 + g + 1)
                if g:
                    pe.wait_ge(S["o_normed"], b * 4 + g)
                else:
                    wait(pe, S["x_added"], b)
                for t in range(TPB):
                    last = pe.transpose(ps_m[:, t * P:(t + 1) * P], oT[:, t * P:(t + 1) * P], core.ident[:, :])
                last.then_inc(S["o_turned"], 1)

            def head(b, par, h, prepare_next):
                scores(b, par, h)
                if h >= 1:
                    values(b, par, h - 1)
                if h in (6, 10, 14):
                    turn_group(b, h // 4 - 1)
                prepare_next()
                if h == HEADS - 1:
                    values(b, par, h)

            def wrap_up(b, slot):
                if slot == 1:
                    turn_group(b, 3)
                if slot == 2:
                    pe.wait_ge(S["o_normed"], b * 4 + 4)
                    for t in range(TPB):
                        last = pe.transpose(ps_m[:, t * P:(t + 1) * P],
                                            att[:, t, :, :].rearrange("p h d -> p (h d)"), core.ident[:, :])
                    last.then_inc(S["a_turned"], 1)
                if slot == 3:
                    pe.wait_ge(S["a_copied"], b + 1)
                    for t in range(TPB):
                        last = pe.matmul(ps_m[:, t * P:(t + 1) * P], aT[:, t * P:(t + 1) * P], wo[:, :],
                                         start=True, stop=True)
                    last.then_inc(S["y_ready"], 1)

            def prepare_all(b, par, slot):
                if not rope and 0 <= slot - MAX < HEADS // 2:
                    first_pass(b, par, 2 * (slot - MAX))
                prepare(b, par, slot)
                if not rope and 0 <= slot - MAX < HEADS // 2:
                    first_pass(b, par, 2 * (slot - MAX) + 1)

            sequences(pe, prepare_all, head, wrap_up)

        @block.scalar
        def _(act):
            def prepare(b, par, slot):
                if slot == 0:
                    act.activation(xb[:, :], core.xT[:, b * BLK:(b + 1) * BLK] if type(b) is int
                                   else core.xT[:, bass.ds(b * BLK, BLK)], ACT.Copy).then_inc(S["xb_ready"], 1)
                if rope and slot == 3:
                    act.wait_ge(S["ss_ready"], b + 1)
                    act.activation(norm[:, :], norm[:, :], ACT.Sqrt).then_inc(S["norm_ready"], 1)
                at = slot - TURN
                if slot == HEADS and not rope:
                    turns = range(FIRST, TURNS)
                elif rope:
                    turns = ()
                else:
                    turns = range(4 * at, 4 * at + 4) if 0 <= at < 2 else ()
                for n in turns:
                    act.wait_ge(S["turned"], b * TURNS + n + 1)
                    what, bank = turn_of(n)
                    dst = (qT6 if what == "q" else kT6)[:, par, 2 * bank:2 * bank + 2, :]
                    act.activation(dst.rearrange("p a k -> p (a k)"), ps_a[:, n % AB, :].bitcast(BF16), ACT.Copy)\
                       .then_inc(S["copied"], 1)

            def head(b, par, h, prepare_next):
                wait(act, S["pv_done"], b * HEADS + h - 1)
                for n, cut in enumerate((slice(0, 512), slice(512, SPAN))):
                    act.wait_ge(S["s_ready"], (b * HEADS + h) * 2 + 1 + n)
                    act.activation(pT[:, h % 2, cut], ps_s[:, cut], ACT.Exp, scale=SCALE).then_inc(S["exp_done"], 1)
                prepare_next()

            sequences(act, prepare, head, lambda b, slot: None)

        @block.vector
        def _(dve):
            dve.wait_ge(S["loaded"], ALL)
            dve.wait_ge(S["const_ready"], 1)
            by = lambda k: part[k][:, :, :].rearrange("p (t h) d -> p t h d", t=TPB)
            wide = lambda a: a[:, :, :].rearrange("p t (o f) -> p t o f", o=1).to_broadcast([P, TPB, HQK, 4])
            src = heads(rot[:, :, :, :]) if rope else heads(qk[:, :, :, :])

            def project(b, par):
                for t in range(TPB):
                    dve.wait_ge(S["qkv_ready"], b * TPB + (t // PER + 1) * PER)
                    dve.tensor_copy(qk[:, t, :, :].rearrange("p h d -> p (h d)"), qkv(t)[:, 0:HQK * HD])
                    dve.tensor_copy(vaug[:, par, t, :, 0:HD],
                                    qkv(t)[:, HQK * HD:QKV].rearrange("p (h d) -> p h d", d=HD))\
                       .then_inc(S["qkv_taken"], 1)
                dve.drain()

            def squares(b):
                dve.tensor_tensor(rest[:, :, :], heads(qk[:, :, :, :]), heads(qk[:, :, :, :]), ALU.mult)
                dve.drain()
                dve.tensor_reduce(norm[:, :], rest[:, :, :], AX.X, ALU.add).then_inc(S["ss_ready"], 1)

            def normalise(b):
                dve.wait_ge(S["norm_ready"], b + 1)
                dve.tensor_scalar(norm[:, :], norm[:, :], 1e-10, None, ALU.add)
                dve.drain()
                dve.reciprocal(norm[:, :], norm[:, :])
                dve.drain()
                dve.tensor_tensor(heads(qk[:, :, :, :]), heads(qk[:, :, :, :]),
                                  norm[:, :].rearrange("p (h o) -> p h o", o=1).to_broadcast([P, TPB * HQK, HD]),
                                  ALU.mult)
                dve.drain()

            def rotate():
                lo, hi = qk[:, :, :, 0:4], qk[:, :, :, 4:8]
                dve.tensor_tensor(rot[:, :, :, 0:4], lo, wide(cos), ALU.mult)
                dve.tensor_tensor(rot[:, :, :, 4:8], hi, wide(cos), ALU.mult)
                dve.tensor_tensor(tmp[:, 0, :, :, :], hi, wide(sin), ALU.mult)
                dve.tensor_tensor(tmp[:, 1, :, :, :], lo, wide(sin), ALU.mult)
                dve.drain()

            def rotated():
                dve.tensor_tensor(rot[:, :, :, 0:4], rot[:, :, :, 0:4], tmp[:, 0, :, :, :], ALU.subtract)
                dve.tensor_tensor(rot[:, :, :, 4:8], rot[:, :, :, 4:8], tmp[:, 1, :, :, :], ALU.add)
                dve.drain()

            def split_high():
                dve.tensor_copy(part[0][:, :, :], src)
                dve.drain()
                dve.tensor_tensor(rest[:, :, :], src, part[0][:, :, :], ALU.subtract)
                dve.drain()

            def split_low():
                dve.tensor_copy(part[1][:, :, :], rest[:, :, :])
                dve.drain()
                dve.tensor_tensor(part[2][:, :, :], rest[:, :, :], part[1][:, :, :], ALU.subtract)
                dve.drain()

            def lay_out(b, ns):
                for n in ns:
                    cut = slice(n * HD, (n + 1) * HD)
                    dve.tensor_copy(q6[:, :, :, cut], by(Q_PARTS[n])[:, :, 0:HEADS, :])
                    kp = by(K_PARTS[n])[:, :, HEADS:HQK, :]
                    if rope:
                        for twin in range(2):
                            last = dve.tensor_copy(k6[:, :, twin::2, cut], kp)
                    else:
                        last = dve.tensor_copy(k6[:, :, :, cut], kp)
                if ns[-1] == 5:
                    last.then_inc(S["parts_ready"], 1)

            def take_max(b, h):
                for u, tiles in enumerate(((3,), (2, 0), (1,))):
                    dve.wait_ge(S["max_scores"], b * PIECES + 3 * h + u + 1)
                    for t in tiles:
                        at = 384 if t == 0 else 0
                        last = dve.tensor_reduce(negm[:, t, h:h + 1], ps_a[:, u, at:at + (t + 1) * P], AX.X, ALU.max,
                                                 negate=True)
                    last.then_inc(S["max_taken"], 1)

            def max_parts(b):
                dve.drain()
                dve.tensor_copy(mpart[0][:, :, :], negm[:, :, :])
                dve.drain()
                dve.tensor_tensor(mrest[:, :, :], negm[:, :, :], mpart[0][:, :, :], ALU.subtract)
                dve.drain()
                dve.tensor_copy(mpart[1][:, :, :], mrest[:, :, :])
                dve.drain()
                dve.tensor_tensor(mpart[2][:, :, :], mrest[:, :, :], mpart[1][:, :, :], ALU.subtract)
                dve.drain()
                for k in range(3):
                    last = dve.tensor_copy(q6[:, :, :, 57 + k:58 + k],
                                           mpart[k][:, :, :].rearrange("p t (h o) -> p t h o", o=1))
                last.then_inc(S["max_parts"], 1)

            def prepare(b, par, slot):
                if slot == PROJECT:
                    project(b, par)
                if rope:
                    steps = {2: lambda: squares(b), 4: lambda: normalise(b), 5: rotate, 6: rotated, 7: split_high,
                             8: split_low, 9: lambda: lay_out(b, range(6))}
                else:
                    steps = {2: split_high, 3: split_low, 4: lambda: lay_out(b, range(3)),
                             5: lambda: lay_out(b, range(3, 6)), HEADS: lambda: max_parts(b)}
                    if 0 <= slot - MAX < HEADS // 2:
                        take_max(b, 2 * (slot - MAX))
                        take_max(b, 2 * (slot - MAX) + 1)
                if slot in steps:
                    steps[slot]()
                if rope and 0 <= slot - TURN < TURNS:
                    n = slot - TURN
                    dve.wait_ge(S["turned"], b * TURNS + n + 1)
                    what, bank = turn_of(n)
                    dst = (qT6 if what == "q" else kT6)[:, par, 2 * bank:2 * bank + 2, :]
                    dve.tensor_copy(dst.rearrange("p a k -> p (a k)"), ps_a[:, n % AB, :].bitcast(BF16))\
                       .then_inc(S["copied"], 1)

            def copy_group(b, g):
                dve.wait_ge(S["pv_done"], b * HEADS + 4 * g + 4)
                wait(dve, S["o_turned"], b * 4 + g)
                dve.tensor_copy(oT[:, :], ps_o[:, g % OB, :]).then_inc(S["o_copied"], 1)

            def divide_group(b, g):
                dve.wait_ge(S["o_turned"], b * 4 + g + 1)
                if g == 0:
                    wait(dve, S["a_turned"], b)
                by_head = ps_m[:, :].rearrange("p (t i c) -> p t i c", t=TPB, i=4)
                dve.reciprocal(rden[:, :, :], by_head[:, :, :, HD:HD + 1].rearrange("p t i o -> p t (i o)"))
                dve.drain()
                dve.tensor_tensor(att[:, :, 4 * g:4 * g + 4, :], by_head[:, :, :, 0:HD],
                                  rden[:, :, :].rearrange("p t (i o) -> p t i o", o=1)
                                  .to_broadcast([P, TPB, 4, HD]), ALU.mult).then_inc(S["o_normed"], 1)

            def head(b, par, h, prepare_next):
                if h in (5, 9, 13):
                    copy_group(b, h // 4 - 1)
                if h in (6, 10, 14):
                    divide_group(b, h // 4 - 1)
                prepare_next()

            def wrap_up(b, slot):
                if slot == 0:
                    copy_group(b, 3)
                if slot == 1:
                    divide_group(b, 3)
                if slot == 2:
                    dve.wait_ge(S["a_turned"], b + 1)
                    dve.tensor_copy(aT[:, :], ps_m[:, :]).then_inc(S["a_copied"], 1)
                if slot == 3:
                    dve.wait_ge(S["y_ready"], b + 1)
                    xr = core.x[:, b * TPB:(b + 1) * TPB, :] if type(b) is int else core.x[:, bass.ds(b * TPB, TPB), :]
                    dve.tensor_tensor(xr, xr, ps_m[:, :].rearrange("p (t d) -> p t d", t=TPB), ALU.add)\
                       .then_inc(S["x_added"], 1)

            sequences(dve, prepare, head, wrap_up)


def layer1_attention(core, A):
    layernorm(core, "l1a_ln")
    causal_attention(core, "l1a", A["L1_wqkv"], A["L1_wo"], A["c_masks"], "rope", (A["c_cos"], A["c_sin"]))


def layer3_attention(core, A):
    causal_attention(core, "l3a", A["L3_wqkv"], A["L3_wo"], A["c_masks"], "alibi", (A["c_q_tail"], A["c_k_tail"]))


LAND, REG = 64, 1e-6
COLS = LAND + HD + 1
RROWS = 6 * HD + 6


def landmark_sums(core, name, A, qT_all, land_all, w_dram, z_dram):
    nc = core.nc
    PAIRS, H2 = HEADS // 2, 2 * HEADS
    S = {n: core.sem(f"{name}_{n}") for n in (
        "loaded", "const_ready", "onehot_ready", "seq_done", "xb_ready", "qkv_ready", "parts_ready", "turned", "copied",
        "gathered", "land_ready", "w_ready", "w_clamped", "w_exped", "w_full", "dist_ready", "clamped", "phi_ready",
        "z_ready", "z_taken", "z_turned", "z_full", "saved")}
    with ExitStack() as ctx:
        sb = lambda n, s, dt=F32: core.sb(name + "_" + n, s, dt, ctx)
        wqkv, bias = sb("wqkv", [P, 3 * D]), sb("bias", [P, 3 * D])
        identb = sb("identb", [P, P], BF16)
        regeye = sb("regeye", [LAND, LAND])
        temp, scale = sb("temp", [P, 1]), sb("scale", [P, 1])
        idx_i, idx, neg = sb("idx_i", [P, LAND], I32), sb("idx", [P, LAND]), sb("neg", [P, LAND])
        pos_i, pos = sb("pos_i", [P, TPB], I32), sb("pos", [P, TPB])
        onehot = sb("onehot", [P, TPB, LAND], BF16)
        xb = sb("xb", [P, BLK])
        qk, rest = sb("qk", [P, TPB * H2, HD]), sb("rest", [P, TPB * H2, HD])
        part = [sb(f"part{k}", [P, TPB * H2, HD], BF16) for k in range(3)]
        sq, sqrest = sb("sq", [P, TPB * H2]), sb("sqrest", [P, TPB * H2])
        sqpart = [sb(f"sqpart{k}", [P, TPB * H2], BF16) for k in range(3)]
        x6 = sb("x6", [P, TPB, H2, ROWS6], BF16)
        l6 = sb("l6", [P, TPB, HEADS, ROWS6], BF16)
        kT6 = sb("kT6", [P, PAIRS, BLK], BF16)
        land = sb("land", [P, PAIRS, P], BF16)
        kland = sb("kland", [P, PAIRS, LAND], BF16)
        vaug = sb("vaug", [P, TPB, PAIRS, 32])
        zT = sb("zT", [P, 2, P])
        phi = sb("phi", [P, TPB, PAIRS, P])
        w_sb = sb("w", [LAND, HEADS, LAND])
        z_sb = sb("z", [P, PAIRS, HD + 1])
        ps = core.ps(name + "_ps", [P, 8, 512], ctx=ctx)
        block = ctx.enter_context(nc.Block())
        by_head = lambda a: a[:, :, :].rearrange("p (t h) d -> p t h d", t=TPB)
        one = lambda a: a[:, :].rearrange("p (t h o) -> p t h o", t=TPB, o=1)
        BANK_OF_TURN = (4, 5, 6, 7, 0, 1, 2, 3)

        @block.sync
        def _(sp):
            for dst, src in ((wqkv[:, :], A["L0_wqkv"]), (bias[:, :], A["L0_bqkv"].to_broadcast([P, 3 * D])),
                             (identb[:, :], A["c_masks"][2]), (regeye[:, :], A["c_regeye"]),
                             (temp[:, :], A["L0_temp"].to_broadcast([P, 1])),
                             (idx_i[:, :], A["L0_idx"].to_broadcast([P, LAND]))):
                sp.dma_start(dst, src).then_inc(S["loaded"], 16)
            sp.sem_inc(S["seq_done"], 1)
            with sp.Fori(0, BATCH) as b:
                sp.wait_ge(S["w_full"], b + 1)
                sp.dma_start(w_dram[bass.ds(b * HEADS, HEADS)].rearrange("h i k -> i h k"), w_sb[:, :, :])\
                  .then_inc(S["saved"], 16)
                sp.wait_ge(S["z_full"], b + 1)
                for h2 in range(2):
                    zd = z_dram[bass.ds(b, 1), :, h2, :, :].rearrange("o a k c -> k (o a) c")
                    sp.dma_start(zd, z_sb[64 * h2:64 * h2 + 64, :, :]).then_inc(S["saved"], 16)
                sp.wait_ge(S["saved"], b * 48 + 48)
                sp.sem_inc(S["seq_done"], 1)

        @block.gpsimd
        def _(pool):
            pool.iota(pos_i[:, :], [[P, TPB]], base=0, channel_multiplier=1)
            pool.memset(x6[:, :, :, :], 0.0)
            pool.memset(l6[:, :, :, :], 0.0)
            pool.memset(land[:, :, :], 0.0)
            pool.memset(vaug[:, :, :, :], 0.0)
            pool.drain()
            pool.memset(x6[:, :, :, 51:54], 1.0)
            pool.memset(l6[:, :, :, 48:51], 1.0)
            pool.memset(vaug[:, :, :, 16:17], 1.0)
            pool.drain()
            pool.sem_inc(S["const_ready"], 1)

        @block.tensor
        def _(pe):
            pe.wait_ge(S["onehot_ready"], 1)
            def project(b):
                pe.wait_ge(S["xb_ready"], b + 1)
                for t in range(TPB):
                    last = pe.matmul(ps[:, t, 0:3 * D], xb[:, t * P:(t + 1) * P], wqkv[:, :], start=True, stop=True)
                last.then_inc(S["qkv_ready"], 1)

            def sequence(b, another):
                pe.wait_ge(S["parts_ready"], b + 1)
                for n in range(8):
                    for a in range(2):
                        for t in range(TPB):
                            at = (a * TPB + t) * P
                            last = pe.transpose(
                                ps[:, BANK_OF_TURN[n], :].bitcast(BF16)[:, at:at + P],
                                x6[:, t, 4 * n + 2 * a:4 * n + 2 * a + 2, :].rearrange("p h r -> p (h r)"), identb[:, :])
                    last.then_inc(S["turned"], 1)
                pe.wait_ge(S["copied"], b * 8 + 2)
                for bank, src, h0 in ((4, l6, 0), (5, x6, HEADS)):
                    for a in range(PAIRS):
                        for t in range(TPB):
                            last = pe.matmul(ps[:, bank, a * LAND:(a + 1) * LAND],
                                             src[:, t, h0 + 2 * a:h0 + 2 * a + 2, :].rearrange("p h r -> p (h r)"),
                                             onehot[:, t, :], start=(t == 0), stop=(t == TPB - 1))
                last.then_inc(S["gathered"], 1)
                pe.wait_ge(S["land_ready"], b + 1)
                pe.wait_ge(S["copied"], b * 8 + 4)
                for a in range(PAIRS):
                    last = pe.matmul(ps[0:LAND, 6 + a // 4, (a % 4) * P:(a % 4 + 1) * P], kland[:, a, :], land[:, a, :],
                                     start=True, stop=True)
                last.then_inc(S["w_ready"], 1)
                pe.wait_ge(S["copied"], b * 8 + 8)
                for t in range(TPB):
                    if t >= 2:
                        pe.wait_ge(S["clamped"], b * TPB + t - 1)
                    for a in range(PAIRS):
                        last = pe.matmul(ps[:, 2 * (t % 2) + a // 4, (a % 4) * P:(a % 4 + 1) * P],
                                         kT6[:, a, t * P:(t + 1) * P], land[:, a, :], start=True, stop=True)
                    last.then_inc(S["dist_ready"], 1)
                if another:
                    pe.wait_ge(S["clamped"], b * TPB + TPB)
                    project(b + 1)
                pe.wait_ge(S["phi_ready"], b * TPB + TPB)
                for a in range(PAIRS):
                    rows, cols = slice(32 * (a % 4), 32 * (a % 4) + 32), slice((a // 4) * P, (a // 4 + 1) * P)
                    for t in range(TPB):
                        last = pe.matmul(ps[rows, 4, cols], vaug[:, t, a, :], phi[:, t, a, :],
                                         start=(t == 0), stop=(t == TPB - 1))
                last.then_inc(S["z_ready"], 1)
                pe.wait_ge(S["z_taken"], b + 1)
                for g in range(2):
                    last = pe.transpose(ps[:, 5, g * P:(g + 1) * P], zT[:, g, :], core.ident[:, :])
                last.then_inc(S["z_turned"], 1)

            project(0)
            with pe.Fori(0, BATCH - 1) as b:
                sequence(b, True)
            sequence(BATCH - 1, False)

        @block.scalar
        def _(act):
            act.wait_ge(S["onehot_ready"], 1)
            def copy_x(b):
                act.activation(xb[:, :], core.xT[:, bass.ds(b * BLK, BLK)], ACT.Copy).then_inc(S["xb_ready"], 1)

            def sequence(b, another):
                for n in range(8):
                    act.wait_ge(S["turned"], b * 8 + n + 1)
                    src = ps[:, BANK_OF_TURN[n], :].bitcast(BF16)
                    if n < 4:
                        dst = qT_all[:, bass.ds(b * (PAIRS * BLK) + n * 2 * BLK, 2 * BLK)]
                    else:
                        dst = kT6[:, 2 * (n - 4):2 * (n - 4) + 2, :].rearrange("p a k -> p (a k)")
                    act.activation(dst, src, ACT.Copy).then_inc(S["copied"], 1)
                if another:
                    copy_x(b + 1)
                act.wait_ge(S["w_clamped"], b + 1)
                act.activation(w_sb[:, :, :], w_sb[:, :, :], ACT.Exp, scale=scale[0:LAND, 0:1]).then_inc(S["w_exped"], 1)
                for t in range(TPB):
                    act.wait_ge(S["clamped"], b * TPB + t + 1)
                    act.activation(phi[:, t, :, :], phi[:, t, :, :], ACT.Exp, scale=scale[:, 0:1])\
                       .then_inc(S["phi_ready"], 1)

            copy_x(0)
            with act.Fori(0, BATCH - 1) as b:
                sequence(b, True)
            sequence(BATCH - 1, False)

        @block.vector
        def _(dve):
            dve.wait_ge(S["loaded"], 96)
            dve.wait_ge(S["const_ready"], 1)
            dve.tensor_copy(idx[:, :], idx_i[:, :])
            dve.tensor_copy(pos[:, :], pos_i[:, :])
            dve.reciprocal(scale[:, :], temp[:, :])
            dve.drain()
            dve.tensor_scalar(neg[:, :], idx[:, :], 0.0, float(SEQ), ALU.is_lt, ALU.mult)
            dve.tensor_scalar(scale[:, :], scale[:, :], -1.0, None, ALU.mult)
            dve.drain()
            dve.tensor_tensor(idx[:, :], idx[:, :], neg[:, :], ALU.add)
            dve.drain()
            dve.tensor_scalar(idx[:, :], idx[:, :], 0.0, float(SEQ - 1), ALU.max, ALU.min)
            dve.drain()
            for t in range(TPB):
                last = dve.tensor_scalar(onehot[:, t, :], idx[:, :], pos[:, t:t + 1], None, ALU.is_equal)
            last.then_inc(S["onehot_ready"], 1)
            def split(b):
                dve.wait_ge(S["qkv_ready"], b + 1)
                for t in range(TPB):
                    dve.tensor_tensor(by_head(qk)[:, t, :, :].rearrange("p h d -> p (h d)"), ps[:, t, 0:2 * D],
                                      bias[:, 0:2 * D], ALU.add)
                dve.drain()
                dve.tensor_tensor(rest[:, :, :], qk[:, :, :], qk[:, :, :], ALU.mult)
                dve.tensor_copy(part[0][:, :, :], qk[:, :, :])
                dve.drain()
                dve.tensor_reduce(sq[:, :], rest[:, :, :], AX.X, ALU.add)
                dve.drain()
                dve.tensor_tensor(rest[:, :, :], qk[:, :, :], part[0][:, :, :], ALU.subtract)
                dve.tensor_copy(sqpart[0][:, :], sq[:, :])
                dve.drain()
                dve.tensor_copy(part[1][:, :, :], rest[:, :, :])
                dve.tensor_tensor(sqrest[:, :], sq[:, :], sqpart[0][:, :], ALU.subtract)
                dve.drain()
                dve.tensor_tensor(part[2][:, :, :], rest[:, :, :], part[1][:, :, :], ALU.subtract)
                dve.tensor_copy(sqpart[1][:, :], sqrest[:, :])
                dve.drain()
                dve.tensor_tensor(sqpart[2][:, :], sqrest[:, :], sqpart[1][:, :], ALU.subtract)
                dve.drain()

            def take_values():
                for t in range(TPB):
                    dve.tensor_tensor(vaug[:, t, :, 0:16], ps[:, t, 2 * D:3 * D].rearrange("p (a c) -> p a c", a=PAIRS),
                                      bias[:, 2 * D:3 * D].rearrange("p (a c) -> p a c", a=PAIRS), ALU.add)

            def lay_out():
                for n in range(6):
                    cut = slice(n * HD, (n + 1) * HD)
                    dve.tensor_copy(x6[:, :, :, cut], by_head(part[Q_PARTS[n]]))
                    dve.tensor_scalar(l6[:, :, :, cut], by_head(part[K_PARTS[n]])[:, :, HEADS:H2, :], -2.0, None, ALU.mult)
                for k in range(3):
                    dve.tensor_copy(x6[:, :, :, 48 + k:49 + k], one(sqpart[k]))
                    last = dve.tensor_copy(l6[:, :, :, 51 + k:52 + k], one(sqpart[k])[:, :, HEADS:H2, :])
                last.then_inc(S["parts_ready"], 1)

            def sequence(b, another):
                dve.wait_ge(S["gathered"], b + 1)
                for h2 in range(2):
                    rows, cols = slice(64 * h2, 64 * h2 + 64), slice(LAND * h2, LAND * h2 + LAND)
                    dve.tensor_copy(land[rows, :, cols], ps[rows, 4, :].rearrange("p (a k) -> p a k", a=PAIRS))
                dve.tensor_copy(kland[:, :, :], ps[:, 5, :].rearrange("p (a k) -> p a k", a=PAIRS)).then_inc(S["land_ready"], 1)
                dve.drain()
                dve.tensor_copy(land_all[:, bass.ds(b * (PAIRS * P), PAIRS * P)],
                                land[:, :, :].rearrange("p a k -> p (a k)"))
                dve.wait_ge(S["seq_done"], b + 1)
                dve.wait_ge(S["w_ready"], b + 1)
                dve.tensor_scalar(w_sb[:, :, :].rearrange("p h k -> p (h k)"),
                                  ps[0:LAND, 6:8, :].rearrange("p n k -> p (n k)"), 0.0, None, ALU.max)\
                   .then_inc(S["w_clamped"], 1)
                for t in range(TPB):
                    dve.wait_ge(S["dist_ready"], b * TPB + t + 1)
                    z = 2 * (t % 2)
                    dve.tensor_scalar(phi[:, t, :, :].rearrange("p a k -> p (a k)"),
                                      ps[:, z:z + 2, :].rearrange("p n k -> p (n k)"), 0.0, None, ALU.max)\
                       .then_inc(S["clamped"], 1)
                dve.wait_ge(S["w_exped"], b + 1)
                dve.tensor_tensor(w_sb[:, :, :], w_sb[:, :, :],
                                  regeye[:, :].rearrange("p (o k) -> p o k", o=1).to_broadcast([LAND, HEADS, LAND]),
                                  ALU.add).then_inc(S["w_full"], 1)
                if another:
                    split(b + 1)
                dve.wait_ge(S["z_ready"], b + 1)
                dve.tensor_copy(zT[:, :, :].rearrange("p g k -> p (g k)"), ps[:, 4, 0:2 * P]).then_inc(S["z_taken"], 1)
                if another:
                    take_values()
                dve.wait_ge(S["z_turned"], b + 1)
                zv = ps[:, 5, 0:PAIRS * 32].rearrange("p (a c) -> p a c", a=PAIRS)
                for h2 in range(2):
                    rows = slice(64 * h2, 64 * h2 + 64)
                    dve.tensor_copy(z_sb[rows, :, 0:HD], zv[rows, :, HD * h2:HD * h2 + HD])
                    last = dve.tensor_copy(z_sb[rows, :, HD:HD + 1], zv[rows, :, 16:17])
                last.then_inc(S["z_full"], 1)
                if another:
                    lay_out()

            split(0)
            take_values()
            lay_out()
            with dve.Fori(0, BATCH - 1) as b:
                sequence(b, True)
            sequence(BATCH - 1, False)


def solve(core, name, w_dram, z_dram, y_dram):
    nc = core.nc
    OWN = 60
    BAND = 13
    loaded, pivot_ready = core.sem(name + "_loaded"), core.sem(name + "_pivot_ready")
    pool_done, solved, saved = core.sem(name + "_pool_done"), core.sem(name + "_solved"), core.sem(name + "_saved")
    with ExitStack() as ctx:
        sb = lambda n, s, dt=F32: core.sb(name + "_" + n, s, dt, ctx)
        m, rinv = sb("m", [P, LAND, COLS]), sb("rinv", [P, LAND])
        y = sb("y", [P, LAND, HD + 1])
        scaled = sb("scaled", [P, OWN, COLS - OWN])
        outer_p = sb("outer_p", [P, LAND, COLS - OWN])
        row_ps = core.ps(name + "_row", [P, 512], ctx=ctx)
        outer = core.ps(name + "_outer", [P, 7 * 512], ctx=ctx)
        block = ctx.enter_context(nc.Block())

        def outer_product(eng, out, col, row, shape):
            return eng.tensor_tensor(out, col.rearrange("p (r o) -> p r o", o=1).to_broadcast(shape),
                                     row.rearrange("p (o c) -> p o c", o=1).to_broadcast(shape), ALU.mult)

        @block.sync
        def _(sp):
            sp.dma_start(m[:, :, 0:LAND], w_dram).then_inc(loaded, 16)
            sp.dma_start(m[:, :, LAND:COLS], z_dram.rearrange("b a h k c -> (b a h) k c")).then_inc(loaded, 16)
            sp.wait_ge(solved, 1)
            sp.dma_start(y_dram.rearrange("b a h k c -> (b a h) k c"), y[:, :, :]).then_inc(saved, 16)
            sp.wait_ge(saved, 16)

        @block.vector
        def _(dve):
            dve.wait_ge(loaded, 32)
            for k in range(LAND):
                end = OWN if k < OWN else COLS
                last_row = OWN if k < OWN else LAND
                if k == OWN:
                    dve.wait_ge(pool_done, OWN)
                dve.reciprocal(rinv[:, k:k + 1], m[:, k, k:k + 1])
                dve.drain()
                w, n = end - k - 1, last_row - k - 1
                if w:
                    dve.tensor_scalar(row_ps[:, 0:w], m[:, k, k + 1:end], rinv[:, k:k + 1], None, ALU.mult)
                    dve.drain()
                bands, at = [], 0
                for band in range(max(1, round(n / BAND)) if n else 0):
                    r0 = k + 1 + band * n // max(1, round(n / BAND))
                    r1 = k + 1 + (band + 1) * n // max(1, round(n / BAND))
                    size = (r1 - r0) * (end - r0)
                    bands.append((r0, r1, outer[:, at:at + size].rearrange("p (r c) -> p r c", c=end - r0)))
                    at += size
                for r0, r1, out in bands:
                    outer_product(dve, out, m[:, k, r0:r1], row_ps[:, r0 - k - 1:w], [P, r1 - r0, end - r0])
                dve.drain()
                for r0, r1, out in bands:
                    dve.tensor_tensor(m[:, r0:r1, r0:end], m[:, r0:r1, r0:end], out, ALU.subtract)
                if w:
                    dve.tensor_copy(m[:, k, k + 1:end], row_ps[:, 0:w])
                dve.drain()
                if k < OWN:
                    dve.sem_inc(pivot_ready, 1)
            for k in range(LAND - 1, 0, -1):
                shape = [P, k, HD + 1]
                out = outer[:, 0:k * (HD + 1)].rearrange("p (r c) -> p r c", c=HD + 1)
                outer_product(dve, out, m[:, 0:k, k:k + 1].rearrange("p r o -> p (r o)"), m[:, k, LAND:COLS], shape)
                dve.drain()
                dve.tensor_tensor(m[:, 0:k, LAND:COLS], m[:, 0:k, LAND:COLS], out, ALU.subtract)
                dve.drain()
            dve.tensor_copy(y[:, :, :], m[:, :, LAND:COLS]).then_inc(solved, 1)

        @block.gpsimd
        def _(pool):
            pool.wait_ge(loaded, 32)
            for k in range(OWN):
                pool.wait_ge(pivot_ready, k + 1)
                pool.tensor_scalar(scaled[:, k, :], m[:, k, OWN:COLS], rinv[:, k:k + 1], None, ALU.mult)
                pool.drain()
                n = OWN - 1 - k
                if n:
                    outer_product(pool, outer_p[:, k + 1:OWN, :], m[:, k, k + 1:OWN], m[:, k, OWN:COLS],
                                  [P, n, COLS - OWN])
                outer_product(pool, outer_p[:, OWN:LAND, :], m[:, k, OWN:LAND], scaled[:, k, :],
                              [P, LAND - OWN, COLS - OWN])
                pool.drain()
                rest = m[:, k + 1:LAND, OWN:COLS]
                pool.tensor_tensor(rest, rest, outer_p[:, k + 1:LAND, :], ALU.subtract)
                pool.drain()
            pool.tensor_copy(m[:, 0:OWN, OWN:COLS], scaled[:, :, :])
            pool.drain()
            pool.sem_inc(pool_done, OWN)


def landmark_outputs(core, name, A, qT_all, land_all, y_dram):
    nc = core.nc
    PAIRS = HEADS // 2
    S = {n: core.sem(f"{name}_{n}") for n in (
        "loaded", "const_ready", "y_loaded0", "y_loaded1", "land_ready", "dist_ready", "clamped", "phi_ready", "used",
        "o_copied", "o_turned", "o_normed", "a_turned", "a_copied", "y_ready", "x_added")}
    with ExitStack() as ctx:
        sb = lambda n, s, dt=F32: core.sb(name + "_" + n, s, dt, ctx)
        wo, bo, ones = sb("wo", [P, D]), sb("bo", [1, D]), sb("ones", [1, P])
        temp, scale = sb("temp", [P, 1]), sb("scale", [P, 1])
        land = sb("land", [P, 2, PAIRS, P], BF16)
        y2 = sb("y2", [P, 2, PAIRS, 32])
        phi = sb("phi", [P, 2, BLK])
        oT, att, aT = sb("oT", [P, 2, BLK]), sb("att", [P, TPB, HEADS, HD]), sb("aT", [P, BLK])
        den = sb("den", [P, 2, TPB, 8])
        ps_d = core.ps(name + "_ps_d", [P, 2, 512], ctx=ctx)
        ps_o = core.ps(name + "_ps_o", [P, 2, 512], ctx=ctx)
        ps_t = core.ps(name + "_ps_t", [P, 2, 512], ctx=ctx)
        ps_m = core.ps(name + "_ps_m", [P, 512], ctx=ctx)
        block = ctx.enter_context(nc.Block())

        def wait(eng, sem, value):
            if type(value) is not int or value > 0:
                eng.wait_ge(sem, value)

        def sequences(eng, pair, wrap_up):
            def one(b, par, wrap):
                for a in range(PAIRS):
                    if wrap:
                        wrap_up(b - 1, a)
                    pair(b, par, a)

            one(0, 0, False)
            with eng.Fori(0, (BATCH - 2) // 2) as i:
                one(i * 2 + 1, 1, True)
                one(i * 2 + 2, 0, True)
            one(BATCH - 1, 1, True)
            for a in range(PAIRS):
                wrap_up(BATCH - 1, a)

        @block.sync
        def _(sp):
            sp.dma_start(wo[:, :], A["L0_wo"]).then_inc(S["loaded"], 16)
            sp.dma_start(bo[:, :], A["L0_bo"]).then_inc(S["loaded"], 16)
            sp.dma_start(temp[:, :], A["L0_temp"].to_broadcast([P, 1])).then_inc(S["loaded"], 16)
            sp.wait_ge(S["const_ready"], 1)

            def load_y(b, par):
                for h2 in range(2):
                    src = y_dram[bass.ds(b, 1), :, h2, :, :].rearrange("o a k c -> k (o a) c")
                    sp.dma_start(y2[64 * h2:64 * h2 + 64, par, :, 16 * h2:16 * h2 + HD + 1], src)\
                        .then_inc(S[f"y_loaded{par}"], 16)

            load_y(0, 0)
            load_y(1, 1)
            with sp.Fori(1, BATCH // 2) as i:
                for par in range(2):
                    sp.wait_ge(S["used"], (i * 2 + par - 1) * PAIRS)
                    load_y(i * 2 + par, par)

        @block.gpsimd
        def _(pool):
            pool.memset(y2[:, :, :, :], 0.0)
            pool.memset(ones[:, :], 1.0)
            pool.drain()
            pool.sem_inc(S["const_ready"], 1)

        @block.tensor
        def _(pe):
            pe.wait_ge(S["loaded"], 48)
            pe.wait_ge(S["const_ready"], 1)

            def outputs(b, par, a):
                if a == 0:
                    pe.wait_ge(S[f"y_loaded{par}"], (b - par) * 16 + 32)
                if a % 4 == 0:
                    wait(pe, S["o_copied"], b * 2 + a // 4 - 1)
                pe.wait_ge(S["phi_ready"], b * PAIRS + a + 1)
                pe.matmul(ps_o[32 * (a % 4):32 * (a % 4) + 32, a // 4, :], y2[:, par, a, :], phi[:, a % 2, :],
                          start=True, stop=True).then_inc(S["used"], 1)

            def pair(b, par, a):
                if a == 0:
                    pe.wait_ge(S["land_ready"], b + 1)
                wait(pe, S["clamped"], b * PAIRS + a - 1)
                pe.matmul(ps_d[:, a % 2, :], land[:, par, a, :], qT_all[:, bass.ds((b * PAIRS + a) * BLK, BLK)],
                          start=True, stop=True).then_inc(S["dist_ready"], 1)
                if a >= 1:
                    outputs(b, par, a - 1)
                if a == PAIRS - 1:
                    outputs(b, par, a)

            def wrap_up(b, slot):
                if slot == 1:
                    pe.wait_ge(S["o_copied"], b * 2 + 2)
                    for g in range(2):
                        for t in range(TPB):
                            last = pe.transpose(ps_t[:, g, t * P:(t + 1) * P], oT[:, g, t * P:(t + 1) * P],
                                                core.ident[:, :])
                        last.then_inc(S["o_turned"], 1)
                if slot == 3:
                    pe.wait_ge(S["o_normed"], b * 2 + 2)
                    for t in range(TPB):
                        last = pe.transpose(ps_m[:, t * P:(t + 1) * P], att[:, t, :, :].rearrange("p h d -> p (h d)"),
                                            core.ident[:, :])
                    last.then_inc(S["a_turned"], 1)
                if slot == 5:
                    pe.wait_ge(S["a_copied"], b + 1)
                    for t in range(TPB):
                        pe.matmul(ps_m[:, t * P:(t + 1) * P], aT[:, t * P:(t + 1) * P], wo[:, :],
                                  start=True, stop=False)
                        last = pe.matmul(ps_m[:, t * P:(t + 1) * P], ones[:, :], bo[:, :], start=False, stop=True)
                    last.then_inc(S["y_ready"], 1)

            sequences(pe, pair, wrap_up)

        @block.scalar
        def _(act):
            def copy_land(b, par):
                act.activation(land[:, par, :, :].rearrange("p a k -> p (a k)"),
                               land_all[:, bass.ds(b * (PAIRS * P), PAIRS * P)], ACT.Copy).then_inc(S["land_ready"], 1)

            def pair(b, par, a):
                act.wait_ge(S["clamped"], b * PAIRS + a + 1)
                act.activation(phi[:, a % 2, :], phi[:, a % 2, :], ACT.Exp, scale=scale[:, 0:1])\
                   .then_inc(S["phi_ready"], 1)
                if a == 3 and not (type(b) is int and b == BATCH - 1):
                    copy_land(b + 1, 1 - par)

            copy_land(0, 0)
            sequences(act, pair, lambda b, slot: None)

        @block.vector
        def _(dve):
            dve.wait_ge(S["loaded"], 48)
            dve.reciprocal(scale[:, :], temp[:, :])
            dve.drain()
            dve.tensor_scalar(scale[:, :], scale[:, :], -1.0, None, ALU.mult)
            dve.drain()

            def pair(b, par, a):
                dve.wait_ge(S["dist_ready"], b * PAIRS + a + 1)
                wait(dve, S["used"], b * PAIRS + a - 1)
                dve.tensor_scalar(phi[:, a % 2, :], ps_d[:, a % 2, :], 0.0, None, ALU.max).then_inc(S["clamped"], 1)
                if a == 5:
                    dve.wait_ge(S["used"], b * PAIRS + 4)
                    dve.tensor_copy(oT[:, 0, :], ps_o[:, 0, :]).then_inc(S["o_copied"], 1)

            def wrap_up(b, slot):
                if slot == 0:
                    dve.wait_ge(S["used"], b * PAIRS + PAIRS)
                    dve.tensor_copy(oT[:, 1, :], ps_o[:, 1, :]).then_inc(S["o_copied"], 1)
                if slot in (1, 2):
                    g = slot - 1
                    dve.wait_ge(S["o_turned"], b * 2 + g + 1)
                    bh = ps_t[:, g, :].rearrange("p (t i c) -> p t i c", t=TPB, i=8)
                    dve.tensor_scalar(den[:, g, :, :], bh[:, :, :, HD:HD + 1].rearrange("p t i o -> p t (i o)"), 1e-10,
                                      None, ALU.max)
                    dve.drain()
                    dve.reciprocal(den[:, g, :, :], den[:, g, :, :])
                    dve.drain()
                    dve.tensor_tensor(att[:, :, 8 * g:8 * g + 8, :], bh[:, :, :, 0:HD],
                                      den[:, g, :, :].rearrange("p t (i o) -> p t i o", o=1)
                                      .to_broadcast([P, TPB, 8, HD]), ALU.mult).then_inc(S["o_normed"], 1)
                if slot == 4:
                    dve.wait_ge(S["a_turned"], b + 1)
                    dve.tensor_copy(aT[:, :], ps_m[:, :]).then_inc(S["a_copied"], 1)
                if slot == 6:
                    dve.wait_ge(S["y_ready"], b + 1)
                    xr = core.x[:, bass.ds(b * TPB, TPB), :]
                    dve.tensor_tensor(xr, xr, ps_m[:, :].rearrange("p (t d) -> p t d", t=TPB), ALU.add)\
                       .then_inc(S["x_added"], 1)

            sequences(dve, pair, wrap_up)


def layer0_attention(core, A):
    layernorm(core, "l0a_ln")
    with ExitStack() as ctx:
        qT_all = core.sb("l0a_qT_all", [P, BATCH * (HEADS // 2) * BLK], BF16, ctx)
        land_all = core.sb("l0a_land_all", [P, BATCH * (HEADS // 2) * P], BF16, ctx)
        w_dram = core.dram("l0a_w_dram", [BATCH * HEADS, LAND, LAND])
        z_dram = core.dram("l0a_z_dram", [BATCH, HEADS // 2, 2, LAND, HD + 1])
        y_dram = core.dram("l0a_y_dram", [BATCH, HEADS // 2, 2, LAND, HD + 1])
        landmark_sums(core, "l0s", A, qT_all, land_all, w_dram, z_dram)
        solve(core, "l0v", w_dram, z_dram, y_dram)
        landmark_outputs(core, "l0o", A, qT_all, land_all, y_dram)


RHEADS, RD, CHUNK = 4, 32, 32
CHUNKS = SEQ // CHUNK


def chunk_products(core, name, A, store):
    nc = core.nc
    S = {n: core.sem(f"{name}_{n}") for n in (
        "loaded", "const_ready", "taps_ready", "seq_done", "conv_ready", "ctrl_ready", "silu_done", "square_done", "gates_done",
        "spread_ready", "ss_ready", "norm_ready", "recip_ready", "r_turned", "r_copied", "expanded", "kdiag_ready",
        "prod_ready", "l_ready", "all_read", "l_saved", "qkv_read", "spread_taken")}
    with ExitStack() as ctx:
        sb = lambda n, s, dt=F32: core.sb(name + "_" + n, s, dt, ctx)
        w_in, w_taps = sb("w_in", [P, 3, D]), sb("w_taps", [P, 3, 4, D])
        w_ctrl, b8, bog = sb("w_ctrl", [P, 8 + D]), sb("b8", [8, 1]), sb("bog", [P, 1])
        chunk_c = sb("chunk_c", [P, 4, SEQ])
        ones4, pick_ab, pick_r = sb("ones4", [P, RHEADS]), sb("pick_ab", [8, 2, P]), sb("pick_r", [32, 8, P])
        qkv_s, sq = sb("qkv_s", [P, 2, 3, SEQ]), sb("sq", [P, 2, SEQ])
        gates8 = sb("gates8", [8, SEQ])
        a_all, a_in, a_start, b_all = (sb(n, [P, SEQ]) for n in ("a_all", "a_in", "a_start", "b_all"))
        dec, gam, dec_b, gam_b = (sb(n, [P, SEQ]) for n in ("dec", "gam", "dec_b", "gam_b"))
        nrm, rT = sb("nrm", [P, 32]), sb("rT", [32, P])
        kq_n, ktok = sb("kq_n", [P, 2, SEQ]), sb("ktok", [P, SEQ])
        kdiag = sb("kdiag", [P, CHUNKS, P])
        l_sb = sb("l_sb", [P, CHUNKS, CHUNK])
        ps = core.ps(name + "_ps", [P, 8, 512], ctx=ctx)
        block = ctx.enter_context(nc.Block())
        chunks = lambda a: a.rearrange("p (c t) -> p c t", t=CHUNK)
        NOT_START, START, SAME, BEFORE = range(4)

        @block.sync
        def _(sp):
            for dst, src in ((w_in[:, :, :], A["L2_w_in"]), (w_taps[:, :, :, :].rearrange("p s j f -> p (s j f)"), A["L2_taps"].to_broadcast([P, 12 * D])),
                             (w_ctrl[:, :], A["L2_w_ctrl"]), (b8[:, :], A["L2_b8"]), (bog[:, :], A["L2_bog"]),
                             (chunk_c[:, :, :], A["c_chunk"]), (ones4[:, :], A["c_ones4"]), (pick_ab[:, :, :], A["c_pick_ab"]),
                             (pick_r[:, :, :], A["c_pick_r"])):
                sp.dma_start(dst, src).then_inc(S["loaded"], 16)
            sp.sem_inc(S["seq_done"], 1)
            with sp.Fori(0, BATCH) as b:
                sp.wait_ge(S["l_ready"], b + 1)
                for h in range(RHEADS):
                    dst = store.l_dram[bass.ds(b, 1), h].rearrange("o c s t -> (o s) c t")
                    sp.dma_start(dst, l_sb[32 * h:32 * h + 32, :, :]).then_inc(S["l_saved"], 16)
                sp.wait_ge(S["l_saved"], b * 64 + 64)
                sp.sem_inc(S["seq_done"], 1)

        ALL = 16 * 9

        @block.gpsimd
        def _(pool):
            pool.memset(kdiag[:, :, :], 0.0)
            pool.drain()
            pool.sem_inc(S["const_ready"], 1)

        @block.tensor
        def _(pe):
            pe.wait_ge(S["taps_ready"], 1)
            pe.wait_ge(S["loaded"], ALL)
            def convolve(b, parts):
                if 1 in parts:
                    pe.wait_ge(S["silu_done"], b * 3 + 3)
                for s in parts:
                    for j in range(4):
                        last = pe.matmul(ps[:, s, j:SEQ], w_taps[:, s, j, :], core.xT[:, bass.ds(b * SEQ, SEQ - j)],
                                         start=(j == 0), stop=(j == 3))
                    last.then_inc(S["conv_ready"], 1)

            def products_of(b, another):
                for s in range(2):
                    pe.wait_ge(S["square_done"], b * 2 + s + 1)
                    for t in range(TPB):
                        at = (s * TPB + t) * RHEADS
                        last = pe.matmul(ps[:, 7, at:at + RHEADS], sq[:, s, t * P:(t + 1) * P], ones4[:, :],
                                         start=True, stop=True)
                last.then_inc(S["ss_ready"], 1)
                pe.wait_ge(S["recip_ready"], b + 1)
                pe.transpose(ps[0:32, 7, P:2 * P], nrm[:, :], core.ident[:, :]).then_inc(S["r_turned"], 1)
                pe.wait_ge(S["all_read"], b + 1)
                xb = core.xT[:, bass.ds(b * SEQ, SEQ)]
                pe.matmul(ps[:, 4, :], w_ctrl[:, 8:8 + D], xb, start=True, stop=True)
                pe.matmul(ps[0:8, 3, :], w_ctrl[:, 0:8], xb, start=True, stop=True).then_inc(S["ctrl_ready"], 1)
                pe.wait_ge(S["r_copied"], b + 1)
                pe.wait_ge(S["spread_taken"], b + 1)
                for s in range(2):
                    for t in range(TPB):
                        last = pe.matmul(ps[:, 5 + s, t * P:(t + 1) * P], pick_r[:, s * TPB + t, :], rT[:, :],
                                         start=True, stop=True)
                last.then_inc(S["expanded"], 1)
                if another:
                    convolve(b + 1, (1,))
                pe.wait_ge(S["gates_done"], b + 1)
                pe.wait_ge(S["kdiag_ready"], b + 1)
                for k in range(2):
                    last = pe.matmul(ps[:, 5 + k, :], pick_ab[:, k, :], gates8[:, :], start=True, stop=True)
                last.then_inc(S["spread_ready"], 1)
                if another:
                    convolve(b + 1, (0,))
                for c in range(CHUNKS):
                    last = pe.matmul(ps[:, 3 + c // 8, (c % 8) * 64:(c % 8 + 1) * 64], kdiag[:, c, :],
                                     kq_n[:, :, c * CHUNK:(c + 1) * CHUNK], start=True, stop=True)
                last.then_inc(S["prod_ready"], 1)
                if another:
                    convolve(b + 1, (2,))

            convolve(0, (1, 0, 2))
            with pe.Fori(0, BATCH - 1) as b:
                products_of(b, True)
            products_of(BATCH - 1, False)

        @block.scalar
        def _(act):
            def functions_of(b, u):
                act.wait_ge(S["qkv_read"], b + 1)
                for n, s in enumerate((1, 0, 2)):
                    act.wait_ge(S["conv_ready"], b * 3 + n + 1)
                    act.activation(qkv_s[:, u, s, :], ps[:, s, :], ACT.Silu).then_inc(S["silu_done"], 1)
                act.drain()
                for n, s in enumerate((1, 0)):
                    act.activation(sq[:, n, :], qkv_s[:, u, s, :], ACT.Square).then_inc(S["square_done"], 1)
                act.wait_ge(S["ss_ready"], b + 1)
                act.activation(nrm[:, :], ps[:, 7, 0:32], ACT.Sqrt).then_inc(S["norm_ready"], 1)
                act.wait_ge(S["ctrl_ready"], b + 1)
                act.activation(store.og[:, bass.ds(b * SEQ, SEQ)], ps[:, 4, :], ACT.Sigmoid, bias=bog[:, 0:1])
                act.activation(gates8[:, :], ps[0:8, 3, :], ACT.Sigmoid, bias=b8[:, 0:1]).then_inc(S["gates_done"], 1)

            act.wait_ge(S["loaded"], ALL)
            act.sem_inc(S["silu_done"], 3)
            with act.Fori(0, BATCH // 2) as i:
                for u in range(2):
                    functions_of(i * 2 + u, u)

        @block.vector
        def _(dve):
            dve.wait_ge(S["loaded"], ALL)
            dve.wait_ge(S["const_ready"], 1)
            for s in range(3):
                last = dve.tensor_tensor(w_taps[:, s, :, :], w_taps[:, s, :, :],
                                         w_in[:, s, :].rearrange("p (o f) -> p o f", o=1).to_broadcast([P, 4, D]), ALU.mult)
            last.then_inc(S["taps_ready"], 1)
            dve.sem_inc(S["qkv_read"], 2)
            dve.sem_inc(S["spread_taken"], 1)
            dve.sem_inc(S["all_read"], 1)

            def operands_of(b, u):
                dve.wait_ge(S["norm_ready"], b + 1)
                dve.tensor_scalar(nrm[:, :], nrm[:, :], 1e-6, None, ALU.max)
                dve.drain()
                dve.reciprocal(nrm[:, :], nrm[:, :]).then_inc(S["recip_ready"], 1)
                dve.wait_ge(S["r_turned"], b + 1)
                dve.tensor_copy(rT[:, :], ps[0:32, 7, P:2 * P]).then_inc(S["r_copied"], 1)
                dve.wait_ge(S["expanded"], b + 1)
                dve.tensor_tensor(kq_n[:, 0, :], qkv_s[:, u, 1, :], ps[:, 5, :], ALU.mult)
                dve.tensor_tensor(kq_n[:, 1, :], qkv_s[:, u, 0, :], ps[:, 6, :], ALU.mult)
                dve.drain()
                for h in range(RHEADS):
                    rows = slice(32 * h, 32 * h + 32)
                    last = dve.tensor_copy(kdiag[rows, :, 32 * h:32 * h + 32], chunks(kq_n[rows, 0, :]))
                last.then_inc(S["kdiag_ready"], 1)
                dve.transpose(ktok[:, :], kq_n[:, 0, :])
                dve.wait_ge(S["spread_ready"], b + 1)
                dve.tensor_scalar(a_all[:, :], ps[:, 5, :], 0.01, None, ALU.add)
                dve.tensor_copy(b_all[:, :], ps[:, 6, :]).then_inc(S["spread_taken"], 1)
                dve.drain()
                dve.tensor_tensor(store.vb[:, :, bass.ds(b, 1), :], chunks(qkv_s[:, u, 2, :]), chunks(b_all[:, :]), ALU.mult)\
                   .then_inc(S["qkv_read"], 1)
                dve.tensor_tensor(a_in[:, :], a_all[:, :], chunk_c[:, NOT_START, :], ALU.mult)
                dve.tensor_tensor(a_start[:, :], a_all[:, :], chunk_c[:, START, :], ALU.mult)
                dve.drain()
                dve.tensor_tensor_scan(dec[:, :], a_in[:, :], chunk_c[:, SAME, :], 0.0, ALU.mult, ALU.add)
                dve.tensor_tensor_scan(gam[:, :], a_in[:, :], a_start[:, :], 0.0, ALU.mult, ALU.add)
                dve.drain()
                dve.tensor_tensor(dec_b[:, :], dec[:, :], b_all[:, :], ALU.mult)
                dve.tensor_tensor(gam_b[:, :], gam[:, :], b_all[:, :], ALU.mult)
                dve.drain()
                dve.tensor_tensor(dec_b[:, :], dec_b[:, :], chunk_c[:, BEFORE, :], ALU.mult)
                dve.tensor_tensor(store.kq[:, :, bass.ds(b, 1), 0:32], chunks(kq_n[:, 0, :]), chunks(gam_b[:, :]), ALU.mult)
                dve.tensor_tensor(store.kq[:, :, bass.ds(b, 1), 32:64], chunks(kq_n[:, 1, :]), chunks(gam[:, :]), ALU.mult)
                dve.tensor_copy(store.last[:, :, bass.ds(b, 1)], chunks(gam[:, :])[:, :, CHUNK - 1:CHUNK])
                dve.drain()
                dve.tensor_tensor(store.ak[:, :, bass.ds(b, 1), 32:64], chunks(ktok[:, :]),
                                  chunks(dec[:, :])[:, :, CHUNK - 1:CHUNK].to_broadcast([P, CHUNKS, CHUNK]), ALU.mult)
                dve.wait_ge(S["prod_ready"], b + 1)
                dve.wait_ge(S["seq_done"], b + 1)
                prod = ps[:, 3:5, :].rearrange("p n (c k) -> p (n c) k", k=64)
                dve.tensor_tensor(l_sb[:, :, :], prod[:, :, 0:32], chunks(dec_b[:, :]), ALU.mult).then_inc(S["l_ready"], 1)
                dve.tensor_tensor(store.ak[:, :, bass.ds(b, 1), 0:32], prod[:, :, 32:64], chunks(dec[:, :]), ALU.mult)\
                   .then_inc(S["all_read"], 1)

            with dve.Fori(0, BATCH // 2) as i:
                for u in range(2):
                    operands_of(i * 2 + u, u)


def invert_chunks(core, name, l_dram, t_dram):
    nc = core.nc
    SYS, MINE = 4, 3
    loaded, started, done, saved = (core.sem(f"{name}_{n}") for n in ("loaded", "started", "done", "saved"))
    with ExitStack() as ctx:
        sb = lambda n, s, dt=F32: core.sb(name + "_" + n, s, dt, ctx)
        l_sb, t_sb = sb("l", [P, SYS, CHUNK, CHUNK]), sb("t", [P, SYS, CHUNK, CHUNK])
        outer_p = sb("outer_p", [P, 1, CHUNK * CHUNK // 4 + CHUNK])
        outer = core.ps(name + "_outer", [P, MINE * 512], ctx=ctx)
        block = ctx.enter_context(nc.Block())

        def rows_off(eng, s0, n, buf):
            for j in range(CHUNK - 1):
                shape = [P, n, j + 1, CHUNK - 1 - j]
                size = shape[2] * shape[3]
                out = buf(n, size).rearrange("p s (l i) -> p s l i", i=shape[3])
                eng.tensor_tensor(out, l_sb[:, s0:s0 + n, j:j + 1, j + 1:CHUNK].to_broadcast(shape),
                                  t_sb[:, s0:s0 + n, 0:j + 1, j:j + 1].to_broadcast(shape), ALU.mult)
                eng.drain()
                rest = t_sb[:, s0:s0 + n, 0:j + 1, j + 1:CHUNK]
                eng.tensor_tensor(rest, rest, out, ALU.subtract)
                eng.drain()
            eng.sem_inc(done, 1)

        @block.sync
        def _(sp):
            sp.dma_start(l_sb[:, :, :, :], l_dram.rearrange("b h (g c) s t -> (b h g) c s t", c=SYS)).then_inc(loaded, 16)
            sp.wait_ge(done, 2)
            sp.dma_start(t_dram.rearrange("b h (g c) s t -> (b h g) c s t", c=SYS), t_sb[:, :, :, :]).then_inc(saved, 16)
            sp.wait_ge(saved, 16)

        @block.gpsimd
        def _(pool):
            pool.memset(t_sb[:, :, :, :], 0.0)
            pool.drain()
            pool.memset(t_sb[:, :, :, :].rearrange("p c s t -> p c (s t)")[:, :, 0:CHUNK * CHUNK:CHUNK + 1], 1.0)
            pool.drain()
            pool.sem_inc(started, 1)
            pool.wait_ge(loaded, 16)
            rows_off(pool, MINE, 1, lambda n, size: outer_p[:, :, 0:size])

        @block.vector
        def _(dve):
            dve.wait_ge(started, 1)
            dve.wait_ge(loaded, 16)
            rows_off(dve, 0, MINE, lambda n, size: outer[:, :].rearrange("p (s k) -> p s k", s=MINE)[:, :, 0:size])


def chunk_recurrence(core, name, store, t_dram, o_all):
    nc = core.nc
    HB = BATCH // 2
    S = {n: core.sem(f"{name}_{n}") for n in (
        "loaded", "const_ready", "operands", "step_done", "s_ready", "so_ready", "x_ready", "o1_done", "u_ready", "u_diag_a", "u_diag_v",
        "c_ready", "s_turned", "s_diag_a", "s_diag_v")}
    with ExitStack() as ctx:
        sb = lambda n, s, dt=F32: core.sb(name + "_" + n, s, dt, ctx)
        t_all = sb("t_all", [P, BATCH, CHUNKS, CHUNK])
        kq, ak = sb("kq", [P, 2, BATCH, 64]), sb("ak", [P, 2, BATCH, 64])
        tdiag = sb("tdiag", [P, 2, BATCH, P])
        state, turned = sb("state", [P, BATCH, RD]), sb("turned", [P, BATCH, RD])
        sdiag, udiag = sb("sdiag", [P, BATCH, P]), sb("udiag", [P, BATCH, P])
        xT, xtok, o1 = sb("xT", [P, BATCH, RD]), sb("xtok", [P, BATCH, RD]), sb("o1", [P, BATCH, RD])
        ps_a = core.ps(name + "_ps_a", [P, 2, 512], ctx=ctx)
        ps_u = core.ps(name + "_ps_u", [P, 2, 512], ctx=ctx)
        ps_c = core.ps(name + "_ps_c", [P, 2, 512], ctx=ctx)
        block = ctx.enter_context(nc.Block())
        of = lambda ps, g, w: ps[:, g, 0:HB * w].rearrange("p (b k) -> p b k", b=HB)

        def load(eng, heads_of):
            with eng.Fori(0, BATCH) as b:
                for h in heads_of:
                    dst = t_all[32 * h:32 * h + 32, bass.ds(b, 1), :, :].rearrange("s o c t -> s (o c) t")
                    eng.dma_start(dst, t_dram[bass.ds(b, 1), h].rearrange("o c s t -> s (o c) t")).then_inc(S["loaded"], 16)

        @block.sync
        def _(sp):
            load(sp, (0, 1))

        @block.gpsimd
        def _(pool):
            pool.memset(sdiag[:, :, :], 0.0)
            pool.memset(udiag[:, :, :], 0.0)
            pool.memset(tdiag[:, :, :, :], 0.0)
            pool.memset(state[:, :, :], 0.0)
            pool.drain()
            pool.sem_inc(S["const_ready"], 1)

        @block.tensor
        def _(pe):
            pe.wait_ge(S["const_ready"], 1)
            with pe.Fori(0, CHUNKS // 2) as r:
                for k in range(2):
                    pe.wait_ge(S["operands"], r * 2 + k + 1)
                    for g in range(2):
                        n = 2 * k + g
                        pe.wait_ge(S["s_diag_a"], r * 4 + n + 1)
                        pe.wait_ge(S["s_diag_v"], r * 4 + n + 1)
                        for b in range(HB * g, HB * g + HB):
                            last = pe.matmul(of(ps_a, g, 64)[:, b - HB * g, :], sdiag[:, b, :], kq[:, k, b, :],
                                             start=True, stop=True)
                        last.then_inc(S["so_ready"], 1)
                    for g in range(2):
                        n = 2 * k + g
                        pe.wait_ge(S["x_ready"], r * 4 + n + 1)
                        for b in range(HB * g, HB * g + HB):
                            last = pe.matmul(of(ps_u, g, RD)[:, b - HB * g, :], tdiag[:, k, b, :], xtok[:, b, :],
                                             start=True, stop=True)
                        last.then_inc(S["u_ready"], 1)
                    for g in range(2):
                        n = 2 * k + g
                        pe.wait_ge(S["u_diag_a"], r * 4 + n + 1)
                        pe.wait_ge(S["u_diag_v"], r * 4 + n + 1)
                        for b in range(HB * g, HB * g + HB):
                            last = pe.matmul(of(ps_c, g, 64)[:, b - HB * g, :], udiag[:, b, :], ak[:, k, b, :],
                                             start=True, stop=True)
                        last.then_inc(S["c_ready"], 1)

        @block.scalar
        def _(act):
            load(act, (2, 3))
            act.wait_ge(S["const_ready"], 1)
            act.wait_ge(S["loaded"], 64 * BATCH)
            act.sem_inc(S["s_diag_a"], 2)

            def copy_operands(c, k):
                act.wait_ge(S["step_done"], c + 1)
                act.activation(kq[:, k, :, :], store.kq[:, bass.ds(c, 1), :, :].rearrange("p o b k -> p (o b) k"), ACT.Copy)
                act.activation(ak[:, k, :, :], store.ak[:, bass.ds(c, 1), :, :].rearrange("p o b k -> p (o b) k"), ACT.Copy)

            def spread_operands(c, k):
                for h in range(RHEADS):
                    rows = slice(32 * h, 32 * h + 32)
                    act.activation(tdiag[rows, k, :, 32 * h:32 * h + 32],
                                   t_all[rows, :, bass.ds(c, 1), :].rearrange("p b o k -> p b (o k)"), ACT.Copy)
                act.drain()
                act.sem_inc(S["operands"], 1)

            def step(c, k, another):
                for g in range(2):
                    act.wait_ge(S["x_ready"], c * 2 + g + 1)
                    act.activation(o1[:, HB * g:HB * g + HB, :], of(ps_a, g, 64)[:, :, 32:64], ACT.Copy)\
                       .then_inc(S["o1_done"], 1)
                if another:
                    copy_operands(c + 1, 1 - k)
                for g in range(2):
                    act.wait_ge(S["u_ready"], c * 2 + g + 1)
                    for h in (2, 3):
                        rows = slice(32 * h, 32 * h + 32)
                        last = act.activation(udiag[rows, HB * g:HB * g + HB, 32 * h:32 * h + 32],
                                              of(ps_u, g, RD)[rows, :, :], ACT.Copy)
                    last.then_inc(S["u_diag_a"], 1)
                if another:
                    spread_operands(c + 1, 1 - k)
                for g in range(2):
                    act.wait_ge(S["s_turned"], c * 2 + g + 1)
                    for h in (2, 3):
                        rows = slice(32 * h, 32 * h + 32)
                        last = act.activation(sdiag[rows, HB * g:HB * g + HB, 32 * h:32 * h + 32],
                                              turned[rows, HB * g:HB * g + HB, :], ACT.Copy)
                    last.then_inc(S["s_diag_a"], 1)

            copy_operands(0, 0)
            spread_operands(0, 0)
            with act.Fori(0, CHUNKS // 2 - 1) as r:
                step(r * 2, 0, True)
                step(r * 2 + 1, 1, True)
            step(CHUNKS - 2, 0, True)
            step(CHUNKS - 1, 1, False)

        @block.vector
        def _(dve):
            dve.wait_ge(S["const_ready"], 1)
            dve.sem_inc(S["step_done"], 2)
            dve.sem_inc(S["s_diag_v"], 2)
            with dve.Fori(0, CHUNKS // 2) as r:
                for k in range(2):
                    c = r * 2 + k
                    for g in range(2):
                        n = 2 * k + g
                        mine = slice(HB * g, HB * g + HB)
                        dve.wait_ge(S["so_ready"], r * 4 + n + 1)
                        dve.tensor_tensor(xT[:, mine, :],
                                          store.vb[:, bass.ds(c, 1), mine, :].rearrange("p o b k -> p (o b) k"),
                                          of(ps_a, g, 64)[:, :, 0:32], ALU.subtract)
                        dve.drain()
                        dve.transpose(xtok[:, mine, :].rearrange("p b k -> p (b k)"),
                                      xT[:, mine, :].rearrange("p b k -> p (b k)")).then_inc(S["x_ready"], 1)
                        dve.tensor_tensor(state[:, mine, :], state[:, mine, :],
                                          store.last[:, bass.ds(c, 1), mine].rearrange("p o (b u) -> p (o b) u", u=1)
                                          .to_broadcast([P, HB, RD]), ALU.mult)
                    for g in range(2):
                        n = 2 * k + g
                        dve.wait_ge(S["u_ready"], r * 4 + n + 1)
                        for h in (0, 1):
                            rows = slice(32 * h, 32 * h + 32)
                            last = dve.tensor_copy(udiag[rows, HB * g:HB * g + HB, 32 * h:32 * h + 32],
                                                   of(ps_u, g, RD)[rows, :, :])
                        last.then_inc(S["u_diag_v"], 1)
                    for g in range(2):
                        n = 2 * k + g
                        mine = slice(HB * g, HB * g + HB)
                        dve.wait_ge(S["c_ready"], r * 4 + n + 1)
                        dve.tensor_tensor(state[:, mine, :], state[:, mine, :], of(ps_c, g, 64)[:, :, 32:64], ALU.add)
                        dve.drain()
                        dve.transpose(turned[:, mine, :].rearrange("p b k -> p (b k)"),
                                      state[:, mine, :].rearrange("p b k -> p (b k)")).then_inc(S["s_turned"], 1)
                        dve.wait_ge(S["o1_done"], r * 4 + n + 1)
                        dve.tensor_tensor(o_all[:, bass.ds(c, 1), mine, :].rearrange("p o b k -> p (o b) k"), o1[:, mine, :],
                                          of(ps_c, g, 64)[:, :, 0:32], ALU.add)
                        dve.drain()
                        for h in (0, 1):
                            rows = slice(32 * h, 32 * h + 32)
                            last = dve.tensor_copy(sdiag[rows, mine, 32 * h:32 * h + 32], turned[rows, mine, :])
                        last.then_inc(S["s_diag_v"], 1)
                    dve.sem_inc(S["step_done"], 1)


def gated_output(core, name, A, o_all, og):
    nc = core.nc
    S = {n: core.sem(f"{name}_{n}") for n in (
        "loaded", "ramp_exp", "squared", "ss_ready", "root_ready", "recip_ready", "r_turned", "r_copied", "expanded",
        "o_normed", "y_ready", "gated", "turned")}
    with ExitStack() as ctx:
        sb = lambda n, s, dt=F32: core.sb(name + "_" + n, s, dt, ctx)
        w_out, b_out, ramp = sb("w_out", [P, D]), sb("b_out", [P, 1]), sb("ramp", [P, 1])
        ones4, pick = sb("ones4", [P, RHEADS]), sb("pick", [16, TPB, P])
        epsb = sb("eps", [P, 1])
        o_s, sq, on, y = (sb(n, [P, SEQ]) for n in ("o_s", "sq", "on", "y"))
        r, rT = sb("r", [P, 16]), sb("rT", [16, P])
        ps = core.ps(name + "_ps", [P, 4, 512], ctx=ctx)
        block = ctx.enter_context(nc.Block())

        @block.sync
        def _(sp):
            for dst, src in ((w_out[:, :], A["L2_w_out"]), (b_out[:, :], A["L2_b_out"]), (ramp[:, :], A["L2_ramp"]),
                             (ones4[:, :], A["c_ones4"]), (pick[:, :, :], A["c_pick_o"])):
                sp.dma_start(dst, src).then_inc(S["loaded"], 16)

        @block.tensor
        def _(pe):
            def squares(b):
                pe.wait_ge(S["squared"], b + 1)
                for t in range(TPB):
                    last = pe.matmul(ps[:, 0, t * RHEADS:(t + 1) * RHEADS], sq[:, t * P:(t + 1) * P], ones4[:, :],
                                     start=True, stop=True)
                last.then_inc(S["ss_ready"], 1)

            def turn_norms(b):
                pe.wait_ge(S["recip_ready"], b + 1)
                pe.transpose(ps[0:16, 0, P:2 * P], r[:, :], core.ident[:, :]).then_inc(S["r_turned"], 1)

            def expand_norms(b):
                pe.wait_ge(S["r_copied"], b + 1)
                for t in range(TPB):
                    last = pe.matmul(ps[:, 1, t * P:(t + 1) * P], pick[:, t, :], rT[:, :], start=True, stop=True)
                last.then_inc(S["expanded"], 1)

            def sequence(b, another):
                pe.wait_ge(S["o_normed"], b + 2)
                pe.matmul(ps[:, 2, :], w_out[:, :], on[:, :], start=True, stop=True).then_inc(S["y_ready"], 1)
                if another:
                    squares(b + 1)
                    turn_norms(b + 1)
                pe.wait_ge(S["gated"], b + 1)
                for t in range(TPB):
                    last = pe.transpose(ps[:, 3, t * P:(t + 1) * P], y[:, t * P:(t + 1) * P], core.ident[:, :])
                last.then_inc(S["turned"], 1)
                if another:
                    expand_norms(b + 1)

            pe.wait_ge(S["loaded"], 80)
            squares(0)
            turn_norms(0)
            expand_norms(0)
            with pe.Fori(0, BATCH - 1) as b:
                sequence(b, True)
            sequence(BATCH - 1, False)

        @block.scalar
        def _(act):
            def norms(b):
                src = o_all[:, :, bass.ds(b, 1), :].rearrange("p c o t -> p c (o t)")
                act.wait_ge(S["o_normed"], b + 1)
                act.activation(o_s[:, :].rearrange("p (c t) -> p c t", t=CHUNK), src, ACT.Copy)
                act.activation(sq[:, :].rearrange("p (c t) -> p c t", t=CHUNK), src, ACT.Square).then_inc(S["squared"], 1)
                act.wait_ge(S["ss_ready"], b + 1)
                act.activation(r[:, :], ps[:, 0, 0:16], ACT.Sqrt, scale=1.0 / RD, bias=epsb[:, 0:1])\
                   .then_inc(S["root_ready"], 1)

            act.wait_ge(S["loaded"], 80)
            act.activation(ramp[:, :], ramp[:, :], ACT.Sigmoid).then_inc(S["ramp_exp"], 1)
            with act.Fori(0, BATCH) as b:
                norms(b)

        @block.vector
        def _(dve):
            def norms(b):
                dve.wait_ge(S["root_ready"], b + 1)
                dve.reciprocal(r[:, :], r[:, :]).then_inc(S["recip_ready"], 1)
                dve.wait_ge(S["r_turned"], b + 1)
                dve.tensor_copy(rT[:, :], ps[0:16, 0, P:2 * P]).then_inc(S["r_copied"], 1)

            def sequence(b, another):
                dve.wait_ge(S["expanded"], b + 1)
                dve.tensor_tensor(on[:, :], o_s[:, :], ps[:, 1, :], ALU.mult).then_inc(S["o_normed"], 1)
                if another:
                    norms(b + 1)
                dve.wait_ge(S["y_ready"], b + 1)
                dve.tensor_scalar(y[:, :], ps[:, 2, :], b_out[:, 0:1], ramp[:, 0:1], ALU.add, ALU.mult)
                dve.drain()
                dve.tensor_tensor(y[:, :], y[:, :], og[:, bass.ds(b * SEQ, SEQ)], ALU.mult).then_inc(S["gated"], 1)
                dve.wait_ge(S["turned"], b + 1)
                xr = core.x[:, bass.ds(b * TPB, TPB), :]
                dve.tensor_tensor(xr, xr, ps[:, 3, :].rearrange("p (t d) -> p t d", t=TPB), ALU.add)

            dve.memset(epsb[:, :], 1e-6)
            dve.wait_ge(S["ramp_exp"], 1)
            dve.drain()
            dve.sem_inc(S["o_normed"], 1)
            norms(0)
            with dve.Fori(0, BATCH - 1) as b:
                sequence(b, True)
            sequence(BATCH - 1, False)


class ChunkStore:

    def __init__(self, core, ctx):
        self.kq = core.sb("l2a_kq", [P, CHUNKS, BATCH, 64], ctx=ctx)
        self.ak = core.sb("l2a_ak", [P, CHUNKS, BATCH, 64], ctx=ctx)
        self.vb = core.sb("l2a_vb", [P, CHUNKS, BATCH, RD], ctx=ctx)
        self.last = core.sb("l2a_last", [P, CHUNKS, BATCH], ctx=ctx)
        self.l_dram = core.dram("l2a_l_dram", [BATCH, RHEADS, CHUNKS, CHUNK, CHUNK])


def layer2_attention(core, A):
    with ExitStack() as outer:
        og = core.sb("l2a_og", [P, N], ctx=outer)
        o_all = core.xT[:, :].rearrange("p (c b t) -> p c b t", c=CHUNKS, b=BATCH)
        t_dram = core.dram("l2a_t_dram", [BATCH, RHEADS, CHUNKS, CHUNK, CHUNK])
        with ExitStack() as ctx:
            store = ChunkStore(core, ctx)
            store.og = og
            chunk_products(core, "l2p", A, store)
            invert_chunks(core, "l2i", store.l_dram, t_dram)
            chunk_recurrence(core, "l2r", store, t_dram, o_all)
        gated_output(core, "l2g", A, o_all, og)


def place_tokens(core, name, wts, E, span, slots, weights, skip, blk_row=None):
    nc = core.nc
    COLS = TILES * E
    NB = (TABLE_ROWS - 1) // span
    made, masked, summed = core.sem(name + "_made"), core.sem(name + "_masked"), core.sem(name + "_summed")
    with ExitStack() as ctx:
        sb = lambda n, s, dt=F32: core.sb(name + "_" + n, s, dt, ctx)
        before, ones = sb("before", [P, P]), sb("ones", [P, P])
        mask, at, hit = (sb(n, [P, TILES, E]) for n in ("mask", "at", "hit"))
        incl = sb("incl", [P, E, TILES])
        zeros, size, first = sb("zeros", [P, 32]), sb("size", [P, E]), sb("first", [P, E])
        a, b = sb("a", [P, TILES]), sb("b", [P, TILES])
        iota, begun = sb("iota", [P, NB]), sb("begun", [P, NB, E])
        ps_b = core.ps(name + "_ps_b", [P, BLK], ctx=ctx)
        ps_t = core.ps(name + "_ps_t", [P, BLK], ctx=ctx)
        flat = lambda v: v[:, :, :].rearrange("p t e -> p (t e)")
        count = ps_t[:, 0:COLS].rearrange("p (t e) -> p t e", e=E)
        each = lambda v, m: v[:, :].rearrange("p (t o) -> p t o", o=1).to_broadcast([P, m, E])
        by_e = lambda v, m: v[:, :].rearrange("p (o e) -> p o e", o=1).to_broadcast([P, m, E])
        block = ctx.enter_context(nc.Block())

        @block.gpsimd
        def _(pool):
            pool.memset(ones[:, :], 1.0)
            pool.drain()
            pool.affine_select(out=before[:, :], in_=ones[:, :], compare_op=ALU.is_gt, fill=0.0,
                               base=0, pattern=[[1, P]], channel_multiplier=-1)
            pool.iota(iota[:, :], pattern=[[span, NB]], base=0, channel_multiplier=0,
                      allow_small_or_imprecise_dtypes=True)
            pool.iota(a[:, 0:1], pattern=[[0, 1]], base=-P, channel_multiplier=1,
                      allow_small_or_imprecise_dtypes=True)
            pool.drain()
            pool.sem_inc(made, 1)

        @block.tensor
        def _(pe):
            pe.wait_ge(made, 1)
            pe.wait_ge(masked, 1)
            pe.matmul(ps_b[:, 0:COLS], before[:, :], flat(mask), start=True, stop=True)
            pe.matmul(ps_t[:, 0:COLS], ones[:, :], flat(mask), start=True, stop=True).then_inc(summed, 1)

        @block.vector
        def _(dve):
            dve.tensor_scalar(mask[:, :, :], wts[:, :, 0:E], 0.0, None, ALU.is_gt).then_inc(masked, 1)
            if blk_row is not None:
                dve.memset(wts[:, :, E:E + 1], 1.0)
            dve.memset(zeros[:, :], 0.0)
            dve.wait_ge(summed, 1)
            dve.drain()
            for e in range(E):
                dve.tensor_tensor_scan(incl[:, e, :], count[:, :, e], zeros[:, 0:TILES], 0.0, ALU.add, ALU.add)
            dve.drain()
            dve.tensor_scalar(size[:, :], incl[:, :, TILES - 1], span / 2 - 0.5, 1.0 / span, ALU.add, ALU.mult)
            dve.tensor_tensor(at[:, :, :], ps_b[:, 0:COLS].rearrange("p (t e) -> p t e", e=E),
                              incl[:, :, :].rearrange("p e t -> p t e"), ALU.add)
            dve.drain()
            dve.tensor_tensor(at[:, :, :], at[:, :, :], count, ALU.subtract)
            if blk_row is None:
                for e in range(E):
                    last = dve.memset(first[:, e:e + 1], float(e * span))
            else:
                dve.tensor_scalar(size[:, :], size[:, :], 8388608.0, None, ALU.add)
                dve.drain()
                dve.tensor_scalar(size[:, :], size[:, :], -8388608.0, float(span), ALU.add, ALU.mult)
                dve.drain()
                dve.tensor_tensor_scan(first[:, :], size[:, :], zeros[:, 0:E], 0.0, ALU.add, ALU.add)
                dve.drain()
                dve.tensor_tensor(first[:, :], first[:, :], size[:, :], ALU.subtract)
                dve.drain()
                wide = iota[:, :].rearrange("p (n o) -> p n o", o=1).to_broadcast([P, NB, E])
                dve.wait_ge(made, 1)
                dve.tensor_tensor(begun[:, :, :], by_e(first, NB), wide, ALU.is_le)
                dve.tensor_copy(size[:, 0:1], a[:, 0:1])
                dve.drain()
                dve.tensor_reduce(iota[:, :], begun[:, :, :], AX.X, ALU.add)
                dve.drain()
                dve.tensor_scalar(blk_row[:, :], iota[:, :], float(P), size[:, 0:1], ALU.mult, ALU.add)
            dve.drain()
            dve.scalar_tensor_tensor(out=at[:, :, :], in0=at[:, :, :], scalar=1.0, in1=by_e(first, TILES),
                                     op0=ALU.add, op1=ALU.add)
            dve.drain()
            dve.tensor_tensor(at[:, :, :], at[:, :, :], mask[:, :, :], ALU.mult)
            dve.drain()
            dve.tensor_reduce(a[:, :], at[:, :, :], AX.X, ALU.max)
            dve.tensor_reduce(b[:, :], at[:, :, :], AX.X, ALU.add)
            dve.drain()
            dve.tensor_tensor(b[:, :], b[:, :], a[:, :], ALU.subtract)
            dve.tensor_tensor(hit[:, :, :], at[:, :, :], each(a, TILES), ALU.is_equal)
            dve.drain()
            dve.tensor_tensor(hit[:, :, :], hit[:, :, :], wts[:, :, 0:E], ALU.mult)
            for k, v in enumerate((a, b)):
                dve.tensor_copy(slots[:, k, :], v[:, :])
                dve.tensor_scalar(incl[:, k, :], v[:, :], 0.0, 1.0e6, ALU.is_equal, ALU.mult)
            dve.drain()
            for k, v in enumerate((a, b)):
                dve.tensor_tensor(skip[:, k, :], incl[:, k, :], v[:, :], ALU.add)
            dve.tensor_reduce(weights[:, 0, :], hit[:, :, :], AX.X, ALU.add)
            dve.tensor_reduce(weights[:, 1, :], wts[:, :, 0:E], AX.X, ALU.add)
            dve.drain()
            dve.tensor_tensor(weights[:, 1, :], weights[:, 1, :], weights[:, 0, :], ALU.subtract)


def scatter_tokens(core, pool, xn, skip, scattered):
    pool.wait_ge(core.table_filled, 48)
    for k in range(2):
        for t in range(TILES):
            pool.indirect_dma_start(out=core.table_x[:, :], in_=xn[:, t, :], in_offset=None,
                                    out_offset=bass.IndirectOffsetOnAxis(ap=skip[:, k, t:t + 1], axis=0),
                                    bounds_check=TABLE_ROWS - 1, oob_is_err=False).then_inc(scattered, 16)
    pool.wait_ge(scattered, 2 * TILES * 16)


def scatter_block(core, name, xn, skip):
    scattered = core.sem(name + "_scattered")
    with core.nc.Block() as block:

        @block.gpsimd
        def _(pool):
            scatter_tokens(core, pool, xn, skip, scattered)


def shared_expert(core, name, rows, w1_in, b1_in, w2_in, b2_in, xn, skip):
    nc = core.nc
    E, C = b2_in.shape[0], 2
    loaded, gu_ready, gelu_done = core.sem(name + "_loaded"), core.sem(name + "_gu_ready"), core.sem(name + "_gelu_done")
    act_done, y_ready, added = core.sem(name + "_act_done"), core.sem(name + "_y_ready"), core.sem(name + "_added")
    scattered = core.sem(name + "_scattered")
    with ExitStack() as ctx:
        sb = lambda n, s, dt=F32: core.sb(name + "_" + n, s, dt, ctx)
        w1, w2, b1, b2 = sb("w1", [P, 2 * C, P]), sb("w2", [P, C, D]), sb("b1", [P, 2 * C]), sb("b2", [E, D])
        gelu, act_out = sb("gelu", [P, 2, BLK]), sb("act", [P, 2, C, BLK])
        ps_g = core.ps(name + "_ps_g", [P, 2, BLK], ctx=ctx)
        ps_u = core.ps(name + "_ps_u", [P, 2, BLK], ctx=ctx)
        ps_y = core.ps(name + "_ps_y", [P, 2, TPB, D], ctx=ctx)
        block = ctx.enter_context(nc.Block())

        @block.sync
        def _(sp):
            sp.dma_start(w1[:, :, :], w1_in[0]).then_inc(loaded, 16)
            sp.dma_start(w2[:, :, :], w2_in[0]).then_inc(loaded, 16)
            sp.dma_start(b1[:, :], b1_in[0]).then_inc(loaded, 16)
            sp.dma_start(b2[:, :], b2_in).then_inc(loaded, 16)

        @block.gpsimd
        def _(pool):
            scatter_tokens(core, pool, xn, skip, scattered)

        @block.tensor
        def _(pe):
            pe.wait_ge(loaded, 64)

            def down(b):
                pe.wait_ge(act_done, C * (b + 1))
                if b >= 2:
                    pe.wait_ge(added, b - 1)
                for t in range(TPB):
                    for c in range(C):
                        pe.matmul(ps_y[:, b % 2, t, :], act_out[:, b % 2, c, t * P:(t + 1) * P], w2[:, c, :],
                                  start=(c == 0), stop=False)
                    last = pe.matmul(ps_y[:, b % 2, t, :], rows[0:E, b * BLK + t * P:b * BLK + (t + 1) * P],
                                     b2[:, :], start=False, stop=True)
                last.then_inc(y_ready, 1)

            for b in range(NBLK):
                for c in range(C):
                    s = C * b + c
                    if s >= 2:
                        pe.wait_ge(act_done, s - 1)
                    xb = core.xT[:, b * BLK:(b + 1) * BLK]
                    pe.matmul(ps_g[:, s % 2, :], w1[:, c, :], xb, start=True, stop=True)
                    pe.matmul(ps_u[:, s % 2, :], w1[:, C + c, :], xb, start=True, stop=True).then_inc(gu_ready, 1)
                if b >= 1:
                    down(b - 1)
            down(NBLK - 1)

        @block.scalar
        def _(act):
            act.wait_ge(loaded, 64)
            for s in range(C * NBLK):
                act.wait_ge(gu_ready, s + 1)
                if s >= 2:
                    act.wait_ge(act_done, s - 1)
                act.activation(gelu[:, s % 2, :], ps_g[:, s % 2, :], ACT.Gelu, bias=b1[:, s % C:s % C + 1])\
                   .then_inc(gelu_done, 1)

        @block.vector
        def _(dve):
            dve.wait_ge(loaded, 64)

            def add(b):
                dve.wait_ge(y_ready, b + 1)
                xb = core.x[:, b * TPB:(b + 1) * TPB, :]
                dve.tensor_tensor(xb, xb, ps_y[:, b % 2, :, :], ALU.add).then_inc(added, 1)

            for b in range(NBLK):
                for c in range(C):
                    s = C * b + c
                    dve.wait_ge(gelu_done, s + 1)
                    if b >= 2:
                        dve.wait_ge(y_ready, b - 1)
                    dve.scalar_tensor_tensor(out=act_out[:, b % 2, c, :], in0=ps_u[:, s % 2, :],
                                             scalar=b1[:, C + c:C + c + 1], in1=gelu[:, s % 2, :],
                                             op0=ALU.add, op1=ALU.mult).then_inc(act_done, 1)
                if b >= 1:
                    add(b - 1)
            add(NBLK - 1)


def slot_ffn(core, name, rounds, sizes, C, func, w_in, w_cols, blk_row=None):
    nc = core.nc
    gathered = blk_row is not None
    U = len(sizes)
    BPW = 1 if gathered else 2
    NW = U // BPW
    MAXT, FROM = max(sizes), [sum(sizes[:k]) * P for k in range(U)]
    ROUND_ROWS = sum(sizes) * P
    x_loaded = [core.sem(f"{name}_x_loaded{k}") for k in range(U)]
    w_loaded = [core.sem(f"{name}_w_loaded{m}") for m in range(NW)]
    y_stored = [core.sem(f"{name}_y_stored{k}") for k in range(U)]
    turned, copied = core.sem(name + "_turned"), core.sem(name + "_copied")
    gu_ready, gate_done, act_done = (core.sem(f"{name}_{n}") for n in ("gu_ready", "gate_done", "act_done"))
    y_ready, y_copied = core.sem(name + "_y_ready"), core.sem(name + "_y_copied")
    with ExitStack() as ctx:
        sb = lambda n, s, dt=F32: core.sb(name + "_" + n, s, dt, ctx)
        w = sb("w", [P, NW, w_cols])
        idx = sb("idx", [P, NW], U32) if gathered else None
        xs, xsT = sb("xs", [P, U, MAXT, D]), sb("xsT", [P, U, MAXT * P])
        gate, act_out = sb("gate", [P, 2, MAXT * P]), sb("act", [P, U, C, MAXT * P])
        y_sb = sb("y", [P, U, MAXT, D])
        ps_t, ps_g, ps_u, ps_y = (core.ps(f"{name}_ps_{n}", [P, 2, BLK], ctx=ctx) for n in ("t", "g", "u", "y"))
        block = ctx.enter_context(nc.Block())
        w1 = lambda k, c: w[:, k // BPW, c * P:(c + 1) * P]
        w2 = lambda k, c: w[:, k // BPW, (2 * C + c) * P:(2 * C + c + 1) * P]
        b1 = lambda k, c: w[:, k // BPW, 3 * C * P + c:3 * C * P + c + 1] if gathered else 0.0

        def slots_of(table, r, k):
            n = sizes[k] * P
            at = slice(1 + FROM[k], 1 + FROM[k] + n) if type(r) is int and r == 0 \
                else bass.ds(r * ROUND_ROWS + (1 + FROM[k]), n)
            return table[at, :].rearrange("(t p) d -> p t d", p=P)

        def load_weights(sp, r, m):
            at = slice(m * P, (m + 1) * P) if type(r) is int and r == 0 else bass.ds(r * (NW * P) + m * P, P)
            sp.dma_start(w[:, m, :], w_in[at, :]).then_inc(w_loaded[m], 16)

        @block.sync
        def _(sp):
            for k in range(U):
                if not gathered and k % BPW == 0:
                    load_weights(sp, 0, k // BPW)
                sp.dma_start(xs[:, k, 0:sizes[k], :], slots_of(core.table_x, 0, k)).then_inc(x_loaded[k], 16)

            def store(r, k):
                sp.wait_ge(y_copied, r * U + (k + 1))
                sp.dma_start(slots_of(core.table_y, r, k), y_sb[:, k, 0:sizes[k], :]).then_inc(y_stored[k], 16)

            with sp.Fori(0, rounds - 1) as r:
                for k in range(U):
                    sp.wait_ge(turned, r * U + (k + 1))
                    sp.dma_start(xs[:, k, 0:sizes[k], :], slots_of(core.table_x, r + 1, k))\
                        .then_inc(x_loaded[k], 16)
                    store(r, k)
                    if not gathered and k % BPW == BPW - 1:
                        sp.wait_ge(y_ready, r * U + (k + 1))
                        load_weights(sp, r + 1, k // BPW)
            for k in range(U):
                store(rounds - 1, k)
            for k in range(U):
                sp.wait_ge(y_stored[k], 16 * rounds + 16)

        @block.gpsimd
        def _(pool):
            if gathered:
                def gather_weights(r, k):
                    at = slice(k, k + 1) if type(r) is int else bass.ds(r * U + k, 1)
                    pool.tensor_copy(idx[:, k:k + 1], blk_row[:, at])
                    pool.drain()
                    pool.indirect_dma_start(out=w[:, k, :], out_offset=None, in_=w_in[:, :],
                                            in_offset=bass.IndirectOffsetOnAxis(ap=idx[:, k:k + 1], axis=0),
                                            bounds_check=w_in.shape[0] - 1, oob_is_err=False)\
                        .then_inc(w_loaded[k], 16)

                for k in range(U):
                    gather_weights(0, k)
                with pool.Fori(1, rounds) as r:
                    for k in range(U):
                        pool.wait_ge(y_ready, r * U + (k + 1 - U))
                        gather_weights(r, k)

        @block.tensor
        def _(pe):
            def turn(r, k, first):
                pe.wait_ge(x_loaded[k], r * 16 + 16)
                if not (first and k < 2):
                    pe.wait_ge(copied, r * U + (k - 1))
                for t in range(sizes[k]):
                    last = pe.transpose(ps_t[:, k % 2, t * P:(t + 1) * P], xs[:, k, t, :], core.ident[:, :])
                last.then_inc(turned, 1)

            def up(r, k, first):
                n = sizes[k] * P
                pe.wait_ge(copied, r * U + (k + 1))
                if k % BPW == 0:
                    pe.wait_ge(w_loaded[k // BPW], r * 16 + 16)
                for c in range(C):
                    q = (k * C + c) % 2
                    if not (first and k * C + c < 2):
                        pe.wait_ge(act_done, r * (U * C) + (k * C + c - 1))
                    pe.matmul(ps_g[:, q, 0:n], w1(k, c), xsT[:, k, 0:n], start=True, stop=True)
                    pe.matmul(ps_u[:, q, 0:n], w1(k, C + c), xsT[:, k, 0:n], start=True, stop=True)\
                        .then_inc(gu_ready, 1)

            def down(r, k, first):
                pe.wait_ge(act_done, r * (U * C) + (k + 1) * C)
                if not (first and k < 2):
                    pe.wait_ge(y_copied, r * U + (k - 1))
                for t in range(sizes[k]):
                    for c in range(C):
                        last = pe.matmul(ps_y[:, k % 2, t * P:(t + 1) * P], act_out[:, k, c, t * P:(t + 1) * P],
                                         w2(k, c), start=(c == 0), stop=(c == C - 1))
                last.then_inc(y_ready, 1)

            for k in range(U):
                turn(0, k, True)
                if k >= 1:
                    up(0, k - 1, True)
                if k >= 2:
                    down(0, k - 2, True)
            with pe.Fori(1, rounds) as r:
                for k in range(U):
                    turn(r, k, False)
                    if k >= 1:
                        up(r, k - 1, False)
                    else:
                        up(r - 1, U - 1, False)
                    if k >= 2:
                        down(r, k - 2, False)
                    else:
                        down(r - 1, U + k - 2, False)
            up(rounds - 1, U - 1, False)
            down(rounds - 1, U - 2, False)
            down(rounds - 1, U - 1, False)

        @block.scalar
        def _(act):
            def copy(r, k):
                n = sizes[k] * P
                act.wait_ge(turned, r * U + (k + 1))
                act.activation(xsT[:, k, 0:n], ps_t[:, k % 2, 0:n], ACT.Copy).then_inc(copied, 1)

            def gates(r, k, first):
                n = sizes[k] * P
                for c in range(C):
                    q = (k * C + c) % 2
                    act.wait_ge(gu_ready, r * (U * C) + (k * C + c + 1))
                    if not (first and k * C + c < 2):
                        act.wait_ge(act_done, r * (U * C) + (k * C + c - 1))
                    act.activation(gate[:, q, 0:n], ps_g[:, q, 0:n], func, bias=b1(k, c)).then_inc(gate_done, 1)

            for k in range(U):
                if gathered:
                    act.wait_ge(w_loaded[k], 16)
                copy(0, k)
                if k >= 1:
                    gates(0, k - 1, True)
            with act.Fori(1, rounds) as r:
                for k in range(U):
                    if gathered:
                        act.wait_ge(w_loaded[k], r * 16 + 16)
                    copy(r, k)
                    if k >= 1:
                        gates(r, k - 1, False)
                    else:
                        gates(r - 1, U - 1, False)
            gates(rounds - 1, U - 1, False)

        @block.vector
        def _(dve):
            def products(r, k, first):
                n = sizes[k] * P
                for c in range(C):
                    q = (k * C + c) % 2
                    dve.wait_ge(gate_done, r * (U * C) + (k * C + c + 1))
                    if c == 0 and gathered:
                        dve.wait_ge(w_loaded[k], r * 16 + 16)
                    if c == 0 and not first:
                        dve.wait_ge(y_ready, r * U + (k + 1 - U))
                    if gathered:
                        dve.scalar_tensor_tensor(out=act_out[:, k, c, 0:n], in0=ps_u[:, q, 0:n],
                                                 scalar=b1(k, C + c), in1=gate[:, q, 0:n],
                                                 op0=ALU.add, op1=ALU.mult).then_inc(act_done, 1)
                    else:
                        dve.tensor_tensor(act_out[:, k, c, 0:n], ps_u[:, q, 0:n], gate[:, q, 0:n], ALU.mult)\
                           .then_inc(act_done, 1)

            def copy_out(r, k, first):
                n = sizes[k] * P
                dve.wait_ge(y_ready, r * U + (k + 1))
                if not first:
                    dve.wait_ge(y_stored[k], r * 16 + 16)
                dve.tensor_copy(y_sb[:, k, 0:sizes[k], :].rearrange("p t d -> p (t d)"), ps_y[:, k % 2, 0:n])\
                   .then_inc(y_copied, 1)

            for k in range(U):
                dve.sem_inc(y_stored[k], 16)
            for k in range(U):
                products(0, k, True)
                if k >= 1:
                    copy_out(0, k - 1, True)
            with dve.Fori(1, rounds) as r:
                for k in range(U):
                    products(r, k, False)
                    if k >= 1:
                        copy_out(r, k - 1, False)
                    else:
                        copy_out(r - 1, U - 1, False)
            copy_out(rounds - 1, U - 1, False)


def layer2_ffn(core, A):
    with ExitStack() as ctx:
        xn = core.sb("l2f_xn", [P, TILES, D], ctx=ctx)
        wts = core.sb("l2f_wts", [P, TILES, 8], ctx=ctx)
        slots, skip = (core.sb("l2f_" + n, [P, 2, TILES], U32, ctx) for n in ("slots", "skip"))
        weights = core.sb("l2f_weights", [P, 2, TILES], ctx=ctx)
        layernorm(core, "l2f_ln", xn)
        route(core, "l2f_route", A["L2_router_w"], None, wts, 8, 2, "probs")
        keep_best(core, "l2f_keep", wts, 640, A["c_same_expert"], A["c_before_expert"], A["c_bits"], False, True)
        place_tokens(core, "l2f_place", wts, 8, 640, slots, weights, skip)
        scatter_block(core, "l2f_scatter", xn, skip)
        slot_ffn(core, "l2f", 4, [3, 2, 3, 2], 4, ACT.Silu, A["L2_w"], 12 * P)
        layernorm(core, "l3a_ln", combined=(slots, weights, 1 + 8 * 640))


def layer1_ffn(core, A):
    NB = (TABLE_ROWS - 1) // 256
    with ExitStack() as ctx:
        xn = core.sb("l1f_xn", [P, TILES, D], ctx=ctx)
        wts = core.sb("l1f_wts", [P, TILES, 13], ctx=ctx)
        slots, skip = (core.sb("l1f_" + n, [P, 2, TILES], U32, ctx) for n in ("slots", "skip"))
        weights = core.sb("l1f_weights", [P, 2, TILES], ctx=ctx)
        blk_row = core.sb("l1f_blk_row", [P, NB], U32, ctx)
        rows = core.sb("l1f_rows", [P, N], ctx=ctx)
        layernorm(core, "l1f_ln", xn)
        route(core, "l1f_route", A["L1_router_w"], A["L1_router_b"], wts, 12, 2, "topk", 1.5)
        place_tokens(core, "l1f_place", wts, 12, 256, slots, weights, skip, blk_row)
        weight_rows(core, "l1f_wr", wts, 13, rows, None)
        shared_expert(core, "l1fs", rows, A["L1_ws1"], A["L1_bs1"], A["L1_ws2"], A["L1_b2"], xn, skip)
        slot_ffn(core, "l1f", NB // 4, [2, 2, 2, 2], 3, ACT.Gelu, A["L1_w"], 9 * P + 6, blk_row)
        layernorm(core, "l2a_ln", combined=(slots, weights, TABLE_ROWS))


def layer3_ffn(core, A):
    layernorm(core, "l3f_ln")
    with ExitStack() as ctx:
        wts = core.sb("l3f_wts", [P, TILES, 8], ctx=ctx)
        rows = core.sb("l3f_rows", [P, N], ctx=ctx)
        rows_dram = core.dram("l3f_rows_dram", [8, N])
        route(core, "l3f_route", A["L3_router_w"], A["L3_router_b"], wts, 8, 4, "topk")
        weight_rows(core, "l3f_wr", wts, 8, rows, rows_dram)
        expert_ffn(core, "l3f", rows, A["L3_w1"], A["L3_w2"], A["L3_b1"], A["L3_b2"], rows_dram, 8, 2)
        add_back(core, "l3f_add", rows)


def packed(inputs):
    g = {k: np.asarray(v) for k, v in inputs.items()}
    c = np.ascontiguousarray

    def w1(w):
        e, d, f = w.shape
        return c(w.reshape(e, d, f // P, P))

    def w2(w):
        e, f, d = w.shape
        return c(w.reshape(e, f // P, P, d).transpose(0, 2, 1, 3))

    def cols(b):
        e, f = b.shape
        return c(b.reshape(e, f // P, P).transpose(0, 2, 1))

    def by_row(*parts):
        return np.concatenate([a.reshape(a.shape[0] * P, -1) for a in parts], 1)

    def gate_first(w):
        h = w.shape[-1] // 2
        return np.concatenate([w[..., h:], w[..., :h]], -1)

    t, e = np.arange(P) // 8, np.arange(P) % 8
    same_e = e[:, None] == e[None, :]
    same_b = (t[:, None] // TPB) == (t[None, :] // TPB)
    earlier = t[:, None] < t[None, :]
    bits = np.zeros((P, 32), np.int32)
    bits[:, 0:31] = [1 << b for b in range(30, -1, -1)]
    bf16 = mybir.dt.np(BF16)
    later = np.arange(P)[:, None] > np.arange(P)[None, :]
    masks = np.stack([np.where(later, -1e30, 0), np.where(later.T, -1e30, 0), np.eye(P)]).astype(bf16)
    half = HD // 2
    inv_freq = np.float32(1.0) / np.float32(10000.0) ** (np.arange(half, dtype=np.float32) / np.float32(half))
    angle = np.arange(SEQ, dtype=np.float32)[:, None] * inv_freq[None, :]
    by_tile = lambda a: c(a.reshape(TPB, P, half).transpose(1, 0, 2))

    def parts(a):
        hi = a.astype(bf16)
        mid = (a - hi.astype(np.float64)).astype(bf16)
        return np.stack([hi, mid, (a - hi.astype(np.float64) - mid.astype(np.float64)).astype(bf16)], -1)

    slope = np.float32(2.0) ** (-np.arange(1, HEADS + 1, dtype=np.float32) / 2)
    pos = np.arange(SEQ, dtype=np.float64)
    steep = slope.astype(np.float64) * np.sqrt(np.float64(HD))
    q_tail = np.zeros((SEQ, HEADS, 16), bf16)
    q_tail[:, :, 0:3] = q_tail[:, :, 3:6] = parts(steep)[None]
    q_tail[:, :, 6:9] = parts(-pos[:, None] * steep[None, :])
    k_tail = np.zeros((SEQ, HEADS, 16), bf16)
    k_tail[:, :, 0:3] = (pos - pos % 2)[:, None, None]
    k_tail[:, :, 3:6] = (pos % 2)[:, None, None]
    k_tail[:, :, 6:12] = 1
    tail = lambda a: c(a.reshape(TPB, P, HEADS, 16).transpose(1, 0, 2, 3).reshape(P, TPB * HEADS, 16))
    col, row = np.arange(SEQ) % CHUNK, (np.arange(P) % CHUNK)[:, None]
    chunk_c = np.stack([np.broadcast_to(a, (P, SEQ)) for a in (col != 0, col == 0, row == col, row < col)], 1)
    chunk_c = c(chunk_c.astype(np.float32))
    quadrant = np.arange(P) // RD
    by_quadrant = c((quadrant[:, None] == np.arange(RHEADS)[None, :]).astype(np.float32))
    pick_ab = np.zeros((8, 2, P), np.float32)
    pick_ab[0:4, 0] = 0.98 * by_quadrant.T
    pick_ab[4:8, 1] = by_quadrant.T

    def pick(n):
        a = np.zeros((n, RHEADS, n, P), np.float32)
        for i in range(n):
            a[i, :, i] = by_quadrant.T
        return a.reshape(n * RHEADS, n, P)

    return {
        "c_masks": masks, "c_cos": by_tile(np.cos(angle)), "c_sin": by_tile(np.sin(angle)),
        "c_q_tail": tail(q_tail), "c_k_tail": tail(k_tail),
        "c_chunk": chunk_c, "c_ones4": by_quadrant, "c_pick_ab": pick_ab, "c_pick_r": pick(8), "c_pick_o": pick(4),
        "L2_w_in": c(g["L2_attn_W_in"].reshape(D, 3, D)),
        "L2_taps": c(np.stack([g["L2_attn_w_q"], g["L2_attn_w_k"], g["L2_attn_w_v"]])[:, :, 0, ::-1]
                     .transpose(0, 2, 1).reshape(1, 12 * D)),
        "L2_w_ctrl": g["L2_attn_W_ctrl"], "L2_b8": c(g["L2_attn_b_ctrl"][:8].reshape(8, 1)),
        "L2_bog": c(g["L2_attn_b_ctrl"][8:].reshape(D, 1)), "L2_w_out": g["L2_attn_W_out"],
        "L2_b_out": g["L2_attn_b_out"].reshape(D, 1), "L2_ramp": g["L2_attn_ramp_logit"].reshape(D, 1),
        "c_regeye": (np.eye(LAND) * REG).astype(np.float32),
        "L0_wqkv": c(np.concatenate([g["L0_attn_Wq"].T, g["L0_attn_Wk"].T, g["L0_attn_Wv"].T], 1)),
        "L0_bqkv": np.concatenate([g["L0_attn_bq"], g["L0_attn_bk"], g["L0_attn_bv"]]).reshape(1, 3 * D),
        "L0_temp": g["L0_attn_temperature"].reshape(1, 1), "L0_idx": g["L0_attn_landmark_idx"].reshape(1, LAND),
        "L0_wo": c(g["L0_attn_Wo"].T), "L0_bo": g["L0_attn_bo"].reshape(1, D),
        "L1_wqkv": g["L1_attn_w_qkv"], "L1_wo": g["L1_attn_w_o"],
        "L3_wqkv": g["L3_attn_Wqkv"], "L3_wo": g["L3_attn_Wout"],
        "x_in": c(g["L0_attn_query"].reshape(N, D)),
        "c_bits": bits,
        "c_same_expert": same_e.astype(np.float32),
        "c_before_expert": (same_e & earlier).astype(np.float32),
        "c_same_batch": (same_e & same_b).astype(np.float32),
        "c_before_batch": (same_e & same_b & earlier).astype(np.float32),
        "L0_router_w": g["L0_ffn_w_gate_w"], "L0_router_b": g["L0_ffn_w_gate_b"].reshape(-1, 1),
        "L0_w1": c(g["L0_ffn_W1"].transpose(1, 0, 2).reshape(D, 2, P)), "L0_b1": c(g["L0_ffn_b1"].reshape(2, P).T),
        "L0_w2": c(g["L0_ffn_W2"].reshape(2, P, D).transpose(1, 0, 2)), "L0_b2": g["L0_ffn_b2"],
        "L1_router_w": g["L1_ffn_Wr"], "L1_router_b": g["L1_ffn_br"].reshape(-1, 1),
        "L1_ws1": w1(gate_first(g["L1_ffn_Ws1"][None])), "L1_ws2": w2(g["L1_ffn_Ws2"][None]),
        "L1_bs1": cols(gate_first(g["L1_ffn_bs1"][None])),
        "L1_w": by_row(w1(gate_first(g["L1_ffn_We1"])), w2(g["L1_ffn_We2"]), cols(gate_first(g["L1_ffn_be1"]))),
        "L1_b2": np.concatenate([g["L1_ffn_be2"], g["L1_ffn_bs2"].reshape(1, D)]),
        "L2_router_w": c(g["L2_ffn_router_w"].T),
        "L2_w": by_row(w1(np.concatenate([g["L2_ffn_wg"], g["L2_ffn_wu"]], 2)), w2(g["L2_ffn_wd"])),
        "L3_router_w": c(g["L3_ffn_router_weight"].T), "L3_router_b": g["L3_ffn_router_bias"].reshape(-1, 1),
        "L3_w1": w1(g["L3_ffn_gate_up_proj"].transpose(0, 2, 1)), "L3_w2": w2(g["L3_ffn_down_proj"].transpose(0, 2, 1)),
        "L3_b1": cols(g["L3_ffn_gate_up_proj_bias"]), "L3_b2": c(g["L3_ffn_down_proj_bias"][:, :, None]),
    }


def forward(nc, A, x_out):
    with ExitStack() as ctx:
        core = Core(nc, ctx)
        start(core, A["x_in"])
        for layer in (layer0_attention, layer0_ffn, layer1_attention, layer1_ffn,
                      layer2_attention, layer2_ffn, layer3_attention, layer3_ffn):
            layer(core, A)
            core.free_sems()
        store(core, x_out)


def kernel(**inputs):
    import concourse.bacc as _bacc
    from concourse.bass_utils import run_bass_kernel_spmd as _run

    arrays = packed(inputs)
    nc = _bacc.Bacc("TRN2", target_bir_lowering=False, num_devices=1)
    A = {k: nc.dram_tensor(k, a.shape, mybir.dt.from_np(a.dtype), kind="ExternalInput").ap()
         for k, a in arrays.items()}
    x_out = nc.dram_tensor("x_out", [N, D], F32, kind="ExternalOutput").ap()
    forward(nc, A, x_out)
    r = _run(nc, [arrays], core_ids=[0])
    return r.results[0]["x_out"].reshape(BATCH, SEQ, D)
```
